# Optimizing a Trainium2 kernel written in Bass

```python
import numpy as np
import jax
import jax.numpy as jnp

def _softmax(x, axis=-1):
    return jax.nn.softmax(x, axis=axis)

def _gelu(x):
    return jax.nn.gelu(x, approximate=True)

def _silu(x):
    return jax.nn.silu(x)

def _sigmoid(x):
    return jax.nn.sigmoid(x)

def _layernorm(x, axis=-1, eps=1e-05):
    m = jnp.mean(x, axis=axis, keepdims=True)
    v = jnp.var(x, axis=axis, keepdims=True)
    return (x - m) / jnp.sqrt(v + eps)

def _scatter_add(tgt, idx, src, axis=0):
    return tgt.at[idx].add(src)

def _segment_sum(src, seg, n):
    return jax.ops.segment_sum(src, seg, n)
kernel_name = 'mk_decoder_preln_d4_seqx_r8_8dcc5b'

def setup_inputs(seed: int=0):
    np.random.seed(seed)
    _w = jnp.asarray

    def _rec_inputs():
        import jax
        import jax.numpy as jnp
        _rk = jax.random.key(seed)
        x = 0.0002417 + 0.9998 * jax.random.normal(jax.random.fold_in(_rk, 1), (4, 512, 128), jnp.float32)
        _lenS = 512 - jax.random.randint(jax.random.fold_in(_rk, 7), (4,), 0, max(1, 512 // 4) + 1, jnp.int32)
        _lenS2 = 77 - jax.random.randint(jax.random.fold_in(_rk, 8), (4,), 0, max(1, 77 // 4) + 1, jnp.int32)
        _ctx_1024P = jax.random.normal(jax.random.fold_in(_rk, 11), (4, 16, 128), jnp.float32)
        _ctx_1024c = jax.random.dirichlet(jax.random.fold_in(_rk, 511), 0.3 * jnp.ones((16,), jnp.float32), (4, 77))
        _ctx_1024t = jnp.einsum('bsk,bkd->bsd', _ctx_1024c, _ctx_1024P)
        _ctx_1024t = _ctx_1024t * jax.lax.rsqrt(jnp.mean(jnp.square(_ctx_1024t)) + 1e-12) * 0.953939
        ctx_1024 = 7.22013e-05 + 1.00017 * (_ctx_1024t + 0.3 * jax.random.normal(jax.random.fold_in(_rk, 611), (4, 77, 128), jnp.float32))
        _validS = jnp.arange(512)[None, :] < _lenS[:, None]
        _validS2 = jnp.arange(77)[None, :] < _lenS2[:, None]
        _causal = jnp.tril(jnp.ones((512, 512), dtype=bool))
        mask_BxS2_bk0 = jnp.logical_not(jnp.broadcast_to(_validS2[:, :], (4, 77)))
        return (x, ctx_1024, mask_BxS2_bk0)
    x, ctx_1024, mask_BxS2_bk0 = _rec_inputs()

    def _L0_attn_setup():
        import jax, jax.numpy as jnp
        import numpy as np
        import math
        B, T, C = (2, 256, 128)
        H = 16
        D = C // H

        def alibi_slopes(n_heads):
            start = 2.0 ** (-2.0 ** (-(math.log2(n_heads) - 3)))
            return jnp.asarray([start * start ** i for i in range(n_heads)], dtype=jnp.float32)
        key = jax.random.key(seed)
        ks = jax.random.split(key, 6)
        x = jax.random.normal(ks[0], (B, T, C), dtype=jnp.float32)
        W_attn = jax.random.normal(ks[1], (C, 3 * C), dtype=jnp.float32) * 0.02
        b_attn = jnp.zeros((3 * C,), dtype=jnp.float32)
        W_proj = jax.random.normal(ks[2], (C, C), dtype=jnp.float32) * 0.02
        b_proj = jnp.zeros((C,), dtype=jnp.float32)
        temperature = jnp.ones((1,), dtype=jnp.float32) * 2.0
        return {'x': x, 'W_attn': W_attn, 'b_attn': b_attn, 'W_proj': W_proj, 'b_proj': b_proj, 'temperature': temperature}
    _L0_attn_all = _L0_attn_setup()
    _L0_attn_in = {k: v for k, v in _L0_attn_all.items() if k in ('W_attn', 'b_attn', 'W_proj', 'b_proj', 'temperature')}
    del _L0_attn_all

    def _L0_xattn_setup():
        import jax, jax.numpy as jnp
        import numpy as np
        D_MODEL = 128
        B, S = (4, 256)
        key = jax.random.key(seed)
        ks = jax.random.split(key, 10)
        s = 1.0 / np.sqrt(D_MODEL)
        return {'k': jax.random.normal(ks[0], (B, S, D_MODEL), jnp.float32), 'v': jax.random.normal(ks[1], (B, S, D_MODEL), jnp.float32), 'q': jax.random.normal(ks[2], (B, S, D_MODEL), jnp.float32), 'Wk': jax.random.normal(ks[3], (D_MODEL, D_MODEL), jnp.float32) * s, 'Wv': jax.random.normal(ks[4], (D_MODEL, D_MODEL), jnp.float32) * s, 'bv': jnp.zeros((D_MODEL,), jnp.float32), 'Wq': jax.random.normal(ks[5], (D_MODEL, D_MODEL), jnp.float32) * s, 'bq': jnp.zeros((D_MODEL,), jnp.float32), 'Wo': jax.random.normal(ks[6], (D_MODEL, D_MODEL), jnp.float32) * s, 'bo': jnp.zeros((D_MODEL,), jnp.float32)}
    _L0_xattn_all = _L0_xattn_setup()
    _L0_xattn_in = {k: v for k, v in _L0_xattn_all.items() if k in ('Wk', 'Wv', 'bv', 'Wq', 'bq', 'Wo', 'bo')}
    del _L0_xattn_all

    def _L0_ffn_setup():
        import jax, jax.numpy as jnp
        import numpy as np
        E = 16
        K = 4
        NG = 4
        TG = 2
        SCALE = 2.5
        NORM_TOPK = True
        H = 128
        I = 64
        SH_I = I * 2
        B, S = (2, 256)
        key = jax.random.key(seed)
        ks = jax.random.split(key, 9)

        def w(k, shape, fan_in):
            return jax.random.normal(k, shape, jnp.float32) * (1.0 / np.sqrt(fan_in))
        return {'hidden_states': jax.random.normal(ks[0], (B, S, H), jnp.float32), 'gate_w': w(ks[1], (E, H), H), 'gate_bias': jnp.zeros((E,), jnp.float32), 'Wg': w(ks[2], (E, I, H), H), 'Wu': w(ks[3], (E, I, H), H), 'Wd': w(ks[4], (E, H, I), I), 'Ws_g': w(ks[5], (SH_I, H), H), 'Ws_u': w(ks[6], (SH_I, H), H), 'Ws_d': w(ks[7], (H, SH_I), SH_I)}
    _L0_ffn_all = _L0_ffn_setup()
    _L0_ffn_in = {k: v for k, v in _L0_ffn_all.items() if k in ('gate_w', 'gate_bias', 'Wg', 'Wu', 'Wd', 'Ws_g', 'Ws_u', 'Ws_d')}
    del _L0_ffn_all

    def _L1_attn_setup():
        import jax, jax.numpy as jnp
        import numpy as np
        NUM_HEADS = 16
        EPS = 1e-06

        def _split_heads(t, h):
            b, s, d = t.shape
            return t.reshape(b, s, h, d // h).transpose(0, 2, 1, 3)
        key = jax.random.key(seed)
        ks = jax.random.split(key, 6)
        b, s, d = (4, 512, 128)
        scale = 1.0 / np.sqrt(d)
        return {'x': jax.random.normal(ks[0], (b, s, d), dtype=jnp.float32), 'wq': jax.random.normal(ks[1], (d, d), dtype=jnp.float32) * scale, 'wk': jax.random.normal(ks[2], (d, d), dtype=jnp.float32) * scale, 'wv': jax.random.normal(ks[3], (d, d), dtype=jnp.float32) * scale, 'wo': jax.random.normal(ks[4], (d, d), dtype=jnp.float32) * scale, 'bo': jnp.zeros((d,), dtype=jnp.float32)}
    _L1_attn_all = _L1_attn_setup()
    _L1_attn_in = {k: v for k, v in _L1_attn_all.items() if k in ('wq', 'wk', 'wv', 'wo', 'bo')}
    del _L1_attn_all

    def _L1_xattn_setup():
        import jax, jax.numpy as jnp
        import numpy as np
        B, L_ENC, L_DEC, D = (16, 64, 128, 128)
        key = jax.random.key(seed)
        k1, k2, k3, k4, k5, k6 = jax.random.split(key, 6)
        encoder_hc = jax.random.normal(k1, (B, L_ENC, D), dtype=jnp.float32)
        decoder_hq = jax.random.normal(k2, (B, L_DEC, D), dtype=jnp.float32)
        w_sim = jax.random.normal(k3, (3 * D,), dtype=jnp.float32) * 0.02
        b_sim = jax.random.normal(k4, (1,), dtype=jnp.float32) * 0.02
        W_qv = jax.random.normal(k5, (4 * D, D), dtype=jnp.float32) * 0.02
        b_qv = jax.random.normal(k6, (D,), dtype=jnp.float32) * 0.02
        return {'encoder_hc': encoder_hc, 'decoder_hq': decoder_hq, 'w_sim': w_sim, 'b_sim': b_sim, 'W_qv': W_qv, 'b_qv': b_qv}
    _L1_xattn_all = _L1_xattn_setup()
    _L1_xattn_in = {k: v for k, v in _L1_xattn_all.items() if k in ('w_sim', 'b_sim', 'W_qv', 'b_qv')}
    del _L1_xattn_all

    def _L1_ffn_setup():
        import jax, jax.numpy as jnp
        import numpy as np
        B, T, C = (1, 512, 128)
        E, K = (64, 8)
        G, TG = (8, 4)
        H, HS = (64, 256)
        STD = 0.02

        def _route(xf, router_w, e_bias):
            S = xf.shape[0]
            scores = jax.nn.sigmoid(xf @ router_w.T)
            sb = scores + e_bias
            epg = E // G
            grp = jax.lax.top_k(sb.reshape(S, G, epg), K // TG)[0].sum(-1)
            gidx = jax.lax.top_k(grp, TG)[1]
            gmask = jnp.zeros((S, G), bool).at[jnp.arange(S)[:, None], gidx].set(True)
            emask = jnp.repeat(gmask, epg, axis=1)
            masked = jnp.where(emask, sb, -jnp.inf)
            topk_idx = jax.lax.top_k(masked, K)[1]
            w = jnp.take_along_axis(scores, topk_idx, axis=1)
            w = w / (w.sum(-1, keepdims=True) + 1e-20)
            return (topk_idx, w)
        key = jax.random.key(seed)
        ks = jax.random.split(key, 9)
        return {'x': jax.random.normal(ks[0], (B, T, C), jnp.float32), 'router_w': jax.random.normal(ks[1], (E, C), jnp.float32) * C ** (-0.5), 'e_bias': jnp.zeros((E,), jnp.float32), 'gate_w': jax.random.normal(ks[2], (E, C, H), jnp.float32) * STD, 'up_w': jax.random.normal(ks[3], (E, C, H), jnp.float32) * STD, 'down_w': jax.random.normal(ks[4], (E, H, C), jnp.float32) * STD, 'sh_gate_w': jax.random.normal(ks[5], (C, HS), jnp.float32) * STD, 'sh_up_w': jax.random.normal(ks[6], (C, HS), jnp.float32) * STD, 'sh_down_w': jax.random.normal(ks[7], (HS, C), jnp.float32) * STD}
    _L1_ffn_all = _L1_ffn_setup()
    _L1_ffn_in = {k: v for k, v in _L1_ffn_all.items() if k in ('router_w', 'e_bias', 'gate_w', 'up_w', 'down_w', 'sh_gate_w', 'sh_up_w', 'sh_down_w')}
    del _L1_ffn_all

    def _L2_attn_setup():
        import jax, jax.numpy as jnp
        import numpy as np
        KEY_DIM = 128
        EMBED_DIM = 128
        key = jax.random.key(seed)
        kx, kw = jax.random.split(key)
        x = jax.random.normal(kx, (4, 256, EMBED_DIM), dtype=jnp.float32)
        W = jax.random.normal(kw, (EMBED_DIM, 3 * KEY_DIM), dtype=jnp.float32)
        return {'x': x, 'W': W}
    _L2_attn_all = _L2_attn_setup()
    _L2_attn_in = {k: v for k, v in _L2_attn_all.items() if k in ('W',)}
    del _L2_attn_all

    def _L2_xattn_setup():
        import jax, jax.numpy as jnp
        import numpy as np
        NUM_HEADS, NUM_KV, HEAD_DIM, WIDTH = (4, 1, 32, 128)
        MASK_FILL = -2.3819763e+38

        def _apply_rope(x, positions, max_wavelength=10000.0):
            d = x.shape[-1]
            freq_exp = 2.0 / d * jnp.arange(d // 2, dtype=jnp.float32)
            timescale = max_wavelength ** freq_exp
            radians = positions[..., None].astype(jnp.float32) / timescale
            radians = radians[..., None, :]
            sin, cos = (jnp.sin(radians), jnp.cos(radians))
            x1, x2 = jnp.split(x, 2, axis=-1)
            out = jnp.concatenate([x1 * cos - x2 * sin, x2 * cos + x1 * sin], axis=-1)
            return out.astype(x.dtype)

        def _rmsnorm(x, scale):
            var = jnp.mean(jnp.square(x.astype(jnp.float32)), axis=-1, keepdims=True)
            normed = x * jax.lax.rsqrt(var + 1e-06)
            return (normed * (1 + scale)).astype(x.dtype)
        key = jax.random.key(seed)
        ks = jax.random.split(key, 7)
        B, T, S = (8, 64, 256)
        return {'x': jax.random.normal(ks[0], (B, T, WIDTH), jnp.float32), 'mem_seq': jax.random.normal(ks[1], (B, S, WIDTH), jnp.float32), 'mem_mask': jax.random.randint(ks[2], (B, S), 0, 2).astype(bool), 'rms_scale': jax.random.normal(ks[3], (WIDTH,), jnp.float32) * 0.02, 'q_w': jax.random.normal(ks[4], (NUM_HEADS, WIDTH, HEAD_DIM), jnp.float32) / np.sqrt(WIDTH), 'kv_w': jax.random.normal(ks[5], (2, NUM_KV, WIDTH, HEAD_DIM), jnp.float32) / np.sqrt(WIDTH), 'out_w': jax.random.normal(ks[6], (NUM_HEADS, HEAD_DIM, WIDTH), jnp.float32) / np.sqrt(NUM_HEADS * HEAD_DIM)}
    _L2_xattn_all = _L2_xattn_setup()
    _L2_xattn_in = {k: v for k, v in _L2_xattn_all.items() if k in ('rms_scale', 'q_w', 'kv_w', 'out_w')}
    del _L2_xattn_all

    def _L2_ffn_setup():
        import jax, jax.numpy as jnp
        import numpy as np
        D, H, P, E, K, F = (128, 16, 64, 8, 2, 512)
        B, S = (2, 256)
        NROT = 32
        BASE = 10000.0
        EPS = 1e-05

        def _ln(x, g, b):
            m = jnp.mean(x, -1, keepdims=True)
            v = jnp.mean(jnp.square(x - m), -1, keepdims=True)
            return (x - m) * jax.lax.rsqrt(v + EPS) * g + b

        def _rope(x):
            xr, xp = (x[..., :NROT], x[..., NROT:])
            half = NROT // 2
            inv = BASE ** (-jnp.arange(half, dtype=jnp.float32) / half)
            ang = jnp.arange(x.shape[2], dtype=jnp.float32)[:, None] * inv[None, :]
            cos, sin = (jnp.cos(ang), jnp.sin(ang))
            x1, x2 = (xr[..., :half], xr[..., half:])
            xr = jnp.concatenate([x1 * cos - x2 * sin, x1 * sin + x2 * cos], -1)
            return jnp.concatenate([xr, xp], -1)

        def _gate(x, Wsel):
            s = jax.nn.sigmoid(jnp.einsum('bsd,hed->bhse', x, Wsel))
            _, idx = jax.lax.top_k(s, K)
            mask = jax.nn.one_hot(idx, E, dtype=s.dtype).sum(-2)
            return s * mask

        def _moe_attn(x, Wq, Wk, Wv, Wo, Wsel_v, Wsel_o):
            q = _rope(jnp.einsum('bsd,hdp->bhsp', x, Wq))
            k = _rope(jnp.einsum('bsd,hdp->bhsp', x, Wk))
            gv = _gate(x, Wsel_v)
            v = jnp.einsum('bsd,bhse,hedp->bhsp', x, gv, Wv)
            att = jax.nn.softmax(jnp.einsum('bhsp,bhtp->bhst', q, k) / np.sqrt(P), axis=-1)
            o = jnp.einsum('bhst,bhtp->bhsp', att, v)
            go = _gate(x, Wsel_o)
            return jnp.einsum('bhsp,bhse,hepd->bsd', o, go, Wo)
        key = jax.random.key(seed)
        ks = jax.random.split(key, 10)
        f = lambda k, sh: jax.random.normal(k, sh, jnp.float32) * 0.02
        return dict(src=jax.random.normal(ks[0], (B, S, D), jnp.float32), Wq=f(ks[1], (H, D, P)), Wk=f(ks[2], (H, D, P)), Wv=f(ks[3], (H, E, D, P)), Wo=f(ks[4], (H, E, P, D)), Wsel_v=f(ks[5], (H, E, D)), Wsel_o=f(ks[6], (H, E, D)), ln1_g=jnp.ones(D, jnp.float32), ln1_b=jnp.zeros(D, jnp.float32), ln2_g=jnp.ones(D, jnp.float32), ln2_b=jnp.zeros(D, jnp.float32), W1=f(ks[7], (D, F)), b1=jnp.zeros(F, jnp.float32), W2=f(ks[8], (F, D)), b2=jnp.zeros(D, jnp.float32))
    _L2_ffn_all = _L2_ffn_setup()
    _L2_ffn_in = {k: v for k, v in _L2_ffn_all.items() if k in ('Wq', 'Wk', 'Wv', 'Wo', 'Wsel_v', 'Wsel_o', 'ln1_g', 'ln1_b', 'ln2_g', 'ln2_b', 'W1', 'b1', 'W2', 'b2')}
    del _L2_ffn_all

    def _L3_attn_setup():
        import jax, jax.numpy as jnp
        import numpy as np
        B, S, H, D = (4, 256, 128, 128)
        key = jax.random.key(seed)
        k0, k1, k2, k3 = jax.random.split(key, 4)
        x = jax.random.normal(k0, (B, S, H), dtype=jnp.float32)
        scale = 1.0 / np.sqrt(H)
        Wq = jax.random.normal(k1, (D, H), dtype=jnp.float32) * scale
        Wk = jax.random.normal(k2, (D, H), dtype=jnp.float32) * scale
        Wv = jax.random.normal(k3, (D, H), dtype=jnp.float32) * scale
        return {'x': x, 'Wq': Wq, 'Wk': Wk, 'Wv': Wv}
    _L3_attn_all = _L3_attn_setup()
    _L3_attn_in = {k: v for k, v in _L3_attn_all.items() if k in ('Wq', 'Wk', 'Wv')}
    del _L3_attn_all

    def _L3_xattn_setup():
        import jax, jax.numpy as jnp
        import numpy as np
        HIDDEN = 128
        HEADS = 16
        HEAD_DIM = 64
        key = jax.random.key(seed)
        ks = jax.random.split(key, 7)
        B, Q, K = (2, 256, 512)
        s = 1.0 / np.sqrt(HIDDEN)
        return {'query': jax.random.normal(ks[0], (B, Q, HIDDEN), dtype=jnp.float32), 'key': jax.random.normal(ks[1], (B, K, HIDDEN), dtype=jnp.float32), 'value': jax.random.normal(ks[2], (B, K, HIDDEN), dtype=jnp.float32), 'w_q': jax.random.normal(ks[3], (HIDDEN, HEADS * HEAD_DIM), dtype=jnp.float32) * s, 'w_k': jax.random.normal(ks[4], (HIDDEN, HEADS * HEAD_DIM), dtype=jnp.float32) * s, 'w_v': jax.random.normal(ks[5], (HIDDEN, HEADS * HEAD_DIM), dtype=jnp.float32) * s, 'w_o': jax.random.normal(ks[6], (HEADS * HEAD_DIM, HIDDEN), dtype=jnp.float32) * s}
    _L3_xattn_all = _L3_xattn_setup()
    _L3_xattn_in = {k: v for k, v in _L3_xattn_all.items() if k in ('w_q', 'w_k', 'w_v', 'w_o')}
    del _L3_xattn_all

    def _L3_ffn_setup():
        import jax, jax.numpy as jnp
        import numpy as np
        D = 128
        I = 64
        E = 32
        K = 4
        T = 2 * 256
        C = 2 * T * K // E
        key = jax.random.key(seed)
        ks = jax.random.split(key, 9)
        bf = jnp.bfloat16
        std = 0.02
        x = jax.random.normal(ks[0], (2, 256, D), dtype=jnp.float32).astype(bf)
        gate_w = (std * jax.random.normal(ks[1], (E, D), dtype=jnp.float32)).astype(bf)
        bias = jnp.zeros((E,), jnp.float32)
        W1 = (std * jax.random.normal(ks[2], (E, D, I), dtype=jnp.float32)).astype(bf)
        W3 = (std * jax.random.normal(ks[3], (E, D, I), dtype=jnp.float32)).astype(bf)
        W2 = (std * jax.random.normal(ks[4], (E, I, D), dtype=jnp.float32)).astype(bf)
        sw1 = (std * jax.random.normal(ks[5], (I, D), dtype=jnp.float32)).astype(bf)
        sw3 = (std * jax.random.normal(ks[6], (I, D), dtype=jnp.float32)).astype(bf)
        sw2 = (std * jax.random.normal(ks[7], (D, I), dtype=jnp.float32)).astype(bf)
        return {'x': x, 'gate_w': gate_w, 'bias': bias, 'W1': W1, 'W3': W3, 'W2': W2, 'sw1': sw1, 'sw3': sw3, 'sw2': sw2}
    _L3_ffn_all = _L3_ffn_setup()
    _L3_ffn_in = {k: v for k, v in _L3_ffn_all.items() if k in ('gate_w', 'bias', 'W1', 'W3', 'W2', 'sw1', 'sw3', 'sw2')}
    del _L3_ffn_all
    return {'x': x, 'ctx_1024': ctx_1024, 'mask_BxS2_bk0': mask_BxS2_bk0, 'L0_attn_W_attn': _L0_attn_in['W_attn'], 'L0_attn_b_attn': _L0_attn_in['b_attn'], 'L0_attn_W_proj': _L0_attn_in['W_proj'], 'L0_attn_b_proj': _L0_attn_in['b_proj'], 'L0_attn_temperature': _L0_attn_in['temperature'], 'L0_xattn_Wk': _L0_xattn_in['Wk'], 'L0_xattn_Wv': _L0_xattn_in['Wv'], 'L0_xattn_bv': _L0_xattn_in['bv'], 'L0_xattn_Wq': _L0_xattn_in['Wq'], 'L0_xattn_bq': _L0_xattn_in['bq'], 'L0_xattn_Wo': _L0_xattn_in['Wo'], 'L0_xattn_bo': _L0_xattn_in['bo'], 'L0_ffn_gate_w': _L0_ffn_in['gate_w'], 'L0_ffn_gate_bias': _L0_ffn_in['gate_bias'], 'L0_ffn_Wg': _L0_ffn_in['Wg'], 'L0_ffn_Wu': _L0_ffn_in['Wu'], 'L0_ffn_Wd': _L0_ffn_in['Wd'], 'L0_ffn_Ws_g': _L0_ffn_in['Ws_g'], 'L0_ffn_Ws_u': _L0_ffn_in['Ws_u'], 'L0_ffn_Ws_d': _L0_ffn_in['Ws_d'], 'L1_attn_wq': _L1_attn_in['wq'], 'L1_attn_wk': _L1_attn_in['wk'], 'L1_attn_wv': _L1_attn_in['wv'], 'L1_attn_wo': _L1_attn_in['wo'], 'L1_attn_bo': _L1_attn_in['bo'], 'L1_xattn_w_sim': _L1_xattn_in['w_sim'], 'L1_xattn_b_sim': _L1_xattn_in['b_sim'], 'L1_xattn_W_qv': _L1_xattn_in['W_qv'], 'L1_xattn_b_qv': _L1_xattn_in['b_qv'], 'L1_ffn_router_w': _L1_ffn_in['router_w'], 'L1_ffn_e_bias': _L1_ffn_in['e_bias'], 'L1_ffn_gate_w': _L1_ffn_in['gate_w'], 'L1_ffn_up_w': _L1_ffn_in['up_w'], 'L1_ffn_down_w': _L1_ffn_in['down_w'], 'L1_ffn_sh_gate_w': _L1_ffn_in['sh_gate_w'], 'L1_ffn_sh_up_w': _L1_ffn_in['sh_up_w'], 'L1_ffn_sh_down_w': _L1_ffn_in['sh_down_w'], 'L2_attn_W': _L2_attn_in['W'], 'L2_xattn_rms_scale': _L2_xattn_in['rms_scale'], 'L2_xattn_q_w': _L2_xattn_in['q_w'], 'L2_xattn_kv_w': _L2_xattn_in['kv_w'], 'L2_xattn_out_w': _L2_xattn_in['out_w'], 'L2_ffn_Wq': _L2_ffn_in['Wq'], 'L2_ffn_Wk': _L2_ffn_in['Wk'], 'L2_ffn_Wv': _L2_ffn_in['Wv'], 'L2_ffn_Wo': _L2_ffn_in['Wo'], 'L2_ffn_Wsel_v': _L2_ffn_in['Wsel_v'], 'L2_ffn_Wsel_o': _L2_ffn_in['Wsel_o'], 'L2_ffn_ln1_g': _L2_ffn_in['ln1_g'], 'L2_ffn_ln1_b': _L2_ffn_in['ln1_b'], 'L2_ffn_ln2_g': _L2_ffn_in['ln2_g'], 'L2_ffn_ln2_b': _L2_ffn_in['ln2_b'], 'L2_ffn_W1': _L2_ffn_in['W1'], 'L2_ffn_b1': _L2_ffn_in['b1'], 'L2_ffn_W2': _L2_ffn_in['W2'], 'L2_ffn_b2': _L2_ffn_in['b2'], 'L3_attn_Wq': _L3_attn_in['Wq'], 'L3_attn_Wk': _L3_attn_in['Wk'], 'L3_attn_Wv': _L3_attn_in['Wv'], 'L3_xattn_w_q': _L3_xattn_in['w_q'], 'L3_xattn_w_k': _L3_xattn_in['w_k'], 'L3_xattn_w_v': _L3_xattn_in['w_v'], 'L3_xattn_w_o': _L3_xattn_in['w_o'], 'L3_ffn_gate_w': _L3_ffn_in['gate_w'], 'L3_ffn_bias': _L3_ffn_in['bias'], 'L3_ffn_W1': _L3_ffn_in['W1'], 'L3_ffn_W3': _L3_ffn_in['W3'], 'L3_ffn_W2': _L3_ffn_in['W2'], 'L3_ffn_sw1': _L3_ffn_in['sw1'], 'L3_ffn_sw3': _L3_ffn_in['sw3'], 'L3_ffn_sw2': _L3_ffn_in['sw2']}

def reference(x, ctx_1024, mask_BxS2_bk0, L0_attn_W_attn, L0_attn_b_attn, L0_attn_W_proj, L0_attn_b_proj, L0_attn_temperature, L0_xattn_Wk, L0_xattn_Wv, L0_xattn_bv, L0_xattn_Wq, L0_xattn_bq, L0_xattn_Wo, L0_xattn_bo, L0_ffn_gate_w, L0_ffn_gate_bias, L0_ffn_Wg, L0_ffn_Wu, L0_ffn_Wd, L0_ffn_Ws_g, L0_ffn_Ws_u, L0_ffn_Ws_d, L1_attn_wq, L1_attn_wk, L1_attn_wv, L1_attn_wo, L1_attn_bo, L1_xattn_w_sim, L1_xattn_b_sim, L1_xattn_W_qv, L1_xattn_b_qv, L1_ffn_router_w, L1_ffn_e_bias, L1_ffn_gate_w, L1_ffn_up_w, L1_ffn_down_w, L1_ffn_sh_gate_w, L1_ffn_sh_up_w, L1_ffn_sh_down_w, L2_attn_W, L2_xattn_rms_scale, L2_xattn_q_w, L2_xattn_kv_w, L2_xattn_out_w, L2_ffn_Wq, L2_ffn_Wk, L2_ffn_Wv, L2_ffn_Wo, L2_ffn_Wsel_v, L2_ffn_Wsel_o, L2_ffn_ln1_g, L2_ffn_ln1_b, L2_ffn_ln2_g, L2_ffn_ln2_b, L2_ffn_W1, L2_ffn_b1, L2_ffn_W2, L2_ffn_b2, L3_attn_Wq, L3_attn_Wk, L3_attn_Wv, L3_xattn_w_q, L3_xattn_w_k, L3_xattn_w_v, L3_xattn_w_o, L3_ffn_gate_w, L3_ffn_bias, L3_ffn_W1, L3_ffn_W3, L3_ffn_W2, L3_ffn_sw1, L3_ffn_sw3, L3_ffn_sw2):
    import jax
    import jax.numpy as jnp

    def _L0_attn_ref(x, W_attn, b_attn, W_proj, b_proj, temperature):
        import jax, jax.numpy as jnp
        import numpy as np
        import math
        B, T, C = (2, 256, 128)
        H = 16
        D = C // H

        def alibi_slopes(n_heads):
            start = 2.0 ** (-2.0 ** (-(math.log2(n_heads) - 3)))
            return jnp.asarray([start * start ** i for i in range(n_heads)], dtype=jnp.float32)
        Bc, Tc, Cc = x.shape
        qkv = x @ W_attn + b_attn
        q, k, v = jnp.split(qkv, 3, axis=-1)
        q = q.reshape(Bc, Tc, H, D)
        k = k.reshape(Bc, Tc, H, D)
        v = v.reshape(Bc, Tc, H, D)
        scale = 1.0 / math.sqrt(D)
        att = jnp.einsum('bqhd,bkhd->bhqk', q, k) * scale
        att = att / temperature
        pos = jnp.arange(Tc, dtype=jnp.float32)
        rel = pos[None, :] - pos[:, None]
        slopes = alibi_slopes(H)
        bias = slopes[:, None, None] * rel[None, :, :]
        causal = pos[None, :] <= pos[:, None]
        bias = jnp.where(causal[None, :, :], bias, -jnp.inf)
        att = att + bias[None, :, :, :]
        w = jax.nn.softmax(att, axis=-1)
        y = jnp.einsum('bhqk,bkhd->bqhd', w, v).reshape(Bc, Tc, Cc)
        return y @ W_proj + b_proj

    def _L0_xattn_ref(k, v, q, Wk, Wv, bv, Wq, bq, Wo, bo):
        import jax, jax.numpy as jnp
        import numpy as np
        D_MODEL = 128
        B, S = (4, 256)
        kp = jnp.einsum('bsd,ed->bse', k, Wk)
        vp = jnp.einsum('bsd,ed->bse', v, Wv) + bv
        qp = jnp.einsum('bsd,ed->bse', q, Wq) + bq
        scale = 1.0 / jnp.sqrt(jnp.float32(kp.shape[-1]))
        scores = jnp.einsum('bqd,bkd->bqk', qp, kp) * scale
        probs = jax.nn.softmax(scores, axis=-1)
        ctx = jnp.einsum('bqk,bkd->bqd', probs, vp)
        return jnp.einsum('bqd,ed->bqe', ctx, Wo) + bo

    def _L0_ffn_ref(hidden_states, gate_w, gate_bias, Wg, Wu, Wd, Ws_g, Ws_u, Ws_d):
        import jax, jax.numpy as jnp
        import numpy as np
        E = 16
        K = 4
        NG = 4
        TG = 2
        SCALE = 2.5
        NORM_TOPK = True
        H = 128
        I = 64
        SH_I = I * 2
        B, S = (2, 256)
        x = hidden_states
        b, s, h = x.shape
        n = b * s
        xf = x.reshape(n, h)
        logits = xf @ gate_w.T
        scores = jax.nn.sigmoid(logits)
        sfc = scores + gate_bias
        epg = E // NG
        grp = sfc.reshape(n, NG, epg)
        g_scores = jax.lax.top_k(grp, 2)[0].sum(-1)
        _, gidx = jax.lax.top_k(g_scores, TG)
        gmask = jax.nn.one_hot(gidx, NG, dtype=sfc.dtype).sum(1)
        emask = jnp.repeat(gmask, epg, axis=1)
        masked = jnp.where(emask > 0, sfc, -jnp.inf)
        _, topk_idx = jax.lax.top_k(masked, K)
        topk_w = jnp.take_along_axis(scores, topk_idx, axis=1)
        if K > 1 and NORM_TOPK:
            topk_w = topk_w / (topk_w.sum(-1, keepdims=True) + 1e-20)
        topk_w = topk_w * SCALE
        cw = (jax.nn.one_hot(topk_idx, E, dtype=topk_w.dtype) * topk_w[..., None]).sum(1)
        hg = jnp.einsum('nh,eih->nei', xf, Wg)
        hu = jnp.einsum('nh,eih->nei', xf, Wu)
        act = jax.nn.silu(hg) * hu
        y = jnp.einsum('nei,ne,ehi->nh', act, cw, Wd)
        shared = jax.nn.silu(xf @ Ws_g.T) * (xf @ Ws_u.T) @ Ws_d.T
        y = y + shared
        return (x + y.reshape(b, s, h)).astype(hidden_states.dtype)

    def _L1_attn_ref(x, wq, wk, wv, wo, bo):
        import jax, jax.numpy as jnp
        import numpy as np
        NUM_HEADS = 16
        EPS = 1e-06

        def _split_heads(t, h):
            b, s, d = t.shape
            return t.reshape(b, s, h, d // h).transpose(0, 2, 1, 3)
        h = NUM_HEADS
        q = _split_heads(x @ wq.T, h)
        k = _split_heads(x @ wk.T, h)
        v = _split_heads(x @ wv.T, h)
        qf = jax.nn.elu(q) + 1.0
        kf = jax.nn.elu(k) + 1.0
        k_sum = jnp.sum(kf, axis=-2)
        denom = jnp.sum(qf * k_sum[:, :, None, :], axis=-1, keepdims=True) + EPS
        kv = jnp.einsum('bhsd,bhse->bhde', kf, v)
        q_kv = jnp.einsum('bhsd,bhde->bhse', qf, kv)
        out = q_kv / denom
        b, _, s, dh = out.shape
        out = out.transpose(0, 2, 1, 3).reshape(b, s, h * dh)
        return out @ wo.T + bo

    def _L1_xattn_ref(encoder_hc, decoder_hq, w_sim, b_sim, W_qv, b_qv):
        import jax, jax.numpy as jnp
        import numpy as np
        B, L_ENC, L_DEC, D = (16, 64, 128, 128)
        d = encoder_hc.shape[-1]
        w1, w2, w3 = (w_sim[:d], w_sim[d:2 * d], w_sim[2 * d:])
        Sim = (encoder_hc @ w1)[:, :, None] + (decoder_hq @ w2)[:, None, :] + jnp.einsum('bid,bjd->bij', encoder_hc * w3, decoder_hq) + b_sim[0]
        A = jax.nn.softmax(Sim, axis=2)
        hq_hat = jnp.einsum('bij,bjd->bid', A, decoder_hq)
        Batt = jax.nn.softmax(jnp.max(Sim, axis=2), axis=1)
        hc_bar = jnp.einsum('bi,bid->bd', Batt, encoder_hc)[:, None, :]
        hc_hat = jnp.broadcast_to(hc_bar, encoder_hc.shape)
        feats = jnp.concatenate([encoder_hc, hq_hat, encoder_hc * hq_hat, encoder_hc * hc_hat], axis=-1)
        hcq = feats @ W_qv + b_qv
        return hcq

    def _L1_ffn_ref(x, router_w, e_bias, gate_w, up_w, down_w, sh_gate_w, sh_up_w, sh_down_w):
        import jax, jax.numpy as jnp
        import numpy as np
        B, T, C = (1, 512, 128)
        E, K = (64, 8)
        G, TG = (8, 4)
        H, HS = (64, 256)
        STD = 0.02

        def _route(xf, router_w, e_bias):
            S = xf.shape[0]
            scores = jax.nn.sigmoid(xf @ router_w.T)
            sb = scores + e_bias
            epg = E // G
            grp = jax.lax.top_k(sb.reshape(S, G, epg), K // TG)[0].sum(-1)
            gidx = jax.lax.top_k(grp, TG)[1]
            gmask = jnp.zeros((S, G), bool).at[jnp.arange(S)[:, None], gidx].set(True)
            emask = jnp.repeat(gmask, epg, axis=1)
            masked = jnp.where(emask, sb, -jnp.inf)
            topk_idx = jax.lax.top_k(masked, K)[1]
            w = jnp.take_along_axis(scores, topk_idx, axis=1)
            w = w / (w.sum(-1, keepdims=True) + 1e-20)
            return (topk_idx, w)
        Bq, Tq, Cq = x.shape
        xf = x.reshape(Bq * Tq, Cq)
        shared = jax.nn.silu(xf @ sh_gate_w) * (xf @ sh_up_w) @ sh_down_w
        topk_idx, w = _route(xf, router_w, e_bias)
        fe = topk_idx.reshape(-1)
        order = jnp.argsort(fe, stable=True)
        tok = order // K
        sorted_x = xf[tok]
        group_sizes = jnp.bincount(fe, length=E).astype(jnp.int32)
        g = jax.lax.ragged_dot(sorted_x, gate_w, group_sizes)
        u = jax.lax.ragged_dot(sorted_x, up_w, group_sizes)
        h = jax.nn.silu(g) * u
        o = jax.lax.ragged_dot(h, down_w, group_sizes)
        o = o * w.reshape(-1)[order][:, None]
        routed = jnp.zeros_like(xf).at[tok].add(o)
        return (shared + routed).reshape(Bq, Tq, Cq)

    def _L2_attn_ref(x, W):
        import jax, jax.numpy as jnp
        import numpy as np
        KEY_DIM = 128
        EMBED_DIM = 128
        key_dim = KEY_DIM
        qkv = jnp.einsum('bsd,de->bse', x, W)
        q = qkv[:, :, :key_dim]
        k = qkv[:, :, key_dim:2 * key_dim]
        v = qkv[:, :, 2 * key_dim:]
        scores = jnp.einsum('bqd,bkd->bqk', q, k) / np.sqrt(key_dim).astype(np.float32)
        attn = jax.nn.softmax(scores, axis=1)
        return jnp.einsum('bqk,bkd->bqd', attn, v)

    def _L2_xattn_ref(x, mem_seq, mem_mask, rms_scale, q_w, kv_w, out_w):
        import jax, jax.numpy as jnp
        import numpy as np
        NUM_HEADS, NUM_KV, HEAD_DIM, WIDTH = (4, 1, 32, 128)
        MASK_FILL = -2.3819763e+38

        def _apply_rope(x, positions, max_wavelength=10000.0):
            d = x.shape[-1]
            freq_exp = 2.0 / d * jnp.arange(d // 2, dtype=jnp.float32)
            timescale = max_wavelength ** freq_exp
            radians = positions[..., None].astype(jnp.float32) / timescale
            radians = radians[..., None, :]
            sin, cos = (jnp.sin(radians), jnp.cos(radians))
            x1, x2 = jnp.split(x, 2, axis=-1)
            out = jnp.concatenate([x1 * cos - x2 * sin, x2 * cos + x1 * sin], axis=-1)
            return out.astype(x.dtype)

        def _rmsnorm(x, scale):
            var = jnp.mean(jnp.square(x.astype(jnp.float32)), axis=-1, keepdims=True)
            normed = x * jax.lax.rsqrt(var + 1e-06)
            return (normed * (1 + scale)).astype(x.dtype)
        B, S, _ = mem_seq.shape
        T = x.shape[1]
        G = NUM_HEADS // NUM_KV
        xn = _rmsnorm(x, rms_scale)
        mn = _rmsnorm(mem_seq, rms_scale)
        q = jnp.einsum('BTD,NDH->BTNH', xn, q_w)
        kv = jnp.einsum('BSD,cKDH->cBSKH', mn, kv_w)
        k, v = (kv[0], kv[1])
        q_pos = jnp.broadcast_to(jnp.arange(S, T + S), (B, T))
        k_pos = jnp.broadcast_to(jnp.arange(S), (B, S))
        q = _apply_rope(q, q_pos) * HEAD_DIM ** (-0.5)
        k = _apply_rope(k, k_pos)
        q = q.reshape(B, T, NUM_KV, G, HEAD_DIM)
        logits = jnp.einsum('BTKGH,BSKH->BKGTS', q, k, preferred_element_type=jnp.float32)
        masked = jnp.where(mem_mask[:, None, None, None, :], logits, MASK_FILL)
        probs = jax.nn.softmax(masked, axis=-1).astype(x.dtype)
        enc = jnp.einsum('BKGTS,BSKH->BTKGH', probs, v).reshape(B, T, NUM_HEADS, HEAD_DIM)
        return jnp.einsum('BTNH,NHD->BTD', enc, out_w)

    def _L2_ffn_ref(src, Wq, Wk, Wv, Wo, Wsel_v, Wsel_o, ln1_g, ln1_b, ln2_g, ln2_b, W1, b1, W2, b2):
        import jax, jax.numpy as jnp
        import numpy as np
        D, H, P, E, K, F = (128, 16, 64, 8, 2, 512)
        B, S = (2, 256)
        NROT = 32
        BASE = 10000.0
        EPS = 1e-05

        def _ln(x, g, b):
            m = jnp.mean(x, -1, keepdims=True)
            v = jnp.mean(jnp.square(x - m), -1, keepdims=True)
            return (x - m) * jax.lax.rsqrt(v + EPS) * g + b

        def _rope(x):
            xr, xp = (x[..., :NROT], x[..., NROT:])
            half = NROT // 2
            inv = BASE ** (-jnp.arange(half, dtype=jnp.float32) / half)
            ang = jnp.arange(x.shape[2], dtype=jnp.float32)[:, None] * inv[None, :]
            cos, sin = (jnp.cos(ang), jnp.sin(ang))
            x1, x2 = (xr[..., :half], xr[..., half:])
            xr = jnp.concatenate([x1 * cos - x2 * sin, x1 * sin + x2 * cos], -1)
            return jnp.concatenate([xr, xp], -1)

        def _gate(x, Wsel):
            s = jax.nn.sigmoid(jnp.einsum('bsd,hed->bhse', x, Wsel))
            _, idx = jax.lax.top_k(s, K)
            mask = jax.nn.one_hot(idx, E, dtype=s.dtype).sum(-2)
            return s * mask

        def _moe_attn(x, Wq, Wk, Wv, Wo, Wsel_v, Wsel_o):
            q = _rope(jnp.einsum('bsd,hdp->bhsp', x, Wq))
            k = _rope(jnp.einsum('bsd,hdp->bhsp', x, Wk))
            gv = _gate(x, Wsel_v)
            v = jnp.einsum('bsd,bhse,hedp->bhsp', x, gv, Wv)
            att = jax.nn.softmax(jnp.einsum('bhsp,bhtp->bhst', q, k) / np.sqrt(P), axis=-1)
            o = jnp.einsum('bhst,bhtp->bhsp', att, v)
            go = _gate(x, Wsel_o)
            return jnp.einsum('bhsp,bhse,hepd->bsd', o, go, Wo)
        src2 = _moe_attn(src, Wq, Wk, Wv, Wo, Wsel_v, Wsel_o)
        src = src + src2
        src = _ln(src, ln1_g, ln1_b)
        src2 = jax.nn.relu(src @ W1 + b1) @ W2 + b2
        src = src + src2
        return _ln(src, ln2_g, ln2_b)

    def _L3_attn_ref(x, Wq, Wk, Wv):
        import jax, jax.numpy as jnp
        import numpy as np
        B, S, H, D = (4, 256, 128, 128)
        b, s, _ = x.shape
        d = Wq.shape[0]
        q = jnp.einsum('bsh,dh->bsd', x, Wq)
        k = jnp.einsum('bsh,dh->bsd', x, Wk)
        v = jnp.einsum('bsh,dh->bsd', x, Wv)
        kT = k.reshape(b, d, s)
        scores = jnp.matmul(q, kT) / jnp.sqrt(jnp.float32(d))
        attn = jax.nn.softmax(scores, axis=0)
        tril = jnp.tril(jnp.ones((s, s), dtype=bool))
        attn_masked = jnp.where(tril[None, :, :], attn, jnp.float32(1e-09))
        return jnp.matmul(attn_masked, v)

    def _L3_xattn_ref(query, key, value, w_q, w_k, w_v, w_o):
        import jax, jax.numpy as jnp
        import numpy as np
        HIDDEN = 128
        HEADS = 16
        HEAD_DIM = 64
        B, Q, _ = query.shape
        Kl = key.shape[1]
        scale = HEAD_DIM ** (-0.5)
        q = (query @ w_q).reshape(B, Q, HEADS, HEAD_DIM).transpose(0, 2, 1, 3)
        k = (key @ w_k).reshape(B, Kl, HEADS, HEAD_DIM).transpose(0, 2, 1, 3)
        v = (value @ w_v).reshape(B, Kl, HEADS, HEAD_DIM).transpose(0, 2, 1, 3)
        scores = jnp.einsum('bhqd,bhkd->bhqk', q, k) * scale
        attn = jax.nn.softmax(scores, axis=-1)
        out = jnp.einsum('bhqk,bhkd->bhqd', attn, v)
        out = out.transpose(0, 2, 1, 3).reshape(B, Q, HEADS * HEAD_DIM)
        return out @ w_o

    def _L3_ffn_ref(x, gate_w, bias, W1, W3, W2, sw1, sw3, sw2):
        import jax, jax.numpy as jnp
        import numpy as np
        D = 128
        I = 64
        E = 32
        K = 4
        T = 2 * 256
        C = 2 * T * K // E
        X = x.reshape(-1, D)
        logits = (X @ gate_w.T).astype(jnp.float32)
        scores = jax.nn.sigmoid(logits)
        _, idx = jax.lax.top_k(scores + bias[None, :], K)
        w = jnp.take_along_axis(scores, idx, axis=-1)
        w = w / jnp.clip(jnp.sum(w, axis=-1, keepdims=True), 1e-12, None)
        w = w.astype(x.dtype)
        eid = idx.reshape(-1)
        onehot = (eid[:, None] == jnp.arange(E)[None, :]).astype(jnp.int32)
        pos = jnp.take_along_axis(jnp.cumsum(onehot, axis=0) - 1, eid[:, None], axis=1)[:, 0]
        valid = pos < C
        posc = jnp.minimum(pos, C - 1)
        Xrep = jnp.repeat(X, K, axis=0)
        xe = jnp.zeros((E, C, D), x.dtype).at[eid, posc].add(jnp.where(valid[:, None], Xrep, jnp.zeros((), x.dtype)))
        h = jax.nn.silu(jnp.einsum('ecd,edi->eci', xe, W1)) * jnp.einsum('ecd,edi->eci', xe, W3)
        ye = jnp.einsum('eci,eid->ecd', h, W2)
        gflat = jnp.where(valid, w.reshape(-1), jnp.zeros((), x.dtype))
        yrows = ye[eid, posc] * gflat[:, None]
        out = yrows.reshape(-1, K, D).sum(axis=1)
        out = out + jax.nn.silu(X @ sw1.T) * (X @ sw3.T) @ sw2.T
        return out.reshape(x.shape)
    x = x + _L0_attn_ref(_layernorm(x, axis=-1), L0_attn_W_attn, L0_attn_b_attn, L0_attn_W_proj, L0_attn_b_proj, L0_attn_temperature)
    x = x + _L0_xattn_ref(ctx_1024, ctx_1024, _layernorm(x, axis=-1), L0_xattn_Wk, L0_xattn_Wv, L0_xattn_bv, L0_xattn_Wq, L0_xattn_bq, L0_xattn_Wo, L0_xattn_bo)
    x = x + _L0_ffn_ref(_layernorm(x, axis=-1), L0_ffn_gate_w, L0_ffn_gate_bias, L0_ffn_Wg, L0_ffn_Wu, L0_ffn_Wd, L0_ffn_Ws_g, L0_ffn_Ws_u, L0_ffn_Ws_d)
    x = x + _L1_attn_ref(_layernorm(x, axis=-1), L1_attn_wq, L1_attn_wk, L1_attn_wv, L1_attn_wo, L1_attn_bo)
    x = x + _L1_xattn_ref(_layernorm(x, axis=-1), ctx_1024, L1_xattn_w_sim, L1_xattn_b_sim, L1_xattn_W_qv, L1_xattn_b_qv)
    x = x + _L1_ffn_ref(_layernorm(x, axis=-1), L1_ffn_router_w, L1_ffn_e_bias, L1_ffn_gate_w, L1_ffn_up_w, L1_ffn_down_w, L1_ffn_sh_gate_w, L1_ffn_sh_up_w, L1_ffn_sh_down_w)
    x = x + _L2_attn_ref(_layernorm(x, axis=-1), L2_attn_W)
    x = x + _L2_xattn_ref(_layernorm(x, axis=-1), ctx_1024, mask_BxS2_bk0, L2_xattn_rms_scale, L2_xattn_q_w, L2_xattn_kv_w, L2_xattn_out_w)
    x = x + _L2_ffn_ref(_layernorm(x, axis=-1), L2_ffn_Wq, L2_ffn_Wk, L2_ffn_Wv, L2_ffn_Wo, L2_ffn_Wsel_v, L2_ffn_Wsel_o, L2_ffn_ln1_g, L2_ffn_ln1_b, L2_ffn_ln2_g, L2_ffn_ln2_b, L2_ffn_W1, L2_ffn_b1, L2_ffn_W2, L2_ffn_b2)
    x = x + _L3_attn_ref(_layernorm(x, axis=-1), L3_attn_Wq, L3_attn_Wk, L3_attn_Wv)
    x = x + _L3_xattn_ref(_layernorm(x, axis=-1), ctx_1024, ctx_1024, L3_xattn_w_q, L3_xattn_w_k, L3_xattn_w_v, L3_xattn_w_o)
    x = x + _L3_ffn_ref(_layernorm(x, axis=-1), L3_ffn_gate_w, L3_ffn_bias, L3_ffn_W1, L3_ffn_W3, L3_ffn_W2, L3_ffn_sw1, L3_ffn_sw3, L3_ffn_sw2)
    return x

_drawn_inputs = setup_inputs


def setup_inputs(seed=0):
    import zlib

    import numpy as np

    out = dict(_drawn_inputs(seed))
    spreads = {'L0_attn_b_attn': (0.0, 0.1),
     'L0_attn_b_proj': (0.0, 0.1),
     'L0_xattn_bv': (0.0, 0.1),
     'L0_xattn_bq': (0.0, 0.1),
     'L0_xattn_bo': (0.0, 0.1),
     'L0_ffn_gate_bias': (0.0, 0.1),
     'L1_attn_bo': (0.0, 0.1),
     'L1_ffn_e_bias': (0.0, 0.8),
     'L2_ffn_ln1_g': (1.0, 0.2),
     'L2_ffn_ln1_b': (0.0, 0.1),
     'L2_ffn_ln2_g': (1.0, 0.2),
     'L2_ffn_ln2_b': (0.0, 0.1),
     'L2_ffn_b1': (0.0, 0.792),
     'L2_ffn_b2': (0.0, 0.1),
     'L3_ffn_bias': (0.0, 0.8)}
    factors = {'L1_ffn_router_w': 8.0,
     'L1_ffn_gate_w': 8.0,
     'L1_ffn_up_w': 8.0,
     'L1_ffn_down_w': 8.0,
     'L1_ffn_sh_gate_w': 3.428,
     'L1_ffn_sh_up_w': 3.323,
     'L1_ffn_sh_down_w': 3.309,
     'L2_xattn_rms_scale': 7.044,
     'L2_ffn_Wq': 8.0,
     'L2_ffn_Wk': 8.0,
     'L2_ffn_Wv': 8.0,
     'L2_ffn_Wo': 8.0,
     'L2_ffn_Wsel_v': 8.0,
     'L2_ffn_Wsel_o': 8.0,
     'L2_ffn_W1': 4.67,
     'L3_xattn_w_q': 3.723,
     'L3_xattn_w_k': 3.844}
    for name, (base, spread) in spreads.items():
        noise = np.random.default_rng([zlib.crc32(name.encode()), seed]).standard_normal(out[name].shape)
        drawn = base * np.exp(spread * noise) if base else spread * noise
        out[name] = jnp.asarray(drawn.astype(out[name].dtype))
    for name, factor in factors.items():
        out[name] = (out[name] * factor).astype(out[name].dtype)
    return out
```

```python
from contextlib import ExitStack

import numpy as np

import concourse.bass as bass
from concourse import mybir

STAGES = tuple(range(12))

B, S, D = 4, 512, 128
P = 128
TPB = S // P
NT = B * TPB
N = B * S
L = 77
F32 = mybir.dt.float32
BF16 = mybir.dt.bfloat16
ALU = mybir.AluOpType
ACT = mybir.ActivationFunctionType
AX = mybir.AxisListType.X
BIG = 1.0e30


class Shared:
    pass


def spread(ap, n):
    return ap.unsqueeze(2).broadcast_to([ap.shape[0], ap.shape[1], n])


def tiled(ap, n):
    return ap.unsqueeze(1).broadcast_to([ap.shape[0], n, ap.shape[1]])


def chain(T, dve):
    def link(ins):
        T.dve_steps += 1
        ins.then_inc(T.dve_step, 1)
        dve.wait_ge(T.dve_step, T.dve_steps)
    return link


def layernorm(nc, T, src, dst, dstT, loads=(), load_sem=None, gain=None, shift=None, eps=1e-5):
    n = T.ln_calls
    T.ln_calls += 1
    with nc.Block() as block:
        @block.sync
        def _(sp):
            for to, frm in loads:
                sp.dma_start(to, frm).then_inc(load_sem, 16)

        @block.vector
        def _(dve):
            link = chain(T, dve)
            link(nc.vector.tensor_reduce(T.ln_sum[:, :], src, axis=AX, op=ALU.add))
            link(nc.vector.tensor_scalar(T.ln_mean[:, :], T.ln_sum[:, :], 1.0 / D, None, ALU.mult))
            link(nc.vector.tensor_tensor(dst, src, spread(T.ln_mean[:, :], D), ALU.subtract))
            link(nc.vector.tensor_tensor(T.ln_sq[:, :, :], dst, dst, ALU.mult))
            link(nc.vector.tensor_reduce(T.ln_sum[:, :], T.ln_sq[:, :, :], axis=AX, op=ALU.add))
            nc.vector.tensor_scalar(T.ln_mean[:, :], T.ln_sum[:, :], 1.0 / D, eps, ALU.mult, ALU.add)\
                .then_inc(T.ln_var, 1)
            dve.wait_ge(T.ln_std, n + 1)
            link(nc.vector.reciprocal(T.ln_rstd[:, :], T.ln_sum[:, :]))
            for c in range(B):
                t = slice(c * TPB, (c + 1) * TPB)
                out = nc.vector.tensor_tensor(dst[:, t, :], dst[:, t, :], spread(T.ln_rstd[:, t], D), ALU.mult)
                if gain is not None:
                    link(out)
                    link(nc.vector.tensor_tensor(dst[:, t, :], dst[:, t, :], tiled(gain, TPB), ALU.mult))
                    out = nc.vector.tensor_tensor(dst[:, t, :], dst[:, t, :], tiled(shift, TPB), ALU.add)
                out.then_inc(T.ln_done, 1)

        @block.tensor
        def _(pe):
            for c in range(B):
                pe.wait_ge(T.ln_done, B * n + c + 1)
                for t in range(TPB):
                    last = nc.tensor.transpose(T.bank[c][:, t * P:(t + 1) * P], dst[:, c * TPB + t, :], T.ident[:, :])
                last.then_inc(T.ln_turned, 1)

        @block.scalar
        def _(act):
            act.wait_ge(T.ln_var, n + 1)
            nc.scalar.activation(T.ln_sum[:, :], T.ln_mean[:, :], ACT.Sqrt).then_inc(T.ln_std, 1)
            for c in range(B):
                act.wait_ge(T.ln_turned, B * n + c + 1)
                nc.scalar.activation(dstT[:, c * S:(c + 1) * S], T.bank[c][:, :], ACT.Copy)


class Stage:
    def __init__(self, nc, name):
        self.nc, self.name, self.ctx, self.sems = nc, name, ExitStack(), []

    def __enter__(self):
        self.ctx.__enter__()
        return self

    def __exit__(self, *a):
        if self.sems:
            with self.nc.Block() as block:
                @block.gpsimd
                def _(pool):
                    for s in self.sems:
                        pool.sem_clear(s)
        return self.ctx.__exit__(*a)

    def sb(self, name, shape, dt=F32):
        return self.ctx.enter_context(self.nc.sbuf_tensor(f"{self.name}_{name}", shape, dt))

    def sem(self, name):
        self.sems.append(self.ctx.enter_context(self.nc.semaphore(f"{self.name}_{name}")))
        return self.sems[-1]


def l0_attention(nc, T, A):
    H, HD = 16, 8
    G, HPG = 4, 4
    UNITS = TPB * H
    slopes = [2.0 ** (-0.5 * (h + 1)) for h in range(H)]
    with Stage(nc, "l0a") as st:
        w = st.sb("w", [P, 2 * G * P + D])
        wproj = st.sb("wproj", [P, D])
        cols = st.sb("cols", [P, 2 * G + 1])
        rows = st.sb("rows", [P, 2 * D])
        rel = st.sb("rel", [P, 2 * S - P])
        alibi = st.sb("alibi", [P, H, 2 * S - P])
        qscale = st.sb("qscale", [P, 1])
        qbias = st.sb("qbias", [P, G])
        xb = st.sb("xb", [P, S])
        q = st.sb("q", [P, G, S])
        k = st.sb("k", [P, G, S])
        v = st.sb("v", [P, TPB, D])
        sc = st.sb("sc", [P, 2, S])
        pr = st.sb("pr", [P, 2, S])
        prT = st.sb("prT", [P, 2, S])
        mx = st.sb("mx", [P, 4])
        nmx = st.sb("nmx", [P, 4])
        rsum = st.sb("rsum", [P, TPB, H])
        rinv = st.sb("rinv", [P, TPB, H])
        y = st.sb("y", [P, TPB, D])
        yT = st.sb("yT", [P, S])
        loaded = st.sem("loaded")
        prepared = st.sem("prepared")
        x_ready, projected, qk_ready, v_ready = (st.sem(n) for n in ("x_ready", "projected", "qk_ready", "v_ready"))
        scored, masked, max_ready, expd, turned, copied_a, copied_v, pv_done, y_ready = (
            st.sem(n) for n in ("scored", "masked", "max_ready", "expd", "turned", "copied_a", "copied_v",
                                "pv_done", "y_ready"))
        y_turned, yT_ready, out_ready, added, rinv_ready = (
            st.sem(n) for n in ("y_turned", "yT_ready", "out_ready", "added", "rinv_ready"))
        score_seen = st.sem("score_seen")
        loads = [(w[:, :], A["l0a_w"]), (wproj[:, :], A["l0a_wproj"]), (cols[:, :], A["l0a_cols"]),
                 (rows[:, :], A["l0a_rows"]), (rel[:, :], A["rel"])]
        layernorm(nc, T, T.X[:, :, :], T.LNX[:, :, :], T.LNT[:, :], loads, loaded)
        pj, sbank, tbank, obank = T.bank[0:2], T.bank[2:4], T.bank[4:6], T.bank[6:8]

        with nc.Block() as block:
            @block.vector
            def _(dve):
                link = chain(T, dve)
                dve.wait_ge(loaded, 16 * len(loads))
                link(nc.vector.reciprocal(qscale[:, :], cols[:, 2 * G:2 * G + 1]))
                link(nc.vector.tensor_scalar(qscale[:, :], qscale[:, :], HD ** -0.5, None, ALU.mult))
                nc.vector.tensor_scalar(qbias[:, :], cols[:, 0:G], qscale[:, 0:1], None, ALU.mult).then_inc(prepared, 1)
                for h in range(H):
                    nc.vector.tensor_scalar(alibi[:, h, :], rel[:, :], slopes[h], None, ALU.mult)
                link(nc.vector.tensor_tensor(T.X[:, :, :], T.X[:, :, :], tiled(rows[:, D:2 * D], NT), ALU.add))
                with dve.Fori(0, B) as b:
                    dve.wait_ge(projected, b * 9 + 9)
                    nc.vector.tensor_tensor(v[:, :, :], pj[0][:, :].rearrange("p (t c) -> p t c", t=TPB),
                                            tiled(rows[:, 0:D], TPB), ALU.add).then_inc(v_ready, 1)
                    for i in range(UNITS + 3):
                        if i < UNITS:
                            tt, h = divmod(i, H)
                            W = (tt + 1) * P
                            u0 = S - P - tt * P
                            dve.wait_ge(scored, b * UNITS + i + 1)
                            if i >= 2:
                                dve.wait_ge(expd, b * UNITS + i - 1)
                            dve.sem_inc(score_seen, 1)
                            nc.vector.tensor_tensor_reduce(
                                out=sc[:, i % 2, 0:W], in0=sbank[i % 2][:, 0:W], in1=alibi[:, h, u0:u0 + W], scale=1.0,
                                scalar=-3.0e38, op0=ALU.add, op1=ALU.max,
                                accum_out=mx[:, i % 4:i % 4 + 1]).then_inc(masked, 1)
                            dve.wait_ge(masked, b * UNITS + i + 1)
                            nc.vector.tensor_scalar(nmx[:, i % 4:i % 4 + 1], mx[:, i % 4:i % 4 + 1], -1.0, None,
                                                    ALU.mult).then_inc(max_ready, 1)
                        j = i - 1
                        if 0 <= j < UNITS and j % 2:
                            W = (j // H + 1) * P
                            dve.wait_ge(turned, b * UNITS + j + 1)
                            nc.vector.tensor_copy(prT[:, 1, 0:W], tbank[1][:, 0:W]).then_inc(copied_v, 1)
                        j = i - 3
                        if j >= 0 and j % H == H - 1:
                            tt = j // H
                            dve.wait_ge(pv_done, b * UNITS + j + 1)
                            nc.vector.reciprocal(rinv[:, tt, :], rsum[:, tt, :]).then_inc(rinv_ready, 1)
                            dve.wait_ge(rinv_ready, b * TPB + tt + 1)
                            nc.vector.tensor_tensor(y[:, tt, :].rearrange("p (h d) -> p h d", h=H),
                                                    obank[tt % 2][:, 0:D].rearrange("p (h d) -> p h d", h=H),
                                                    spread(rinv[:, tt, :], HD), ALU.mult).then_inc(y_ready, 1)
                    dve.wait_ge(out_ready, b + 1)
                    nc.vector.tensor_tensor(T.X[:, bass.ds(b * TPB, TPB), :], T.X[:, bass.ds(b * TPB, TPB), :],
                                            pj[1][:, :].rearrange("p (t c) -> p t c", t=TPB), ALU.add).then_inc(added, 1)

            @block.scalar
            def _(act):
                act.wait_ge(loaded, 16 * len(loads))
                act.wait_ge(prepared, 1)
                with act.Fori(0, B) as b:
                    nc.scalar.activation(xb[:, :], T.LNT[:, bass.ds(b * S, S)], ACT.Copy).then_inc(x_ready, 1)
                    for n in range(2 * G):
                        act.wait_ge(projected, b * 9 + n + 1)
                        if n < G:
                            nc.scalar.activation(q[:, n, :], pj[n % 2][:, :], ACT.Identity, bias=qbias[:, n:n + 1],
                                                 scale=qscale[:, 0:1]).then_inc(qk_ready, 1)
                        else:
                            nc.scalar.activation(k[:, n - G, :], pj[n % 2][:, :], ACT.Identity,
                                                 bias=cols[:, n:n + 1]).then_inc(qk_ready, 1)
                    for i in range(UNITS + 1):
                        if i < UNITS:
                            tt, h = divmod(i, H)
                            W = (tt + 1) * P
                            act.wait_ge(max_ready, b * UNITS + i + 1)
                            if i >= 2:
                                act.wait_ge(turned, b * UNITS + i - 1)
                            nc.scalar.activation(pr[:, i % 2, 0:W], sc[:, i % 2, 0:W], ACT.Exp,
                                                 bias=nmx[:, i % 4:i % 4 + 1],
                                                 accum_out=rsum[:, tt, h:h + 1]).then_inc(expd, 1)
                        j = i - 1
                        if j >= 0 and j % 2 == 0:
                            W = (j // H + 1) * P
                            act.wait_ge(turned, b * UNITS + j + 1)
                            nc.scalar.activation(prT[:, 0, 0:W], tbank[0][:, 0:W], ACT.Copy).then_inc(copied_a, 1)
                    act.wait_ge(y_turned, b + 1)
                    nc.scalar.activation(yT[:, :], pj[0][:, :], ACT.Copy).then_inc(yT_ready, 1)

            @block.tensor
            def _(pe):
                pe.wait_ge(loaded, 16 * len(loads))
                with pe.Fori(0, B) as b:
                    pe.wait_ge(x_ready, b + 1)
                    for n in range(2 * G):
                        if n >= 2:
                            pe.wait_ge(qk_ready, b * 2 * G + n - 1)
                        nc.tensor.matmul(pj[n % 2][:, :], w[:, n * P:(n + 1) * P], xb[:, :], start=True,
                                         stop=True).then_inc(projected, 1)
                    pe.wait_ge(qk_ready, b * 2 * G + 2 * G)
                    for t in range(TPB):
                        last = nc.tensor.matmul(pj[0][:, t * D:(t + 1) * D], xb[:, t * P:(t + 1) * P],
                                                w[:, 2 * G * P:2 * G * P + D], start=True, stop=True)
                    last.then_inc(projected, 1)
                    pe.wait_ge(v_ready, b + 1)
                    for i in range(UNITS + 2):
                        if i < UNITS:
                            tt, h = divmod(i, H)
                            g, r = divmod(h, HPG)
                            W = (tt + 1) * P
                            if i >= 2:
                                pe.wait_ge(masked, b * UNITS + i - 1)
                            nc.tensor.matmul(sbank[i % 2][:, 0:W], q[32 * r:32 * r + 32, g, tt * P:(tt + 1) * P],
                                             k[32 * r:32 * r + 32, g, 0:W], start=True, stop=True,
                                             ).then_inc(scored, 1)
                        j = i - 1
                        if 0 <= j < UNITS:
                            pe.wait_ge(expd, b * UNITS + j + 1)
                            for t in range(j // H + 1):
                                last = nc.tensor.transpose(tbank[j % 2][:, t * P:(t + 1) * P],
                                                           pr[:, j % 2, t * P:(t + 1) * P], T.ident[:, :])
                            last.then_inc(turned, 1)
                        j = i - 2
                        if j >= 0:
                            tt, h = divmod(j, H)
                            pe.wait_ge(copied_v if j % 2 else copied_a, b * (UNITS // 2) + j // 2 + 1)
                            if h == 0 and tt >= 2:
                                pe.wait_ge(y_ready, b * TPB + tt - 1)
                            for t in range(tt + 1):
                                last = nc.tensor.matmul(obank[tt % 2][:, h * HD:(h + 1) * HD],
                                                        prT[:, j % 2, t * P:(t + 1) * P], v[:, t, h * HD:(h + 1) * HD],
                                                        start=(t == 0), stop=(t == tt))
                            last.then_inc(pv_done, 1)
                    pe.wait_ge(y_ready, b * TPB + TPB)
                    for t in range(TPB):
                        last = nc.tensor.transpose(pj[0][:, t * P:(t + 1) * P], y[:, t, :], T.ident[:, :])
                    last.then_inc(y_turned, 1)
                    pe.wait_ge(yT_ready, b + 1)
                    for t in range(TPB):
                        last = nc.tensor.matmul(pj[1][:, t * D:(t + 1) * D], yT[:, t * P:(t + 1) * P], wproj[:, :],
                                                start=True, stop=True)
                    last.then_inc(out_ready, 1)
                    pe.wait_ge(added, b + 1)


def context_attention(nc, T, A, name, H, dk, HB, biased=False, rope=False, normed=False, keep_mask=False):
    HPG = P // dk
    G = H // HPG
    R = 2 if rope else 1
    STEPS = TPB * H // HB
    NP = G * (2 * R + 1) + H
    W = HB * L
    SCALE = dk ** -0.5
    FILL = -2.3819763e38
    with Stage(nc, name) as st:
        wq = st.sb("wq", [P, R, G, P])
        wk = st.sb("wk", [P, R, G, P])
        wv = st.sb("wv", [P, G, P])
        wo = st.sb("wo", [P, G, D])
        loaded = st.sem("loaded")
        loads = [(wq[:, :, :, :], A[f"{name}_wq"]), (wk[:, :, :, :], A[f"{name}_wk"]), (wv[:, :, :], A[f"{name}_wv"]),
                 (wo[:, :, :], A[f"{name}_wo"])]
        if biased:
            cols = st.sb("cols", [P, 2])
            rows = st.sb("rows", [P, D])
            qbias = st.sb("qbias", [P, 1])
            loads += [(cols[:, :], A[f"{name}_cols"]), (rows[:, :], A[f"{name}_rows"])]
        if rope:
            qtrig = st.sb("qtrig", [P, 2, S])
            ktrig = st.sb("ktrig", [P, 2, L])
            qrot = st.sb("qrot", [P, 2, S])
            krot = st.sb("krot", [P, 2, L])
            loads += [(qtrig[:, :, :], A[f"{name}_qtrig"]), (ktrig[:, :, :], A[f"{name}_ktrig"])]
        if normed:
            gain = st.sb("gain", [P, 1])
            rms = st.sb("rms", [P, NT])
            crms = st.sb("crms", [L, B])
            sq = st.sb("sq", [P, NT, D])
            cn = st.sb("cn", [L, B, D])
            loads += [(gain[:, :], A[f"{name}_gain"])]
        if keep_mask:
            keep_bits = st.sb("keep_bits", [P, B, L], mybir.dt.int32)
            keep = st.sb("keep", [P, B, L])
            fill = st.sb("fill", [P, B, L])
            keepb = st.sb("keepb", [P, HB, L])
            fillb = st.sb("fillb", [P, HB, L])
            loads += [(keep_bits[:, :, :], A[f"{name}_keep"])]
        ctxT = st.sb("ctxT", [P, B * L]) if normed else T.CTXT
        q = st.sb("q", [P, G, S])
        k = st.sb("k", [P, G, HPG, L])
        vT = st.sb("vT", [P, G, L])
        vo = st.sb("vo", [L, H, D])
        sc = st.sb("sc", [P, 2, HB, L])
        pr = st.sb("pr", [P, 2, HB, L])
        prT = st.sb("prT", [L, 2, HB * P])
        mx = st.sb("mx", [P, 2, HB])
        rs = st.sb("rs", [P, 2, HB])
        sems = ("prepared", "squared", "rooted", "cturned", "ct_ready", "projected", "taken", "scored", "dstep",
                "centred", "expd", "normal", "turned", "copied", "pv_done", "added", "maskb", "qrotated")
        prepared, squared, rooted, cturned, ct_ready, projected, taken, scored, dstep, centred, expd, normal, turned, \
            copied, pv_done, added, maskb, qrotated = (st.sem(n) for n in sems)
        layernorm(nc, T, T.X[:, :, :], T.LNX[:, :, :], T.LNT[:, :], loads, loaded)
        pj, sbank, tbank, obank = T.bank[0:2], T.bank[2:4], T.bank[4:6], T.bank[6:8]

        with nc.Block() as block:
            @block.vector
            def _(dve):
                link = chain(T, dve)
                dve.wait_ge(loaded, 16 * len(loads))
                link(nc.vector.memset(k[:, :, :, :], 0.0))
                if biased:
                    link(nc.vector.tensor_scalar(qbias[:, :], cols[:, 0:1], SCALE, None, ALU.mult))
                    link(nc.vector.tensor_tensor(T.X[:, :, :], T.X[:, :, :], tiled(rows[:, :], NT), ALU.add))
                if keep_mask:
                    link(nc.vector.tensor_copy(keep[:, :, :], keep_bits[:, :, :]))
                    link(nc.vector.tensor_scalar(fill[:, :, :], keep[:, :, :], -1.0, -FILL, ALU.add, ALU.mult))
                if normed:
                    link(nc.vector.tensor_scalar(gain[:, :], gain[:, :], 1.0, None, ALU.add))
                    for m in (wq[:, :, :, :], wk[:, :, :, :], wv[:, :, :]):
                        link(nc.vector.tensor_scalar(m, m, gain[:, 0:1], None, ALU.mult))
                    link(nc.vector.tensor_tensor(sq[:, :, :], T.LNX[:, :, :], T.LNX[:, :, :], ALU.mult))
                    link(nc.vector.tensor_reduce(rms[:, :], sq[:, :, :], axis=AX, op=ALU.add))
                    link(nc.vector.tensor_scalar(rms[:, :], rms[:, :], 1.0 / D, 1e-6, ALU.mult, ALU.add))
                    link(nc.vector.tensor_tensor(cn[:, :, :], T.CTX[:, :, :], T.CTX[:, :, :], ALU.mult))
                    link(nc.vector.tensor_reduce(crms[:, :], cn[:, :, :], axis=AX, op=ALU.add))
                    nc.vector.tensor_scalar(crms[:, :], crms[:, :], 1.0 / D, 1e-6, ALU.mult, ALU.add).then_inc(squared, 1)
                    dve.wait_ge(rooted, 2)
                    link(nc.vector.reciprocal(rms[:, :], rms[:, :]))
                    link(nc.vector.tensor_scalar(rms[:, :], rms[:, :], SCALE, None, ALU.mult))
                    link(nc.vector.reciprocal(crms[:, :], crms[:, :]))
                    nc.vector.tensor_tensor(cn[:, :, :], T.CTX[:, :, :], spread(crms[:, :], D), ALU.mult)\
                        .then_inc(prepared, 1)

            @block.scalar
            def _(act):
                if normed:
                    act.wait_ge(squared, 1)
                    nc.scalar.activation(rms[:, :], rms[:, :], ACT.Sqrt).then_inc(rooted, 1)
                    nc.scalar.activation(crms[:, :], crms[:, :], ACT.Sqrt).then_inc(rooted, 1)
                    act.wait_ge(cturned, 1)
                    nc.scalar.activation(ctxT[:, :], T.bank[0][:, 0:B * L], ACT.Copy)

            @block.tensor
            def _(pe):
                if normed:
                    pe.wait_ge(prepared, 1)
                    for b in range(B):
                        last = nc.tensor.transpose(T.bank[0][:, b * L:(b + 1) * L], cn[:, b, :], T.ident[0:L, 0:L])
                    last.then_inc(cturned, 1)

        with nc.Block() as block:
            @block.tensor
            def _(pe):
                with pe.Fori(0, B) as b:
                    x = T.LNT[:, bass.ds(b * S, S)]
                    c = ctxT[:, bass.ds(b * L, L)]
                    n = 0

                    def bank_free(n):
                        if n >= 2:
                            pe.wait_ge(taken, b * NP + n - 1)
                    for g in range(G):
                        for r in range(R):
                            bank_free(n)
                            nc.tensor.matmul(pj[n % 2][:, :], wq[:, r, g, :], x, start=True, stop=True).then_inc(projected, 1)
                            n += 1
                    for g in range(G):
                        for r in range(R):
                            bank_free(n)
                            nc.tensor.matmul(pj[n % 2][:, 0:L], wk[:, r, g, :], c, start=True, stop=True).then_inc(projected, 1)
                            n += 1
                    for g in range(G):
                        bank_free(n)
                        nc.tensor.matmul(pj[n % 2][:, 0:L], wv[:, g, :], c, start=True, stop=True).then_inc(projected, 1)
                        n += 1
                    pe.wait_ge(taken, b * NP + n)
                    for h in range(H):
                        g, r = divmod(h, HPG)
                        bank_free(n)
                        nc.tensor.matmul(pj[n % 2][0:L, 0:D], vT[r * dk:(r + 1) * dk, g, :], wo[r * dk:(r + 1) * dk, g, :],
                                         start=True, stop=True).then_inc(projected, 1)
                        n += 1
                    pe.wait_ge(taken, b * NP + NP)
                    for i in range(STEPS + 2):
                        if i < STEPS:
                            tt, hb = divmod(i, H // HB)
                            if i >= 2:
                                pe.wait_ge(centred, b * STEPS + i - 1)
                            for e in range(0, HB, HPG):
                                g = (hb * HB + e) // HPG
                                last = nc.tensor.matmul(sbank[i % 2][:, e * L:(e + HPG) * L], q[:, g, tt * P:(tt + 1) * P],
                                                        k[:, g, :, :], start=True, stop=True)
                            last.then_inc(scored, 1)
                        j = i - 1
                        if 0 <= j < STEPS:
                            pe.wait_ge(normal, b * STEPS + j + 1)
                            for e in range(HB):
                                last = nc.tensor.transpose(tbank[j % 2][0:L, e * P:(e + 1) * P], pr[:, j % 2, e, :],
                                                           T.ident[:, :])
                            last.then_inc(turned, 1)
                        j = i - 2
                        if j >= 0:
                            hb = j % (H // HB)
                            pe.wait_ge(copied, b * STEPS + j + 1)
                            if j >= 2:
                                pe.wait_ge(added, b * STEPS + j - 1)
                            for e in range(HB):
                                last = nc.tensor.matmul(obank[j % 2][:, 0:D], prT[:, j % 2, e * P:(e + 1) * P],
                                                        vo[:, hb * HB + e, :], start=(e == 0), stop=(e == HB - 1))
                            last.then_inc(pv_done, 1)
                    pe.wait_ge(added, b * STEPS + STEPS)

            @block.scalar
            def _(act):
                with act.Fori(0, B) as b:
                    first = 2 * R * G if rope else 0
                    for n in range(first, NP):
                        act.wait_ge(projected, b * NP + n + 1)
                        src = pj[n % 2]
                        if n < G:
                            out = nc.scalar.activation(q[:, n, :], src[:, :], ACT.Identity,
                                                       bias=qbias[:, 0:1] if biased else 0.0, scale=SCALE)
                        elif n < 2 * G * R:
                            for r in range(HPG):
                                rows_ = slice(r * dk, (r + 1) * dk)
                                out = nc.scalar.activation(k[rows_, n - G, r, :], src[rows_, 0:L], ACT.Copy)
                        elif n < (2 * R + 1) * G:
                            out = nc.scalar.activation(vT[:, n - 2 * R * G, :], src[:, 0:L], ACT.Identity,
                                                       bias=cols[:, 1:2] if biased else 0.0)
                        else:
                            out = nc.scalar.activation(vo[:, n - (2 * R + 1) * G, :], src[0:L, 0:D], ACT.Copy)
                        out.then_inc(taken, 1)
                    for i in range(STEPS + 1):
                        if i < STEPS:
                            act.wait_ge(centred, b * STEPS + i + 1)
                            if i >= 2:
                                act.wait_ge(turned, b * STEPS + i - 1)
                            nc.scalar.activation(pr[:, i % 2, :, :], sc[:, i % 2, :, :], ACT.Exp).then_inc(expd, 1)
                        j = i - 1
                        if j >= 0:
                            act.wait_ge(turned, b * STEPS + j + 1)
                            if j >= 2:
                                act.wait_ge(pv_done, b * STEPS + j - 1)
                            nc.scalar.activation(prT[:, j % 2, :], tbank[j % 2][0:L, 0:HB * P], ACT.Copy).then_inc(copied, 1)

            @block.vector
            def _(dve):
                DS = STEPS * (6 if keep_mask else 3)
                with dve.Fori(0, B) as b:
                    count = [0]

                    def link(ins):
                        count[0] += 1
                        ins.then_inc(dstep, 1)
                        dve.wait_ge(dstep, b * DS + count[0])
                    if keep_mask:
                        nc.vector.tensor_copy(keepb[:, :, :], keep[:, bass.ds(b, 1), :].broadcast_to([P, HB, L]))
                        nc.vector.tensor_copy(fillb[:, :, :], fill[:, bass.ds(b, 1), :].broadcast_to([P, HB, L]))\
                            .then_inc(maskb, 1)
                        dve.wait_ge(maskb, b + 1)
                    if rope:
                        for n, (dst, trig, rot, w_) in enumerate(((q, qtrig, qrot, S), (k, ktrig, krot, L))):
                            dve.wait_ge(projected, b * NP + 2 * n + 1)
                            nc.vector.tensor_tensor(rot[:, 0, :], pj[0][:, 0:w_], trig[:, 0, :], ALU.mult).then_inc(taken, 1)
                            dve.wait_ge(projected, b * NP + 2 * n + 2)
                            nc.vector.tensor_tensor(rot[:, 1, :], pj[1][:, 0:w_], trig[:, 1, :], ALU.mult)\
                                .then_inc(qrotated, 1)
                            dve.wait_ge(qrotated, b * 2 + n + 1)
                            if dst is q:
                                out = nc.vector.tensor_tensor(q[:, 0, :], rot[:, 0, :], rot[:, 1, :], ALU.add)
                            else:
                                for r in range(HPG):
                                    rows_ = slice(r * dk, (r + 1) * dk)
                                    out = nc.vector.tensor_tensor(k[rows_, 0, r, :], rot[rows_, 0, :], rot[rows_, 1, :], ALU.add)
                            out.then_inc(taken, 1)
                    for i in range(STEPS + 2):
                        if i < STEPS:
                            tt = i // (H // HB)
                            s = sbank[i % 2][:, 0:W].rearrange("p (e l) -> p e l", e=HB)
                            dve.wait_ge(scored, b * STEPS + i + 1)
                            if i >= 2:
                                dve.wait_ge(expd, b * STEPS + i - 1)
                            z = sc[:, i % 2, :, :]
                            if keep_mask:
                                link(nc.vector.tensor_scalar(z, s, rms[:, bass.ds(b * TPB + tt, 1)], None, ALU.mult))
                                link(nc.vector.tensor_tensor(z, z, keepb[:, :, :], ALU.mult))
                                link(nc.vector.tensor_tensor(z, z, fillb[:, :, :], ALU.add))
                                s = z
                            link(nc.vector.tensor_reduce(mx[:, i % 2, :], s, axis=AX, op=ALU.max))
                            nc.vector.tensor_tensor(z, s, spread(mx[:, i % 2, :], L), ALU.subtract).then_inc(centred, 1)
                        j = i - 1
                        if 0 <= j < STEPS:
                            dve.wait_ge(expd, b * STEPS + j + 1)
                            p = pr[:, j % 2, :, :]
                            link(nc.vector.tensor_reduce(rs[:, j % 2, :], p, axis=AX, op=ALU.add))
                            link(nc.vector.reciprocal(rs[:, j % 2, :], rs[:, j % 2, :]))
                            nc.vector.tensor_tensor(p, p, spread(rs[:, j % 2, :], L), ALU.mult).then_inc(normal, 1)
                        j = i - 2
                        if j >= 0:
                            tt = j // (H // HB)
                            dve.wait_ge(pv_done, b * STEPS + j + 1)
                            if j:
                                dve.wait_ge(added, b * STEPS + j)
                            xt = T.X[:, bass.ds(b * TPB + tt, 1), :]
                            nc.vector.tensor_tensor(xt, xt, obank[j % 2][:, 0:D].unsqueeze(1), ALU.add).then_inc(added, 1)
                    assert count[0] == DS


def pick_max(nc, link, V, rev, m, c, O):
    groups, n = V.shape[1], V.shape[2]
    link(nc.vector.tensor_reduce(m, V, axis=AX, op=ALU.max))
    link(nc.vector.tensor_tensor(c, V, spread(m, n), ALU.is_ge))
    link(nc.vector.tensor_tensor(c, c, tiled(rev, groups), ALU.mult))
    link(nc.vector.tensor_reduce(m, c, axis=AX, op=ALU.max))
    link(nc.vector.tensor_tensor(O, c, spread(m, n), ALU.is_equal))
    link(nc.vector.scalar_tensor_tensor(V, O, -3.0 * BIG, V, ALU.mult, ALU.add))


def expert_ffn(nc, T, A, name, E, K, route, NSH=1, half_weights=False, add_input=False,
               counted=False):
    I = 64
    PAIRS = E // 2
    SLOTS = 4
    BLK = B
    with Stage(nc, name) as st:
        WT = BF16 if half_weights else F32
        router = st.sb("router", [P, E], WT)
        bias = st.sb("bias", [P, E])
        shared_raw = st.sb("shared", [P, NSH, 3 * P], WT)
        score = st.sb("score", [P, NT, E])
        cw = st.sb("cw", [P, NT, E])
        cwT = st.sb("cwT", [E, N])
        wide_router = st.sb("wide_router", [P, E]) if half_weights else router
        shared = st.sb("wide_shared", [P, NSH, 3 * P]) if half_weights else shared_raw
        mask = st.sb("mask", [P, NT, E])
        T.router_bias = bias
        T.chosen, T.counts = st.sem("chosen"), st.sem("counts")
        loaded = st.sem("loaded")
        loads = [(router[:, :], A[f"{name}_router"]), (bias[:, :], A[f"{name}_bias"]),
                 (shared_raw[:, :, :], A[f"{name}_shared"])]
        if counted:
            tri = st.sb("tri", [P, 2, P])
            loads.append((tri[:, :, :], A["tri"]))
        weights = nc.dram_tensor(f"{name}_weights", (E, N), F32, kind="Internal").ap()
        widened, logits, scored, routed, cw_turned, cw_taken, cw_stored = (
            st.sem(n) for n in ("widened", "logits", "scored", "routed", "cw_turned", "cw_taken", "cw_stored"))
        layernorm(nc, T, T.X[:, :, :], T.LNX[:, :, :], T.LNT[:, :], loads, loaded)

        with Stage(nc, f"{name}r") as rt, nc.Block() as block:
            per_bank = 512 // E if E > 32 else NT

            @block.tensor
            def _(pe):
                pe.wait_ge(loaded, 16 * len(loads))
                if half_weights:
                    pe.wait_ge(widened, 2)
                for t in range(NT):
                    bank, at = divmod(t, per_bank)
                    last = nc.tensor.matmul(T.bank[bank][:, at * E:(at + 1) * E], T.LNT[:, t * P:(t + 1) * P],
                                            wide_router[:, :], start=True, stop=True)
                last.then_inc(logits, 1)
                if counted:
                    pe.wait_ge(T.chosen, 1)
                    for i in range(2):
                        nc.tensor.matmul(T.bank[2 + i][:, :], tri[:, i, :], mask[:, :, :].rearrange("p t e -> p (t e)"),
                                         start=True, stop=True).then_inc(T.counts, 1)
                pe.wait_ge(routed, 1)
                for c in range(B):
                    for t in range(TPB):
                        last = nc.tensor.transpose(T.bank[4 + c][0:E, t * P:(t + 1) * P], cw[:, c * TPB + t, :],
                                                   T.ident[:, :])
                    last.then_inc(cw_turned, 1)

            @block.scalar
            def _(act):
                if half_weights:
                    act.wait_ge(loaded, 16 * len(loads))
                    nc.scalar.activation(wide_router[:, :], router[:, :], ACT.Copy).then_inc(widened, 1)
                    nc.scalar.activation(shared[:, :, :], shared_raw[:, :, :], ACT.Copy).then_inc(widened, 1)
                act.wait_ge(logits, 1)
                for n in range(0, NT, per_bank):
                    last = nc.scalar.activation(score[:, n:n + per_bank, :],
                                                T.bank[n // per_bank][:, 0:per_bank * E].rearrange("p (t e) -> p t e", e=E),
                                                ACT.Sigmoid)
                last.then_inc(scored, 1)
                for c in range(B):
                    act.wait_ge(cw_turned, c + 1)
                    nc.scalar.activation(cwT[:, c * S:(c + 1) * S], T.bank[4 + c][0:E, :], ACT.Copy).then_inc(cw_taken, 1)

            @block.vector
            def _(dve):
                dve.wait_ge(loaded, 16 * len(loads))
                dve.wait_ge(scored, 1)
                route(nc, T, rt, dve, chain(T, dve), score, mask, cw)
                dve.sem_inc(routed, 1)

            @block.sync
            def _(sp):
                sp.wait_ge(cw_taken, B)
                sp.dma_start(weights, cwT[:, :]).then_inc(cw_stored, 16)
                sp.wait_ge(cw_stored, 16)

        wslot = [st.sb(f"w{i}", [P, 3 * P]) for i in range(SLOTS)]
        hslot = [st.sb(f"hw{i}", [P, 3 * P], BF16) for i in range(SLOTS)] if half_weights else wslot
        cslot = [st.sb(f"c{i}", [P, N]) for i in range(SLOTS)]
        gate = st.sb("gate", [P, 2, S])
        prod = st.sb("prod", [P, 2, S])
        hid = st.sb("hid", [P, 2, S])
        outT = st.sb("outT", [P, N])
        arrived = [st.sem(f"arrived{i}") for i in range(SLOTS)]
        cw_here = [st.sem(f"cw_here{i}") for i in range(SLOTS)]
        wide = [st.sem(f"wide{i}") for i in range(SLOTS)]
        wide_free = st.sem("wide_free")
        up_done, gated, multiplied, hidden, down_done = (
            st.sem(n) for n in ("up_done", "gated", "multiplied", "hidden", "down_done"))
        taken, turned_back, closed = st.sem("taken"), st.sem("turned_back"), st.sem("closed")
        closing = T.ident if add_input else T.zeros
        acc = T.bank[0:BLK]
        gbank, ubank = T.bank[4:6], T.bank[6:8]
        PRE = NSH * BLK
        PER = SLOTS * BLK
        TURNS = PAIRS // SLOTS
        with nc.Block() as block:
            @block.sync
            def _(sp):
                def fetch(s, turn):
                    sp.dma_start(hslot[s][:, :], A[f"{name}_pairs"][bass.ds(turn * SLOTS + s, 1), :, :]
                                 .rearrange("a p c -> (a p) c")).then_inc(arrived[s], 16)

                def fetch_cw(s, turn):
                    for e in range(2):
                        sp.dma_start(cslot[s][e * I:(e + 1) * I, :],
                                     weights[bass.ds(turn * 2 * SLOTS + 2 * s + e, 1), :].broadcast_to([I, N]))\
                            .then_inc(cw_here[s], 16)
                for s in range(SLOTS):
                    fetch(s, 0)
                    fetch_cw(s, 0)
                with sp.Fori(0, TURNS - 1) as it:
                    for s in range(SLOTS):
                        if half_weights:
                            sp.wait_ge(wide[s], it + 1)
                            fetch(s, it + 1)
                        sp.wait_ge(down_done, it * PER + PRE + (s + 1) * BLK)
                        if not half_weights:
                            fetch(s, it + 1)
                        fetch_cw(s, it + 1)

            if half_weights:
                @block.gpsimd
                def _(pool):
                    for s in range(SLOTS):
                        pool.wait_ge(arrived[s], 16)
                        nc.gpsimd.tensor_copy(wslot[s][:, :], hslot[s][:, :]).then_inc(wide[s], 1)
                    with pool.Fori(0, TURNS - 1) as it:
                        for s in range(SLOTS):
                            pool.wait_ge(arrived[s], it * 16 + 32)
                            pool.wait_ge(down_done, it * PER + PRE + (s + 1) * BLK)
                            pool.sem_inc(wide_free, 1)
                            nc.gpsimd.tensor_copy(wslot[s][:, :], hslot[s][:, :]).then_inc(wide[s], 1)

            @block.tensor
            def _(pe):
                def up(w, blk, k, local):
                    x = T.LNT[:, blk * S:(blk + 1) * S]
                    nc.tensor.matmul(gbank[local % 2][:, :], w[:, 0:P], x, start=True, stop=True)
                    nc.tensor.matmul(ubank[local % 2][:, :], w[:, P:2 * P], x, start=True, stop=True).then_inc(up_done, 1)

                def down(w, blk, local, first, last):
                    return nc.tensor.matmul(acc[blk][:, :], w[:, 2 * P:3 * P], hid[:, local % 2, :], start=first,
                                            stop=last).then_inc(down_done, 1)
                for n in range(PRE):
                    if n >= 2:
                        pe.wait_ge(hidden, n - 1)
                    up(shared[:, n // BLK, :], n % BLK, n, n)
                    if n >= 1:
                        pe.wait_ge(hidden, n)
                        down(shared[:, (n - 1) // BLK, :], (n - 1) % BLK, n - 1, n - 1 < BLK, False)
                pe.wait_ge(hidden, PRE)
                down(shared[:, NSH - 1, :], BLK - 1, PRE - 1, NSH == 1, False)
                with pe.Fori(0, TURNS) as it:
                    for n in range(PER):
                        s, blk = divmod(n, BLK)
                        if blk == 0:
                            if half_weights:
                                pe.wait_ge(wide[s], it + 1)
                            else:
                                pe.wait_ge(arrived[s], it * 16 + 16)
                        pe.wait_ge(hidden, it * PER + PRE + n - 1)
                        up(wslot[s][:, :], blk, 0, n)
                        if n >= 1:
                            pe.wait_ge(hidden, it * PER + PRE + n)
                            m = n - 1
                            down(wslot[m // BLK][:, :], m % BLK, m, False, False)
                    pe.wait_ge(hidden, it * PER + PRE + PER)
                    down(wslot[SLOTS - 1][:, :], BLK - 1, PER - 1, False, False)
                for blk in range(BLK):
                    last = nc.tensor.matmul(acc[blk][:, :], closing[:, :], T.LNT[:, blk * S:(blk + 1) * S], start=False,
                                            stop=True)
                last.then_inc(closed, 1)
                for c in range(B):
                    pe.wait_ge(taken, c + 1)
                    for t in range(TPB):
                        last = nc.tensor.transpose(T.bank[4 + c][:, t * P:(t + 1) * P],
                                                   outT[:, c * S + t * P:c * S + (t + 1) * P], T.ident[:, :])
                    last.then_inc(turned_back, 1)

            @block.scalar
            def _(act):
                def silu(k, local, wait_free):
                    act.wait_ge(up_done, k + 1)
                    if wait_free:
                        act.wait_ge(multiplied, k - 1)
                    nc.scalar.activation(gate[:, local % 2, :], gbank[local % 2][:, :], ACT.Silu).then_inc(gated, 1)
                for n in range(PRE):
                    silu(n, n, n >= 2)
                with act.Fori(0, TURNS) as it:
                    for n in range(PER):
                        silu(it * PER + PRE + n, n, True)
                act.wait_ge(closed, 1)
                for c in range(B):
                    nc.scalar.activation(outT[:, c * S:(c + 1) * S], acc[c][:, :], ACT.Copy).then_inc(taken, 1)

            @block.vector
            def _(dve):
                for n in range(PRE):
                    dve.wait_ge(gated, n + 1)
                    if n >= 2:
                        dve.wait_ge(down_done, n - 1)
                    nc.vector.tensor_tensor(hid[:, n % 2, :], ubank[n % 2][:, :], gate[:, n % 2, :], ALU.mult)\
                        .then_inc(hidden, 1)
                    dve.wait_ge(hidden, n + 1)
                    dve.sem_inc(multiplied, 1)
                with dve.Fori(0, TURNS) as it:
                    for n in range(PER):
                        s, blk = divmod(n, BLK)
                        k = it * PER + PRE + n
                        if blk == 0:
                            dve.wait_ge(cw_here[s], it * 32 + 32)
                        dve.wait_ge(gated, k + 1)
                        nc.vector.tensor_tensor(prod[:, n % 2, :], ubank[n % 2][:, :], gate[:, n % 2, :], ALU.mult)\
                            .then_inc(multiplied, 1)
                        dve.wait_ge(multiplied, k + 1)
                        dve.wait_ge(down_done, k - 1)
                        nc.vector.tensor_tensor(hid[:, n % 2, :], prod[:, n % 2, :], cslot[s][:, blk * S:(blk + 1) * S],
                                                ALU.mult).then_inc(hidden, 1)
                for c in range(B):
                    dve.wait_ge(turned_back, c + 1)
                    x = T.X[:, c * TPB:(c + 1) * TPB, :]
                    nc.vector.tensor_tensor(x, x, T.bank[4 + c][:, :].rearrange("p (t d) -> p t d", t=TPB), ALU.add)


def top_groups_then_experts(nc, T, rt, link, score, bias, NG, TG, K, mask):
    E = score.shape[2]
    n = E // NG
    V = rt.sb("V", [P, NT, E])
    c = rt.sb("c", [P, NT * E])
    O = rt.sb("O", [P, NT * E])
    m = rt.sb("m", [P, NT * NG])
    best = rt.sb("best", [P, NT * NG])
    gs = rt.sb("gs", [P, NT, NG])
    gm = rt.sb("gm", [P, NT])
    sfc = rt.sb("sfc", [P, NT, E])
    rev = T.rev
    def groups(t):
        return t.rearrange("p (g n) -> p g n", n=n)
    Vg = V[:, :, :].rearrange("p t (g n) -> p (t g) n", n=n)
    flat_gs = gs[:, :, :].rearrange("p t g -> p (t g)")
    link(nc.vector.tensor_tensor(sfc[:, :, :], score[:, :, :], tiled(bias[:, :], NT), ALU.add))
    link(nc.vector.tensor_copy(V[:, :, :], sfc[:, :, :]))
    link(nc.vector.tensor_reduce(best[:, :], Vg, axis=AX, op=ALU.max))
    pick_max(nc, link, Vg, rev[:, 64 - n:64], m[:, :], groups(c[:, :]), groups(O[:, :]))
    link(nc.vector.tensor_reduce(m[:, :], Vg, axis=AX, op=ALU.max))
    link(nc.vector.tensor_tensor(flat_gs, best[:, :], m[:, :], ALU.add))
    g = NT * NG
    for _ in range(TG):
        pick_max(nc, link, gs[:, :, :], rev[:, 64 - NG:64], gm[:, :], c[:, 0:g].rearrange("p (t g) -> p t g", g=NG),
                 O[:, 0:g].rearrange("p (t g) -> p t g", g=NG))
    link(nc.vector.tensor_scalar(m[:, :], flat_gs, -2.0 * BIG, BIG, ALU.is_lt, ALU.mult))
    link(nc.vector.tensor_scalar(m[:, :], m[:, :], -BIG, None, ALU.add))
    link(nc.vector.tensor_tensor(Vg, sfc[:, :, :].rearrange("p t (g n) -> p (t g) n", n=n), spread(m[:, :], n), ALU.add))
    choose(nc, T, rt, link, V, K, c, O, gm)
    link(nc.vector.tensor_scalar(mask[:, :, :], V[:, :, :], -2.0 * BIG, None, ALU.is_lt))


def choose(nc, T, rt, link, V, K, c, O, gm):
    E = V.shape[2]
    if K == 8:
        top = rt.sb("top", [P, NT, 8])
        for t in range(NT):
            last = nc.vector.max(top[:, t, :], V[:, t, :])
        link(last)
        for t in range(NT):
            last = nc.vector.match_replace(V[:, t, :], top[:, t, :], V[:, t, :], -3.0 * BIG)
        link(last)
        return
    for _ in range(K):
        pick_max(nc, link, V[:, :, :], T.rev[:, 64 - E:64], gm[:, :], c[:, :].rearrange("p (t e) -> p t e", e=E),
                 O[:, :].rearrange("p (t e) -> p t e", e=E))


def normalized(nc, rt, link, score, mask, cw, scale, floor, clip):
    total = rt.sb("total", [P, NT])
    E = score.shape[2]
    link(nc.vector.tensor_tensor(cw[:, :, :], score[:, :, :], mask[:, :, :], ALU.mult))
    link(nc.vector.tensor_reduce(total[:, :], cw[:, :, :], axis=AX, op=ALU.add))
    link(nc.vector.tensor_scalar(total[:, :], total[:, :], floor, None, ALU.max if clip else ALU.add))
    link(nc.vector.reciprocal(total[:, :], total[:, :]))
    link(nc.vector.tensor_tensor(cw[:, :, :], cw[:, :, :], spread(total[:, :], E), ALU.mult))
    if scale != 1.0:
        link(nc.vector.tensor_scalar(cw[:, :, :], cw[:, :, :], scale, None, ALU.mult))


def l0_moe(nc, T, A):
    def route(nc, T, rt, dve, link, score, mask, cw):
        top_groups_then_experts(nc, T, rt, link, score, T.router_bias, NG=4, TG=2, K=4, mask=mask)
        normalized(nc, rt, link, score, mask, cw, 2.5, 1e-20, False)
    expert_ffn(nc, T, A, "l0m", 16, 4, route, add_input=True)


def l1_moe(nc, T, A):
    def route(nc, T, rt, dve, link, score, mask, cw):
        top_groups_then_experts(nc, T, rt, link, score, T.router_bias, NG=8, TG=4, K=8, mask=mask)
        normalized(nc, rt, link, score, mask, cw, 1.0, 1e-20, False)
    expert_ffn(nc, T, A, "l1m", 64, 8, route, NSH=2)


def l3_moe(nc, T, A):
    E, CAP = 32, 2 * 512 * 4 // 32

    def route(nc, T, rt, dve, link, score, mask, cw):
        V = rt.sb("V", [P, NT, E])
        c, O = rt.sb("c", [P, NT * E]), rt.sb("O", [P, NT * E])
        gm = rt.sb("gm", [P, NT])
        pos = rt.sb("pos", [P, NT, E])
        before = rt.sb("before", [P, NT, E])
        link(nc.vector.tensor_tensor(V[:, :, :], score[:, :, :], tiled(T.router_bias[:, :], NT), ALU.add))
        choose(nc, T, rt, link, V, 4, c, O, gm)
        nc.vector.tensor_scalar(mask[:, :, :], V[:, :, :], -2.0 * BIG, None, ALU.is_lt).then_inc(T.chosen, 1)
        dve.wait_ge(T.chosen, 1)
        normalized(nc, rt, link, score, mask, cw, 1.0, 1e-12, True)
        dve.wait_ge(T.counts, 2)
        link(nc.vector.memset(before[:, 0, :], 0.0))
        for t in range(1, NT):
            link(nc.vector.tensor_tensor(before[:, t, :], before[:, t - 1, :], T.bank[3][:, (t - 1) * E:t * E], ALU.add))
        link(nc.vector.tensor_tensor(pos[:, :, :], before[:, :, :], T.bank[2][:, :].rearrange("p (t e) -> p t e", e=E), ALU.add))
        link(nc.vector.tensor_scalar(pos[:, :, :], pos[:, :, :], float(CAP), None, ALU.is_lt))
        link(nc.vector.tensor_tensor(cw[:, :, :], cw[:, :, :], pos[:, :, :], ALU.mult))
    expert_ffn(nc, T, A, "l3m", 32, 4, route, half_weights=True, counted=True)


def l1_attention(nc, T, A):
    H, HD = 16, 8
    KW = D + H
    with Stage(nc, "l1a") as st:
        wq = st.sb("wq", [P, D])
        wkv = st.sb("wkv", [P, 2 * D])
        wo = st.sb("wo", [P, D])
        bo = st.sb("bo", [P, D])
        same = st.sb("same", [P, KW])
        xb = st.sb("xb", [P, S])
        qm, qe, qf = (st.sb(n, [P, S]) for n in ("qm", "qe", "qf"))
        km, ke, kf = (st.sb(n, [P, TPB, D]) for n in ("km", "ke", "kf"))
        v = st.sb("v", [P, TPB, D + 1])
        kv = st.sb("kv", [P, KW])
        den = st.sb("den", [P, TPB, H])
        y = st.sb("y", [P, TPB, D])
        yT = st.sb("yT", [P, S])
        names = ("loaded", "x_ready", "projected", "mins", "exps", "features", "kv_done", "kv_ready", "out_done",
                 "den_step", "y_ready", "y_turned", "yT_ready", "proj_done", "added", "ones")
        loaded, x_ready, projected, mins, exps, features, kv_done, kv_ready, out_done, den_step, y_ready, y_turned, \
            yT_ready, proj_done, added, ones = (st.sem(n) for n in names)
        loads = [(wq[:, :], A["l1a_wq"]), (wkv[:, :], A["l1a_wkv"]), (wo[:, :], A["l1a_wo"]), (bo[:, :], A["l1a_bo"]),
                 (same[:, :], A["l1a_same"])]
        layernorm(nc, T, T.X[:, :, :], T.LNX[:, :, :], T.LNT[:, :], loads, loaded)
        k_psum = [T.bank[1 + i][:, :].rearrange("p (t c) -> p t c", t=2) for i in range(2)]
        o_psum = [T.bank[4 + i][:, 0:2 * KW].rearrange("p (t c) -> p t c", t=2) for i in range(2)]
        with nc.Block() as block:
            @block.scalar
            def _(act):
                act.wait_ge(ones, 1)
                with act.Fori(0, B) as b:
                    nc.scalar.activation(xb[:, :], T.LNT[:, bass.ds(b * S, S)], ACT.Copy).then_inc(x_ready, 1)
                    act.wait_ge(mins, b + 1)
                    nc.scalar.activation(qe[:, :], qm[:, :], ACT.Exp)
                    nc.scalar.activation(ke[:, :, :], km[:, :, :], ACT.Exp)
                    for i in range(2):
                        last = nc.scalar.activation(v[:, 2 * i:2 * i + 2, 0:D], k_psum[i][:, :, D:2 * D], ACT.Copy)
                    last.then_inc(exps, 1)
                    act.wait_ge(y_turned, b + 1)
                    nc.scalar.activation(yT[:, :], T.bank[6][:, :], ACT.Copy).then_inc(yT_ready, 1)

            @block.tensor
            def _(pe):
                pe.wait_ge(loaded, 16 * len(loads))
                with pe.Fori(0, B) as b:
                    pe.wait_ge(x_ready, b + 1)
                    nc.tensor.matmul(T.bank[0][:, :], wq[:, :], xb[:, :], start=True, stop=True)
                    for t in range(TPB):
                        last = nc.tensor.matmul(k_psum[t // 2][:, t % 2, :], xb[:, t * P:(t + 1) * P], wkv[:, :],
                                                start=True, stop=True)
                    last.then_inc(projected, 1)
                    pe.wait_ge(features, b + 1)
                    for t in range(TPB):
                        last = nc.tensor.matmul(T.bank[3][:, 0:D + 1], kf[:, t, :], v[:, t, :], start=(t == 0),
                                                stop=(t == TPB - 1))
                    last.then_inc(kv_done, 1)
                    pe.wait_ge(kv_ready, b + 1)
                    for t in range(TPB):
                        last = nc.tensor.matmul(o_psum[t // 2][:, t % 2, :], qf[:, t * P:(t + 1) * P], kv[:, :],
                                                start=True, stop=True)
                    last.then_inc(out_done, 1)
                    pe.wait_ge(y_ready, b + 1)
                    for t in range(TPB):
                        last = nc.tensor.transpose(T.bank[6][:, t * P:(t + 1) * P], y[:, t, :], T.ident[:, :])
                    last.then_inc(y_turned, 1)
                    pe.wait_ge(yT_ready, b + 1)
                    for t in range(TPB):
                        last = nc.tensor.matmul(T.bank[7][:, t * D:(t + 1) * D], yT[:, t * P:(t + 1) * P], wo[:, :],
                                                start=True, stop=True)
                    last.then_inc(proj_done, 1)
                    pe.wait_ge(added, b + 1)

            @block.vector
            def _(dve):
                link = chain(T, dve)
                nc.vector.memset(v[:, :, :], 1.0).then_inc(ones, 1)
                dve.wait_ge(loaded, 16 * len(loads))
                link(nc.vector.tensor_tensor(T.X[:, :, :], T.X[:, :, :], tiled(bo[:, :], NT), ALU.add))
                with dve.Fori(0, B) as b:
                    dve.wait_ge(projected, b + 1)
                    nc.vector.tensor_scalar(qm[:, :], T.bank[0][:, :], 0.0, None, ALU.min)
                    for i in range(2):
                        last = nc.vector.tensor_scalar(km[:, 2 * i:2 * i + 2, :], k_psum[i][:, :, 0:D], 0.0, None, ALU.min)
                    last.then_inc(mins, 1)
                    dve.wait_ge(exps, b + 1)
                    nc.vector.scalar_tensor_tensor(qf[:, :], T.bank[0][:, :], 0.0, qe[:, :], ALU.max, ALU.add)
                    for i in range(2):
                        last = nc.vector.scalar_tensor_tensor(kf[:, 2 * i:2 * i + 2, :], k_psum[i][:, :, 0:D], 0.0,
                                                              ke[:, 2 * i:2 * i + 2, :], ALU.max, ALU.add)
                    last.then_inc(features, 1)
                    dve.wait_ge(kv_done, b + 1)
                    nc.vector.tensor_tensor(kv[:, 0:D], T.bank[3][:, 0:D], same[:, 0:D], ALU.mult)
                    nc.vector.tensor_scalar(kv[:, D:KW], same[:, D:KW], T.bank[3][:, D:D + 1], None, ALU.mult)\
                        .then_inc(kv_ready, 1)
                    dve.wait_ge(out_done, b + 1)
                    for i in range(2):
                        last = nc.vector.tensor_scalar(den[:, 2 * i:2 * i + 2, :], o_psum[i][:, :, D:KW], 1e-6, None, ALU.add)
                    last.then_inc(den_step, 1)
                    dve.wait_ge(den_step, b * 2 + 1)
                    nc.vector.reciprocal(den[:, :, :], den[:, :, :]).then_inc(den_step, 1)
                    dve.wait_ge(den_step, b * 2 + 2)
                    for t in range(TPB):
                        last = nc.vector.tensor_tensor(y[:, t, :].rearrange("p (h d) -> p h d", h=H),
                                                       o_psum[t // 2][:, t % 2, 0:D].rearrange("p (h d) -> p h d", h=H),
                                                       spread(den[:, t, :], HD), ALU.mult)
                    last.then_inc(y_ready, 1)
                    dve.wait_ge(proj_done, b + 1)
                    x = T.X[:, bass.ds(b * TPB, TPB), :]
                    nc.vector.tensor_tensor(x, x, T.bank[7][:, :].rearrange("p (t c) -> p t c", t=TPB), ALU.add)\
                        .then_inc(added, 1)


def l1_coattention(nc, T, A):
    with Stage(nc, "l1c") as st:
        cols = st.sb("cols", [P, 4])
        w = st.sb("w", [P, 4, D])
        bias = st.sb("bias", [P, D])
        c3 = st.sb("c3", [P, B * L])
        w2 = st.sb("w2", [P, P])
        drow = st.sb("drow", [P, B, L])
        sim = st.sb("sim", [P, 2, TPB, L])
        mx = st.sb("mx", [P, NT])
        rs = st.sb("rs", [P, NT])
        prT = st.sb("prT", [L, 2, S])
        hq = st.sb("hq", [P, 2, S])
        ehq = st.sb("ehq", [P, 2, S])
        row = st.sb("row", [1, 2, S])
        rowmax = st.sb("rowmax", [1, B])
        rowsum = st.sb("rowsum", [1, B])
        ecol = st.sb("ecol", [P, NT])
        w14 = st.sb("w14", [P, B, D])
        names = ("loaded", "prepared", "drow_done", "drow_ready", "sim_done", "centred", "expd", "normal", "turned",
                 "prT_ready", "hq_done", "hq_ready", "row_done", "rowmax_ready", "row_exp", "row_ready", "col_done",
                 "col_ready", "hc_done", "w_ready", "out_done", "added", "hq_taken")
        loaded, prepared, drow_done, drow_ready, sim_done, centred, expd, normal, turned, prT_ready, hq_done, hq_ready, \
            row_done, rowmax_ready, row_exp, row_ready, col_done, col_ready, hc_done, w_ready, out_done, added, \
            hq_taken = (st.sem(n) for n in names)
        loads = [(cols[:, :], A["l1c_cols"]), (w[:, :, :], A["l1c_w"]), (bias[:, :], A["l1c_bias"])]
        layernorm(nc, T, T.X[:, :, :], T.LNX[:, :, :], T.LNT[:, :], loads, loaded)
        with nc.Block() as block:
            @block.tensor
            def _(pe):
                pe.wait_ge(prepared, 1)
                nc.tensor.matmul(T.bank[0][:, 0:B * L], w2[:, :], T.CTXT[:, :], start=True, stop=True).then_inc(drow_done, 1)
                pe.wait_ge(drow_ready, 1)
                for b in range(B):
                    if b >= 2:
                        pe.wait_ge(centred, b - 1)
                    for t in range(TPB):
                        n = b * TPB + t
                        last = nc.tensor.matmul(T.bank[b % 2][:, t * L:(t + 1) * L], T.LNT[:, n * P:(n + 1) * P],
                                                c3[:, b * L:(b + 1) * L], start=True, stop=True)
                    last.then_inc(sim_done, 1)
                    pe.wait_ge(normal, b + 1)
                    for t in range(TPB):
                        last = nc.tensor.transpose(T.bank[2][0:L, t * P:(t + 1) * P], sim[:, b % 2, t, :], T.ident[:, :])
                    last.then_inc(turned, 1)
                    for t in range(TPB):
                        n = b * TPB + t
                        last = nc.tensor.matmul(T.bank[4][0:1, t * P:(t + 1) * P], mx[:, n:n + 1], T.ident[:, :],
                                                start=True, stop=True)
                    last.then_inc(row_done, 1)
                    pe.wait_ge(prT_ready, b + 1)
                    nc.tensor.matmul(T.bank[3][:, :], T.CTX[:, b, :], prT[:, b % 2, :], start=True, stop=True).then_inc(hq_done, 1)
                    pe.wait_ge(row_ready, b + 1)
                    for t in range(TPB):
                        last = nc.tensor.matmul(T.bank[5][:, t:t + 1], row[0:1, b % 2, t * P:(t + 1) * P],
                                                T.ident[0:1, 0:1], start=True, stop=True)
                    last.then_inc(col_done, 1)
                    pe.wait_ge(col_ready, b + 1)
                    for t in range(TPB):
                        n = b * TPB + t
                        last = nc.tensor.matmul(T.bank[7][:, 0:1], T.LNX[:, n, :], ecol[:, n:n + 1], start=(t == 0),
                                                stop=(t == TPB - 1))
                    last.then_inc(hc_done, 1)
                    pe.wait_ge(w_ready, b + 1)
                    pe.wait_ge(hq_ready, b + 1)
                    for t in range(TPB):
                        n = b * TPB + t
                        cut = slice(t * P, (t + 1) * P)
                        o = T.bank[6][:, t * D:(t + 1) * D]
                        nc.tensor.matmul(o, T.LNT[:, n * P:(n + 1) * P], w14[:, b, :], start=True, stop=False)
                        nc.tensor.matmul(o, hq[:, b % 2, cut], w[:, 1, :], start=False, stop=False)
                        last = nc.tensor.matmul(o, ehq[:, b % 2, cut], w[:, 2, :], start=False, stop=True)
                    last.then_inc(out_done, 1)
                    pe.wait_ge(added, b + 1)

            @block.scalar
            def _(act):
                for b in range(B):
                    act.wait_ge(centred, b + 1)
                    nc.scalar.activation(sim[:, b % 2, :, :], sim[:, b % 2, :, :], ACT.Exp).then_inc(expd, 1)
                    act.wait_ge(turned, b + 1)
                    nc.scalar.activation(prT[:, b % 2, :], T.bank[2][0:L, :], ACT.Copy).then_inc(prT_ready, 1)
                    act.wait_ge(rowmax_ready, b + 1)
                    nc.scalar.activation(row[0:1, b % 2, :], T.bank[4][0:1, :], ACT.Exp, bias=rowmax[0:1, b:b + 1],
                                         accum_out=rowsum[0:1, b:b + 1]).then_inc(row_exp, 1)
                    act.wait_ge(col_done, b + 1)
                    nc.scalar.activation(ecol[:, b * TPB:(b + 1) * TPB], T.bank[5][:, 0:TPB], ACT.Copy).then_inc(col_ready, 1)

            @block.vector
            def _(dve):
                link = chain(T, dve)
                dve.wait_ge(loaded, 16 * len(loads))
                nc.vector.tensor_scalar(c3[:, :], T.CTXT[:, :], cols[:, 2:3], cols[:, 0:1], ALU.mult, ALU.add)
                nc.vector.tensor_scalar(w2[:, :], T.zeros[:, :], cols[:, 1:2], None, ALU.add).then_inc(prepared, 1)
                link(nc.vector.tensor_tensor(T.X[:, :, :], T.X[:, :, :], tiled(bias[:, :], NT), ALU.add))
                dve.wait_ge(drow_done, 1)
                nc.vector.tensor_scalar(drow[:, :, :], T.bank[0][:, 0:B * L].rearrange("p (b l) -> p b l", b=B),
                                        cols[:, 3:4], None, ALU.add).then_inc(drow_ready, 1)
                dve.wait_ge(drow_ready, 1)
                for b in range(B):
                    z = sim[:, b % 2, :, :]
                    m = mx[:, b * TPB:(b + 1) * TPB]
                    r = rs[:, b * TPB:(b + 1) * TPB]
                    dve.wait_ge(sim_done, b + 1)
                    link(nc.vector.tensor_tensor(z, T.bank[b % 2][:, 0:TPB * L].rearrange("p (t l) -> p t l", t=TPB),
                                                 tiled(drow[:, b, :], TPB), ALU.add))
                    link(nc.vector.tensor_reduce(m, z, axis=AX, op=ALU.max))
                    nc.vector.tensor_tensor(z, z, spread(m, L), ALU.subtract).then_inc(centred, 1)
                    dve.wait_ge(expd, b + 1)
                    link(nc.vector.tensor_reduce(r, z, axis=AX, op=ALU.add))
                    link(nc.vector.reciprocal(r, r))
                    nc.vector.tensor_tensor(z, z, spread(r, L), ALU.mult).then_inc(normal, 1)
                    dve.wait_ge(row_done, b + 1)
                    nc.vector.tensor_reduce(rowmax[0:1, b:b + 1], T.bank[4][0:1, :], axis=AX, op=ALU.max, negate=True)\
                        .then_inc(rowmax_ready, 1)
                    dve.wait_ge(hq_done, b + 1)
                    nc.vector.tensor_copy(hq[:, b % 2, :], T.bank[3][:, :])
                    nc.vector.tensor_tensor(ehq[:, b % 2, :], T.bank[3][:, :], T.LNT[:, b * S:(b + 1) * S], ALU.mult)\
                        .then_inc(hq_ready, 1)
                    dve.wait_ge(row_exp, b + 1)
                    link(nc.vector.reciprocal(rowsum[0:1, b:b + 1], rowsum[0:1, b:b + 1]))
                    nc.vector.tensor_scalar(row[0:1, b % 2, :], row[0:1, b % 2, :], rowsum[0:1, b:b + 1], None, ALU.mult)\
                        .then_inc(row_ready, 1)
                    dve.wait_ge(hc_done, b + 1)
                    nc.vector.scalar_tensor_tensor(w14[:, b, :], w[:, 3, :], T.bank[7][:, 0:1], w[:, 0, :], ALU.mult,
                                                   ALU.add).then_inc(w_ready, 1)
                    dve.wait_ge(out_done, b + 1)
                    x = T.X[:, b * TPB:(b + 1) * TPB, :]
                    nc.vector.tensor_tensor(x, x, T.bank[6][:, :].rearrange("p (t d) -> p t d", t=TPB), ALU.add)\
                        .then_inc(added, 1)


def l2_attention(nc, T, A):
    with Stage(nc, "l2a") as st:
        w = st.sb("w", [P, 3 * D])
        xb = st.sb("xb", [P, S])
        q, k = st.sb("q", [P, S]), st.sb("k", [P, S])
        v = st.sb("v", [P, TPB, D])
        e = st.sb("e", [P, TPB, S])
        nmx, rs = st.sb("nmx", [P, TPB]), st.sb("rs", [P, TPB])
        names = ("loaded", "x_ready", "projected", "qk_ready", "scored", "max_ready", "expd", "v_scaled", "out_done",
                 "added", "v_step")
        loaded, x_ready, projected, qk_ready, scored, max_ready, expd, v_scaled, out_done, added, v_step = (
            st.sem(n) for n in names)
        loads = [(w[:, :], A["l2a_w"])]
        layernorm(nc, T, T.X[:, :, :], T.LNX[:, :, :], T.LNT[:, :], loads, loaded)
        with nc.Block() as block:
            @block.tensor
            def _(pe):
                pe.wait_ge(loaded, 16)
                with pe.Fori(0, B) as b:
                    pe.wait_ge(x_ready, b + 1)
                    for i in range(2):
                        nc.tensor.matmul(T.bank[i][:, :], w[:, i * D:(i + 1) * D], xb[:, :], start=True, stop=True)\
                            .then_inc(projected, 1)
                    for t in range(TPB):
                        last = nc.tensor.matmul(T.bank[2][:, t * D:(t + 1) * D], xb[:, t * P:(t + 1) * P],
                                                w[:, 2 * D:3 * D], start=True, stop=True)
                    last.then_inc(projected, 1)
                    pe.wait_ge(qk_ready, b + 1)
                    for t in range(TPB):
                        nc.tensor.matmul(T.bank[3 + t][:, :], k[:, t * P:(t + 1) * P], q[:, :], start=True, stop=True)\
                            .then_inc(scored, 1)
                    pe.wait_ge(v_scaled, b + 1)
                    for t in range(TPB):
                        for j in range(TPB):
                            last = nc.tensor.matmul(T.bank[7][:, t * D:(t + 1) * D], e[:, j, t * P:(t + 1) * P], v[:, j, :],
                                                    start=(j == 0), stop=(j == TPB - 1))
                    last.then_inc(out_done, 1)
                    pe.wait_ge(added, b + 1)

            @block.scalar
            def _(act):
                with act.Fori(0, B) as b:
                    nc.scalar.activation(xb[:, :], T.LNT[:, bass.ds(b * S, S)], ACT.Copy).then_inc(x_ready, 1)
                    act.wait_ge(projected, b * 3 + 2)
                    nc.scalar.activation(q[:, :], T.bank[0][:, :], ACT.Copy, scale=D ** -0.5)
                    nc.scalar.activation(k[:, :], T.bank[1][:, :], ACT.Copy).then_inc(qk_ready, 1)
                    for t in range(TPB):
                        act.wait_ge(max_ready, b * TPB + t + 1)
                        nc.scalar.activation(e[:, t, :], T.bank[3 + t][:, :], ACT.Exp, bias=nmx[:, t:t + 1],
                                             accum_out=rs[:, t:t + 1]).then_inc(expd, 1)

            @block.vector
            def _(dve):
                with dve.Fori(0, B) as b:
                    for t in range(TPB):
                        dve.wait_ge(scored, b * TPB + t + 1)
                        nc.vector.tensor_reduce(nmx[:, t:t + 1], T.bank[3 + t][:, :], axis=AX, op=ALU.max, negate=True)\
                            .then_inc(max_ready, 1)
                    dve.wait_ge(expd, b * TPB + TPB)
                    nc.vector.reciprocal(rs[:, :], rs[:, :]).then_inc(v_step, 1)
                    dve.wait_ge(v_step, b + 1)
                    nc.vector.tensor_tensor(v[:, :, :], T.bank[2][:, :].rearrange("p (t d) -> p t d", t=TPB),
                                            spread(rs[:, :], D), ALU.mult).then_inc(v_scaled, 1)
                    dve.wait_ge(out_done, b + 1)
                    x = T.X[:, bass.ds(b * TPB, TPB), :]
                    nc.vector.tensor_tensor(x, x, T.bank[7][:, :].rearrange("p (t c) -> p t c", t=TPB), ALU.add)\
                        .then_inc(added, 1)


def l3_attention(nc, T, A):
    EPS = 1e-9
    with Stage(nc, "l3a") as st:
        w = st.sb("w", [P, 3 * D])
        tril = st.sb("tril", [P, 2, P])
        eps = st.sb("eps", [P, P])
        q = st.sb("q", [P, N])
        k = st.sb("k", [P, N])
        v = st.sb("v", [P, NT, D])
        m = st.sb("m", [P, S])
        z = st.sb("z", [P, B, S])
        zT = st.sb("zT", [P, B, S])
        total = st.sb("total", [P, S])
        names = ("loaded", "projected", "taken", "scored", "first", "centred", "expd", "normal", "turned", "zT_ready",
                 "out_done", "added", "eps_ready")
        loaded, projected, taken, scored, first, centred, expd, normal, turned, zT_ready, out_done, added, eps_ready = (
            st.sem(n) for n in names)
        loads = [(w[:, :], A["l3a_w"]), (tril[:, :, :], A["tril"])]
        layernorm(nc, T, T.X[:, :, :], T.LNX[:, :, :], T.LNT[:, :], loads, loaded)
        with nc.Block() as block:
            @block.tensor
            def _(pe):
                pe.wait_ge(loaded, 16 * len(loads))
                for b in range(B):
                    for i in range(3):
                        n = 3 * b + i
                        if n >= 6:
                            pe.wait_ge(taken, n - 5)
                        bank = T.bank[n % 6]
                        xT = T.LNT[:, b * S:(b + 1) * S]
                        if i == 0:
                            last = nc.tensor.matmul(bank[:, :], w[:, 0:D], xT, start=True, stop=True)
                        for t in range(TPB if i else 0):
                            x = xT.rearrange("p (r c) -> p c r", c=TPB)[:, t, :] if i == 1 else xT[:, t * P:(t + 1) * P]
                            last = nc.tensor.matmul(bank[:, t * D:(t + 1) * D], x, w[:, i * D:(i + 1) * D], start=True,
                                                    stop=True)
                        last.then_inc(projected, 1)
                pe.wait_ge(taken, 3 * B)
                pe.wait_ge(eps_ready, 1)
                for t in range(TPB):
                    W = (t + 1) * P
                    if t:
                        pe.wait_ge(centred, t)
                    for b in range(B):
                        last = nc.tensor.matmul(T.bank[b][:, 0:W], q[:, b * S + t * P:b * S + (t + 1) * P],
                                                k[:, b * S:b * S + W], start=True, stop=True)
                    last.then_inc(scored, 1)
                    pe.wait_ge(normal, t + 1)
                    for b in range(B):
                        n = t * B + b
                        if n >= 2:
                            pe.wait_ge(zT_ready, n - 1)
                        for j in range(t + 1):
                            last = nc.tensor.transpose(T.bank[4 + n % 2][:, j * P:(j + 1) * P], z[:, b, j * P:(j + 1) * P],
                                                       T.ident[:, :])
                        last.then_inc(turned, 1)
                    pe.wait_ge(zT_ready, B * (t + 1))
                    if t >= 2:
                        pe.wait_ge(added, t - 1)
                    for b in range(B):
                        for j in range(TPB):
                            p = zT[:, b, j * P:(j + 1) * P] if j <= t else eps[:, :]
                            last = nc.tensor.matmul(T.bank[6 + t % 2][:, b * D:(b + 1) * D], p, v[:, b * TPB + j, :],
                                                    start=(j == 0), stop=(j == TPB - 1))
                    last.then_inc(out_done, 1)

            @block.scalar
            def _(act):
                for n in range(3 * B):
                    b, i = divmod(n, 3)
                    act.wait_ge(projected, n + 1)
                    src = T.bank[n % 6][:, :]
                    if i == 0:
                        out = nc.scalar.activation(q[:, b * S:(b + 1) * S], src, ACT.Copy, scale=D ** -0.5)
                    elif i == 1:
                        out = nc.scalar.activation(k[:, b * S:(b + 1) * S], src, ACT.Copy)
                    else:
                        out = nc.scalar.activation(v[:, b * TPB:(b + 1) * TPB, :],
                                                   src.rearrange("p (t d) -> p t d", t=TPB), ACT.Copy)
                    out.then_inc(taken, 1)
                for t in range(TPB):
                    W = (t + 1) * P
                    act.wait_ge(scored, t + 1)
                    if t:
                        act.wait_ge(centred, t)
                    nc.scalar.activation(m[:, 0:W], T.bank[0][:, 0:W], ACT.Copy).then_inc(first, 1)
                    act.wait_ge(centred, t + 1)
                    nc.scalar.activation(z[:, :, 0:W], z[:, :, 0:W], ACT.Exp).then_inc(expd, 1)
                    for b in range(B):
                        act.wait_ge(turned, B * t + b + 1)
                        nc.scalar.activation(zT[:, b, 0:W], T.bank[4 + b % 2][:, 0:W], ACT.Copy).then_inc(zT_ready, 1)

            @block.vector
            def _(dve):
                link = chain(T, dve)
                nc.vector.memset(eps[:, :], EPS).then_inc(eps_ready, 1)
                dve.wait_ge(loaded, 16 * len(loads))
                for t in range(TPB):
                    W = (t + 1) * P
                    dve.wait_ge(first, t + 1)
                    mm = m[:, 0:W]
                    for b in range(1, B):
                        link(nc.vector.tensor_tensor(mm, T.bank[b][:, 0:W], mm, ALU.max))
                    if t:
                        dve.wait_ge(turned, B * t)
                    for b in range(B):
                        last = nc.vector.tensor_tensor(z[:, b, 0:W], T.bank[b][:, 0:W], mm, ALU.subtract)
                    last.then_inc(centred, 1)
                    dve.wait_ge(expd, t + 1)
                    link(nc.vector.tensor_reduce(total[:, 0:W], z[:, :, 0:W].rearrange("p b w -> p w b"), axis=AX, op=ALU.add))
                    link(nc.vector.reciprocal(total[:, 0:W], total[:, 0:W]))
                    link(nc.vector.tensor_tensor(z[:, :, 0:W], z[:, :, 0:W], tiled(total[:, 0:W], B), ALU.mult))
                    last_block = z[:, :, t * P:W]
                    link(nc.vector.tensor_tensor(last_block, last_block, tiled(tril[:, 0, :], B), ALU.mult))
                    nc.vector.tensor_tensor(last_block, last_block, tiled(tril[:, 1, :], B), ALU.add).then_inc(normal, 1)
                    dve.wait_ge(out_done, t + 1)
                    x = T.X[:, :, :].rearrange("p (b t) d -> p t b d", b=B)[:, t, :, :]
                    nc.vector.tensor_tensor(x, x, T.bank[6 + t % 2][:, :].rearrange("p (b d) -> p b d", b=B), ALU.add)\
                        .then_inc(added, 1)


def l2_moe_attention(nc, T, A):
    H, HD, E = 16, 64, 8
    PAIRS, SLOTS = H // 2, 2
    TURNS = PAIRS // SLOTS
    GROUPS = SLOTS * B
    UPG = 2 * TPB
    UNITS = GROUPS * UPG
    PIECES = 4 + UPG
    QK = 4 * P
    WV = QK + 2 * E * HD
    WTOT = WV + 2 * 4 * D
    F = 4 * D
    with Stage(nc, "l2m") as st:
        gates = st.sb("gates", [P, NT, 2, H, E])
        ln1, ln2 = st.sb("ln1", [P, 2, D]), st.sb("ln2", [P, 2, D])
        b1, b2 = st.sb("b1", [P, 4]), st.sb("b2", [P, D])
        trig = st.sb("trig", [P, 4, S])
        loaded = st.sem("loaded")
        loads = [(ln1[:, :, :], A["l2m_ln1"]), (ln2[:, :, :], A["l2m_ln2"]), (b1[:, :], A["l2m_b1"]), (b2[:, :], A["l2m_b2"]),
                 (trig[:, :, :], A["l2m_trig"])]

        with Stage(nc, "l2g") as sg:
            wsel = sg.sb("wsel", [P, 2 * H * E])
            V = sg.sb("V", [P, NT * 2 * H, E])
            c = sg.sb("c", [P, NT * 2 * H, E])
            O = sg.sb("O", [P, NT * 2 * H, E])
            m = sg.sb("m", [P, NT * 2 * H])
            logits, squashed = sg.sem("logits"), sg.sem("squashed")
            flat = gates[:, :, :, :, :].rearrange("p t v h e -> p (t v h) e")
            layernorm(nc, T, T.X[:, :, :], T.LNX[:, :, :], T.LNT[:, :], loads + [(wsel[:, :], A["l2m_wsel"])], loaded)
            with nc.Block() as block:
                @block.tensor
                def _(pe):
                    pe.wait_ge(loaded, 16 * len(loads) + 16)
                    for t in range(NT):
                        nc.tensor.matmul(T.bank[t // 2][:, t % 2 * 256:t % 2 * 256 + 256], T.LNT[:, t * P:(t + 1) * P],
                                         wsel[:, :], start=True, stop=True).then_inc(logits, 1)

                @block.scalar
                def _(act):
                    for i in range(NT // 2):
                        act.wait_ge(logits, 2 * i + 2)
                        nc.scalar.activation(gates[:, 2 * i:2 * i + 2, :, :, :].rearrange("p t v h e -> p (t v h e)"),
                                             T.bank[i][:, :], ACT.Sigmoid).then_inc(squashed, 1)

                @block.vector
                def _(dve):
                    link = chain(T, dve)
                    dve.wait_ge(squashed, NT // 2)
                    link(nc.vector.tensor_copy(V[:, :, :], flat))
                    for _ in range(2):
                        pick_max(nc, link, V[:, :, :], T.rev[:, 64 - E:64], m[:, :], c[:, :, :], O[:, :, :])
                    link(nc.vector.tensor_scalar(c[:, :, :], V[:, :, :], -2.0 * BIG, None, ALU.is_lt))
                    link(nc.vector.tensor_tensor(flat, flat, c[:, :, :], ALU.mult))

        with Stage(nc, "l2h") as sh:
            slot = [sh.sb(f"w{i}", [P, WTOT]) for i in range(SLOTS)]
            plain, rotated = sh.sb("plain", [P, 2, S]), sh.sb("rotated", [P, 2, S])
            q, k = sh.sb("q", [P, 2, S]), sh.sb("k", [P, 2, S])
            vg = sh.sb("vg", [P, 2, E, HD])
            vs = sh.sb("vs", [P, 2, E // 2, HD])
            v = sh.sb("v", [P, 2, UPG, HD])
            pr, prT = sh.sb("pr", [P, 2, S]), sh.sb("prT", [P, 2, S])
            og, ogT = sh.sb("og", [P, 2, E, HD]), sh.sb("ogT", [P, 2, S])
            nmx, rs = sh.sb("nmx", [P, 4]), sh.sb("rs", [P, 4])
            go = sh.sb("go", [P, 4, E])
            gv_h = sh.sb("gv_h", [P, NT, 2 * SLOTS, E])
            go_h = sh.sb("go_h", [P, NT, 2 * SLOTS, E])
            arrived = [sh.sem(f"arrived{i}") for i in range(SLOTS)]
            names = ("gates_ready", "made", "read", "rot_step", "roped", "v_gated", "v_step", "v_ready", "scored", "maxed",
                     "expd", "turned", "copied", "pv_done", "o_step", "gated", "g_turned", "g_copied", "y_done", "added")
            gates_ready, made, read, rot_step, roped, v_gated, v_step, v_ready, scored, maxed, expd, turned, copied, pv_done, \
                o_step, gated, g_turned, g_copied, y_done, added = (sh.sem(n) for n in names)
            pj, sbank, tbank, obank, ybank = T.bank[0:2], T.bank[2:4], T.bank[4:6], T.bank[6], T.bank[7]

            def pieces_at(i):
                g, r = divmod(i, UPG)
                if g + 1 >= GROUPS or i < 0 or r >= PIECES // 2:
                    return []
                return [(g + 1, 2 * r), (g + 1, 2 * r + 1)]
            START = [(0, n) for n in range(PIECES)]

            with nc.Block() as block:
                @block.sync
                def _(sp):
                    for s in range(SLOTS):
                        sp.dma_start(slot[s][:, :], A["l2m_w"][s, :, :]).then_inc(arrived[s], 16)
                    with sp.Fori(0, TURNS - 1) as it:
                        for s in range(SLOTS):
                            sp.wait_ge(y_done, it * UNITS + (s + 1) * UNITS // SLOTS)
                            sp.dma_start(slot[s][:, :], A["l2m_w"][bass.ds(it * SLOTS + SLOTS + s, 1), :, :]
                                         .rearrange("a p c -> (a p) c")).then_inc(arrived[s], 16)

                @block.tensor
                def _(pe):
                    with pe.Fori(0, TURNS) as it:
                        def make(g, n):
                            s, b = divmod(g, B)
                            at = g * PIECES + n
                            if n == 0 and b == 0:
                                pe.wait_ge(arrived[s], it * 16 + 16)
                            if at >= 2:
                                pe.wait_ge(read, it * GROUPS * PIECES + at - 1)
                            if n < 4:
                                out = nc.tensor.matmul(pj[at % 2][:, :], slot[s][:, n * P:(n + 1) * P],
                                                       T.LNT[:, b * S:(b + 1) * S], start=True, stop=True)
                            else:
                                h, t = divmod(n - 4, TPB)
                                out = nc.tensor.matmul(pj[at % 2][:, :], T.LNT[:, b * S + t * P:b * S + (t + 1) * P],
                                                       slot[s][:, QK + h * S:QK + (h + 1) * S], start=True, stop=True)
                            out.then_inc(made, 1)
                        for g, n in START:
                            make(g, n)
                        for i in range(UNITS + 4):
                            if i < UNITS:
                                g, u = divmod(i, UPG)
                                h, t = divmod(u, TPB)
                                if u == 0:
                                    pe.wait_ge(roped, it * 2 * GROUPS + 2 * g + 2)
                                if i >= 2:
                                    pe.wait_ge(expd, it * UNITS + i - 1)
                                rows = slice(h * HD, (h + 1) * HD)
                                nc.tensor.matmul(sbank[i % 2][:, :], q[rows, g % 2, t * P:(t + 1) * P], k[rows, g % 2, :],
                                                 start=True, stop=True).then_inc(scored, 1)
                            j = i - 1
                            if 0 <= j < UNITS:
                                pe.wait_ge(expd, it * UNITS + j + 1)
                                if j >= 1:
                                    pe.wait_ge(copied, it * UNITS + j)
                                for t in range(TPB):
                                    last = nc.tensor.transpose(tbank[0][:, t * P:(t + 1) * P],
                                                               pr[:, j % 2, t * P:(t + 1) * P], T.ident[:, :])
                                last.then_inc(turned, 1)
                            j = i - 2
                            if 0 <= j < UNITS:
                                g, u = divmod(j, UPG)
                                pe.wait_ge(copied, it * UNITS + j + 1)
                                if u == 0:
                                    pe.wait_ge(v_ready, it * UNITS + (g + 1) * UPG)
                                if j >= 1:
                                    pe.wait_ge(gated, it * UNITS + j)
                                for t in range(TPB):
                                    last = nc.tensor.matmul(obank[:, 0:HD], prT[:, j % 2, t * P:(t + 1) * P],
                                                            v[:, g % 2, u // TPB * TPB + t, :], start=(t == 0),
                                                            stop=(t == TPB - 1))
                                last.then_inc(pv_done, 1)
                            j = i - 3
                            if 0 <= j < UNITS:
                                pe.wait_ge(gated, it * UNITS + j + 1)
                                if j >= 1:
                                    pe.wait_ge(g_copied, it * UNITS + j)
                                for t in range(4):
                                    last = nc.tensor.transpose(tbank[1][:, t * P:(t + 1) * P],
                                                               og[:, j % 2, 2 * t:2 * t + 2, :].rearrange("p e d -> p (e d)"),
                                                               T.ident[:, :])
                                last.then_inc(g_turned, 1)
                            j = i - 4
                            if j >= 0:
                                s, h = j // (B * UPG), j % UPG // TPB
                                pe.wait_ge(g_copied, it * UNITS + j + 1)
                                if j >= 1:
                                    pe.wait_ge(added, it * UNITS + j)
                                for t in range(4):
                                    at = WV + (h * 4 + t) * D
                                    last = nc.tensor.matmul(ybank[:, 0:D], ogT[:, j % 2, t * P:(t + 1) * P],
                                                            slot[s][:, at:at + D], start=(t == 0), stop=(t == 3))
                                last.then_inc(y_done, 1)
                            for g, n in pieces_at(i):
                                make(g, n)
                        pe.wait_ge(added, it * UNITS + UNITS)

                @block.scalar
                def _(act):
                    with act.Fori(0, TURNS) as it:
                        for i in range(UNITS + 3):
                            if i < UNITS:
                                act.wait_ge(maxed, it * UNITS + i + 1)
                                if i >= 2:
                                    act.wait_ge(turned, it * UNITS + i - 1)
                                nc.scalar.activation(pr[:, i % 2, :], sbank[i % 2][:, :], ACT.Exp, bias=nmx[:, i % 4:i % 4 + 1],
                                                     accum_out=rs[:, i % 4:i % 4 + 1]).then_inc(expd, 1)
                            j = i - 1
                            if 0 <= j < UNITS:
                                act.wait_ge(turned, it * UNITS + j + 1)
                                if j >= 2:
                                    act.wait_ge(pv_done, it * UNITS + j - 1)
                                nc.scalar.activation(prT[:, j % 2, :], tbank[0][:, :], ACT.Copy).then_inc(copied, 1)
                            j = i - 3
                            if j >= 0:
                                act.wait_ge(g_turned, it * UNITS + j + 1)
                                if j >= 2:
                                    act.wait_ge(y_done, it * UNITS + j - 1)
                                nc.scalar.activation(ogT[:, j % 2, :], tbank[1][:, :], ACT.Copy).then_inc(g_copied, 1)

                @block.vector
                def _(dve):
                    with dve.Fori(0, TURNS) as it:
                        heads = slice(0, 2 * SLOTS)
                        nc.vector.tensor_copy(gv_h[:, :, :, :], gates[:, :, 0, bass.ds(it * 2 * SLOTS, 2 * SLOTS), :])
                        nc.vector.tensor_copy(go_h[:, :, :, :], gates[:, :, 1, bass.ds(it * 2 * SLOTS, 2 * SLOTS), :])\
                            .then_inc(gates_ready, 1)
                        dve.wait_ge(gates_ready, it + 1)

                        def take(g, n):
                            s, b = divmod(g, B)
                            at = g * PIECES + n
                            dve.wait_ge(made, it * GROUPS * PIECES + at + 1)
                            if n < 4:
                                kind, part = divmod(n, 2)
                                dst = (plain, rotated)[part][:, kind, :]
                                if at >= PIECES and part == 0:
                                    dve.wait_ge(roped, it * 2 * GROUPS + 2 * g - 1 + kind)
                                nc.vector.tensor_tensor(dst, pj[at % 2][:, :], trig[:, n, :], ALU.mult).then_inc(read, 1)
                                if part:
                                    dve.wait_ge(read, it * GROUPS * PIECES + at + 1)
                                    nc.vector.tensor_tensor((q, k)[kind][:, g % 2, :], plain[:, kind, :], rotated[:, kind, :],
                                                            ALU.add).then_inc(roped, 1)
                            else:
                                u = g * UPG + n - 4
                                h, t = divmod(n - 4, TPB)
                                if u >= 2:
                                    dve.wait_ge(v_step, it * 2 * UNITS + 2 * u - 3)
                                nc.vector.tensor_tensor(vg[:, u % 2, :, :], pj[at % 2][:, :].rearrange("p (e d) -> p e d", e=E),
                                                        spread(gv_h[:, b * TPB + t, 2 * s + h, :], HD), ALU.mult)\
                                    .then_inc(read, 1)
                        for g, n in START:
                            take(g, n)
                        for i in range(UNITS + 5):
                            if i < UNITS:
                                dve.wait_ge(scored, it * UNITS + i + 1)
                                nc.vector.tensor_reduce(nmx[:, i % 4:i % 4 + 1], sbank[i % 2][:, :], axis=AX, op=ALU.max,
                                                        negate=True).then_inc(maxed, 1)
                            j = i - 2
                            if 0 <= j < UNITS:
                                g, u = divmod(j, UPG)
                                s, b = divmod(g, B)
                                h, t = divmod(u, TPB)
                                dve.wait_ge(expd, it * UNITS + j + 1)
                                nc.vector.reciprocal(rs[:, j % 4:j % 4 + 1], rs[:, j % 4:j % 4 + 1]).then_inc(o_step, 1)
                                dve.wait_ge(o_step, it * 2 * UNITS + 2 * j + 1)
                                nc.vector.tensor_scalar(go[:, j % 4, :], go_h[:, b * TPB + t, 2 * s + h, :],
                                                        rs[:, j % 4:j % 4 + 1], None, ALU.mult).then_inc(o_step, 1)
                                dve.wait_ge(o_step, it * 2 * UNITS + 2 * j + 2)
                                if j >= 2:
                                    dve.wait_ge(g_turned, it * UNITS + j - 1)
                                dve.wait_ge(pv_done, it * UNITS + j + 1)
                                nc.vector.tensor_tensor(og[:, j % 2, :, :], tiled(obank[:, 0:HD], E),
                                                        spread(go[:, j % 4, :], HD), ALU.mult).then_inc(gated, 1)
                            j = i - 5
                            if j >= 0:
                                b, t = j // UPG % B, j % TPB
                                dve.wait_ge(y_done, it * UNITS + j + 1)
                                if j >= TPB:
                                    dve.wait_ge(added, it * UNITS + j - TPB + 1)
                                acc = T.LNX[:, b * TPB + t, :]
                                nc.vector.tensor_tensor(acc, acc, ybank[:, 0:D], ALU.add).then_inc(added, 1)
                            for g, n in pieces_at(i):
                                take(g, n)

                @block.gpsimd
                def _(pool):
                    with pool.Fori(0, TURNS) as it:
                        for u in range(UNITS):
                            g, n = divmod(u, UPG)
                            pool.wait_ge(read, it * GROUPS * PIECES + g * PIECES + 4 + n + 1)
                            nc.gpsimd.tensor_tensor(vs[:, u % 2, :, :], vg[:, u % 2, 0:4, :], vg[:, u % 2, 4:8, :], ALU.add)\
                                .then_inc(v_step, 1)
                            pool.wait_ge(v_step, it * 2 * UNITS + 2 * u + 1)
                            nc.gpsimd.tensor_tensor(vs[:, u % 2, 0:2, :], vs[:, u % 2, 0:2, :], vs[:, u % 2, 2:4, :], ALU.add)\
                                .then_inc(v_step, 1)
                            pool.wait_ge(v_step, it * 2 * UNITS + 2 * u + 2)
                            if g >= 2 and n == 0:
                                pool.wait_ge(pv_done, it * UNITS + (g - 1) * UPG)
                            nc.gpsimd.tensor_tensor(v[:, g % 2, n, :], vs[:, u % 2, 0, :], vs[:, u % 2, 1, :], ALU.add)\
                                .then_inc(v_ready, 1)

        with Stage(nc, "l2f") as sf:
            w1 = sf.sb("w1", [P, F])
            w2 = sf.sb("w2", [P, 4, D])
            hid = sf.sb("hid", [P, 2, 4, S])
            names = ("loaded", "up_done", "hidden", "down_done", "added")
            w_loaded, up_done, hidden, down_done, added = (sf.sem(n) for n in names)
            layernorm(nc, T, T.LNX[:, :, :], T.LNX[:, :, :], T.LNT[:, :], [(w1[:, :], A["l2m_w1"]), (w2[:, :, :], A["l2m_w2"])],
                      w_loaded, ln1[:, 0, :], ln1[:, 1, :])
            with nc.Block() as block:
                @block.tensor
                def _(pe):
                    pe.wait_ge(w_loaded, 32)
                    for c in range(B + 1):
                        for f in range(4 if c < B else 0):
                            n = 4 * c + f
                            if n >= 4:
                                pe.wait_ge(hidden, n - 3)
                            nc.tensor.matmul(T.bank[f][:, :], w1[:, f * P:(f + 1) * P], T.LNT[:, c * S:(c + 1) * S],
                                             start=True, stop=True).then_inc(up_done, 1)
                        if c:
                            d = c - 1
                            pe.wait_ge(hidden, 4 * c)
                            if d >= 2:
                                pe.wait_ge(added, d - 1)
                            for t in range(TPB):
                                for f in range(4):
                                    last = nc.tensor.matmul(T.bank[4 + d % 2][:, t * D:(t + 1) * D],
                                                            hid[:, d % 2, f, t * P:(t + 1) * P], w2[:, f, :], start=(f == 0),
                                                            stop=(f == 3))
                            last.then_inc(down_done, 1)

                @block.scalar
                def _(act):
                    for n in range(4 * B):
                        c, f = divmod(n, 4)
                        act.wait_ge(up_done, n + 1)
                        if c >= 2:
                            act.wait_ge(down_done, c - 1)
                        nc.scalar.activation(hid[:, c % 2, f, :], T.bank[f][:, :], ACT.Relu, bias=b1[:, f:f + 1]).then_inc(hidden, 1)

                @block.vector
                def _(dve):
                    link = chain(T, dve)
                    link(nc.vector.tensor_tensor(T.LNX[:, :, :], T.LNX[:, :, :], tiled(b2[:, :], NT), ALU.add))
                    for c in range(B):
                        dve.wait_ge(down_done, c + 1)
                        x = T.LNX[:, c * TPB:(c + 1) * TPB, :]
                        nc.vector.tensor_tensor(x, x, T.bank[4 + c % 2][:, :].rearrange("p (t d) -> p t d", t=TPB), ALU.add)\
                            .then_inc(added, 1)
        layernorm(nc, T, T.LNX[:, :, :], T.LNX[:, :, :], T.LNT[:, :], gain=ln2[:, 0, :], shift=ln2[:, 1, :])
        with nc.Block() as block:
            @block.vector
            def _(dve):
                nc.vector.tensor_tensor(T.X[:, :, :], T.X[:, :, :], T.LNX[:, :, :], ALU.add)


def build(nc, A, out):
    T = Shared()
    T.dve_steps = T.ln_calls = 0
    with ExitStack() as ctx:
        def sb(name, shape, dt=F32):
            return ctx.enter_context(nc.sbuf_tensor(name, shape, dt))

        T.X = sb("X", [P, NT, D])
        T.LNX = sb("LNX", [P, NT, D])
        T.LNT = sb("LNT", [P, N])
        T.CTX = sb("CTX", [L, B, D])
        T.CTXT = sb("CTXT", [P, B * L])
        T.ident = sb("ident", [P, P])
        T.zeros = sb("zeros", [P, P])
        T.rev = sb("rev", [P, 64])
        T.ln_sq = sb("ln_sq", [P, NT, D])
        T.ln_sum, T.ln_mean, T.ln_rstd = (sb(n, [P, NT]) for n in ("ln_sum", "ln_mean", "ln_rstd"))
        T.bank = [ctx.enter_context(nc.psum_tensor(f"bank{i}", [P, 512], F32)) for i in range(8)]
        T.dve_step, T.ln_var, T.ln_std, T.ln_done, T.ln_turned, inputs, stored = (
            ctx.enter_context(nc.semaphore(n))
            for n in ("dve_step", "ln_var", "ln_std", "ln_done", "ln_turned", "inputs", "stored"))
        with nc.Block() as block:
            @block.sync
            def _(sp):
                for to, frm in ((T.X[:, :, :], A["x"]), (T.CTX[:, :, :], A["ctx"]), (T.CTXT[:, :], A["ctxT"]),
                                (T.ident[:, :], A["ident"]), (T.rev[:, :], A["rev"])):
                    sp.dma_start(to, frm).then_inc(inputs, 16)
                sp.wait_ge(inputs, 80)

            @block.vector
            def _(dve):
                nc.vector.memset(T.zeros[:, :], 0.0)

        stages = [
            lambda: l0_attention(nc, T, A),
            lambda: context_attention(nc, T, A, "l0x", H=1, dk=128, HB=1, biased=True),
            lambda: l0_moe(nc, T, A),
            lambda: l1_attention(nc, T, A),
            lambda: l1_coattention(nc, T, A),
            lambda: l1_moe(nc, T, A),
            lambda: l2_attention(nc, T, A),
            lambda: context_attention(nc, T, A, "l2x", H=4, dk=32, HB=4, rope=True, normed=True, keep_mask=True),
            lambda: l2_moe_attention(nc, T, A),
            lambda: l3_attention(nc, T, A),
            lambda: context_attention(nc, T, A, "l3x", H=16, dk=64, HB=4),
            lambda: l3_moe(nc, T, A),
        ]
        for n in STAGES:
            stages[n]()
        with nc.Block() as block:
            @block.sync
            def _(sp):
                sp.dma_start(out, T.X[:, :, :]).then_inc(stored, 16)
                sp.wait_ge(stored, 16)


def _rope_tables(positions, half, base):
    angle = positions[None, :].astype(np.float32) * (base ** (-np.arange(half, dtype=np.float32) / half))[:, None]
    return np.cos(angle.astype(np.float32)), np.sin(angle.astype(np.float32))


def _layouts(a):
    f = {}

    def rep(v, n=P):
        return np.broadcast_to(v.reshape(1, -1), (n, v.size))

    def tok(x):
        return x.reshape(NT, P, D).transpose(1, 0, 2)

    ctx = a["ctx_1024"]
    f["x"] = tok(a["x"])
    f["ctx"] = ctx.transpose(1, 0, 2)
    f["ctxT"] = ctx.transpose(2, 0, 1).reshape(D, B * L)
    f["ident"] = np.eye(P, dtype=np.float32)

    w, bias = a["L0_attn_W_attn"], a["L0_attn_b_attn"]

    def pad(m):
        z = np.zeros(m.shape[:-1] + (8, 4, 32), m.dtype)
        z[..., 0:8] = m.reshape(m.shape[:-1] + (8, 4, 8))
        return z.reshape(m.shape[:-1] + (8, 128))
    f["l0a_w"] = np.concatenate([pad(w[:, :256]).reshape(D, 1024), w[:, 256:]], axis=1)
    f["l0a_cols"] = np.concatenate([pad(bias[:256]).T, rep(a["L0_attn_temperature"])], axis=1)
    f["l0a_rows"] = np.concatenate([rep(bias[256:]), rep(a["L0_attn_b_proj"])], axis=1)
    f["l0a_wproj"] = a["L0_attn_W_proj"]
    u = np.arange(2 * S - P)[None, :] - (S - P) - np.arange(P)[:, None]
    f["rel"] = np.where(u <= 0, u, -BIG).astype(np.float32)

    f["l0x_wq"] = a["L0_xattn_Wq"].T.reshape(D, 1, 1, P)
    f["l0x_wk"] = a["L0_xattn_Wk"].T.reshape(D, 1, 1, P)
    f["l0x_wv"] = a["L0_xattn_Wv"].T.reshape(D, 1, P)
    f["l0x_wo"] = a["L0_xattn_Wo"].T.reshape(P, 1, D)
    f["l0x_cols"] = np.stack([a["L0_xattn_bq"], a["L0_xattn_bv"]], axis=1)
    f["l0x_rows"] = rep(a["L0_xattn_bo"])

    qw = a["L2_xattn_q_w"].transpose(1, 0, 2)
    kw = np.broadcast_to(a["L2_xattn_kv_w"][0, 0][:, None, :], (D, 4, 32))
    vw = np.broadcast_to(a["L2_xattn_kv_w"][1, 0][:, None, :], (D, 4, 32))

    def halves(m):
        return np.concatenate([m[..., 16:], m[..., :16]], axis=-1)
    f["l2x_wq"] = np.stack([qw.reshape(D, P), halves(qw).reshape(D, P)], axis=1).reshape(D, 2, 1, P)
    f["l2x_wk"] = np.stack([kw.reshape(D, P), halves(kw).reshape(D, P)], axis=1).reshape(D, 2, 1, P)
    f["l2x_wv"] = vw.reshape(D, 1, P)
    f["l2x_wo"] = a["L2_xattn_out_w"].reshape(P, 1, D)
    for n, pos in (("l2x_qtrig", np.arange(L, L + S)), ("l2x_ktrig", np.arange(L))):
        cos, sin = _rope_tables(pos, 16, 10000.0)
        f[n] = np.stack([np.tile(np.concatenate([cos, cos]), (4, 1)), np.tile(np.concatenate([-sin, sin]), (4, 1))], axis=1)
    f["l2x_gain"] = a["L2_xattn_rms_scale"].reshape(D, 1)
    f["l2x_keep"] = np.broadcast_to(a["mask_BxS2_bk0"].astype(np.int32)[None], (P, B, L))

    f["l3x_wq"] = a["L3_xattn_w_q"].reshape(D, 1, 8, P)
    f["l3x_wk"] = a["L3_xattn_w_k"].reshape(D, 1, 8, P)
    f["l3x_wv"] = a["L3_xattn_w_v"].reshape(D, 8, P)
    f["l3x_wo"] = a["L3_xattn_w_o"].reshape(8, P, D).transpose(1, 0, 2)

    def native(g, u, d):
        e = g.shape[0]
        def cols(m):
            return m.reshape(e // 2, 2, D, 64).transpose(0, 2, 1, 3).reshape(e // 2, D, P)
        return np.concatenate([cols(g), cols(u), d.reshape(e // 2, P, D)], axis=2)

    def turned(m):
        return m.transpose(0, 2, 1)
    f["rev"] = rep(np.arange(64, 0, -1, dtype=np.float32))
    f["tri"] = np.stack([np.triu(np.ones((P, P), np.float32), 1), np.ones((P, P), np.float32)], axis=1)
    f["l0m_router"] = a["L0_ffn_gate_w"].T
    f["l0m_bias"] = rep(a["L0_ffn_gate_bias"])
    f["l0m_pairs"] = native(turned(a["L0_ffn_Wg"]), turned(a["L0_ffn_Wu"]), turned(a["L0_ffn_Wd"]))
    f["l0m_shared"] = np.concatenate([a["L0_ffn_Ws_g"].T, a["L0_ffn_Ws_u"].T, a["L0_ffn_Ws_d"].T], axis=1).reshape(D, 1, 3 * P)
    f["l1m_router"] = a["L1_ffn_router_w"].T
    f["l1m_bias"] = rep(a["L1_ffn_e_bias"])
    f["l1m_pairs"] = native(a["L1_ffn_gate_w"], a["L1_ffn_up_w"], a["L1_ffn_down_w"])
    f["l1m_shared"] = np.stack([np.concatenate([a["L1_ffn_sh_gate_w"][:, s], a["L1_ffn_sh_up_w"][:, s],
                                                a["L1_ffn_sh_down_w"][s, :]], axis=1)
                                for s in (slice(0, P), slice(P, 2 * P))], axis=1)
    f["l3m_router"] = a["L3_ffn_gate_w"].T
    f["l3m_bias"] = rep(a["L3_ffn_bias"])
    f["l3m_pairs"] = native(a["L3_ffn_W1"], a["L3_ffn_W3"], a["L3_ffn_W2"])
    half = np.zeros((P, 1, 3 * P), f["l3m_pairs"].dtype)
    half[:, 0, 0:64] = a["L3_ffn_sw1"].T
    half[:, 0, P:P + 64] = a["L3_ffn_sw3"].T
    half[0:64, 0, 2 * P:3 * P] = a["L3_ffn_sw2"].T
    f["l3m_shared"] = half

    f["l1a_wq"] = a["L1_attn_wq"].T
    f["l1a_wkv"] = np.concatenate([a["L1_attn_wk"].T, a["L1_attn_wv"].T], axis=1)
    f["l1a_wo"] = a["L1_attn_wo"].T
    f["l1a_bo"] = rep(a["L1_attn_bo"])
    r = np.arange(P)
    f["l1a_same"] = np.concatenate([r[:, None] // 8 == r[None, :] // 8, r[:, None] // 8 == np.arange(16)[None, :]],
                                   axis=1).astype(np.float32)
    f["l1c_cols"] = np.concatenate([a["L1_xattn_w_sim"].reshape(3, D).T, rep(a["L1_xattn_b_sim"])], axis=1)
    f["l1c_w"] = a["L1_xattn_W_qv"].reshape(4, D, D).transpose(1, 0, 2)
    f["l1c_bias"] = rep(a["L1_xattn_b_qv"])

    f["l2a_w"] = a["L2_attn_W"]

    def pair_cols(m):
        return m.reshape(8, 2, D, 64).transpose(0, 2, 1, 3).reshape(8, D, P)

    def rotated_cols(m):
        return np.concatenate([m[..., 16:32], m[..., :16], m[..., 32:]], axis=-1)
    wq, wk = a["L2_ffn_Wq"], a["L2_ffn_Wk"]
    wv = a["L2_ffn_Wv"].transpose(0, 2, 1, 3).reshape(8, 2, D, 512).transpose(0, 2, 1, 3).reshape(8, D, 1024)
    wo = a["L2_ffn_Wo"].reshape(8, 2, 4, P, D).transpose(0, 3, 1, 2, 4).reshape(8, P, 1024)
    f["l2m_w"] = np.concatenate([pair_cols(wq), pair_cols(rotated_cols(wq)), pair_cols(wk), pair_cols(rotated_cols(wk)), wv, wo],
                                axis=2)
    f["l2m_wsel"] = np.concatenate([a["L2_ffn_Wsel_v"].reshape(P, D).T, a["L2_ffn_Wsel_o"].reshape(P, D).T], axis=1)
    cos, sin = _rope_tables(np.arange(S), 16, 10000.0)
    cos = np.tile(np.concatenate([cos, cos, np.ones((32, S), np.float32)]), (2, 1))
    sin = np.tile(np.concatenate([-sin, sin, np.zeros((32, S), np.float32)]), (2, 1))
    f["l2m_trig"] = np.stack([cos / 8, sin / 8, cos, sin], axis=1).astype(np.float32)
    for n in ("1", "2"):
        f["l2m_ln" + n] = np.stack([rep(a[f"L2_ffn_ln{n}_g"]), rep(a[f"L2_ffn_ln{n}_b"])], axis=1)
    f["l2m_w1"] = a["L2_ffn_W1"]
    f["l2m_b1"] = a["L2_ffn_b1"].reshape(4, P).T
    f["l2m_w2"] = a["L2_ffn_W2"].reshape(4, P, D).transpose(1, 0, 2)
    f["l2m_b2"] = rep(a["L2_ffn_b2"])

    f["l3a_w"] = np.concatenate([a["L3_attn_Wq"].T, a["L3_attn_Wk"].T, a["L3_attn_Wv"].T], axis=1)
    low = np.tril(np.ones((P, P), np.float32))
    f["tril"] = np.stack([low, (1 - low) * np.float32(1e-9)], axis=1)
    return {n: np.ascontiguousarray(v) for n, v in f.items()}


def kernel(**inputs):
    import concourse.bacc as bacc
    from concourse.bass_utils import run_bass_kernel_spmd

    arrays = _layouts({n: np.asarray(v) for n, v in inputs.items()})
    nc = bacc.Bacc("TRN2", target_bir_lowering=False, num_devices=1)
    A = {n: nc.dram_tensor(f"in_{n}", v.shape, mybir.dt.from_np(v.dtype), kind="ExternalInput").ap()
         for n, v in arrays.items()}
    out = nc.dram_tensor("out", (P, NT, D), F32, kind="ExternalOutput").ap()
    build(nc, A, out)
    r = run_bass_kernel_spmd(nc, [{f"in_{n}": v for n, v in arrays.items()}], core_ids=[0])
    return np.ascontiguousarray(r.results[0]["out"].transpose(1, 0, 2)).reshape(B, S, D)
```

```python
from contextlib import ExitStack

import numpy as np

import concourse.bass as bass
from concourse import mybir

STAGES = tuple(range(12))

B, S, D = 4, 512, 128
P = 128
TPB = S // P
NT = B * TPB
N = B * S
L = 77
F32 = mybir.dt.float32
F32R = mybir.dt.float32r
BF16 = mybir.dt.bfloat16
ALU = mybir.AluOpType
ACT = mybir.ActivationFunctionType
AX = mybir.AxisListType.X
BIG = 1.0e30


class Shared:
    pass


def spread(ap, n):
    return ap.unsqueeze(2).broadcast_to([ap.shape[0], ap.shape[1], n])


def tiled(ap, n):
    return ap.unsqueeze(1).broadcast_to([ap.shape[0], n, ap.shape[1]])


def chain(T, dve):
    def link(ins):
        T.dve_steps += 1
        ins.then_inc(T.dve_step, 1)
        dve.wait_ge(T.dve_step, T.dve_steps)
    return link


def layernorm(nc, T, src, dst, dstT, loads=(), load_sem=None, gain=None, shift=None, eps=1e-5):
    n = T.ln_calls
    T.ln_calls += 1
    n_affine = T.ln_affine_calls
    T.ln_affine_calls += gain is not None
    with nc.Block() as block:
        @block.sync
        def _(sp):
            for to, frm in loads:
                sp.dma_start(to, frm).then_inc(load_sem, 16)

        @block.vector
        def _(dve):
            link = chain(T, dve)
            for t in range(NT):
                out = nc.vector.bn_stats(T.ln_stats[:, t, :], src[:, t, :])
            link(out)
            for t in range(NT):
                out = nc.vector.bn_aggr(T.ln_mv[:, t, :], T.ln_stats[:, t, :])
            link(out)
            nc.vector.tensor_scalar(T.ln_var_eps[:, :], T.ln_mv[:, :, 1], eps, None, ALU.add).then_inc(T.ln_var, 1)
            dve.wait_ge(T.ln_std, n + 1)
            link(nc.vector.reciprocal(T.ln_rstd[:, :], T.ln_var_eps[:, :]))
            nc.vector.scalar_tensor_tensor(T.ln_shift[:, :], T.ln_mv[:, :, 0], -1.0, T.ln_rstd[:, :], ALU.mult, ALU.mult)\
                .then_inc(T.ln_scaled, 1)
            dve.wait_ge(T.ln_scaled, n + 1)
            for t in range(NT):
                if t % 2 == 0:
                    nc.vector.tensor_scalar(dst[:, t, :], src[:, t, :], T.ln_rstd[:, t:t + 1], T.ln_shift[:, t:t + 1],
                                            ALU.mult, ALU.add).then_inc(T.ln_even, 1)
            if gain is not None:
                for c in range(B):
                    ts = slice(c * TPB, (c + 1) * TPB)
                    dve.wait_ge(T.ln_even, NT // 2 * n + TPB // 2 * (c + 1))
                    dve.wait_ge(T.ln_odd, NT // 2 * n + TPB // 2 * (c + 1))
                    link(nc.vector.tensor_tensor(dst[:, ts, :], dst[:, ts, :], tiled(gain, TPB), ALU.mult))
                    nc.vector.tensor_tensor(dst[:, ts, :], dst[:, ts, :], tiled(shift, TPB), ALU.add).then_inc(T.ln_affine, 1)
            for c in range(1, B, 2):
                dve.wait_ge(T.ln_turned, B * n + c + 1)
                nc.vector.tensor_copy(dstT[:, c * S:(c + 1) * S], T.bank[c][:, :])

        @block.tensor
        def _(pe):
            for c in range(B):
                pe.wait_ge(T.ln_even, NT // 2 * n + TPB // 2 * (c + 1))
                pe.wait_ge(T.ln_odd, NT // 2 * n + TPB // 2 * (c + 1))
                if gain is not None:
                    pe.wait_ge(T.ln_affine, B * n_affine + c + 1)
                for t in range(TPB):
                    last = nc.tensor.transpose(T.bank[c][:, t * P:(t + 1) * P], dst[:, c * TPB + t, :], T.ident[:, :])
                last.then_inc(T.ln_turned, 1)

        @block.scalar
        def _(act):
            act.wait_ge(T.ln_var, n + 1)
            nc.scalar.activation(T.ln_var_eps[:, :], T.ln_var_eps[:, :], ACT.Sqrt).then_inc(T.ln_std, 1)
            act.wait_ge(T.ln_scaled, n + 1)
            for t in range(1, NT, 2):
                nc.scalar.activation(dst[:, t, :], src[:, t, :], ACT.Identity, bias=T.ln_shift[:, t:t + 1],
                                     scale=T.ln_rstd[:, t:t + 1]).then_inc(T.ln_odd, 1)
            for c in range(0, B, 2):
                act.wait_ge(T.ln_turned, B * n + c + 1)
                nc.scalar.activation(dstT[:, c * S:(c + 1) * S], T.bank[c][:, :], ACT.Copy)


class Stage:
    def __init__(self, nc, name):
        self.nc, self.name, self.ctx, self.sems = nc, name, ExitStack(), []

    def __enter__(self):
        self.ctx.__enter__()
        return self

    def __exit__(self, *a):
        if self.sems and a[0] is None:
            with self.nc.Block() as block:
                @block.gpsimd
                def _(pool):
                    for s in self.sems:
                        pool.sem_clear(s)
        return self.ctx.__exit__(*a)

    def sb(self, name, shape, dt=F32):
        return self.ctx.enter_context(self.nc.sbuf_tensor(f"{self.name}_{name}", shape, dt))

    def sem(self, name):
        self.sems.append(self.ctx.enter_context(self.nc.semaphore(f"{self.name}_{name}")))
        return self.sems[-1]


def l0_attention(nc, T, A):
    H, HD = 16, 8
    G, HPG = 4, 4
    UNITS = TPB * H
    POOL_HEADS = 4
    TLAG, VLAG, RING = 2, 4, 4
    slopes = [2.0 ** (-0.5 * (h + 1)) for h in range(H)]
    with Stage(nc, "l0a") as st:
        w = st.sb("w", [P, 2 * G * P + D])
        wproj = st.sb("wproj", [P, D])
        cols = st.sb("cols", [P, 2 * G + 3])
        rows = st.sb("rows", [P, 2 * D])
        rel = st.sb("rel", [P, 2 * S - P])
        alibi = st.sb("alibi", [P, H, 2 * S - P])
        qscale = st.sb("qscale", [P, 1])
        qbias = st.sb("qbias", [P, G])
        xb = st.sb("xb", [P, S])
        raw = st.sb("raw", [P, 2 * G, S])
        qk = st.sb("qk", [P, 2 * G, S], F32R)
        v = st.sb("v", [P, TPB, H * (P + HD)])
        sc = st.sb("sc", [P, RING, S])
        pr = st.sb("pr", [P, RING, S])
        prT = st.sb("prT", [P, RING, S])
        nmx = st.sb("nmx", [P, RING])
        rsum = st.sb("rsum", [P, TPB, H])
        rinv = st.sb("rinv", [P, TPB, H])
        rrep = st.sb("rrep", [P, 2, D])
        rinvT = st.sb("rinvT", [P, 2, P])
        yT = st.sb("yT", [P, S])
        loaded = st.sem("loaded")
        prepared = st.sem("prepared")
        x_ready, projected, q_raw, k_raw, high, split, v_ready = (
            st.sem(n) for n in ("x_ready", "projected", "q_raw", "k_raw", "high", "split", "v_ready"))
        scored, masked, expd, turned, copied_a, copied_v, pv_done, yT_ready = (
            st.sem(n) for n in ("scored", "masked", "expd", "turned", "copied_a", "copied_v",
                                "pv_done", "yT_ready"))
        rrep_ready, r_turned, rinvT_ready, out_ready, added, rinv_ready = (
            st.sem(n) for n in ("rrep_ready", "r_turned", "rinvT_ready", "out_ready", "added", "rinv_ready"))
        score_seen, cleared = st.sem("score_seen"), st.sem("cleared")
        loads = [(w[:, :], A["l0a_w"]), (wproj[:, :], A["l0a_wproj"]), (cols[:, :], A["l0a_cols"]),
                 (rows[:, :], A["l0a_rows"]), (rel[:, :], A["rel"])]
        layernorm(nc, T, T.X[:, :, :], T.LNX[:, :, :], T.LNT[:, :], loads, loaded)
        low_rows = (cols[:, 2 * G + 1:2 * G + 2], cols[:, 2 * G + 2:2 * G + 3])
        pj, sbank, tbank, obank, rbank = T.bank, T.bank[0:4], T.bank[4:6], T.bank[6:7], T.bank[7]

        with nc.Block() as block:
            @block.vector
            def _(dve):
                link = chain(T, dve)
                dve.wait_ge(loaded, 16 * len(loads))
                link(nc.vector.reciprocal(qscale[:, :], cols[:, 2 * G:2 * G + 1]))
                link(nc.vector.tensor_scalar(qscale[:, :], qscale[:, :], -(HD ** -0.5), None, ALU.mult))
                nc.vector.tensor_scalar(qbias[:, :], cols[:, 0:G], qscale[:, 0:1], None, ALU.mult).then_inc(prepared, 1)
                for h in range(H - POOL_HEADS):
                    nc.vector.tensor_scalar(alibi[:, h, :], rel[:, :], slopes[h], None, ALU.mult)
                link(nc.vector.tensor_tensor(T.X[:, :, :], T.X[:, :, :], tiled(rows[:, D:2 * D], NT), ALU.add))
                with dve.Fori(0, B) as b:
                    for n in range(2 * G):
                        if n < G:
                            dve.wait_ge(projected, b * 9 + G + n + 1)
                            nc.vector.tensor_scalar(raw[:, G + n, :], pj[G + n][:, :], cols[:, G + n:G + n + 1], None, ALU.add)\
                                .then_inc(k_raw, 1)
                        dve.wait_ge(high, b * 2 * G + n + 1)
                        nc.vector.scalar_tensor_tensor(qk[:, n, :], qk[:, n, :], low_rows[n // G], raw[:, n, :], ALU.mult,
                                                       ALU.add).then_inc(split, 1)
                    dve.wait_ge(projected, b * 9 + 9)
                    dve.wait_ge(cleared, 1)
                    for t in range(TPB):
                        nc.vector.tensor_tensor(v[:, t, :].rearrange("p (h c) -> p h c", h=H)[:, :, 0:HD],
                                                pj[0][:, t * D:(t + 1) * D].rearrange("p (h d) -> p h d", h=H),
                                                rows[:, 0:D].rearrange("p (h d) -> p h d", h=H), ALU.add).then_inc(v_ready, 1)
                    for i in range(UNITS + VLAG + 1):
                        if i < UNITS:
                            tt, h = divmod(i, H)
                            W = (tt + 1) * P
                            u0 = S - P - tt * P
                            dve.wait_ge(scored, b * UNITS + i + 1)
                            if i >= RING:
                                dve.wait_ge(expd, b * UNITS + i - RING + 1)
                            dve.sem_inc(score_seen, 1)
                            nc.vector.tensor_tensor_reduce(
                                out=sc[:, i % RING, 0:W], in0=alibi[:, h, u0:u0 + W], in1=sbank[i % 4][:, 0:W], scale=1.0,
                                scalar=3.0e38, op0=ALU.add, op1=ALU.min,
                                accum_out=nmx[:, i % RING:i % RING + 1]).then_inc(masked, 1)
                        j = i - TLAG
                        if 0 <= j < UNITS and j % 2:
                            W = (j // H + 1) * P
                            dve.wait_ge(turned, b * UNITS + j + 1)
                            if j >= RING:
                                dve.wait_ge(pv_done, b * UNITS + j - RING + 1)
                            nc.vector.tensor_copy(prT[:, j % RING, 0:W], tbank[1][:, 0:W]).then_inc(copied_v, 1)
                        j = i - 1
                        if 0 <= j < UNITS and j % H == H - 1:
                            tt = j // H
                            dve.wait_ge(expd, b * UNITS + j + 1)
                            nc.vector.reciprocal(rinv[:, tt, :], rsum[:, tt, :]).then_inc(rinv_ready, 1)
                            dve.wait_ge(rinv_ready, b * TPB + tt + 1)
                            if tt >= 2:
                                dve.wait_ge(r_turned, b * TPB + tt - 1)
                            nc.vector.tensor_copy(rrep[:, tt % 2, :].rearrange("p (h d) -> p h d", h=H),
                                                  spread(rinv[:, tt, :], HD)).then_inc(rrep_ready, 1)
                        j = i - VLAG - 1
                        if j >= 0 and j % H == H - 1:
                            tt = j // H
                            dve.wait_ge(pv_done, b * UNITS + j + 1)
                            dve.wait_ge(rinvT_ready, b * TPB + tt + 1)
                            nc.vector.tensor_tensor(yT[:, tt * P:(tt + 1) * P], obank[0][:, tt * P:(tt + 1) * P],
                                                    rinvT[:, tt % 2, :], ALU.mult).then_inc(yT_ready, 1)
                    dve.wait_ge(out_ready, b + 1)
                    nc.vector.tensor_tensor(T.X[:, bass.ds(b * TPB, TPB), :], T.X[:, bass.ds(b * TPB, TPB), :],
                                            pj[1][:, :].rearrange("p (t c) -> p t c", t=TPB), ALU.add).then_inc(added, 1)

            @block.gpsimd
            def _(pool):
                nc.gpsimd.memset(v[:, :, :], 0.0)
                pool.wait_ge(loaded, 16 * len(loads))
                for h in range(H - POOL_HEADS, H):
                    out = nc.gpsimd.tensor_scalar(alibi[:, h, :], rel[:, :], slopes[h], None, ALU.mult)
                out.then_inc(cleared, 1)

            @block.scalar
            def _(act):
                act.wait_ge(loaded, 16 * len(loads))
                act.wait_ge(prepared, 1)
                with act.Fori(0, B) as b:
                    nc.scalar.activation(xb[:, :], T.LNT[:, bass.ds(b * S, S)], ACT.Copy).then_inc(x_ready, 1)
                    for n in range(G):
                        act.wait_ge(projected, b * 9 + n + 1)
                        nc.scalar.activation(raw[:, n, :], pj[n][:, :], ACT.Identity, bias=qbias[:, n:n + 1],
                                             scale=qscale[:, 0:1]).then_inc(q_raw, 1)
                        act.wait_ge(q_raw, b * G + n + 1)
                        nc.scalar.activation(qk[:, n, :], raw[:, n, :], ACT.Copy).then_inc(high, 1)
                    for n in range(G):
                        act.wait_ge(k_raw, b * G + n + 1)
                        nc.scalar.activation(qk[:, G + n, :], raw[:, G + n, :], ACT.Copy).then_inc(high, 1)
                    for i in range(UNITS + TLAG):
                        if i < UNITS:
                            tt, h = divmod(i, H)
                            W = (tt + 1) * P
                            act.wait_ge(masked, b * UNITS + i + 1)
                            if i >= RING:
                                act.wait_ge(turned, b * UNITS + i - RING + 1)
                            nc.scalar.activation(pr[:, i % RING, 0:W], sc[:, i % RING, 0:W], ACT.Exp,
                                                 bias=nmx[:, i % RING:i % RING + 1], scale=-1.0,
                                                 accum_out=rsum[:, tt, h:h + 1]).then_inc(expd, 1)
                        j = i - TLAG
                        if j >= 0 and j % 2 == 0:
                            W = (j // H + 1) * P
                            act.wait_ge(turned, b * UNITS + j + 1)
                            if j >= RING:
                                act.wait_ge(pv_done, b * UNITS + j - RING + 1)
                            nc.scalar.activation(prT[:, j % RING, 0:W], tbank[0][:, 0:W], ACT.Copy).then_inc(copied_a, 1)
                        if 0 <= j < UNITS and j % H == H - 1:
                            tt = j // H
                            act.wait_ge(r_turned, b * TPB + tt + 1)
                            if tt >= 2:
                                act.wait_ge(yT_ready, b * TPB + tt - 1)
                            nc.scalar.activation(rinvT[:, tt % 2, :], rbank[:, 0:P], ACT.Copy).then_inc(rinvT_ready, 1)

            @block.tensor
            def _(pe):
                pe.wait_ge(loaded, 16 * len(loads))
                with pe.Fori(0, B) as b:
                    pe.wait_ge(x_ready, b + 1)
                    for n in range(2 * G):
                        nc.tensor.matmul(pj[n][:, :], w[:, n * P:(n + 1) * P], xb[:, :], start=True,
                                         stop=True).then_inc(projected, 1)
                    pe.wait_ge(q_raw, b * G + 1)
                    for t in range(TPB):
                        last = nc.tensor.matmul(pj[0][:, t * D:(t + 1) * D], xb[:, t * P:(t + 1) * P],
                                                w[:, 2 * G * P:2 * G * P + D], start=True, stop=True)
                    last.then_inc(projected, 1)
                    pe.wait_ge(split, (b + 1) * 2 * G)
                    pe.wait_ge(v_ready, (b + 1) * TPB)
                    for i in range(UNITS + VLAG):
                        if i < UNITS:
                            tt, h = divmod(i, H)
                            g, r = divmod(h, HPG)
                            W = (tt + 1) * P
                            if i >= 4:
                                pe.wait_ge(masked, b * UNITS + i - 3)
                            nc.tensor.matmul(sbank[i % 4][:, 0:W], qk[32 * r:32 * r + 32, g, tt * P:(tt + 1) * P],
                                             qk[32 * r:32 * r + 32, G + g, 0:W], start=True, stop=True,
                                             ).then_inc(scored, 1)
                        j = i - TLAG
                        if 0 <= j < UNITS:
                            pe.wait_ge(expd, b * UNITS + j + 1)
                            if j >= 2:
                                pe.wait_ge(copied_v if j % 2 else copied_a, b * (UNITS // 2) + j // 2)
                            for t in range(j // H + 1):
                                last = nc.tensor.transpose(tbank[j % 2][:, t * P:(t + 1) * P],
                                                           pr[:, j % RING, t * P:(t + 1) * P], T.ident[:, :])
                            last.then_inc(turned, 1)
                        j = i - VLAG
                        if j >= 0:
                            tt, h = divmod(j, H)
                            pe.wait_ge(copied_v if j % 2 else copied_a, b * (UNITS // 2) + j // 2 + 1)
                            if h == 0 and tt >= 1:
                                pe.wait_ge(yT_ready, b * TPB + tt)
                            for t in range(tt + 1):
                                last = nc.tensor.matmul(obank[0][:, tt * P:(tt + 1) * P], v[:, t, h * P:(h + 1) * P],
                                                        prT[:, j % RING, t * P:(t + 1) * P], start=(h == 0 and t == 0),
                                                        stop=(h == H - 1 and t == tt))
                            last.then_inc(pv_done, 1)
                        j = i - TLAG - 1
                        if 0 <= j < UNITS and j % H == H - 1:
                            tt = j // H
                            pe.wait_ge(rrep_ready, b * TPB + tt + 1)
                            if tt >= 1:
                                pe.wait_ge(rinvT_ready, b * TPB + tt)
                            nc.tensor.transpose(rbank[:, 0:P], rrep[:, tt % 2, :], T.ident[:, :]).then_inc(r_turned, 1)
                    pe.wait_ge(yT_ready, b * TPB + TPB)
                    for t in range(TPB):
                        last = nc.tensor.matmul(pj[1][:, t * D:(t + 1) * D], yT[:, t * P:(t + 1) * P], wproj[:, :],
                                                start=True, stop=True)
                    last.then_inc(out_ready, 1)
                    pe.wait_ge(added, b + 1)


def context_attention(nc, T, A, name, H, dk, HB, biased=False, rope=False, normed=False, keep_mask=False):
    HPG = P // dk
    G = H // HPG
    R = 2 if rope else 1
    STEPS = TPB * H // HB
    VB = min(G, 4)
    NV = HPG * (G // VB)
    NP = G * (2 * R + 1) + NV
    HT = H // HB
    TLAG, VLAG, RING = 3, 5, 4
    W = HB * L
    SCALE = dk ** -0.5
    FILL = -2.3819763e38
    with Stage(nc, name) as st:
        wq = st.sb("wq", [P, R, G, P])
        wk = st.sb("wk", [P, R, G, P])
        wv = st.sb("wv", [P, G, P])
        wo = st.sb("wo", [P, G, D])
        loaded = st.sem("loaded")
        loads = [(wq[:, :, :, :], A[f"{name}_wq"]), (wk[:, :, :, :], A[f"{name}_wk"]), (wv[:, :, :], A[f"{name}_wv"]),
                 (wo[:, :, :], A[f"{name}_wo"])]
        if biased:
            cols = st.sb("cols", [P, 2])
            rows = st.sb("rows", [P, D])
            qbias = st.sb("qbias", [P, 1])
            loads += [(cols[:, :], A[f"{name}_cols"]), (rows[:, :], A[f"{name}_rows"])]
        if rope:
            qtrig = st.sb("qtrig", [P, 2, S])
            ktrig = st.sb("ktrig", [P, 2, L])
            qrot = st.sb("qrot", [P, 2, S])
            krot = st.sb("krot", [P, 2, L])
            loads += [(qtrig[:, :, :], A[f"{name}_qtrig"]), (ktrig[:, :, :], A[f"{name}_ktrig"])]
        if normed:
            gain = st.sb("gain", [P, 1])
            rms = st.sb("rms", [P, NT])
            crms = st.sb("crms", [L, B])
            sq = st.sb("sq", [P, NT, D])
            cn = st.sb("cn", [L, B, D])
            loads += [(gain[:, :], A[f"{name}_gain"])]
        if keep_mask:
            keep_bits = st.sb("keep_bits", [P, B, L], mybir.dt.int32)
            keep = st.sb("keep", [P, B, L])
            fill = st.sb("fill", [P, B, L])
            keepb = st.sb("keepb", [P, HB, L])
            fillb = st.sb("fillb", [P, HB, L])
            loads += [(keep_bits[:, :, :], A[f"{name}_keep"])]
        ctxT = st.sb("ctxT", [P, B * L]) if normed else T.CTXT
        q = st.sb("q", [P, G, S])
        k = st.sb("k", [P, G, HPG, L])
        vT = st.sb("vT", [P, G, L])
        vo = st.sb("vo", [L, H, D])
        sc = st.sb("sc", [P, 2, HB, L])
        pr = st.sb("pr", [P, RING, HB, L])
        prT = st.sb("prT", [L, RING, HB * P])
        mx = st.sb("mx", [P, 2, HB])
        rs = st.sb("rs", [P, RING, HB])
        sems = ("prepared", "squared", "rooted", "cturned", "ct_ready", "projected", "taken_a", "taken_v", "scored", "dstep",
                "centred", "expd", "summed", "normal", "turned", "copied", "pv_done", "added", "maskb", "qrotated")
        prepared, squared, rooted, cturned, ct_ready, projected, taken_a, taken_v, scored, dstep, centred, expd, summed, normal, turned, \
            copied, pv_done, added, maskb, qrotated = (st.sem(n) for n in sems)
        layernorm(nc, T, T.X[:, :, :], T.LNX[:, :, :], T.LNT[:, :], loads, loaded)
        pj, sbank, tbank, obank = T.bank, T.bank[0:2], T.bank[2:4], T.bank[4:6]
        by_dve = [n < 2 * R * G if rope else n % 2 == 1 for n in range(NP)]
        NTV = sum(by_dve)
        NTA = NP - NTV

        with nc.Block() as block:
            @block.vector
            def _(dve):
                link = chain(T, dve)
                dve.wait_ge(loaded, 16 * len(loads))
                link(nc.vector.memset(k[:, :, :, :], 0.0))
                if biased:
                    link(nc.vector.tensor_scalar(qbias[:, :], cols[:, 0:1], SCALE, None, ALU.mult))
                    link(nc.vector.tensor_tensor(T.X[:, :, :], T.X[:, :, :], tiled(rows[:, :], NT), ALU.add))
                if keep_mask:
                    link(nc.vector.tensor_copy(keep[:, :, :], keep_bits[:, :, :]))
                    link(nc.vector.tensor_scalar(fill[:, :, :], keep[:, :, :], -1.0, -FILL, ALU.add, ALU.mult))
                if normed:
                    link(nc.vector.tensor_scalar(gain[:, :], gain[:, :], 1.0, None, ALU.add))
                    for m in (wq[:, :, :, :], wk[:, :, :, :], wv[:, :, :]):
                        link(nc.vector.tensor_scalar(m, m, gain[:, 0:1], None, ALU.mult))
                    link(nc.vector.tensor_tensor(sq[:, :, :], T.LNX[:, :, :], T.LNX[:, :, :], ALU.mult))
                    link(nc.vector.tensor_reduce(rms[:, :], sq[:, :, :], axis=AX, op=ALU.add))
                    link(nc.vector.tensor_scalar(rms[:, :], rms[:, :], 1.0 / D, 1e-6, ALU.mult, ALU.add))
                    link(nc.vector.tensor_tensor(cn[:, :, :], T.CTX[:, :, :], T.CTX[:, :, :], ALU.mult))
                    link(nc.vector.tensor_reduce(crms[:, :], cn[:, :, :], axis=AX, op=ALU.add))
                    nc.vector.tensor_scalar(crms[:, :], crms[:, :], 1.0 / D, 1e-6, ALU.mult, ALU.add).then_inc(squared, 1)
                    dve.wait_ge(rooted, 2)
                    link(nc.vector.reciprocal(rms[:, :], rms[:, :]))
                    link(nc.vector.tensor_scalar(rms[:, :], rms[:, :], SCALE, None, ALU.mult))
                    link(nc.vector.reciprocal(crms[:, :], crms[:, :]))
                    nc.vector.tensor_tensor(cn[:, :, :], T.CTX[:, :, :], spread(crms[:, :], D), ALU.mult)\
                        .then_inc(prepared, 1)

            @block.scalar
            def _(act):
                if normed:
                    act.wait_ge(squared, 1)
                    nc.scalar.activation(rms[:, :], rms[:, :], ACT.Sqrt).then_inc(rooted, 1)
                    nc.scalar.activation(crms[:, :], crms[:, :], ACT.Sqrt).then_inc(rooted, 1)
                    act.wait_ge(cturned, 1)
                    nc.scalar.activation(ctxT[:, :], T.bank[0][:, 0:B * L], ACT.Copy)

            @block.tensor
            def _(pe):
                if normed:
                    pe.wait_ge(prepared, 1)
                    for b in range(B):
                        last = nc.tensor.transpose(T.bank[0][:, b * L:(b + 1) * L], cn[:, b, :], T.ident[0:L, 0:L])
                    last.then_inc(cturned, 1)

        with nc.Block() as block:
            @block.tensor
            def _(pe):
                with pe.Fori(0, B) as b:
                    x = T.LNT[:, bass.ds(b * S, S)]
                    c = ctxT[:, bass.ds(b * L, L)]
                    n = 0

                    def read_up_to(m):
                        if any(by_dve[:m + 1]):
                            pe.wait_ge(taken_v, b * NTV + sum(by_dve[:m + 1]))
                        if not all(by_dve[:m + 1]):
                            pe.wait_ge(taken_a, b * NTA + m + 1 - sum(by_dve[:m + 1]))

                    def bank_free(n):
                        if n >= 8:
                            read_up_to(n - 8)
                    for g in range(G):
                        for r in range(R):
                            bank_free(n)
                            nc.tensor.matmul(pj[n % 8][:, :], wq[:, r, g, :], x, start=True, stop=True).then_inc(projected, 1)
                            n += 1
                    for g in range(G):
                        for r in range(R):
                            bank_free(n)
                            nc.tensor.matmul(pj[n % 8][:, 0:L], wk[:, r, g, :], c, start=True, stop=True).then_inc(projected, 1)
                            n += 1
                    for g in range(G):
                        bank_free(n)
                        nc.tensor.matmul(pj[n % 8][:, 0:L], wv[:, g, :], c, start=True, stop=True).then_inc(projected, 1)
                        n += 1
                    read_up_to(n - 1)
                    for r in range(HPG):
                        for g0 in range(0, G, VB):
                            for e in range(VB):
                                last = nc.tensor.matmul(pj[n % 8][0:L, e * D:(e + 1) * D], vT[r * dk:(r + 1) * dk, g0 + e, :],
                                                        wo[r * dk:(r + 1) * dk, g0 + e, :], start=True, stop=True)
                            last.then_inc(projected, 1)
                            n += 1
                    read_up_to(NP - 1)
                    for i in range(STEPS + VLAG):
                        if i < STEPS:
                            tt, hb = divmod(i, HT)
                            if i >= 2:
                                pe.wait_ge(centred, b * STEPS + i - 1)
                            for e in range(0, HB, HPG):
                                g = (hb * HB + e) // HPG
                                last = nc.tensor.matmul(sbank[i % 2][:, e * L:(e + HPG) * L], q[:, g, tt * P:(tt + 1) * P],
                                                        k[:, g, :, :], start=True, stop=True)
                            last.then_inc(scored, 1)
                        j = i - TLAG
                        if 0 <= j < STEPS:
                            pe.wait_ge(normal, b * STEPS + j + 1)
                            if j >= 2:
                                pe.wait_ge(copied, b * STEPS + j - 1)
                            for e in range(HB):
                                last = nc.tensor.transpose(tbank[j % 2][0:L, e * P:(e + 1) * P], pr[:, j % RING, e, :],
                                                           T.ident[:, :])
                            last.then_inc(turned, 1)
                        j = i - VLAG
                        if j >= 0:
                            tt, hb = divmod(j, HT)
                            pe.wait_ge(copied, b * STEPS + j + 1)
                            if hb == 0 and tt >= 2:
                                pe.wait_ge(added, b * TPB + tt - 1)
                            for e in range(HB):
                                last = nc.tensor.matmul(obank[tt % 2][:, 0:D], prT[:, j % RING, e * P:(e + 1) * P],
                                                        vo[:, hb * HB + e, :], start=(hb == 0 and e == 0),
                                                        stop=(hb == HT - 1 and e == HB - 1))
                            last.then_inc(pv_done, 1)
                    pe.wait_ge(added, b * TPB + TPB)

            def take(engine, b, n):
                src = pj[n % 8]
                if n < G:
                    return engine(q[:, n, :], src[:, :], qbias[:, 0:1] if biased else None, SCALE)
                if n < 2 * G * R:
                    for r in range(HPG):
                        rows_ = slice(r * dk, (r + 1) * dk)
                        out = engine(k[rows_, n - G, r, :], src[rows_, 0:L], None, 1.0)
                    return out
                if n < (2 * R + 1) * G:
                    return engine(vT[:, n - 2 * R * G, :], src[:, 0:L], cols[:, 1:2] if biased else None, 1.0)
                r, c = divmod(n - (2 * R + 1) * G, G // VB)
                dst = vo[:, :, :].rearrange("p (g r) d -> p g r d", r=HPG)[:, c * VB:(c + 1) * VB, r, :]
                return engine(dst, src[0:L, 0:VB * D].rearrange("p (g d) -> p g d", g=VB), None, 1.0)

            @block.scalar
            def _(act):
                def move(to, frm, bias, scale):
                    if bias is None:
                        return nc.scalar.activation(to, frm, ACT.Copy, scale=scale)
                    return nc.scalar.activation(to, frm, ACT.Identity, bias=bias, scale=scale)
                with act.Fori(0, B) as b:
                    for n in range(NP):
                        if not by_dve[n]:
                            act.wait_ge(projected, b * NP + n + 1)
                            take(move, b, n).then_inc(taken_a, 1)
                    for i in range(STEPS + TLAG):
                        if i < STEPS:
                            act.wait_ge(centred, b * STEPS + i + 1)
                            if i >= RING:
                                act.wait_ge(turned, b * STEPS + i - RING + 1)
                            nc.scalar.activation(pr[:, i % RING, :, :], sc[:, i % 2, :, :], ACT.Exp).then_inc(expd, 1)
                        j = i - TLAG
                        if j >= 0:
                            act.wait_ge(turned, b * STEPS + j + 1)
                            if j >= RING:
                                act.wait_ge(pv_done, b * STEPS + j - RING + 1)
                            nc.scalar.activation(prT[:, j % RING, :], tbank[j % 2][0:L, 0:HB * P], ACT.Copy)\
                                .then_inc(copied, 1)

            @block.gpsimd
            def _(pool):
                with pool.Fori(0, B) as b:
                    for i in range(STEPS):
                        pool.wait_ge(summed, b * STEPS + i + 1)
                        p = pr[:, i % RING, :, :]
                        nc.gpsimd.tensor_tensor(p, p, spread(rs[:, i % RING, :], L), ALU.mult).then_inc(normal, 1)

            @block.vector
            def _(dve):
                DS = STEPS * (5 if keep_mask else 2)

                def move(to, frm, bias, scale):
                    if bias is None:
                        return nc.vector.tensor_scalar(to, frm, scale, None, ALU.mult)
                    return nc.vector.tensor_scalar(to, frm, scale, bias, ALU.mult, ALU.add)
                with dve.Fori(0, B) as b:
                    count = [0]

                    def link(ins):
                        count[0] += 1
                        ins.then_inc(dstep, 1)
                        dve.wait_ge(dstep, b * DS + count[0])
                    if keep_mask:
                        nc.vector.tensor_copy(keepb[:, :, :], keep[:, bass.ds(b, 1), :].broadcast_to([P, HB, L]))
                        nc.vector.tensor_copy(fillb[:, :, :], fill[:, bass.ds(b, 1), :].broadcast_to([P, HB, L]))\
                            .then_inc(maskb, 1)
                        dve.wait_ge(maskb, b + 1)
                    if rope:
                        for n, (dst, trig, rot, w_) in enumerate(((q, qtrig, qrot, S), (k, ktrig, krot, L))):
                            dve.wait_ge(projected, b * NP + 2 * n + 1)
                            nc.vector.tensor_tensor(rot[:, 0, :], pj[2 * n][:, 0:w_], trig[:, 0, :], ALU.mult)\
                                .then_inc(taken_v, 1)
                            dve.wait_ge(projected, b * NP + 2 * n + 2)
                            nc.vector.tensor_tensor(rot[:, 1, :], pj[2 * n + 1][:, 0:w_], trig[:, 1, :], ALU.mult)\
                                .then_inc(qrotated, 1)
                            dve.wait_ge(qrotated, b * 2 + n + 1)
                            if dst is q:
                                out = nc.vector.tensor_tensor(q[:, 0, :], rot[:, 0, :], rot[:, 1, :], ALU.add)
                            else:
                                for r in range(HPG):
                                    rows_ = slice(r * dk, (r + 1) * dk)
                                    out = nc.vector.tensor_tensor(k[rows_, 0, r, :], rot[rows_, 0, :], rot[rows_, 1, :], ALU.add)
                            out.then_inc(taken_v, 1)
                    else:
                        for n in range(NP):
                            if by_dve[n]:
                                dve.wait_ge(projected, b * NP + n + 1)
                                take(move, b, n).then_inc(taken_v, 1)
                    for i in range(STEPS + VLAG + 1):
                        if i < STEPS:
                            tt = i // HT
                            s = sbank[i % 2][:, 0:W].rearrange("p (e l) -> p e l", e=HB)
                            dve.wait_ge(scored, b * STEPS + i + 1)
                            if i >= 2:
                                dve.wait_ge(expd, b * STEPS + i - 1)
                            z = sc[:, i % 2, :, :]
                            if keep_mask:
                                link(nc.vector.tensor_scalar(z, s, rms[:, bass.ds(b * TPB + tt, 1)], None, ALU.mult))
                                link(nc.vector.tensor_tensor(z, z, keepb[:, :, :], ALU.mult))
                                link(nc.vector.tensor_tensor(z, z, fillb[:, :, :], ALU.add))
                                s = z
                            link(nc.vector.tensor_reduce(mx[:, i % 2, :], s, axis=AX, op=ALU.max))
                            nc.vector.tensor_tensor(z, s, spread(mx[:, i % 2, :], L), ALU.subtract).then_inc(centred, 1)
                        j = i - 1
                        if 0 <= j < STEPS:
                            dve.wait_ge(expd, b * STEPS + j + 1)
                            link(nc.vector.tensor_reduce(rs[:, j % RING, :], pr[:, j % RING, :, :], axis=AX, op=ALU.add))
                            nc.vector.reciprocal(rs[:, j % RING, :], rs[:, j % RING, :]).then_inc(summed, 1)
                        j = i - VLAG - 1
                        if j >= 0 and j % HT == HT - 1:
                            tt = j // HT
                            dve.wait_ge(pv_done, b * STEPS + j + 1)
                            xt = T.X[:, bass.ds(b * TPB + tt, 1), :]
                            nc.vector.tensor_tensor(xt, xt, obank[tt % 2][:, 0:D].unsqueeze(1), ALU.add).then_inc(added, 1)
                    assert count[0] == DS


def pick_max(nc, link, V, rev, m, c, O):
    groups, n = V.shape[1], V.shape[2]
    link(nc.vector.tensor_reduce(m, V, axis=AX, op=ALU.max))
    link(nc.vector.tensor_tensor(c, V, spread(m, n), ALU.is_ge))
    link(nc.vector.tensor_tensor(c, c, tiled(rev, groups), ALU.mult))
    link(nc.vector.tensor_reduce(m, c, axis=AX, op=ALU.max))
    link(nc.vector.tensor_tensor(O, c, spread(m, n), ALU.is_equal))
    link(nc.vector.scalar_tensor_tensor(V, O, -3.0 * BIG, V, ALU.mult, ALU.add))


def expert_ffn(nc, T, A, name, E, K, route, NSH=1, half_weights=False, add_input=False,
               counted=False):
    I = 64
    PAIRS = E // 2
    SLOTS = 4
    BLK = B
    PRE = NSH * BLK
    PER = SLOTS * BLK
    TURNS = PAIRS // SLOTS
    DLAG, RING = 4, 8
    with Stage(nc, name) as st:
        WT = BF16 if half_weights else F32
        router = st.sb("router", [P, E], WT)
        bias = st.sb("bias", [P, E])
        shared_raw = st.sb("shared", [P, NSH, 3 * P], WT)
        score = st.sb("score", [P, NT, E])
        cw = st.sb("cw", [P, NT, E])
        cwT = st.sb("cwT", [E, N])
        wide_router = st.sb("wide_router", [P, E]) if half_weights else router
        x_hi, x_lo = st.sb("x_hi", [P, N], F32R), st.sb("x_lo", [P, N], F32R)
        shared_hi = st.sb("shared_hi", [P, NSH, 3 * P], F32R)
        wslot = [st.sb(f"w{i}", [P, 3 * P], WT) for i in range(SLOTS)]
        w_hi = [st.sb(f"w_hi{i}", [P, 3 * P], F32R) for i in range(SLOTS)]
        if not half_weights:
            shared_lo = st.sb("shared_lo", [P, NSH, 3 * P], F32R)
            w_lo = [st.sb(f"w_lo{i}", [P, 3 * P], F32R) for i in range(SLOTS)]
        arrived = [st.sem(f"arrived{i}") for i in range(SLOTS)]
        w_high = [st.sem(f"w_high{i}") for i in range(SLOTS)]
        w_low = w_high if half_weights else [st.sem(f"w_low{i}") for i in range(SLOTS)]
        x_high, shared_high = st.sem("x_high"), st.sem("shared_high")

        def fetch(sp, s, turn):
            sp.dma_start(wslot[s][:, :], A[f"{name}_pairs"][bass.ds(turn * SLOTS + s, 1), :, :]
                         .rearrange("a p c -> (a p) c")).then_inc(arrived[s], 16)
        mask = st.sb("mask", [P, NT, E])
        T.router_bias = bias
        T.chosen, T.counts = st.sem("chosen"), st.sem("counts")
        loaded = st.sem("loaded")
        loads = [(router[:, :], A[f"{name}_router"]), (bias[:, :], A[f"{name}_bias"]),
                 (shared_raw[:, :, :], A[f"{name}_shared"])]
        if counted:
            tri = st.sb("tri", [P, 2, P])
            loads.append((tri[:, :, :], A["tri"]))
        weights = nc.dram_tensor(f"{name}_weights", (E, N), F32, kind="Internal").ap()
        widened, logits, scored, routed, cw_turned, cw_taken, cw_stored = (
            st.sem(n) for n in ("widened", "logits", "scored", "routed", "cw_turned", "cw_taken", "cw_stored"))
        layernorm(nc, T, T.X[:, :, :], T.LNX[:, :, :], T.LNT[:, :], loads, loaded)

        with Stage(nc, f"{name}r") as rt, nc.Block() as block:
            per_bank = 512 // E if E > 32 else NT

            @block.tensor
            def _(pe):
                pe.wait_ge(loaded, 16 * len(loads))
                if half_weights:
                    pe.wait_ge(widened, 1)
                for t in range(NT):
                    bank, at = divmod(t, per_bank)
                    last = nc.tensor.matmul(T.bank[bank][:, at * E:(at + 1) * E], T.LNT[:, t * P:(t + 1) * P],
                                            wide_router[:, :], start=True, stop=True)
                last.then_inc(logits, 1)
                if counted:
                    pe.wait_ge(T.chosen, 1)
                    for i in range(2):
                        nc.tensor.matmul(T.bank[2 + i][:, :], tri[:, i, :], mask[:, :, :].rearrange("p t e -> p (t e)"),
                                         start=True, stop=True).then_inc(T.counts, 1)
                pe.wait_ge(routed, 1)
                for c in range(B):
                    for t in range(TPB):
                        last = nc.tensor.transpose(T.bank[4 + c][0:E, t * P:(t + 1) * P], cw[:, c * TPB + t, :],
                                                   T.ident[:, :])
                    last.then_inc(cw_turned, 1)

            @block.scalar
            def _(act):
                act.wait_ge(loaded, 16 * len(loads))
                if half_weights:
                    nc.scalar.activation(wide_router[:, :], router[:, :], ACT.Copy).then_inc(widened, 1)
                for c in range(B):
                    nc.scalar.activation(x_hi[:, c * S:(c + 1) * S], T.LNT[:, c * S:(c + 1) * S], ACT.Copy).then_inc(x_high, 1)
                act.wait_ge(logits, 1)
                for n in range(0, NT, per_bank):
                    last = nc.scalar.activation(score[:, n:n + per_bank, :],
                                                T.bank[n // per_bank][:, 0:per_bank * E].rearrange("p (t e) -> p t e", e=E),
                                                ACT.Sigmoid)
                last.then_inc(scored, 1)
                nc.scalar.activation(shared_hi[:, :, :], shared_raw[:, :, :], ACT.Copy).then_inc(shared_high, 1)
                if not half_weights:
                    for s in range(SLOTS - 1):
                        act.wait_ge(arrived[s], 16)
                        nc.scalar.activation(w_hi[s][:, :], wslot[s][:, :], ACT.Copy).then_inc(w_high[s], 1)
                for c in range(B):
                    act.wait_ge(cw_turned, c + 1)
                    nc.scalar.activation(cwT[:, c * S:(c + 1) * S], T.bank[4 + c][0:E, :], ACT.Copy).then_inc(cw_taken, 1)

            @block.vector
            def _(dve):
                dve.wait_ge(loaded, 16 * len(loads))
                dve.wait_ge(scored, 1)
                route(nc, T, rt, dve, chain(T, dve), score, mask, cw)
                dve.sem_inc(routed, 1)

            @block.gpsimd
            def _(pool):
                for c in range(B):
                    cols = slice(c * S, (c + 1) * S)
                    pool.wait_ge(x_high, c + 1)
                    nc.gpsimd.tensor_tensor(x_lo[:, cols], T.LNT[:, cols], x_hi[:, cols], ALU.subtract)
                if not half_weights:
                    pool.wait_ge(shared_high, 1)
                    nc.gpsimd.tensor_tensor(shared_lo[:, :, :], shared_raw[:, :, :], shared_hi[:, :, :], ALU.subtract)
                for s in range(SLOTS - 1):
                    if half_weights:
                        pool.wait_ge(arrived[s], 16)
                        nc.gpsimd.tensor_copy(w_hi[s][:, :], wslot[s][:, :]).then_inc(w_high[s], 1)
                    else:
                        pool.wait_ge(w_high[s], 1)
                        nc.gpsimd.tensor_tensor(w_lo[s][:, :], wslot[s][:, :], w_hi[s][:, :], ALU.subtract).then_inc(w_low[s], 1)

            @block.sync
            def _(sp):
                for s in range(SLOTS):
                    fetch(sp, s, 0)
                sp.wait_ge(cw_taken, B)
                sp.dma_start(weights, cwT[:, :]).then_inc(cw_stored, 16)
                sp.wait_ge(cw_stored, 16)

        cslot = [st.sb(f"c{i}", [P, N]) for i in range(SLOTS)]
        gate = st.sb("gate", [P, 2, S])
        prod = st.sb("prod", [P, 2, S])
        hid = st.sb("hid", [P, 4, S])
        hid_hi, hid_lo = st.sb("hid_hi", [P, RING, S], F32R), st.sb("hid_lo", [P, RING, S], F32R)
        outT = st.sb("outT", [P, N])
        cw_here = [st.sem(f"cw_here{i}") for i in range(SLOTS)]
        up_done, gated, multiplied, hidden, hid_high, hid_low, down_done, split_free = (
            st.sem(n) for n in ("up_done", "gated", "multiplied", "hidden", "hid_high", "hid_low", "down_done", "split_free"))
        taken, turned_back, closed = st.sem("taken"), st.sem("turned_back"), st.sem("closed")
        closing = T.ident if add_input else T.zeros
        acc = T.bank[0:BLK]
        gbank, ubank = T.bank[4:6], T.bank[6:8]

        def steps(engine, step):
            for n in range(-PRE, DLAG):
                step(0, n, False)
            with engine.Fori(0, TURNS - 1) as it:
                for n in range(DLAG, DLAG + PER):
                    step(it, n, False)
            for n in range(DLAG, DLAG + PER):
                step(TURNS - 1, n, True)

        def split_at(n, last):
            for s in range(SLOTS - 1):
                if n == (s + 1) * BLK + DLAG + 2 and not last:
                    return s, 1
            return (SLOTS - 1, 0) if n == DLAG + 2 else None

        def halves(n):
            if n < 0:
                e = (n + PRE) // BLK
                return shared_hi[:, e, :], None if half_weights else shared_lo[:, e, :]
            s = n // BLK % SLOTS
            return w_hi[s][:, :], None if half_weights else w_lo[s][:, :]

        with nc.Block() as block:
            @block.sync
            def _(sp):
                def fetch_cw(s, turn):
                    for e in range(2):
                        sp.dma_start(cslot[s][e * I:(e + 1) * I, :],
                                     weights[bass.ds(turn * 2 * SLOTS + 2 * s + e, 1), :].broadcast_to([I, N]))\
                            .then_inc(cw_here[s], 16)
                for s in range(SLOTS):
                    fetch_cw(s, 0)
                with sp.Fori(0, TURNS - 1) as it:
                    for s in range(SLOTS):
                        sp.wait_ge(w_low[s], it + 1)
                        fetch(sp, s, it + 1)
                        sp.wait_ge(down_done, it * PER + PRE + (s + 1) * BLK)
                        fetch_cw(s, it + 1)

            @block.tensor
            def _(pe):
                def product(out, w, w_cols, hi, lo, first, last, lo_ready=None):
                    wh, wl = w
                    nc.tensor.matmul(out, wh[:, w_cols], hi, start=first, stop=False)
                    if wl is not None:
                        nc.tensor.matmul(out, wl[:, w_cols], hi, start=False, stop=False)
                    if lo_ready is not None:
                        pe.wait_ge(hid_low, lo_ready)
                    return nc.tensor.matmul(out, wh[:, w_cols], lo, start=False, stop=last)

                def step(it, n, last):
                    k = it * PER + PRE + n
                    if n < PER or not last:
                        s, blk = n // BLK % SLOTS, n % BLK
                        if n >= 0 and blk == 0:
                            pe.wait_ge(w_low[s], it + n // PER + 1)
                        if n + PRE >= 2:
                            pe.wait_ge(multiplied, k - 1)
                        x = slice(blk * S, (blk + 1) * S)
                        product(gbank[n % 2][:, :], halves(n), slice(0, P), x_hi[:, x], x_lo[:, x], True, True)
                        product(ubank[n % 2][:, :], halves(n), slice(P, 2 * P), x_hi[:, x], x_lo[:, x], True, True)\
                            .then_inc(up_done, 1)
                    m = n - DLAG
                    if m + PRE >= 0:
                        at = (m + PRE) % RING
                        pe.wait_ge(hid_high, k - DLAG + 1)
                        product(acc[m % BLK][:, :], halves(m), slice(2 * P, 3 * P), hid_hi[:, at, :], hid_lo[:, at, :],
                                m + PRE < BLK, False, k - DLAG + 1).then_inc(down_done, 1)
                steps(pe, step)
                for blk in range(BLK):
                    last = nc.tensor.matmul(acc[blk][:, :], closing[:, :], T.LNT[:, blk * S:(blk + 1) * S], start=False,
                                            stop=True)
                last.then_inc(closed, 1)
                for c in range(B):
                    pe.wait_ge(taken, c + 1)
                    for t in range(TPB):
                        last = nc.tensor.transpose(T.bank[4 + c][:, t * P:(t + 1) * P],
                                                   outT[:, c * S + t * P:c * S + (t + 1) * P], T.ident[:, :])
                    last.then_inc(turned_back, 1)

            @block.scalar
            def _(act):
                def step(it, n, last):
                    k = it * PER + PRE + n
                    if n < PER or not last:
                        act.wait_ge(up_done, k + 1)
                        if n + PRE >= 2:
                            act.wait_ge(multiplied, k - 1)
                        nc.scalar.activation(gate[:, n % 2, :], gbank[n % 2][:, :], ACT.Silu).then_inc(gated, 1)
                    m = n - 1
                    if m + PRE >= 0 and (m < PER or not last):
                        act.wait_ge(hidden, k)
                        if n + PRE > DLAG + 1:
                            act.wait_ge(down_done, k - DLAG - 1)
                        nc.scalar.activation(hid_hi[:, (m + PRE) % RING, :], hid[:, (m + PRE) % 4, :], ACT.Copy)\
                            .then_inc(hid_high, 1)
                    if split_at(n, last) and not half_weights:
                        s, ahead = split_at(n, last)
                        act.wait_ge(arrived[s], it * 16 + 16 * ahead + 16)
                        act.wait_ge(down_done, k - DLAG - 1)
                        nc.scalar.activation(w_hi[s][:, :], wslot[s][:, :], ACT.Copy).then_inc(w_high[s], 1)
                steps(act, step)
                act.wait_ge(closed, 1)
                for c in range(B):
                    nc.scalar.activation(outT[:, c * S:(c + 1) * S], acc[c][:, :], ACT.Copy).then_inc(taken, 1)

            @block.gpsimd
            def _(pool):
                def step(it, n, last):
                    k = it * PER + PRE + n
                    if n < PER or not last:
                        pool.wait_ge(hid_high, k + 1)
                        if n + PRE > DLAG + 1:
                            pool.wait_ge(down_done, k - DLAG - 1)
                        at = (n + PRE) % RING
                        nc.gpsimd.tensor_tensor(hid_lo[:, at, :], hid[:, (n + PRE) % 4, :], hid_hi[:, at, :], ALU.subtract)\
                            .then_inc(hid_low, 1)
                    if split_at(n, last):
                        s, ahead = split_at(n, last)
                        if half_weights:
                            pool.wait_ge(arrived[s], it * 16 + 16 * ahead + 16)
                            pool.wait_ge(down_done, k - DLAG - 1)
                            pool.sem_inc(split_free, 1)
                            nc.gpsimd.tensor_copy(w_hi[s][:, :], wslot[s][:, :]).then_inc(w_high[s], 1)
                        else:
                            pool.wait_ge(w_high[s], it + ahead + 1)
                            nc.gpsimd.tensor_tensor(w_lo[s][:, :], wslot[s][:, :], w_hi[s][:, :], ALU.subtract)\
                                .then_inc(w_low[s], 1)
                steps(pool, step)

            @block.vector
            def _(dve):
                def step(it, n, last):
                    if n >= PER and last:
                        return
                    k = it * PER + PRE + n
                    h = hid[:, (n + PRE) % 4, :]
                    if n < 0:
                        dve.wait_ge(gated, k + 1)
                        if k >= 4:
                            dve.wait_ge(hid_low, k - 3)
                        nc.vector.tensor_tensor(h, ubank[n % 2][:, :], gate[:, n % 2, :], ALU.mult).then_inc(hidden, 1)
                        dve.wait_ge(hidden, k + 1)
                        dve.sem_inc(multiplied, 1)
                        return
                    s, blk = n // BLK % SLOTS, n % BLK
                    if blk == 0:
                        dve.wait_ge(cw_here[s], it * 32 + 32 * (n // PER) + 32)
                    dve.wait_ge(gated, k + 1)
                    dve.wait_ge(hidden, k - 1)
                    nc.vector.tensor_tensor(prod[:, n % 2, :], ubank[n % 2][:, :], gate[:, n % 2, :], ALU.mult)\
                        .then_inc(multiplied, 1)
                    dve.wait_ge(multiplied, k + 1)
                    dve.wait_ge(hid_low, k - 3)
                    nc.vector.tensor_tensor(h, prod[:, n % 2, :], cslot[s][:, blk * S:(blk + 1) * S], ALU.mult)\
                        .then_inc(hidden, 1)
                steps(dve, step)
                for c in range(B):
                    dve.wait_ge(turned_back, c + 1)
                    x = T.X[:, c * TPB:(c + 1) * TPB, :]
                    nc.vector.tensor_tensor(x, x, T.bank[4 + c][:, :].rearrange("p (t d) -> p t d", t=TPB), ALU.add)


def top_groups_then_experts(nc, T, rt, link, score, bias, NG, TG, K, mask):
    E = score.shape[2]
    n = E // NG
    V = rt.sb("V", [P, NT, E])
    c = rt.sb("c", [P, NT * E])
    O = rt.sb("O", [P, NT * E])
    m = rt.sb("m", [P, NT * NG])
    best = rt.sb("best", [P, NT * NG])
    gs = rt.sb("gs", [P, NT, NG])
    gm = rt.sb("gm", [P, NT])
    sfc = rt.sb("sfc", [P, NT, E])
    rev = T.rev
    def groups(t):
        return t.rearrange("p (g n) -> p g n", n=n)
    Vg = V[:, :, :].rearrange("p t (g n) -> p (t g) n", n=n)
    flat_gs = gs[:, :, :].rearrange("p t g -> p (t g)")
    link(nc.vector.tensor_tensor(sfc[:, :, :], score[:, :, :], tiled(bias[:, :], NT), ALU.add))
    link(nc.vector.tensor_copy(V[:, :, :], sfc[:, :, :]))
    link(nc.vector.tensor_reduce(best[:, :], Vg, axis=AX, op=ALU.max))
    pick_max(nc, link, Vg, rev[:, 64 - n:64], m[:, :], groups(c[:, :]), groups(O[:, :]))
    link(nc.vector.tensor_reduce(m[:, :], Vg, axis=AX, op=ALU.max))
    link(nc.vector.tensor_tensor(flat_gs, best[:, :], m[:, :], ALU.add))
    g = NT * NG
    for _ in range(TG):
        pick_max(nc, link, gs[:, :, :], rev[:, 64 - NG:64], gm[:, :], c[:, 0:g].rearrange("p (t g) -> p t g", g=NG),
                 O[:, 0:g].rearrange("p (t g) -> p t g", g=NG))
    link(nc.vector.tensor_scalar(m[:, :], flat_gs, -2.0 * BIG, BIG, ALU.is_lt, ALU.mult))
    link(nc.vector.tensor_scalar(m[:, :], m[:, :], -BIG, None, ALU.add))
    link(nc.vector.tensor_tensor(Vg, sfc[:, :, :].rearrange("p t (g n) -> p (t g) n", n=n), spread(m[:, :], n), ALU.add))
    choose(nc, T, rt, link, V, K, c, O, gm)
    link(nc.vector.tensor_scalar(mask[:, :, :], V[:, :, :], -2.0 * BIG, None, ALU.is_lt))


def choose(nc, T, rt, link, V, K, c, O, gm):
    E = V.shape[2]
    if K == 8:
        top = rt.sb("top", [P, NT, 8])
        for t in range(NT):
            last = nc.vector.max(top[:, t, :], V[:, t, :])
        link(last)
        for t in range(NT):
            last = nc.vector.match_replace(V[:, t, :], top[:, t, :], V[:, t, :], -3.0 * BIG)
        link(last)
        return
    for _ in range(K):
        pick_max(nc, link, V[:, :, :], T.rev[:, 64 - E:64], gm[:, :], c[:, :].rearrange("p (t e) -> p t e", e=E),
                 O[:, :].rearrange("p (t e) -> p t e", e=E))


def normalized(nc, rt, link, score, mask, cw, scale, floor, clip):
    total = rt.sb("total", [P, NT])
    E = score.shape[2]
    link(nc.vector.tensor_tensor(cw[:, :, :], score[:, :, :], mask[:, :, :], ALU.mult))
    link(nc.vector.tensor_reduce(total[:, :], cw[:, :, :], axis=AX, op=ALU.add))
    link(nc.vector.tensor_scalar(total[:, :], total[:, :], floor, None, ALU.max if clip else ALU.add))
    link(nc.vector.reciprocal(total[:, :], total[:, :]))
    link(nc.vector.tensor_tensor(cw[:, :, :], cw[:, :, :], spread(total[:, :], E), ALU.mult))
    if scale != 1.0:
        link(nc.vector.tensor_scalar(cw[:, :, :], cw[:, :, :], scale, None, ALU.mult))


def l0_moe(nc, T, A):
    def route(nc, T, rt, dve, link, score, mask, cw):
        top_groups_then_experts(nc, T, rt, link, score, T.router_bias, NG=4, TG=2, K=4, mask=mask)
        normalized(nc, rt, link, score, mask, cw, 2.5, 1e-20, False)
    expert_ffn(nc, T, A, "l0m", 16, 4, route, add_input=True)


def l1_moe(nc, T, A):
    def route(nc, T, rt, dve, link, score, mask, cw):
        top_groups_then_experts(nc, T, rt, link, score, T.router_bias, NG=8, TG=4, K=8, mask=mask)
        normalized(nc, rt, link, score, mask, cw, 1.0, 1e-20, False)
    expert_ffn(nc, T, A, "l1m", 64, 8, route, NSH=2)


def l3_moe(nc, T, A):
    E, CAP = 32, 2 * 512 * 4 // 32

    def route(nc, T, rt, dve, link, score, mask, cw):
        V = rt.sb("V", [P, NT, E])
        c, O = rt.sb("c", [P, NT * E]), rt.sb("O", [P, NT * E])
        gm = rt.sb("gm", [P, NT])
        pos = rt.sb("pos", [P, NT, E])
        before = rt.sb("before", [P, NT, E])
        link(nc.vector.tensor_tensor(V[:, :, :], score[:, :, :], tiled(T.router_bias[:, :], NT), ALU.add))
        choose(nc, T, rt, link, V, 4, c, O, gm)
        nc.vector.tensor_scalar(mask[:, :, :], V[:, :, :], -2.0 * BIG, None, ALU.is_lt).then_inc(T.chosen, 1)
        dve.wait_ge(T.chosen, 1)
        normalized(nc, rt, link, score, mask, cw, 1.0, 1e-12, True)
        dve.wait_ge(T.counts, 2)
        link(nc.vector.memset(before[:, 0, :], 0.0))
        for t in range(1, NT):
            link(nc.vector.tensor_tensor(before[:, t, :], before[:, t - 1, :], T.bank[3][:, (t - 1) * E:t * E], ALU.add))
        link(nc.vector.tensor_tensor(pos[:, :, :], before[:, :, :], T.bank[2][:, :].rearrange("p (t e) -> p t e", e=E), ALU.add))
        link(nc.vector.tensor_scalar(pos[:, :, :], pos[:, :, :], float(CAP), None, ALU.is_lt))
        link(nc.vector.tensor_tensor(cw[:, :, :], cw[:, :, :], pos[:, :, :], ALU.mult))
    expert_ffn(nc, T, A, "l3m", 32, 4, route, half_weights=True, counted=True)


def l1_attention(nc, T, A):
    H, HD = 16, 8
    KW = D + H
    with Stage(nc, "l1a") as st:
        wq = st.sb("wq", [P, D])
        wkv = st.sb("wkv", [P, 2 * D])
        wo = st.sb("wo", [P, D])
        bo = st.sb("bo", [P, D])
        same = st.sb("same", [P, KW])
        xb = st.sb("xb", [P, S])
        qm, qe, qf = (st.sb(n, [P, S]) for n in ("qm", "qe", "qf"))
        km, ke, kf = (st.sb(n, [P, TPB, D]) for n in ("km", "ke", "kf"))
        v = st.sb("v", [P, TPB, D + 1])
        kv = st.sb("kv", [P, KW])
        den = st.sb("den", [P, TPB, H])
        y = st.sb("y", [P, TPB, D])
        yT = st.sb("yT", [P, S])
        names = ("loaded", "x_ready", "projected", "mins", "exps", "features", "kv_done", "kv_ready", "out_done",
                 "den_step", "y_ready", "y_turned", "yT_ready", "proj_done", "added", "ones")
        loaded, x_ready, projected, mins, exps, features, kv_done, kv_ready, out_done, den_step, y_ready, y_turned, \
            yT_ready, proj_done, added, ones = (st.sem(n) for n in names)
        loads = [(wq[:, :], A["l1a_wq"]), (wkv[:, :], A["l1a_wkv"]), (wo[:, :], A["l1a_wo"]), (bo[:, :], A["l1a_bo"]),
                 (same[:, :], A["l1a_same"])]
        layernorm(nc, T, T.X[:, :, :], T.LNX[:, :, :], T.LNT[:, :], loads, loaded)
        k_psum = [T.bank[1 + i][:, :].rearrange("p (t c) -> p t c", t=2) for i in range(2)]
        o_psum = [T.bank[4 + i][:, 0:2 * KW].rearrange("p (t c) -> p t c", t=2) for i in range(2)]
        with nc.Block() as block:
            @block.scalar
            def _(act):
                act.wait_ge(ones, 1)
                with act.Fori(0, B) as b:
                    nc.scalar.activation(xb[:, :], T.LNT[:, bass.ds(b * S, S)], ACT.Copy).then_inc(x_ready, 1)
                    act.wait_ge(mins, b + 1)
                    nc.scalar.activation(qe[:, :], qm[:, :], ACT.Exp)
                    nc.scalar.activation(ke[:, :, :], km[:, :, :], ACT.Exp)
                    for i in range(2):
                        last = nc.scalar.activation(v[:, 2 * i:2 * i + 2, 0:D], k_psum[i][:, :, D:2 * D], ACT.Copy)
                    last.then_inc(exps, 1)
                    act.wait_ge(y_turned, b + 1)
                    nc.scalar.activation(yT[:, :], T.bank[6][:, :], ACT.Copy).then_inc(yT_ready, 1)

            @block.tensor
            def _(pe):
                pe.wait_ge(loaded, 16 * len(loads))
                with pe.Fori(0, B) as b:
                    pe.wait_ge(x_ready, b + 1)
                    nc.tensor.matmul(T.bank[0][:, :], wq[:, :], xb[:, :], start=True, stop=True)
                    for t in range(TPB):
                        last = nc.tensor.matmul(k_psum[t // 2][:, t % 2, :], xb[:, t * P:(t + 1) * P], wkv[:, :],
                                                start=True, stop=True)
                    last.then_inc(projected, 1)
                    pe.wait_ge(features, b + 1)
                    for t in range(TPB):
                        last = nc.tensor.matmul(T.bank[3][:, 0:D + 1], kf[:, t, :], v[:, t, :], start=(t == 0),
                                                stop=(t == TPB - 1))
                    last.then_inc(kv_done, 1)
                    pe.wait_ge(kv_ready, b + 1)
                    for t in range(TPB):
                        last = nc.tensor.matmul(o_psum[t // 2][:, t % 2, :], qf[:, t * P:(t + 1) * P], kv[:, :],
                                                start=True, stop=True)
                    last.then_inc(out_done, 1)
                    pe.wait_ge(y_ready, b + 1)
                    for t in range(TPB):
                        last = nc.tensor.transpose(T.bank[6][:, t * P:(t + 1) * P], y[:, t, :], T.ident[:, :])
                    last.then_inc(y_turned, 1)
                    pe.wait_ge(yT_ready, b + 1)
                    for t in range(TPB):
                        last = nc.tensor.matmul(T.bank[7][:, t * D:(t + 1) * D], yT[:, t * P:(t + 1) * P], wo[:, :],
                                                start=True, stop=True)
                    last.then_inc(proj_done, 1)
                    pe.wait_ge(added, b + 1)

            @block.vector
            def _(dve):
                link = chain(T, dve)
                nc.vector.memset(v[:, :, :], 1.0).then_inc(ones, 1)
                dve.wait_ge(loaded, 16 * len(loads))
                link(nc.vector.tensor_tensor(T.X[:, :, :], T.X[:, :, :], tiled(bo[:, :], NT), ALU.add))
                with dve.Fori(0, B) as b:
                    dve.wait_ge(projected, b + 1)
                    nc.vector.tensor_scalar(qm[:, :], T.bank[0][:, :], 0.0, None, ALU.min)
                    for i in range(2):
                        last = nc.vector.tensor_scalar(km[:, 2 * i:2 * i + 2, :], k_psum[i][:, :, 0:D], 0.0, None, ALU.min)
                    last.then_inc(mins, 1)
                    dve.wait_ge(exps, b + 1)
                    nc.vector.scalar_tensor_tensor(qf[:, :], T.bank[0][:, :], 0.0, qe[:, :], ALU.max, ALU.add)
                    for i in range(2):
                        last = nc.vector.scalar_tensor_tensor(kf[:, 2 * i:2 * i + 2, :], k_psum[i][:, :, 0:D], 0.0,
                                                              ke[:, 2 * i:2 * i + 2, :], ALU.max, ALU.add)
                    last.then_inc(features, 1)
                    dve.wait_ge(kv_done, b + 1)
                    nc.vector.tensor_tensor(kv[:, 0:D], T.bank[3][:, 0:D], same[:, 0:D], ALU.mult)
                    nc.vector.tensor_scalar(kv[:, D:KW], same[:, D:KW], T.bank[3][:, D:D + 1], None, ALU.mult)\
                        .then_inc(kv_ready, 1)
                    dve.wait_ge(out_done, b + 1)
                    for i in range(2):
                        last = nc.vector.tensor_scalar(den[:, 2 * i:2 * i + 2, :], o_psum[i][:, :, D:KW], 1e-6, None, ALU.add)
                    last.then_inc(den_step, 1)
                    dve.wait_ge(den_step, b * 2 + 1)
                    nc.vector.reciprocal(den[:, :, :], den[:, :, :]).then_inc(den_step, 1)
                    dve.wait_ge(den_step, b * 2 + 2)
                    for t in range(TPB):
                        last = nc.vector.tensor_tensor(y[:, t, :].rearrange("p (h d) -> p h d", h=H),
                                                       o_psum[t // 2][:, t % 2, 0:D].rearrange("p (h d) -> p h d", h=H),
                                                       spread(den[:, t, :], HD), ALU.mult)
                    last.then_inc(y_ready, 1)
                    dve.wait_ge(proj_done, b + 1)
                    x = T.X[:, bass.ds(b * TPB, TPB), :]
                    nc.vector.tensor_tensor(x, x, T.bank[7][:, :].rearrange("p (t c) -> p t c", t=TPB), ALU.add)\
                        .then_inc(added, 1)


def l1_coattention(nc, T, A):
    with Stage(nc, "l1c") as st:
        cols = st.sb("cols", [P, 4])
        w = st.sb("w", [P, 4, D])
        bias = st.sb("bias", [P, D])
        c3 = st.sb("c3", [P, B * L])
        w2 = st.sb("w2", [P, P])
        drow = st.sb("drow", [P, B, L])
        sim = st.sb("sim", [P, 2, TPB, L])
        mx = st.sb("mx", [P, NT])
        rs = st.sb("rs", [P, NT])
        prT = st.sb("prT", [L, 2, S])
        hq = st.sb("hq", [P, 2, S])
        ehq = st.sb("ehq", [P, 2, S])
        row = st.sb("row", [1, 2, S])
        rowmax = st.sb("rowmax", [1, B])
        rowsum = st.sb("rowsum", [1, B])
        ecol = st.sb("ecol", [P, NT])
        w14 = st.sb("w14", [P, B, D])
        names = ("loaded", "prepared", "drow_done", "drow_ready", "sim_done", "centred", "expd", "normal", "turned",
                 "prT_ready", "hq_done", "hq_ready", "row_done", "rowmax_ready", "row_exp", "row_ready", "col_done",
                 "col_ready", "hc_done", "w_ready", "out_done", "added", "hq_taken")
        loaded, prepared, drow_done, drow_ready, sim_done, centred, expd, normal, turned, prT_ready, hq_done, hq_ready, \
            row_done, rowmax_ready, row_exp, row_ready, col_done, col_ready, hc_done, w_ready, out_done, added, \
            hq_taken = (st.sem(n) for n in names)
        loads = [(cols[:, :], A["l1c_cols"]), (w[:, :, :], A["l1c_w"]), (bias[:, :], A["l1c_bias"])]
        layernorm(nc, T, T.X[:, :, :], T.LNX[:, :, :], T.LNT[:, :], loads, loaded)
        with nc.Block() as block:
            @block.tensor
            def _(pe):
                pe.wait_ge(prepared, 1)
                nc.tensor.matmul(T.bank[0][:, 0:B * L], w2[:, :], T.CTXT[:, :], start=True, stop=True).then_inc(drow_done, 1)
                pe.wait_ge(drow_ready, 1)
                for b in range(B):
                    if b >= 2:
                        pe.wait_ge(centred, b - 1)
                    for t in range(TPB):
                        n = b * TPB + t
                        last = nc.tensor.matmul(T.bank[b % 2][:, t * L:(t + 1) * L], T.LNT[:, n * P:(n + 1) * P],
                                                c3[:, b * L:(b + 1) * L], start=True, stop=True)
                    last.then_inc(sim_done, 1)
                    pe.wait_ge(normal, b + 1)
                    for t in range(TPB):
                        last = nc.tensor.transpose(T.bank[2][0:L, t * P:(t + 1) * P], sim[:, b % 2, t, :], T.ident[:, :])
                    last.then_inc(turned, 1)
                    for t in range(TPB):
                        n = b * TPB + t
                        last = nc.tensor.matmul(T.bank[4][0:1, t * P:(t + 1) * P], mx[:, n:n + 1], T.ident[:, :],
                                                start=True, stop=True)
                    last.then_inc(row_done, 1)
                    pe.wait_ge(prT_ready, b + 1)
                    nc.tensor.matmul(T.bank[3][:, :], T.CTX[:, b, :], prT[:, b % 2, :], start=True, stop=True).then_inc(hq_done, 1)
                    pe.wait_ge(row_ready, b + 1)
                    for t in range(TPB):
                        last = nc.tensor.matmul(T.bank[5][:, t:t + 1], row[0:1, b % 2, t * P:(t + 1) * P],
                                                T.ident[0:1, 0:1], start=True, stop=True)
                    last.then_inc(col_done, 1)
                    pe.wait_ge(col_ready, b + 1)
                    for t in range(TPB):
                        n = b * TPB + t
                        last = nc.tensor.matmul(T.bank[7][:, 0:1], T.LNX[:, n, :], ecol[:, n:n + 1], start=(t == 0),
                                                stop=(t == TPB - 1))
                    last.then_inc(hc_done, 1)
                    pe.wait_ge(w_ready, b + 1)
                    pe.wait_ge(hq_ready, b + 1)
                    for t in range(TPB):
                        n = b * TPB + t
                        cut = slice(t * P, (t + 1) * P)
                        o = T.bank[6][:, t * D:(t + 1) * D]
                        nc.tensor.matmul(o, T.LNT[:, n * P:(n + 1) * P], w14[:, b, :], start=True, stop=False)
                        nc.tensor.matmul(o, hq[:, b % 2, cut], w[:, 1, :], start=False, stop=False)
                        last = nc.tensor.matmul(o, ehq[:, b % 2, cut], w[:, 2, :], start=False, stop=True)
                    last.then_inc(out_done, 1)
                    pe.wait_ge(added, b + 1)

            @block.scalar
            def _(act):
                for b in range(B):
                    act.wait_ge(centred, b + 1)
                    nc.scalar.activation(sim[:, b % 2, :, :], sim[:, b % 2, :, :], ACT.Exp).then_inc(expd, 1)
                    act.wait_ge(turned, b + 1)
                    nc.scalar.activation(prT[:, b % 2, :], T.bank[2][0:L, :], ACT.Copy).then_inc(prT_ready, 1)
                    act.wait_ge(rowmax_ready, b + 1)
                    nc.scalar.activation(row[0:1, b % 2, :], T.bank[4][0:1, :], ACT.Exp, bias=rowmax[0:1, b:b + 1],
                                         accum_out=rowsum[0:1, b:b + 1]).then_inc(row_exp, 1)
                    act.wait_ge(col_done, b + 1)
                    nc.scalar.activation(ecol[:, b * TPB:(b + 1) * TPB], T.bank[5][:, 0:TPB], ACT.Copy).then_inc(col_ready, 1)

            @block.vector
            def _(dve):
                link = chain(T, dve)
                dve.wait_ge(loaded, 16 * len(loads))
                nc.vector.tensor_scalar(c3[:, :], T.CTXT[:, :], cols[:, 2:3], cols[:, 0:1], ALU.mult, ALU.add)
                nc.vector.tensor_scalar(w2[:, :], T.zeros[:, :], cols[:, 1:2], None, ALU.add).then_inc(prepared, 1)
                link(nc.vector.tensor_tensor(T.X[:, :, :], T.X[:, :, :], tiled(bias[:, :], NT), ALU.add))
                dve.wait_ge(drow_done, 1)
                nc.vector.tensor_scalar(drow[:, :, :], T.bank[0][:, 0:B * L].rearrange("p (b l) -> p b l", b=B),
                                        cols[:, 3:4], None, ALU.add).then_inc(drow_ready, 1)
                dve.wait_ge(drow_ready, 1)
                for b in range(B):
                    z = sim[:, b % 2, :, :]
                    m = mx[:, b * TPB:(b + 1) * TPB]
                    r = rs[:, b * TPB:(b + 1) * TPB]
                    dve.wait_ge(sim_done, b + 1)
                    link(nc.vector.tensor_tensor(z, T.bank[b % 2][:, 0:TPB * L].rearrange("p (t l) -> p t l", t=TPB),
                                                 tiled(drow[:, b, :], TPB), ALU.add))
                    link(nc.vector.tensor_reduce(m, z, axis=AX, op=ALU.max))
                    nc.vector.tensor_tensor(z, z, spread(m, L), ALU.subtract).then_inc(centred, 1)
                    dve.wait_ge(expd, b + 1)
                    link(nc.vector.tensor_reduce(r, z, axis=AX, op=ALU.add))
                    link(nc.vector.reciprocal(r, r))
                    nc.vector.tensor_tensor(z, z, spread(r, L), ALU.mult).then_inc(normal, 1)
                    dve.wait_ge(row_done, b + 1)
                    nc.vector.tensor_reduce(rowmax[0:1, b:b + 1], T.bank[4][0:1, :], axis=AX, op=ALU.max, negate=True)\
                        .then_inc(rowmax_ready, 1)
                    dve.wait_ge(hq_done, b + 1)
                    nc.vector.tensor_copy(hq[:, b % 2, :], T.bank[3][:, :])
                    nc.vector.tensor_tensor(ehq[:, b % 2, :], T.bank[3][:, :], T.LNT[:, b * S:(b + 1) * S], ALU.mult)\
                        .then_inc(hq_ready, 1)
                    dve.wait_ge(row_exp, b + 1)
                    link(nc.vector.reciprocal(rowsum[0:1, b:b + 1], rowsum[0:1, b:b + 1]))
                    nc.vector.tensor_scalar(row[0:1, b % 2, :], row[0:1, b % 2, :], rowsum[0:1, b:b + 1], None, ALU.mult)\
                        .then_inc(row_ready, 1)
                    dve.wait_ge(hc_done, b + 1)
                    nc.vector.scalar_tensor_tensor(w14[:, b, :], w[:, 3, :], T.bank[7][:, 0:1], w[:, 0, :], ALU.mult,
                                                   ALU.add).then_inc(w_ready, 1)
                    dve.wait_ge(out_done, b + 1)
                    x = T.X[:, b * TPB:(b + 1) * TPB, :]
                    nc.vector.tensor_tensor(x, x, T.bank[6][:, :].rearrange("p (t d) -> p t d", t=TPB), ALU.add)\
                        .then_inc(added, 1)


def l2_attention(nc, T, A):
    with Stage(nc, "l2a") as st:
        w = st.sb("w", [P, 3 * D])
        xb = st.sb("xb", [P, S])
        q, k = st.sb("q", [P, S]), st.sb("k", [P, S])
        v = st.sb("v", [P, TPB, D])
        e = st.sb("e", [P, TPB, S])
        nmx, rs = st.sb("nmx", [P, TPB]), st.sb("rs", [P, TPB])
        names = ("loaded", "x_ready", "projected", "qk_ready", "scored", "max_ready", "expd", "v_scaled", "out_done",
                 "added", "v_step")
        loaded, x_ready, projected, qk_ready, scored, max_ready, expd, v_scaled, out_done, added, v_step = (
            st.sem(n) for n in names)
        loads = [(w[:, :], A["l2a_w"])]
        layernorm(nc, T, T.X[:, :, :], T.LNX[:, :, :], T.LNT[:, :], loads, loaded)
        with nc.Block() as block:
            @block.tensor
            def _(pe):
                pe.wait_ge(loaded, 16)
                with pe.Fori(0, B) as b:
                    pe.wait_ge(x_ready, b + 1)
                    for i in range(2):
                        nc.tensor.matmul(T.bank[i][:, :], w[:, i * D:(i + 1) * D], xb[:, :], start=True, stop=True)\
                            .then_inc(projected, 1)
                    for t in range(TPB):
                        last = nc.tensor.matmul(T.bank[2][:, t * D:(t + 1) * D], xb[:, t * P:(t + 1) * P],
                                                w[:, 2 * D:3 * D], start=True, stop=True)
                    last.then_inc(projected, 1)
                    pe.wait_ge(qk_ready, b + 1)
                    for t in range(TPB):
                        nc.tensor.matmul(T.bank[3 + t][:, :], k[:, t * P:(t + 1) * P], q[:, :], start=True, stop=True)\
                            .then_inc(scored, 1)
                    pe.wait_ge(v_scaled, b + 1)
                    for t in range(TPB):
                        for j in range(TPB):
                            last = nc.tensor.matmul(T.bank[7][:, t * D:(t + 1) * D], e[:, j, t * P:(t + 1) * P], v[:, j, :],
                                                    start=(j == 0), stop=(j == TPB - 1))
                    last.then_inc(out_done, 1)
                    pe.wait_ge(added, b + 1)

            @block.scalar
            def _(act):
                with act.Fori(0, B) as b:
                    nc.scalar.activation(xb[:, :], T.LNT[:, bass.ds(b * S, S)], ACT.Copy).then_inc(x_ready, 1)
                    act.wait_ge(projected, b * 3 + 2)
                    nc.scalar.activation(q[:, :], T.bank[0][:, :], ACT.Copy, scale=D ** -0.5)
                    nc.scalar.activation(k[:, :], T.bank[1][:, :], ACT.Copy).then_inc(qk_ready, 1)
                    for t in range(TPB):
                        act.wait_ge(max_ready, b * TPB + t + 1)
                        nc.scalar.activation(e[:, t, :], T.bank[3 + t][:, :], ACT.Exp, bias=nmx[:, t:t + 1],
                                             accum_out=rs[:, t:t + 1]).then_inc(expd, 1)

            @block.vector
            def _(dve):
                with dve.Fori(0, B) as b:
                    for t in range(TPB):
                        dve.wait_ge(scored, b * TPB + t + 1)
                        nc.vector.tensor_reduce(nmx[:, t:t + 1], T.bank[3 + t][:, :], axis=AX, op=ALU.max, negate=True)\
                            .then_inc(max_ready, 1)
                    dve.wait_ge(expd, b * TPB + TPB)
                    nc.vector.reciprocal(rs[:, :], rs[:, :]).then_inc(v_step, 1)
                    dve.wait_ge(v_step, b + 1)
                    nc.vector.tensor_tensor(v[:, :, :], T.bank[2][:, :].rearrange("p (t d) -> p t d", t=TPB),
                                            spread(rs[:, :], D), ALU.mult).then_inc(v_scaled, 1)
                    dve.wait_ge(out_done, b + 1)
                    x = T.X[:, bass.ds(b * TPB, TPB), :]
                    nc.vector.tensor_tensor(x, x, T.bank[7][:, :].rearrange("p (t c) -> p t c", t=TPB), ALU.add)\
                        .then_inc(added, 1)


def l3_attention(nc, T, A):
    EPS = 1e-9
    with Stage(nc, "l3a") as st:
        w = st.sb("w", [P, 3 * D])
        tril = st.sb("tril", [P, 2, P])
        eps = st.sb("eps", [P, P])
        q = st.sb("q", [P, N])
        k = st.sb("k", [P, N])
        v = st.sb("v", [P, NT, D])
        m = st.sb("m", [P, S])
        z = st.sb("z", [P, B, S])
        zT = st.sb("zT", [P, B, S])
        total = st.sb("total", [P, S])
        names = ("loaded", "projected", "taken", "scored", "first", "centred", "expd", "normal", "turned", "zT_ready",
                 "out_done", "added", "eps_ready")
        loaded, projected, taken, scored, first, centred, expd, normal, turned, zT_ready, out_done, added, eps_ready = (
            st.sem(n) for n in names)
        loads = [(w[:, :], A["l3a_w"]), (tril[:, :, :], A["tril"])]
        layernorm(nc, T, T.X[:, :, :], T.LNX[:, :, :], T.LNT[:, :], loads, loaded)
        with nc.Block() as block:
            @block.tensor
            def _(pe):
                pe.wait_ge(loaded, 16 * len(loads))
                for b in range(B):
                    for i in range(3):
                        n = 3 * b + i
                        if n >= 6:
                            pe.wait_ge(taken, n - 5)
                        bank = T.bank[n % 6]
                        xT = T.LNT[:, b * S:(b + 1) * S]
                        if i == 0:
                            last = nc.tensor.matmul(bank[:, :], w[:, 0:D], xT, start=True, stop=True)
                        for t in range(TPB if i else 0):
                            x = xT.rearrange("p (r c) -> p c r", c=TPB)[:, t, :] if i == 1 else xT[:, t * P:(t + 1) * P]
                            last = nc.tensor.matmul(bank[:, t * D:(t + 1) * D], x, w[:, i * D:(i + 1) * D], start=True,
                                                    stop=True)
                        last.then_inc(projected, 1)
                pe.wait_ge(taken, 3 * B)
                pe.wait_ge(eps_ready, 1)
                for t in range(TPB):
                    W = (t + 1) * P
                    if t:
                        pe.wait_ge(centred, t)
                    for b in range(B):
                        last = nc.tensor.matmul(T.bank[b][:, 0:W], q[:, b * S + t * P:b * S + (t + 1) * P],
                                                k[:, b * S:b * S + W], start=True, stop=True)
                    last.then_inc(scored, 1)
                    pe.wait_ge(normal, t + 1)
                    for b in range(B):
                        n = t * B + b
                        if n >= 2:
                            pe.wait_ge(zT_ready, n - 1)
                        for j in range(t + 1):
                            last = nc.tensor.transpose(T.bank[4 + n % 2][:, j * P:(j + 1) * P], z[:, b, j * P:(j + 1) * P],
                                                       T.ident[:, :])
                        last.then_inc(turned, 1)
                    pe.wait_ge(zT_ready, B * (t + 1))
                    if t >= 2:
                        pe.wait_ge(added, t - 1)
                    for b in range(B):
                        for j in range(TPB):
                            p = zT[:, b, j * P:(j + 1) * P] if j <= t else eps[:, :]
                            last = nc.tensor.matmul(T.bank[6 + t % 2][:, b * D:(b + 1) * D], p, v[:, b * TPB + j, :],
                                                    start=(j == 0), stop=(j == TPB - 1))
                    last.then_inc(out_done, 1)

            @block.scalar
            def _(act):
                for n in range(3 * B):
                    b, i = divmod(n, 3)
                    act.wait_ge(projected, n + 1)
                    src = T.bank[n % 6][:, :]
                    if i == 0:
                        out = nc.scalar.activation(q[:, b * S:(b + 1) * S], src, ACT.Copy, scale=D ** -0.5)
                    elif i == 1:
                        out = nc.scalar.activation(k[:, b * S:(b + 1) * S], src, ACT.Copy)
                    else:
                        out = nc.scalar.activation(v[:, b * TPB:(b + 1) * TPB, :],
                                                   src.rearrange("p (t d) -> p t d", t=TPB), ACT.Copy)
                    out.then_inc(taken, 1)
                for t in range(TPB):
                    W = (t + 1) * P
                    act.wait_ge(scored, t + 1)
                    if t:
                        act.wait_ge(centred, t)
                    nc.scalar.activation(m[:, 0:W], T.bank[0][:, 0:W], ACT.Copy).then_inc(first, 1)
                    act.wait_ge(centred, t + 1)
                    nc.scalar.activation(z[:, :, 0:W], z[:, :, 0:W], ACT.Exp).then_inc(expd, 1)
                    for b in range(B):
                        act.wait_ge(turned, B * t + b + 1)
                        nc.scalar.activation(zT[:, b, 0:W], T.bank[4 + b % 2][:, 0:W], ACT.Copy).then_inc(zT_ready, 1)

            @block.vector
            def _(dve):
                link = chain(T, dve)
                nc.vector.memset(eps[:, :], EPS).then_inc(eps_ready, 1)
                dve.wait_ge(loaded, 16 * len(loads))
                for t in range(TPB):
                    W = (t + 1) * P
                    dve.wait_ge(first, t + 1)
                    mm = m[:, 0:W]
                    for b in range(1, B):
                        link(nc.vector.tensor_tensor(mm, T.bank[b][:, 0:W], mm, ALU.max))
                    if t:
                        dve.wait_ge(turned, B * t)
                    for b in range(B):
                        last = nc.vector.tensor_tensor(z[:, b, 0:W], T.bank[b][:, 0:W], mm, ALU.subtract)
                    last.then_inc(centred, 1)
                    dve.wait_ge(expd, t + 1)
                    link(nc.vector.tensor_reduce(total[:, 0:W], z[:, :, 0:W].rearrange("p b w -> p w b"), axis=AX, op=ALU.add))
                    link(nc.vector.reciprocal(total[:, 0:W], total[:, 0:W]))
                    link(nc.vector.tensor_tensor(z[:, :, 0:W], z[:, :, 0:W], tiled(total[:, 0:W], B), ALU.mult))
                    last_block = z[:, :, t * P:W]
                    link(nc.vector.tensor_tensor(last_block, last_block, tiled(tril[:, 0, :], B), ALU.mult))
                    nc.vector.tensor_tensor(last_block, last_block, tiled(tril[:, 1, :], B), ALU.add).then_inc(normal, 1)
                    dve.wait_ge(out_done, t + 1)
                    x = T.X[:, :, :].rearrange("p (b t) d -> p t b d", b=B)[:, t, :, :]
                    nc.vector.tensor_tensor(x, x, T.bank[6 + t % 2][:, :].rearrange("p (b d) -> p b d", b=B), ALU.add)\
                        .then_inc(added, 1)


def l2_moe_attention(nc, T, A):
    H, HD, E = 16, 64, 8
    PAIRS, SLOTS = H // 2, 2
    TURNS = PAIRS // SLOTS
    TH = 2 * SLOTS
    PICKS = 14
    GROUPS = SLOTS * B
    UPG = 2 * TPB
    UNITS = GROUPS * UPG
    SPLIT_1, SPLIT_0, PICK = 14, 44, 20
    LEAD = UPG + 2
    PIECES = 4 + UPG
    QK = 4 * P
    WV = QK + 2 * E * HD
    WTOT = WV + 2 * 4 * D
    F = 4 * D
    with Stage(nc, "l2m") as st:
        gates = st.sb("gates", [P, NT, 2, H, E])
        ln1, ln2 = st.sb("ln1", [P, 2, D]), st.sb("ln2", [P, 2, D])
        b1, b2 = st.sb("b1", [P, 4]), st.sb("b2", [P, D])
        trig = st.sb("trig", [P, 4, S])
        loaded = st.sem("loaded")
        loads = [(ln1[:, :, :], A["l2m_ln1"]), (ln2[:, :, :], A["l2m_ln2"]), (b1[:, :], A["l2m_b1"]), (b2[:, :], A["l2m_b2"]),
                 (trig[:, :, :], A["l2m_trig"])]

        with Stage(nc, "l2h") as sh:
            wsel = sh.sb("wsel", [P, 2 * H * E])
            left = sh.sb("left", [P, NT, 2, TH, E])
            seen = sh.sb("seen", [P, NT, 2, TH, E])
            pick = sh.sb("pick", [P, NT, 2, TH, E])
            best = sh.sb("best", [P, NT * 2 * TH])
            x_hi, x_lo = sh.sb("x_hi", [P, N], F32R), sh.sb("x_lo", [P, N], F32R)
            w_hi = [sh.sb(f"w_hi{i}", [P, WV], F32R) for i in range(SLOTS)]
            w_lo = [sh.sb(f"w_lo{i}", [P, WV], F32R) for i in range(SLOTS)]
            slot = [sh.sb(f"w{i}", [P, WTOT]) for i in range(SLOTS)]
            plain, rotated = sh.sb("plain", [P, 2, S]), sh.sb("rotated", [P, 2, S])
            qk = sh.sb("qk", [P, 2, S])
            qk_hi, qk_lo = sh.sb("qk_hi", [P, 2, 2, S], F32R), sh.sb("qk_lo", [P, 2, 2, S], F32R)
            vg = sh.sb("vg", [P, 2, E, HD])
            vs = sh.sb("vs", [P, 2, E // 2, HD])
            v = sh.sb("v", [P, 2, UPG, HD])
            pr, prT = sh.sb("pr", [P, 2, S]), sh.sb("prT", [P, 2, S])
            og, ogT = sh.sb("og", [P, 2, E, HD]), sh.sb("ogT", [P, 2, S])
            nmx, rs = sh.sb("nmx", [P, 4]), sh.sb("rs", [P, 4])
            go = sh.sb("go", [P, 4, E])
            gv_h = [sh.sb(f"gv{i}", [P, NT, 2, E]) for i in range(SLOTS)]
            go_h = [sh.sb(f"go{i}", [P, NT, 2, E]) for i in range(SLOTS)]
            arrived = [sh.sem(f"arrived{i}") for i in range(SLOTS)]
            logits, squashed, pick_step, x_high, x_low, w_high, w_low, qk_high, qk_low = (
                sh.sem(n) for n in ("logits", "squashed", "pick_step", "x_high", "x_low", "w_high", "w_low", "qk_high", "qk_low"))
            names = ("gates_ready", "made", "read", "rot_step", "roped", "v_gated", "v_step", "v_ready", "scored", "maxed",
                     "expd", "turned", "copied", "pv_done", "o_step", "gated", "g_turned", "g_copied", "y_done", "added")
            gates_ready, made, read, rot_step, roped, v_gated, v_step, v_ready, scored, maxed, expd, turned, copied, pv_done, \
                o_step, gated, g_turned, g_copied, y_done, added = (sh.sem(n) for n in names)
            pj, sbank, tbank, obank, ybank = T.bank[0:2], T.bank[2:4], T.bank[4:6], T.bank[6], T.bank[7]

            def pieces_at(i, last):
                g, r = divmod(i, UPG)
                if last and g + 1 >= GROUPS:
                    return []
                return [(g + 1, n) for n in range(PIECES * r // UPG, PIECES * (r + 1) // UPG)]
            START = [(0, n) for n in range(PIECES)]

            def place(n):
                g, u = divmod(n, UPG)
                return g // B % SLOTS, u // TPB, g % B, u % TPB

            def turns(engine, step):
                for i in range(LEAD):
                    step(0, i, False)
                with engine.Fori(0, TURNS - 1) as it:
                    for i in range(LEAD, LEAD + UNITS):
                        step(it, i, False)
                for i in range(LEAD, UNITS + 5):
                    step(TURNS - 1, i, True)

            def due(i, lag, last):
                return i >= lag and (i - lag < UNITS or not last)

            layernorm(nc, T, T.X[:, :, :], T.LNX[:, :, :], T.LNT[:, :], loads + [(wsel[:, :], A["l2m_wsel"])], loaded)
            with nc.Block() as block:
                @block.sync
                def _(sp):
                    for s in range(SLOTS):
                        sp.dma_start(slot[s][:, :], A["l2m_w"][s, :, :]).then_inc(arrived[s], 16)
                    with sp.Fori(0, TURNS - 1) as it:
                        for s in range(SLOTS):
                            sp.wait_ge(y_done, it * UNITS + (s + 1) * UNITS // SLOTS)
                            sp.dma_start(slot[s][:, :], A["l2m_w"][bass.ds(it * SLOTS + SLOTS + s, 1), :, :]
                                         .rearrange("a p c -> (a p) c")).then_inc(arrived[s], 16)

                @block.tensor
                def _(pe):
                    def make(it, g, n):
                        s, b = g // B % SLOTS, g % B
                        at = g * PIECES + n
                        if n == 0 and b == 0:
                            pe.wait_ge(w_low, it * SLOTS + g // GROUPS * SLOTS + s + 1)
                        if at >= 2:
                            pe.wait_ge(read, it * GROUPS * PIECES + at - 1)
                        halves = ((x_hi, w_hi[s]), (x_lo, w_hi[s]), (x_hi, w_lo[s]))
                        for p, (x, w) in enumerate(halves):
                            if n < 4:
                                out = nc.tensor.matmul(pj[at % 2][:, :], w[:, n * P:(n + 1) * P], x[:, b * S:(b + 1) * S],
                                                       start=(p == 0), stop=(p == 2))
                            else:
                                h, t = divmod(n - 4, TPB)
                                out = nc.tensor.matmul(pj[at % 2][:, :], x[:, b * S + t * P:b * S + (t + 1) * P],
                                                       w[:, QK + h * S:QK + (h + 1) * S], start=(p == 0), stop=(p == 2))
                        out.then_inc(made, 1)

                    def step(it, i, last):
                        if due(i, 0, last):
                            g, u = divmod(i, UPG)
                            h, t = divmod(u, TPB)
                            if u == 0:
                                pe.wait_ge(qk_low, it * 2 * GROUPS + 2 * g + 2)
                            if i >= 2:
                                pe.wait_ge(expd, it * UNITS + i - 1)
                            rows = slice(h * HD, (h + 1) * HD)
                            halves = ((qk_hi, qk_hi), (qk_lo, qk_hi), (qk_hi, qk_lo))
                            for p, (q, k) in enumerate(halves):
                                out = nc.tensor.matmul(sbank[i % 2][:, :], q[rows, g % 2, 0, t * P:(t + 1) * P],
                                                       k[rows, g % 2, 1, :], start=(p == 0), stop=(p == 2))
                            out.then_inc(scored, 1)
                        j = i - 1
                        if due(i, 1, last):
                            pe.wait_ge(expd, it * UNITS + j + 1)
                            if j >= 1:
                                pe.wait_ge(copied, it * UNITS + j)
                            for t in range(TPB):
                                out = nc.tensor.transpose(tbank[0][:, t * P:(t + 1) * P], pr[:, j % 2, t * P:(t + 1) * P],
                                                          T.ident[:, :])
                            out.then_inc(turned, 1)
                        j = i - 2
                        if due(i, 2, last):
                            g, u = divmod(j, UPG)
                            pe.wait_ge(copied, it * UNITS + j + 1)
                            if u % TPB == 0:
                                pe.wait_ge(v_ready, it * UNITS + j + TPB)
                            if j >= 1:
                                pe.wait_ge(gated, it * UNITS + j)
                            for t in range(TPB):
                                out = nc.tensor.matmul(obank[:, 0:HD], prT[:, j % 2, t * P:(t + 1) * P],
                                                       v[:, g % 2, u // TPB * TPB + t, :], start=(t == 0),
                                                       stop=(t == TPB - 1))
                            out.then_inc(pv_done, 1)
                        j = i - 3
                        if due(i, 3, last):
                            pe.wait_ge(gated, it * UNITS + j + 1)
                            if j >= 1:
                                pe.wait_ge(g_copied, it * UNITS + j)
                            for t in range(4):
                                out = nc.tensor.transpose(tbank[1][:, t * P:(t + 1) * P],
                                                          og[:, j % 2, 2 * t:2 * t + 2, :].rearrange("p e d -> p (e d)"),
                                                          T.ident[:, :])
                            out.then_inc(g_turned, 1)
                        for g, n in pieces_at(i, last):
                            make(it, g, n)
                        j = i - 4
                        if due(i, 4, last):
                            s, h, _, _ = place(j)
                            pe.wait_ge(g_copied, it * UNITS + j + 1)
                            if j >= 1:
                                pe.wait_ge(added, it * UNITS + j)
                            for t in range(4):
                                at = WV + (h * 4 + t) * D
                                out = nc.tensor.matmul(ybank[:, 0:D], ogT[:, j % 2, t * P:(t + 1) * P],
                                                       slot[s][:, at:at + D], start=(t == 0), stop=(t == 3))
                            out.then_inc(y_done, 1)
                    pe.wait_ge(loaded, 16 * len(loads) + 16)
                    for t in range(NT):
                        nc.tensor.matmul(T.bank[t // 2][:, t % 2 * 256:t % 2 * 256 + 256], T.LNT[:, t * P:(t + 1) * P],
                                         wsel[:, :], start=True, stop=True).then_inc(logits, 1)
                    pe.wait_ge(squashed, NT // 2)
                    pe.wait_ge(x_low, B)
                    for g, n in START:
                        make(0, g, n)
                    turns(pe, step)

                @block.scalar
                def _(act):
                    def split_weights(it, s):
                        act.wait_ge(arrived[s], it * 16 + 16)
                        nc.scalar.activation(w_hi[s][:, :], slot[s][:, 0:WV], ACT.Copy).then_inc(w_high, 1)

                    def split_qk(it, g, kind):
                        act.wait_ge(roped, it * 2 * GROUPS + 2 * g + kind + 1)
                        nc.scalar.activation(qk_hi[:, g % 2, kind, :], qk[:, kind, :], ACT.Copy).then_inc(qk_high, 1)

                    def step(it, i, last):
                        if i == SPLIT_1:
                            act.wait_ge(made, it * GROUPS * PIECES + PIECES)
                            split_weights(it, 1)
                        if i == SPLIT_0 and not last:
                            act.wait_ge(made, it * GROUPS * PIECES + B * PIECES)
                            split_weights(it + 1, 0)
                        if due(i, 0, last):
                            act.wait_ge(maxed, it * UNITS + i + 1)
                            if i >= 2:
                                act.wait_ge(turned, it * UNITS + i - 1)
                            nc.scalar.activation(pr[:, i % 2, :], sbank[i % 2][:, :], ACT.Exp, bias=nmx[:, i % 4:i % 4 + 1],
                                                 accum_out=rs[:, i % 4:i % 4 + 1]).then_inc(expd, 1)
                        j = i - 1
                        if due(i, 1, last):
                            act.wait_ge(turned, it * UNITS + j + 1)
                            if j >= 2:
                                act.wait_ge(pv_done, it * UNITS + j - 1)
                            nc.scalar.activation(prT[:, j % 2, :], tbank[0][:, :], ACT.Copy).then_inc(copied, 1)
                        j = i - 3
                        if due(i, 3, last):
                            act.wait_ge(g_turned, it * UNITS + j + 1)
                            if j >= 2:
                                act.wait_ge(y_done, it * UNITS + j - 1)
                            nc.scalar.activation(ogT[:, j % 2, :], tbank[1][:, :], ACT.Copy).then_inc(g_copied, 1)
                        g, r = divmod(i, UPG)
                        if r in (2, 3) and not (last and g + 1 >= GROUPS):
                            split_qk(it, g + 1, r - 2)
                    for c in range(B):
                        nc.scalar.activation(x_hi[:, c * S:(c + 1) * S], T.LNT[:, c * S:(c + 1) * S], ACT.Copy)\
                            .then_inc(x_high, 1)
                    for i in range(NT // 2):
                        act.wait_ge(logits, 2 * i + 2)
                        nc.scalar.activation(gates[:, 2 * i:2 * i + 2, :, :, :].rearrange("p t v h e -> p (t v h e)"),
                                             T.bank[i][:, :], ACT.Sigmoid).then_inc(squashed, 1)
                    split_weights(0, 0)
                    split_qk(0, 0, 0)
                    split_qk(0, 0, 1)
                    turns(act, step)

                @block.vector
                def _(dve):
                    def pick_gates(it, k):
                        if k:
                            dve.wait_ge(pick_step, it * PICKS + k)
                        V, c, O = (t[:, :, :, :, :].rearrange("p t v h e -> p (t v h) e") for t in (left, seen, pick))
                        m = best[:, :]
                        if k == 0:
                            out = nc.vector.tensor_copy(left[:, :, :, :, :], gates[:, :, :, bass.ds(it * TH, TH), :])
                        elif k == PICKS - 1:
                            out = nc.vector.tensor_scalar(c, V, -2.0 * BIG, None, ALU.is_lt)
                        elif k % 6 == 1:
                            out = nc.vector.tensor_reduce(m, V, axis=AX, op=ALU.max)
                        elif k % 6 == 2:
                            out = nc.vector.tensor_tensor(c, V, spread(m, E), ALU.is_ge)
                        elif k % 6 == 3:
                            out = nc.vector.tensor_tensor(c, c, tiled(T.rev[:, 64 - E:64], NT * 2 * TH), ALU.mult)
                        elif k % 6 == 4:
                            out = nc.vector.tensor_reduce(m, c, axis=AX, op=ALU.max)
                        elif k % 6 == 5:
                            out = nc.vector.tensor_tensor(O, c, spread(m, E), ALU.is_equal)
                        else:
                            out = nc.vector.scalar_tensor_tensor(V, O, -3.0 * BIG, V, ALU.mult, ALU.add)
                        out.then_inc(pick_step, 1)

                    def fetch_gates(it, s, n):
                        heads = bass.ds(it * TH + 2 * s, 2)
                        mine = slice(2 * s, 2 * s + 2)
                        nc.vector.tensor_tensor(gv_h[s][:, :, :, :], gates[:, :, 0, heads, :], seen[:, :, 0, mine, :], ALU.mult)
                        nc.vector.tensor_tensor(go_h[s][:, :, :, :], gates[:, :, 1, heads, :], seen[:, :, 1, mine, :], ALU.mult)\
                            .then_inc(gates_ready, 1)
                        dve.wait_ge(gates_ready, n)

                    def take(it, g, n):
                        s, b = g // B % SLOTS, g % B
                        at = g * PIECES + n
                        dve.wait_ge(made, it * GROUPS * PIECES + at + 1)
                        if n < 4:
                            kind, part = divmod(n, 2)
                            dst = (plain, rotated)[part][:, kind, :]
                            if at >= PIECES and part == 0:
                                dve.wait_ge(roped, it * 2 * GROUPS + 2 * g - 1 + kind)
                            nc.vector.tensor_tensor(dst, pj[at % 2][:, :], trig[:, n, :], ALU.mult).then_inc(read, 1)
                            if part:
                                dve.wait_ge(read, it * GROUPS * PIECES + at + 1)
                                if g:
                                    dve.wait_ge(qk_low, it * 2 * GROUPS + 2 * g - 1 + kind)
                                nc.vector.tensor_tensor(qk[:, kind, :], plain[:, kind, :], rotated[:, kind, :],
                                                        ALU.add).then_inc(roped, 1)
                        else:
                            u = g * UPG + n - 4
                            h, t = divmod(n - 4, TPB)
                            if u >= 2:
                                dve.wait_ge(v_step, it * 2 * UNITS + 2 * u - 3)
                            nc.vector.tensor_tensor(vg[:, u % 2, :, :], pj[at % 2][:, :].rearrange("p (e d) -> p e d", e=E),
                                                    spread(gv_h[s][:, b * TPB + t, h, :], HD), ALU.mult).then_inc(read, 1)

                    def step(it, i, last):
                        j = i - 5
                        if due(i, 5, last):
                            _, _, b, t = place(j)
                            dve.wait_ge(y_done, it * UNITS + j + 1)
                            if j >= TPB:
                                dve.wait_ge(added, it * UNITS + j - TPB + 1)
                            acc = T.LNX[:, b * TPB + t, :]
                            nc.vector.tensor_tensor(acc, acc, ybank[:, 0:D], ALU.add).then_inc(added, 1)
                        if due(i, 0, last):
                            dve.wait_ge(scored, it * UNITS + i + 1)
                            nc.vector.tensor_reduce(nmx[:, i % 4:i % 4 + 1], sbank[i % 2][:, :], axis=AX, op=ALU.max,
                                                    negate=True).then_inc(maxed, 1)
                        j = i - 2
                        if due(i, 2, last):
                            s, h, b, t = place(j)
                            dve.wait_ge(expd, it * UNITS + j + 1)
                            nc.vector.reciprocal(rs[:, j % 4:j % 4 + 1], rs[:, j % 4:j % 4 + 1]).then_inc(o_step, 1)
                            dve.wait_ge(o_step, it * 2 * UNITS + 2 * j + 1)
                            nc.vector.tensor_scalar(go[:, j % 4, :], go_h[s][:, b * TPB + t, h, :], rs[:, j % 4:j % 4 + 1],
                                                    None, ALU.mult).then_inc(o_step, 1)
                            dve.wait_ge(o_step, it * 2 * UNITS + 2 * j + 2)
                            if j >= 2:
                                dve.wait_ge(g_turned, it * UNITS + j - 1)
                            dve.wait_ge(pv_done, it * UNITS + j + 1)
                            nc.vector.tensor_tensor(og[:, j % 2, :, :], tiled(obank[:, 0:HD], E), spread(go[:, j % 4, :], HD),
                                                    ALU.mult).then_inc(gated, 1)
                        if 0 <= i - PICK < PICKS and not last:
                            if i == PICK:
                                dve.wait_ge(gates_ready, it * SLOTS + SLOTS)
                            pick_gates(it + 1, i - PICK)
                        for s in range(SLOTS):
                            if i == (s + 1) * UNITS // SLOTS + 5 and not last:
                                dve.wait_ge(gated, it * UNITS + (s + 1) * UNITS // SLOTS)
                                dve.wait_ge(read, it * GROUPS * PIECES + (s + 1) * B * PIECES)
                                if s == 0:
                                    dve.wait_ge(pick_step, it * PICKS + 2 * PICKS)
                                fetch_gates(it + 1, s, it * SLOTS + SLOTS + s + 1)
                        for g, n in pieces_at(i, last):
                            take(it, g, n)
                    for c in range(B):
                        cols = slice(c * S, (c + 1) * S)
                        dve.wait_ge(x_high, c + 1)
                        nc.vector.tensor_tensor(x_lo[:, cols], T.LNT[:, cols], x_hi[:, cols], ALU.subtract).then_inc(x_low, 1)
                    dve.wait_ge(squashed, NT // 2)
                    for n in range(PICKS):
                        pick_gates(0, n)
                    dve.wait_ge(pick_step, PICKS)
                    for s in range(SLOTS):
                        fetch_gates(0, s, s + 1)
                    for g, n in START:
                        take(0, g, n)
                    turns(dve, step)
                    dve.wait_ge(added, TURNS * UNITS)

                @block.gpsimd
                def _(pool):
                    def split_weights(it, s, later):
                        pool.wait_ge(w_high, it * SLOTS + later * SLOTS + s + 1)
                        nc.gpsimd.tensor_tensor(w_lo[s][:, :], slot[s][:, 0:WV], w_hi[s][:, :], ALU.subtract).then_inc(w_low, 1)

                    def sum_experts(it, u, last):
                        g, n = divmod(u, UPG)
                        if u == SPLIT_1 + UPG:
                            split_weights(it, 1, 0)
                        if u == SPLIT_0 + UPG and not last:
                            split_weights(it, 0, 1)
                        for kind in range(2 if n == 0 else 0):
                            pool.wait_ge(qk_high, it * 2 * GROUPS + 2 * g + kind + 1)
                            nc.gpsimd.tensor_tensor(qk_lo[:, g % 2, kind, :], qk[:, kind, :], qk_hi[:, g % 2, kind, :],
                                                    ALU.subtract).then_inc(qk_low, 1)
                        pool.wait_ge(read, it * GROUPS * PIECES + g * PIECES + 4 + n + 1)
                        nc.gpsimd.tensor_tensor(vs[:, u % 2, :, :], vg[:, u % 2, 0:4, :], vg[:, u % 2, 4:8, :], ALU.add)\
                            .then_inc(v_step, 1)
                        pool.wait_ge(v_step, it * 2 * UNITS + 2 * u + 1)
                        nc.gpsimd.tensor_tensor(vs[:, u % 2, 0:2, :], vs[:, u % 2, 0:2, :], vs[:, u % 2, 2:4, :], ALU.add)\
                            .then_inc(v_step, 1)
                        pool.wait_ge(v_step, it * 2 * UNITS + 2 * u + 2)
                        if g >= 2 and n == 0:
                            pool.wait_ge(pv_done, it * UNITS + (g - 1) * UPG)
                        nc.gpsimd.tensor_tensor(v[:, g % 2, n, :], vs[:, u % 2, 0, :], vs[:, u % 2, 1, :], ALU.add)\
                            .then_inc(v_ready, 1)
                    split_weights(0, 0, 0)
                    for u in range(2 * UPG):
                        sum_experts(0, u, False)
                    with pool.Fori(0, TURNS - 1) as it:
                        for u in range(2 * UPG, 2 * UPG + UNITS):
                            sum_experts(it, u, False)
                    for u in range(2 * UPG, UNITS):
                        sum_experts(TURNS - 1, u, True)

        with Stage(nc, "l2f") as sf:
            w1 = sf.sb("w1", [P, F])
            w2 = sf.sb("w2", [P, 4, D])
            hid = sf.sb("hid", [P, 2, 4, S])
            names = ("loaded", "up_done", "hidden", "down_done", "added")
            w_loaded, up_done, hidden, down_done, added = (sf.sem(n) for n in names)
            layernorm(nc, T, T.LNX[:, :, :], T.LNX[:, :, :], T.LNT[:, :], [(w1[:, :], A["l2m_w1"]), (w2[:, :, :], A["l2m_w2"])],
                      w_loaded, ln1[:, 0, :], ln1[:, 1, :])
            with nc.Block() as block:
                @block.tensor
                def _(pe):
                    pe.wait_ge(w_loaded, 32)
                    for c in range(B + 1):
                        for f in range(4 if c < B else 0):
                            n = 4 * c + f
                            if n >= 4:
                                pe.wait_ge(hidden, n - 3)
                            nc.tensor.matmul(T.bank[f][:, :], w1[:, f * P:(f + 1) * P], T.LNT[:, c * S:(c + 1) * S],
                                             start=True, stop=True).then_inc(up_done, 1)
                        if c:
                            d = c - 1
                            pe.wait_ge(hidden, 4 * c)
                            if d >= 2:
                                pe.wait_ge(added, d - 1)
                            for t in range(TPB):
                                for f in range(4):
                                    last = nc.tensor.matmul(T.bank[4 + d % 2][:, t * D:(t + 1) * D],
                                                            hid[:, d % 2, f, t * P:(t + 1) * P], w2[:, f, :], start=(f == 0),
                                                            stop=(f == 3))
                            last.then_inc(down_done, 1)

                @block.scalar
                def _(act):
                    for n in range(4 * B):
                        c, f = divmod(n, 4)
                        act.wait_ge(up_done, n + 1)
                        if c >= 2:
                            act.wait_ge(down_done, c - 1)
                        nc.scalar.activation(hid[:, c % 2, f, :], T.bank[f][:, :], ACT.Relu, bias=b1[:, f:f + 1]).then_inc(hidden, 1)

                @block.vector
                def _(dve):
                    link = chain(T, dve)
                    link(nc.vector.tensor_tensor(T.LNX[:, :, :], T.LNX[:, :, :], tiled(b2[:, :], NT), ALU.add))
                    for c in range(B):
                        dve.wait_ge(down_done, c + 1)
                        x = T.LNX[:, c * TPB:(c + 1) * TPB, :]
                        nc.vector.tensor_tensor(x, x, T.bank[4 + c % 2][:, :].rearrange("p (t d) -> p t d", t=TPB), ALU.add)\
                            .then_inc(added, 1)
        layernorm(nc, T, T.LNX[:, :, :], T.LNX[:, :, :], T.LNT[:, :], gain=ln2[:, 0, :], shift=ln2[:, 1, :])
        with nc.Block() as block:
            @block.vector
            def _(dve):
                nc.vector.tensor_tensor(T.X[:, :, :], T.X[:, :, :], T.LNX[:, :, :], ALU.add)


def build(nc, A, out):
    T = Shared()
    T.dve_steps = T.ln_calls = T.ln_affine_calls = 0
    with ExitStack() as ctx:
        def sb(name, shape, dt=F32):
            return ctx.enter_context(nc.sbuf_tensor(name, shape, dt))

        T.X = sb("X", [P, NT, D])
        T.LNX = sb("LNX", [P, NT, D])
        T.LNT = sb("LNT", [P, N])
        T.CTX = sb("CTX", [L, B, D])
        T.CTXT = sb("CTXT", [P, B * L])
        T.ident = sb("ident", [P, P])
        T.zeros = sb("zeros", [P, P])
        T.rev = sb("rev", [P, 64])
        T.ln_stats = sb("ln_stats", [P, NT, 6])
        T.ln_mv = sb("ln_mv", [P, NT, 2])
        T.ln_var_eps, T.ln_rstd, T.ln_shift = (sb(n, [P, NT]) for n in ("ln_var_eps", "ln_rstd", "ln_shift"))
        T.bank = [ctx.enter_context(nc.psum_tensor(f"bank{i}", [P, 512], F32)) for i in range(8)]
        T.dve_step, T.ln_var, T.ln_std, T.ln_scaled, T.ln_even, T.ln_odd, T.ln_affine, T.ln_turned, inputs, stored = (
            ctx.enter_context(nc.semaphore(n))
            for n in ("dve_step", "ln_var", "ln_std", "ln_scaled", "ln_even", "ln_odd", "ln_affine", "ln_turned", "inputs", "stored"))
        with nc.Block() as block:
            @block.sync
            def _(sp):
                for to, frm in ((T.X[:, :, :], A["x"]), (T.CTX[:, :, :], A["ctx"]), (T.CTXT[:, :], A["ctxT"]),
                                (T.ident[:, :], A["ident"]), (T.rev[:, :], A["rev"])):
                    sp.dma_start(to, frm).then_inc(inputs, 16)
                sp.wait_ge(inputs, 80)

            @block.vector
            def _(dve):
                nc.vector.memset(T.zeros[:, :], 0.0)

        stages = [
            lambda: l0_attention(nc, T, A),
            lambda: context_attention(nc, T, A, "l0x", H=1, dk=128, HB=1, biased=True),
            lambda: l0_moe(nc, T, A),
            lambda: l1_attention(nc, T, A),
            lambda: l1_coattention(nc, T, A),
            lambda: l1_moe(nc, T, A),
            lambda: l2_attention(nc, T, A),
            lambda: context_attention(nc, T, A, "l2x", H=4, dk=32, HB=4, rope=True, normed=True, keep_mask=True),
            lambda: l2_moe_attention(nc, T, A),
            lambda: l3_attention(nc, T, A),
            lambda: context_attention(nc, T, A, "l3x", H=16, dk=64, HB=4),
            lambda: l3_moe(nc, T, A),
        ]
        for n in STAGES:
            stages[n]()
        with nc.Block() as block:
            @block.sync
            def _(sp):
                sp.dma_start(out, T.X[:, :, :]).then_inc(stored, 16)
                sp.wait_ge(stored, 16)


def _rope_tables(positions, half, base):
    angle = positions[None, :].astype(np.float32) * (base ** (-np.arange(half, dtype=np.float32) / half))[:, None]
    return np.cos(angle.astype(np.float32)), np.sin(angle.astype(np.float32))


def _layouts(a):
    f = {}

    def rep(v, n=P):
        return np.broadcast_to(v.reshape(1, -1), (n, v.size))

    def tok(x):
        return x.reshape(NT, P, D).transpose(1, 0, 2)

    ctx = a["ctx_1024"]
    f["x"] = tok(a["x"])
    f["ctx"] = ctx.transpose(1, 0, 2)
    f["ctxT"] = ctx.transpose(2, 0, 1).reshape(D, B * L)
    f["ident"] = np.eye(P, dtype=np.float32)

    w, bias = a["L0_attn_W_attn"], a["L0_attn_b_attn"]

    def copies(m):
        z = np.broadcast_to(m.reshape(m.shape[:-1] + (8, 4, 1, 8)), m.shape[:-1] + (8, 4, 4, 8))
        return z.reshape(m.shape[:-1] + (8, 128))
    copy = np.arange(P) // 8 % 4
    low = np.stack([-(copy // 2), -(copy % 2)], axis=1).astype(np.float32)
    f["l0a_w"] = np.concatenate([copies(w[:, :256]).reshape(D, 1024), w[:, 256:]], axis=1)
    f["l0a_cols"] = np.concatenate([copies(bias[:256]).T, rep(a["L0_attn_temperature"]), low], axis=1)
    f["l0a_rows"] = np.concatenate([rep(bias[256:]), rep(a["L0_attn_b_proj"])], axis=1)
    f["l0a_wproj"] = a["L0_attn_W_proj"]
    u = np.arange(2 * S - P)[None, :] - (S - P) - np.arange(P)[:, None]
    f["rel"] = np.where(u <= 0, -u, BIG).astype(np.float32)

    f["l0x_wq"] = a["L0_xattn_Wq"].T.reshape(D, 1, 1, P)
    f["l0x_wk"] = a["L0_xattn_Wk"].T.reshape(D, 1, 1, P)
    f["l0x_wv"] = a["L0_xattn_Wv"].T.reshape(D, 1, P)
    f["l0x_wo"] = a["L0_xattn_Wo"].T.reshape(P, 1, D)
    f["l0x_cols"] = np.stack([a["L0_xattn_bq"], a["L0_xattn_bv"]], axis=1)
    f["l0x_rows"] = rep(a["L0_xattn_bo"])

    qw = a["L2_xattn_q_w"].transpose(1, 0, 2)
    kw = np.broadcast_to(a["L2_xattn_kv_w"][0, 0][:, None, :], (D, 4, 32))
    vw = np.broadcast_to(a["L2_xattn_kv_w"][1, 0][:, None, :], (D, 4, 32))

    def halves(m):
        return np.concatenate([m[..., 16:], m[..., :16]], axis=-1)
    f["l2x_wq"] = np.stack([qw.reshape(D, P), halves(qw).reshape(D, P)], axis=1).reshape(D, 2, 1, P)
    f["l2x_wk"] = np.stack([kw.reshape(D, P), halves(kw).reshape(D, P)], axis=1).reshape(D, 2, 1, P)
    f["l2x_wv"] = vw.reshape(D, 1, P)
    f["l2x_wo"] = a["L2_xattn_out_w"].reshape(P, 1, D)
    for n, pos in (("l2x_qtrig", np.arange(L, L + S)), ("l2x_ktrig", np.arange(L))):
        cos, sin = _rope_tables(pos, 16, 10000.0)
        f[n] = np.stack([np.tile(np.concatenate([cos, cos]), (4, 1)), np.tile(np.concatenate([-sin, sin]), (4, 1))], axis=1)
    f["l2x_gain"] = a["L2_xattn_rms_scale"].reshape(D, 1)
    f["l2x_keep"] = np.broadcast_to(a["mask_BxS2_bk0"].astype(np.int32)[None], (P, B, L))

    f["l3x_wq"] = a["L3_xattn_w_q"].reshape(D, 1, 8, P)
    f["l3x_wk"] = a["L3_xattn_w_k"].reshape(D, 1, 8, P)
    f["l3x_wv"] = a["L3_xattn_w_v"].reshape(D, 8, P)
    f["l3x_wo"] = a["L3_xattn_w_o"].reshape(8, P, D).transpose(1, 0, 2)

    def native(g, u, d):
        e = g.shape[0]
        def cols(m):
            return m.reshape(e // 2, 2, D, 64).transpose(0, 2, 1, 3).reshape(e // 2, D, P)
        return np.concatenate([cols(g), cols(u), d.reshape(e // 2, P, D)], axis=2)

    def turned(m):
        return m.transpose(0, 2, 1)
    f["rev"] = rep(np.arange(64, 0, -1, dtype=np.float32))
    f["tri"] = np.stack([np.triu(np.ones((P, P), np.float32), 1), np.ones((P, P), np.float32)], axis=1)
    f["l0m_router"] = a["L0_ffn_gate_w"].T
    f["l0m_bias"] = rep(a["L0_ffn_gate_bias"])
    f["l0m_pairs"] = native(turned(a["L0_ffn_Wg"]), turned(a["L0_ffn_Wu"]), turned(a["L0_ffn_Wd"]))
    f["l0m_shared"] = np.concatenate([a["L0_ffn_Ws_g"].T, a["L0_ffn_Ws_u"].T, a["L0_ffn_Ws_d"].T], axis=1).reshape(D, 1, 3 * P)
    f["l1m_router"] = a["L1_ffn_router_w"].T
    f["l1m_bias"] = rep(a["L1_ffn_e_bias"])
    f["l1m_pairs"] = native(a["L1_ffn_gate_w"], a["L1_ffn_up_w"], a["L1_ffn_down_w"])
    f["l1m_shared"] = np.stack([np.concatenate([a["L1_ffn_sh_gate_w"][:, s], a["L1_ffn_sh_up_w"][:, s],
                                                a["L1_ffn_sh_down_w"][s, :]], axis=1)
                                for s in (slice(0, P), slice(P, 2 * P))], axis=1)
    f["l3m_router"] = a["L3_ffn_gate_w"].T
    f["l3m_bias"] = rep(a["L3_ffn_bias"])
    f["l3m_pairs"] = native(a["L3_ffn_W1"], a["L3_ffn_W3"], a["L3_ffn_W2"])
    half = np.zeros((P, 1, 3 * P), f["l3m_pairs"].dtype)
    half[:, 0, 0:64] = a["L3_ffn_sw1"].T
    half[:, 0, P:P + 64] = a["L3_ffn_sw3"].T
    half[0:64, 0, 2 * P:3 * P] = a["L3_ffn_sw2"].T
    f["l3m_shared"] = half

    f["l1a_wq"] = a["L1_attn_wq"].T
    f["l1a_wkv"] = np.concatenate([a["L1_attn_wk"].T, a["L1_attn_wv"].T], axis=1)
    f["l1a_wo"] = a["L1_attn_wo"].T
    f["l1a_bo"] = rep(a["L1_attn_bo"])
    r = np.arange(P)
    f["l1a_same"] = np.concatenate([r[:, None] // 8 == r[None, :] // 8, r[:, None] // 8 == np.arange(16)[None, :]],
                                   axis=1).astype(np.float32)
    f["l1c_cols"] = np.concatenate([a["L1_xattn_w_sim"].reshape(3, D).T, rep(a["L1_xattn_b_sim"])], axis=1)
    f["l1c_w"] = a["L1_xattn_W_qv"].reshape(4, D, D).transpose(1, 0, 2)
    f["l1c_bias"] = rep(a["L1_xattn_b_qv"])

    f["l2a_w"] = a["L2_attn_W"]

    def pair_cols(m):
        return m.reshape(8, 2, D, 64).transpose(0, 2, 1, 3).reshape(8, D, P)

    def rotated_cols(m):
        return np.concatenate([m[..., 16:32], m[..., :16], m[..., 32:]], axis=-1)
    wq, wk = a["L2_ffn_Wq"], a["L2_ffn_Wk"]
    wv = a["L2_ffn_Wv"].transpose(0, 2, 1, 3).reshape(8, 2, D, 512).transpose(0, 2, 1, 3).reshape(8, D, 1024)
    wo = a["L2_ffn_Wo"].reshape(8, 2, 4, P, D).transpose(0, 3, 1, 2, 4).reshape(8, P, 1024)
    f["l2m_w"] = np.concatenate([pair_cols(wq), pair_cols(rotated_cols(wq)), pair_cols(wk), pair_cols(rotated_cols(wk)), wv, wo],
                                axis=2)
    f["l2m_wsel"] = np.concatenate([a["L2_ffn_Wsel_v"].reshape(P, D).T, a["L2_ffn_Wsel_o"].reshape(P, D).T], axis=1)
    cos, sin = _rope_tables(np.arange(S), 16, 10000.0)
    cos = np.tile(np.concatenate([cos, cos, np.ones((32, S), np.float32)]), (2, 1))
    sin = np.tile(np.concatenate([-sin, sin, np.zeros((32, S), np.float32)]), (2, 1))
    f["l2m_trig"] = np.stack([cos / 8, sin / 8, cos, sin], axis=1).astype(np.float32)
    for n in ("1", "2"):
        f["l2m_ln" + n] = np.stack([rep(a[f"L2_ffn_ln{n}_g"]), rep(a[f"L2_ffn_ln{n}_b"])], axis=1)
    f["l2m_w1"] = a["L2_ffn_W1"]
    f["l2m_b1"] = a["L2_ffn_b1"].reshape(4, P).T
    f["l2m_w2"] = a["L2_ffn_W2"].reshape(4, P, D).transpose(1, 0, 2)
    f["l2m_b2"] = rep(a["L2_ffn_b2"])

    f["l3a_w"] = np.concatenate([a["L3_attn_Wq"].T, a["L3_attn_Wk"].T, a["L3_attn_Wv"].T], axis=1)
    low = np.tril(np.ones((P, P), np.float32))
    f["tril"] = np.stack([low, (1 - low) * np.float32(1e-9)], axis=1)
    return {n: np.ascontiguousarray(v) for n, v in f.items()}


def kernel(**inputs):
    import concourse.bacc as bacc
    from concourse.bass_utils import run_bass_kernel_spmd

    arrays = _layouts({n: np.asarray(v) for n, v in inputs.items()})
    nc = bacc.Bacc("TRN2", target_bir_lowering=False, num_devices=1)
    A = {n: nc.dram_tensor(f"in_{n}", v.shape, mybir.dt.from_np(v.dtype), kind="ExternalInput").ap()
         for n, v in arrays.items()}
    out = nc.dram_tensor("out", (P, NT, D), F32, kind="ExternalOutput").ap()
    build(nc, A, out)
    r = run_bass_kernel_spmd(nc, [{f"in_{n}": v for n, v in arrays.items()}], core_ids=[0])
    return np.ascontiguousarray(r.results[0]["out"].transpose(1, 0, 2)).reshape(B, S, D)
```

```python
from contextlib import ExitStack

import numpy as np

import concourse.bass as bass
from concourse import mybir

STAGES = tuple(range(12))

B, S, D = 4, 512, 128
P = 128
TPB = S // P
NT = B * TPB
N = B * S
L = 77
F32 = mybir.dt.float32
F32R = mybir.dt.float32r
BF16 = mybir.dt.bfloat16
ALU = mybir.AluOpType
ACT = mybir.ActivationFunctionType
AX = mybir.AxisListType.X
BIG = 1.0e30


class Shared:
    pass


def spread(ap, n):
    return ap.unsqueeze(2).broadcast_to([ap.shape[0], ap.shape[1], n])


def tiled(ap, n):
    return ap.unsqueeze(1).broadcast_to([ap.shape[0], n, ap.shape[1]])


def chain(T, dve):
    def link(ins):
        T.dve_steps += 1
        ins.then_inc(T.dve_step, 1)
        dve.wait_ge(T.dve_step, T.dve_steps)
    return link


def layernorm(nc, T, src, dst, dstT, loads=(), load_sem=None, gain=None, shift=None, eps=1e-5, zeros=()):
    n = T.ln_calls
    T.ln_calls += 1
    n_affine = T.ln_affine_calls
    T.ln_affine_calls += gain is not None
    with nc.Block() as block:
        @block.sync
        def _(sp):
            for to, frm in loads:
                sp.dma_start(to, frm).then_inc(load_sem, 16)

        @block.gpsimd
        def _(pool):
            for sems, _ in T.used:
                for s in sems:
                    pool.sem_clear(s)
            for buffer in zeros:
                nc.gpsimd.memset(buffer, 0.0)

        @block.vector
        def _(dve):
            link = chain(T, dve)
            for t in range(NT):
                out = nc.vector.bn_stats(T.ln_stats[:, t, :], src[:, t, :])
            link(out)
            for t in range(NT):
                out = nc.vector.bn_aggr(T.ln_mv[:, t, :], T.ln_stats[:, t, :])
            link(out)
            nc.vector.tensor_scalar(T.ln_var_eps[:, :], T.ln_mv[:, :, 1], eps, None, ALU.add).then_inc(T.ln_var, 1)
            dve.wait_ge(T.ln_std, n + 1)
            link(nc.vector.reciprocal(T.ln_rstd[:, :], T.ln_var_eps[:, :]))
            nc.vector.scalar_tensor_tensor(T.ln_shift[:, :], T.ln_mv[:, :, 0], -1.0, T.ln_rstd[:, :], ALU.mult, ALU.mult)\
                .then_inc(T.ln_scaled, 1)
            dve.wait_ge(T.ln_scaled, n + 1)
            for t in range(NT):
                if t % 2 == 0:
                    nc.vector.tensor_scalar(dst[:, t, :], src[:, t, :], T.ln_rstd[:, t:t + 1], T.ln_shift[:, t:t + 1],
                                            ALU.mult, ALU.add).then_inc(T.ln_even, 1)
            if gain is not None:
                for c in range(B):
                    ts = slice(c * TPB, (c + 1) * TPB)
                    dve.wait_ge(T.ln_even, NT // 2 * n + TPB // 2 * (c + 1))
                    dve.wait_ge(T.ln_odd, NT // 2 * n + TPB // 2 * (c + 1))
                    link(nc.vector.tensor_tensor(dst[:, ts, :], dst[:, ts, :], tiled(gain, TPB), ALU.mult))
                    nc.vector.tensor_tensor(dst[:, ts, :], dst[:, ts, :], tiled(shift, TPB), ALU.add).then_inc(T.ln_affine, 1)
            for c in range(1, B, 2):
                dve.wait_ge(T.ln_turned, B * n + c + 1)
                nc.vector.tensor_copy(dstT[:, c * S:(c + 1) * S], T.bank[c][:, :])

        @block.tensor
        def _(pe):
            for c in range(B):
                pe.wait_ge(T.ln_even, NT // 2 * n + TPB // 2 * (c + 1))
                pe.wait_ge(T.ln_odd, NT // 2 * n + TPB // 2 * (c + 1))
                if gain is not None:
                    pe.wait_ge(T.ln_affine, B * n_affine + c + 1)
                for t in range(TPB):
                    last = nc.tensor.transpose(T.bank[c][:, t * P:(t + 1) * P], dst[:, c * TPB + t, :], T.ident[:, :])
                last.then_inc(T.ln_turned, 1)

        @block.scalar
        def _(act):
            act.wait_ge(T.ln_var, n + 1)
            nc.scalar.activation(T.ln_var_eps[:, :], T.ln_var_eps[:, :], ACT.Sqrt).then_inc(T.ln_std, 1)
            act.wait_ge(T.ln_scaled, n + 1)
            for t in range(1, NT, 2):
                nc.scalar.activation(dst[:, t, :], src[:, t, :], ACT.Identity, bias=T.ln_shift[:, t:t + 1],
                                     scale=T.ln_rstd[:, t:t + 1]).then_inc(T.ln_odd, 1)
            for c in range(0, B, 2):
                act.wait_ge(T.ln_turned, B * n + c + 1)
                nc.scalar.activation(dstT[:, c * S:(c + 1) * S], T.bank[c][:, :], ACT.Copy)
    for _, held in T.used:
        held.close()
    T.used = []


class Stage:
    def __init__(self, nc, T, name):
        self.nc, self.T, self.name, self.ctx, self.held, self.sems = nc, T, name, ExitStack(), ExitStack(), []

    def __enter__(self):
        self.ctx.__enter__()
        return self

    def __exit__(self, *a):
        if self.sems:
            self.T.used.append((self.sems, self.held))
        return self.ctx.__exit__(*a)

    def sb(self, name, shape, dt=F32):
        return self.ctx.enter_context(self.nc.sbuf_tensor(f"{self.name}_{name}", shape, dt))

    def sem(self, name):
        self.sems.append(self.held.enter_context(self.nc.semaphore(f"{self.name}_{name}")))
        return self.sems[-1]


def l0_attention(nc, T, A):
    H, HD = 16, 8
    G, HPG = 4, 4
    UNITS = TPB * H
    POOL_HEADS = 4
    TLAG, VLAG, RING = 2, 4, 4
    slopes = [2.0 ** (-0.5 * (h + 1)) for h in range(H)]
    with Stage(nc, T, "l0a") as st:
        w = st.sb("w", [P, 2 * G * P + D])
        wproj = st.sb("wproj", [P, D])
        cols = st.sb("cols", [P, 2 * G + 3])
        rows = st.sb("rows", [P, 2 * D])
        rel = st.sb("rel", [P, 2 * S - P])
        alibi = st.sb("alibi", [P, H, 2 * S - P])
        qscale = st.sb("qscale", [P, 1])
        qbias = st.sb("qbias", [P, G])
        xb = st.sb("xb", [P, S])
        raw = st.sb("raw", [P, 2 * G, S])
        qk = st.sb("qk", [P, 2 * G, S], F32R)
        v = st.sb("v", [P, TPB, H * (P + HD)])
        sc = st.sb("sc", [P, RING, S])
        pr = st.sb("pr", [P, RING, S])
        prT = st.sb("prT", [P, RING, S])
        nmx = st.sb("nmx", [P, RING])
        rsum = st.sb("rsum", [P, TPB, H])
        rinv = st.sb("rinv", [P, TPB, H])
        rrep = st.sb("rrep", [P, 2, D])
        rinvT = st.sb("rinvT", [P, 2, P])
        yT = st.sb("yT", [P, S])
        loaded = st.sem("loaded")
        prepared = st.sem("prepared")
        x_ready, projected, q_raw, k_raw, high, split, v_ready = (
            st.sem(n) for n in ("x_ready", "projected", "q_raw", "k_raw", "high", "split", "v_ready"))
        scored, masked, expd, turned, copied_a, copied_v, pv_done, yT_ready = (
            st.sem(n) for n in ("scored", "masked", "expd", "turned", "copied_a", "copied_v",
                                "pv_done", "yT_ready"))
        rrep_ready, r_turned, rinvT_ready, out_ready, added, rinv_ready = (
            st.sem(n) for n in ("rrep_ready", "r_turned", "rinvT_ready", "out_ready", "added", "rinv_ready"))
        score_seen, alibi_ready = st.sem("score_seen"), st.sem("alibi_ready")
        loads = [(w[:, :], A["l0a_w"]), (wproj[:, :], A["l0a_wproj"]), (cols[:, :], A["l0a_cols"]),
                 (rows[:, :], A["l0a_rows"]), (rel[:, :], A["rel"])]
        layernorm(nc, T, T.X[:, :, :], T.LNX[:, :, :], T.LNT[:, :], loads, loaded, zeros=[v[:, :, :]])
        low_rows = (cols[:, 2 * G + 1:2 * G + 2], cols[:, 2 * G + 2:2 * G + 3])
        pj, sbank, tbank, obank, rbank = T.bank, T.bank[0:4], T.bank[4:6], T.bank[6:7], T.bank[7]

        with nc.Block() as block:
            @block.vector
            def _(dve):
                link = chain(T, dve)
                dve.wait_ge(loaded, 16 * len(loads))
                link(nc.vector.reciprocal(qscale[:, :], cols[:, 2 * G:2 * G + 1]))
                link(nc.vector.tensor_scalar(qscale[:, :], qscale[:, :], -(HD ** -0.5), None, ALU.mult))
                nc.vector.tensor_scalar(qbias[:, :], cols[:, 0:G], qscale[:, 0:1], None, ALU.mult).then_inc(prepared, 1)
                for h in range(H - POOL_HEADS):
                    nc.vector.tensor_scalar(alibi[:, h, :], rel[:, :], slopes[h], None, ALU.mult)
                link(nc.vector.tensor_tensor(T.X[:, :, :], T.X[:, :, :], tiled(rows[:, D:2 * D], NT), ALU.add))
                with dve.Fori(0, B) as b:
                    def split_group(g):
                        for n in (g, G + g):
                            dve.wait_ge(high, b * 2 * G + n + 1)
                            nc.vector.scalar_tensor_tensor(qk[:, n, :], qk[:, n, :], low_rows[n // G], raw[:, n, :], ALU.mult,
                                                           ALU.add).then_inc(split, 1)
                    for n in range(G):
                        dve.wait_ge(projected, b * 9 + G + n + 1)
                        nc.vector.tensor_scalar(raw[:, G + n, :], pj[G + n][:, :], cols[:, G + n:G + n + 1], None, ALU.add)\
                            .then_inc(k_raw, 1)
                    dve.wait_ge(projected, b * 9 + 9)
                    dve.wait_ge(alibi_ready, 1)
                    for t in range(TPB):
                        nc.vector.tensor_tensor(v[:, t, :].rearrange("p (h c) -> p h c", h=H)[:, :, 0:HD],
                                                pj[0][:, t * D:(t + 1) * D].rearrange("p (h d) -> p h d", h=H),
                                                rows[:, 0:D].rearrange("p (h d) -> p h d", h=H), ALU.add).then_inc(v_ready, 1)
                    split_group(0)
                    for i in range(UNITS + VLAG + 1):
                        if i < H and i % HPG == 1 and i // HPG + 1 < G:
                            split_group(i // HPG + 1)
                        if i < UNITS:
                            tt, h = divmod(i, H)
                            W = (tt + 1) * P
                            u0 = S - P - tt * P
                            dve.wait_ge(scored, b * UNITS + i + 1)
                            if i >= RING:
                                dve.wait_ge(expd, b * UNITS + i - RING + 1)
                            dve.sem_inc(score_seen, 1)
                            nc.vector.tensor_tensor_reduce(
                                out=sc[:, i % RING, 0:W], in0=alibi[:, h, u0:u0 + W], in1=sbank[i % 4][:, 0:W], scale=1.0,
                                scalar=3.0e38, op0=ALU.add, op1=ALU.min,
                                accum_out=nmx[:, i % RING:i % RING + 1]).then_inc(masked, 1)
                        j = i - TLAG
                        if 0 <= j < UNITS and j % 2:
                            W = (j // H + 1) * P
                            dve.wait_ge(turned, b * UNITS + j + 1)
                            if j >= RING:
                                dve.wait_ge(pv_done, b * UNITS + j - RING + 1)
                            nc.vector.tensor_copy(prT[:, j % RING, 0:W], tbank[1][:, 0:W]).then_inc(copied_v, 1)
                        j = i - 1
                        if 0 <= j < UNITS and j % H == H - 1:
                            tt = j // H
                            dve.wait_ge(expd, b * UNITS + j + 1)
                            nc.vector.reciprocal(rinv[:, tt, :], rsum[:, tt, :]).then_inc(rinv_ready, 1)
                            dve.wait_ge(rinv_ready, b * TPB + tt + 1)
                            if tt >= 2:
                                dve.wait_ge(r_turned, b * TPB + tt - 1)
                            nc.vector.tensor_copy(rrep[:, tt % 2, :].rearrange("p (h d) -> p h d", h=H),
                                                  spread(rinv[:, tt, :], HD)).then_inc(rrep_ready, 1)
                        j = i - VLAG - 1
                        if j >= 0 and j % H == H - 1:
                            tt = j // H
                            dve.wait_ge(pv_done, b * UNITS + j + 1)
                            dve.wait_ge(rinvT_ready, b * TPB + tt + 1)
                            nc.vector.tensor_tensor(yT[:, tt * P:(tt + 1) * P], obank[0][:, tt * P:(tt + 1) * P],
                                                    rinvT[:, tt % 2, :], ALU.mult).then_inc(yT_ready, 1)
                    dve.wait_ge(out_ready, b + 1)
                    nc.vector.tensor_tensor(T.X[:, bass.ds(b * TPB, TPB), :], T.X[:, bass.ds(b * TPB, TPB), :],
                                            pj[1][:, :].rearrange("p (t c) -> p t c", t=TPB), ALU.add).then_inc(added, 1)

            @block.gpsimd
            def _(pool):
                pool.wait_ge(loaded, 16 * len(loads))
                for h in range(H - POOL_HEADS, H):
                    out = nc.gpsimd.tensor_scalar(alibi[:, h, :], rel[:, :], slopes[h], None, ALU.mult)
                out.then_inc(alibi_ready, 1)

            @block.scalar
            def _(act):
                act.wait_ge(loaded, 16 * len(loads))
                act.wait_ge(prepared, 1)
                with act.Fori(0, B) as b:
                    nc.scalar.activation(xb[:, :], T.LNT[:, bass.ds(b * S, S)], ACT.Copy).then_inc(x_ready, 1)
                    for n in range(G):
                        act.wait_ge(projected, b * 9 + n + 1)
                        nc.scalar.activation(raw[:, n, :], pj[n][:, :], ACT.Identity, bias=qbias[:, n:n + 1],
                                             scale=qscale[:, 0:1]).then_inc(q_raw, 1)
                        act.wait_ge(q_raw, b * G + n + 1)
                        nc.scalar.activation(qk[:, n, :], raw[:, n, :], ACT.Copy).then_inc(high, 1)
                    for n in range(G):
                        act.wait_ge(k_raw, b * G + n + 1)
                        nc.scalar.activation(qk[:, G + n, :], raw[:, G + n, :], ACT.Copy).then_inc(high, 1)
                    for i in range(UNITS + TLAG):
                        if i < UNITS:
                            tt, h = divmod(i, H)
                            W = (tt + 1) * P
                            act.wait_ge(masked, b * UNITS + i + 1)
                            if i >= RING:
                                act.wait_ge(turned, b * UNITS + i - RING + 1)
                            nc.scalar.activation(pr[:, i % RING, 0:W], sc[:, i % RING, 0:W], ACT.Exp,
                                                 bias=nmx[:, i % RING:i % RING + 1], scale=-1.0,
                                                 accum_out=rsum[:, tt, h:h + 1]).then_inc(expd, 1)
                        j = i - TLAG
                        if j >= 0 and j % 2 == 0:
                            W = (j // H + 1) * P
                            act.wait_ge(turned, b * UNITS + j + 1)
                            if j >= RING:
                                act.wait_ge(pv_done, b * UNITS + j - RING + 1)
                            nc.scalar.activation(prT[:, j % RING, 0:W], tbank[0][:, 0:W], ACT.Copy).then_inc(copied_a, 1)
                        if 0 <= j < UNITS and j % H == H - 1:
                            tt = j // H
                            act.wait_ge(r_turned, b * TPB + tt + 1)
                            if tt >= 2:
                                act.wait_ge(yT_ready, b * TPB + tt - 1)
                            nc.scalar.activation(rinvT[:, tt % 2, :], rbank[:, 0:P], ACT.Copy).then_inc(rinvT_ready, 1)

            @block.tensor
            def _(pe):
                pe.wait_ge(loaded, 16 * len(loads))
                with pe.Fori(0, B) as b:
                    pe.wait_ge(x_ready, b + 1)
                    for n in range(2 * G):
                        nc.tensor.matmul(pj[n][:, :], w[:, n * P:(n + 1) * P], xb[:, :], start=True,
                                         stop=True).then_inc(projected, 1)
                    pe.wait_ge(q_raw, b * G + 1)
                    for t in range(TPB):
                        last = nc.tensor.matmul(pj[0][:, t * D:(t + 1) * D], xb[:, t * P:(t + 1) * P],
                                                w[:, 2 * G * P:2 * G * P + D], start=True, stop=True)
                    last.then_inc(projected, 1)
                    pe.wait_ge(q_raw, b * G + G)
                    pe.wait_ge(k_raw, b * G + G)
                    pe.wait_ge(v_ready, (b + 1) * TPB)
                    for i in range(UNITS + VLAG):
                        if i < UNITS:
                            tt, h = divmod(i, H)
                            g, r = divmod(h, HPG)
                            W = (tt + 1) * P
                            if tt == 0 and r == 0:
                                pe.wait_ge(split, b * 2 * G + 2 * g + 2)
                            if i >= 4:
                                pe.wait_ge(masked, b * UNITS + i - 3)
                            nc.tensor.matmul(sbank[i % 4][:, 0:W], qk[32 * r:32 * r + 32, g, tt * P:(tt + 1) * P],
                                             qk[32 * r:32 * r + 32, G + g, 0:W], start=True, stop=True,
                                             ).then_inc(scored, 1)
                        j = i - TLAG
                        if 0 <= j < UNITS:
                            pe.wait_ge(expd, b * UNITS + j + 1)
                            if j >= 2:
                                pe.wait_ge(copied_v if j % 2 else copied_a, b * (UNITS // 2) + j // 2)
                            for t in range(j // H + 1):
                                last = nc.tensor.transpose(tbank[j % 2][:, t * P:(t + 1) * P],
                                                           pr[:, j % RING, t * P:(t + 1) * P], T.ident[:, :])
                            last.then_inc(turned, 1)
                        j = i - VLAG
                        if j >= 0:
                            tt, h = divmod(j, H)
                            pe.wait_ge(copied_v if j % 2 else copied_a, b * (UNITS // 2) + j // 2 + 1)
                            if h == 0 and tt >= 1:
                                pe.wait_ge(yT_ready, b * TPB + tt)
                            for t in range(tt + 1):
                                last = nc.tensor.matmul(obank[0][:, tt * P:(tt + 1) * P], v[:, t, h * P:(h + 1) * P],
                                                        prT[:, j % RING, t * P:(t + 1) * P], start=(h == 0 and t == 0),
                                                        stop=(h == H - 1 and t == tt))
                            last.then_inc(pv_done, 1)
                        j = i - TLAG - 1
                        if 0 <= j < UNITS and j % H == H - 1:
                            tt = j // H
                            pe.wait_ge(rrep_ready, b * TPB + tt + 1)
                            if tt >= 1:
                                pe.wait_ge(rinvT_ready, b * TPB + tt)
                            nc.tensor.transpose(rbank[:, 0:P], rrep[:, tt % 2, :], T.ident[:, :]).then_inc(r_turned, 1)
                    pe.wait_ge(yT_ready, b * TPB + TPB)
                    for t in range(TPB):
                        last = nc.tensor.matmul(pj[1][:, t * D:(t + 1) * D], yT[:, t * P:(t + 1) * P], wproj[:, :],
                                                start=True, stop=True)
                    last.then_inc(out_ready, 1)
                    pe.wait_ge(added, b + 1)


def context_attention(nc, T, A, name, H, dk, HB, biased=False, rope=False, normed=False, keep_mask=False):
    HPG = P // dk
    G = H // HPG
    R = 2 if rope else 1
    STEPS = TPB * H // HB
    VB = min(G, 4)
    NV = HPG * (G // VB)
    NP = G * (2 * R + 1) + NV
    HT = H // HB
    NS = B * STEPS
    TLAG, VLAG, RING = 3, 5, 4
    W = HB * L
    SCALE = dk ** -0.5
    FILL = -2.3819763e38
    with Stage(nc, T, name) as st:
        wq = st.sb("wq", [P, R, G, P])
        wk = st.sb("wk", [P, R, G, P])
        wv = st.sb("wv", [P, G, P])
        wo = st.sb("wo", [P, G, D])
        loaded = st.sem("loaded")
        loads = [(wq[:, :, :, :], A[f"{name}_wq"]), (wk[:, :, :, :], A[f"{name}_wk"]), (wv[:, :, :], A[f"{name}_wv"]),
                 (wo[:, :, :], A[f"{name}_wo"])]
        if biased:
            cols = st.sb("cols", [P, 2])
            rows = st.sb("rows", [P, D])
            qbias = st.sb("qbias", [P, 1])
            loads += [(cols[:, :], A[f"{name}_cols"]), (rows[:, :], A[f"{name}_rows"])]
        if rope:
            qtrig = st.sb("qtrig", [P, 2, S])
            ktrig = st.sb("ktrig", [P, 2, L])
            qrot = st.sb("qrot", [P, 2, S])
            krot = st.sb("krot", [P, 2, L])
            loads += [(qtrig[:, :, :], A[f"{name}_qtrig"]), (ktrig[:, :, :], A[f"{name}_ktrig"])]
        if normed:
            gain = st.sb("gain", [P, 1])
            rms = st.sb("rms", [P, NT])
            crms = st.sb("crms", [L, B])
            sq = st.sb("sq", [P, NT, D])
            cn = st.sb("cn", [L, B, D])
            loads += [(gain[:, :], A[f"{name}_gain"])]
        if keep_mask:
            keep_bits = st.sb("keep_bits", [P, B, L], mybir.dt.int32)
            keep = st.sb("keep", [P, B, L])
            fill = st.sb("fill", [P, B, L])
            loads += [(keep_bits[:, :, :], A[f"{name}_keep"])]
        ctxT = st.sb("ctxT", [P, B * L]) if normed else T.CTXT
        q = st.sb("q", [P, 2, G, S])
        k = st.sb("k", [P, 2, G, HPG, L])
        vT = st.sb("vT", [P, G, L])
        vo = st.sb("vo", [L, B, H, D])
        sc = st.sb("sc", [P, 2, HB, L])
        pr = st.sb("pr", [P, RING, HB, L])
        prT = st.sb("prT", [L, RING, HB * P])
        mx = st.sb("mx", [P, 2, HB])
        rs = st.sb("rs", [P, RING, HB])
        sems = ("prepared", "squared", "rooted", "cturned", "projected", "taken_a", "taken_v", "scored",
                "centred", "expd", "summed", "normal", "turned", "copied", "pv_done", "added", "rotated")
        prepared, squared, rooted, cturned, projected, taken_a, taken_v, scored, centred, expd, summed, normal, turned, \
            copied, pv_done, added, rotated = (st.sem(n) for n in sems)
        layernorm(nc, T, T.X[:, :, :], T.LNX[:, :, :], T.LNT[:, :], loads, loaded, zeros=[k[:, :, :, :, :]])
        sbank, tbank, obank, pj = T.bank[0:2], T.bank[2:4], T.bank[4:6], T.bank[6:8]
        by_dve = [n < 2 * R * G if rope else n % 2 == 1 for n in range(NP)]
        NTV = sum(by_dve)
        NTA = NP - NTV

        with nc.Block() as block:
            @block.vector
            def _(dve):
                link = chain(T, dve)
                dve.wait_ge(loaded, 16 * len(loads))
                if biased:
                    link(nc.vector.tensor_scalar(qbias[:, :], cols[:, 0:1], SCALE, None, ALU.mult))
                    link(nc.vector.tensor_tensor(T.X[:, :, :], T.X[:, :, :], tiled(rows[:, :], NT), ALU.add))
                if keep_mask:
                    link(nc.vector.tensor_copy(keep[:, :, :], keep_bits[:, :, :]))
                    link(nc.vector.tensor_scalar(fill[:, :, :], keep[:, :, :], -1.0, -FILL, ALU.add, ALU.mult))
                if normed:
                    link(nc.vector.tensor_scalar(gain[:, :], gain[:, :], 1.0, None, ALU.add))
                    for m in (wq[:, :, :, :], wk[:, :, :, :], wv[:, :, :]):
                        link(nc.vector.tensor_scalar(m, m, gain[:, 0:1], None, ALU.mult))
                    link(nc.vector.tensor_tensor(sq[:, :, :], T.LNX[:, :, :], T.LNX[:, :, :], ALU.mult))
                    link(nc.vector.tensor_reduce(rms[:, :], sq[:, :, :], axis=AX, op=ALU.add))
                    link(nc.vector.tensor_scalar(rms[:, :], rms[:, :], 1.0 / D, 1e-6, ALU.mult, ALU.add))
                    link(nc.vector.tensor_tensor(cn[:, :, :], T.CTX[:, :, :], T.CTX[:, :, :], ALU.mult))
                    link(nc.vector.tensor_reduce(crms[:, :], cn[:, :, :], axis=AX, op=ALU.add))
                    nc.vector.tensor_scalar(crms[:, :], crms[:, :], 1.0 / D, 1e-6, ALU.mult, ALU.add).then_inc(squared, 1)
                    dve.wait_ge(rooted, 2)
                    link(nc.vector.reciprocal(rms[:, :], rms[:, :]))
                    link(nc.vector.tensor_scalar(rms[:, :], rms[:, :], SCALE, None, ALU.mult))
                    link(nc.vector.reciprocal(crms[:, :], crms[:, :]))
                    nc.vector.tensor_tensor(cn[:, :, :], T.CTX[:, :, :], spread(crms[:, :], D), ALU.mult)\
                        .then_inc(prepared, 1)

            @block.scalar
            def _(act):
                if normed:
                    act.wait_ge(squared, 1)
                    nc.scalar.activation(rms[:, :], rms[:, :], ACT.Sqrt).then_inc(rooted, 1)
                    nc.scalar.activation(crms[:, :], crms[:, :], ACT.Sqrt).then_inc(rooted, 1)
                    act.wait_ge(cturned, 1)
                    nc.scalar.activation(ctxT[:, :], T.bank[0][:, 0:B * L], ACT.Copy)

            @block.tensor
            def _(pe):
                if normed:
                    pe.wait_ge(prepared, 1)
                    for b in range(B):
                        last = nc.tensor.transpose(T.bank[0][:, b * L:(b + 1) * L], cn[:, b, :], T.ident[0:L, 0:L])
                    last.then_inc(cturned, 1)

        def pieces_at(i):
            b, r = divmod(i, STEPS)
            return [(b + 1, n) for n in range(NP * r // STEPS, NP * (r + 1) // STEPS)] if b + 1 < B else []
        START = [(0, n) for n in range(NP)]

        with nc.Block() as block:
            @block.tensor
            def _(pe):
                def read_up_to(b, m):
                    v = sum(by_dve[:m + 1])
                    if b * NTV + v:
                        pe.wait_ge(taken_v, b * NTV + v)
                    if b * NTA + m + 1 - v:
                        pe.wait_ge(taken_a, b * NTA + m + 1 - v)

                def project(b, n):
                    x = T.LNT[:, b * S:(b + 1) * S]
                    c = ctxT[:, b * L:(b + 1) * L]
                    at = b * NP + n
                    bank = pj[at % 2]
                    if at >= 2:
                        read_up_to(*divmod(at - 2, NP))
                    if n < R * G:
                        g, r = divmod(n, R)
                        last = nc.tensor.matmul(bank[:, :], wq[:, r, g, :], x, start=True, stop=True)
                    elif n < 2 * R * G:
                        g, r = divmod(n - R * G, R)
                        last = nc.tensor.matmul(bank[:, 0:L], wk[:, r, g, :], c, start=True, stop=True)
                    elif n < (2 * R + 1) * G:
                        last = nc.tensor.matmul(bank[:, 0:L], wv[:, n - 2 * R * G, :], c, start=True, stop=True)
                    else:
                        m = n - (2 * R + 1) * G
                        if m == 0:
                            read_up_to(b, n - 1)
                        r, g0 = divmod(m, G // VB)
                        for e in range(VB):
                            g = g0 * VB + e
                            last = nc.tensor.matmul(bank[0:L, e * D:(e + 1) * D], vT[r * dk:(r + 1) * dk, g, :],
                                                    wo[r * dk:(r + 1) * dk, g, :], start=True, stop=True)
                    last.then_inc(projected, 1)
                for b, n in START:
                    project(b, n)
                for i in range(NS + VLAG):
                    if i < NS:
                        b, r = divmod(i, STEPS)
                        tt, hb = divmod(r, HT)
                        if r == 0:
                            read_up_to(b, 2 * R * G - 1)
                            if rope:
                                pe.wait_ge(rotated, 2 * b + 2)
                        if i >= 2:
                            pe.wait_ge(centred, i - 1)
                        for e in range(0, HB, HPG):
                            g = (hb * HB + e) // HPG
                            last = nc.tensor.matmul(sbank[i % 2][:, e * L:(e + HPG) * L], q[:, b % 2, g, tt * P:(tt + 1) * P],
                                                    k[:, b % 2, g, :, :], start=True, stop=True)
                        last.then_inc(scored, 1)
                    j = i - TLAG
                    if 0 <= j < NS:
                        pe.wait_ge(normal, j + 1)
                        if j >= 2:
                            pe.wait_ge(copied, j - 1)
                        for e in range(HB):
                            last = nc.tensor.transpose(tbank[j % 2][0:L, e * P:(e + 1) * P], pr[:, j % RING, e, :],
                                                       T.ident[:, :])
                        last.then_inc(turned, 1)
                    j = i - VLAG
                    if j >= 0:
                        b, tile, hb = j // STEPS, j // HT, j % HT
                        pe.wait_ge(copied, j + 1)
                        if j % STEPS == 0:
                            read_up_to(b, NP - 1)
                        if hb == 0 and tile >= 2:
                            pe.wait_ge(added, tile - 1)
                        for e in range(HB):
                            last = nc.tensor.matmul(obank[tile % 2][:, 0:D], prT[:, j % RING, e * P:(e + 1) * P],
                                                    vo[:, b, hb * HB + e, :], start=(hb == 0 and e == 0),
                                                    stop=(hb == HT - 1 and e == HB - 1))
                        last.then_inc(pv_done, 1)
                    for b, n in pieces_at(i):
                        project(b, n)

            def take(move, b, n):
                src = pj[(b * NP + n) % 2]
                if n < G:
                    return move(q[:, b % 2, n, :], src[:, :], qbias[:, 0:1] if biased else None, SCALE)
                if n < 2 * G * R:
                    for r in range(HPG):
                        rows_ = slice(r * dk, (r + 1) * dk)
                        out = move(k[rows_, b % 2, n - G, r, :], src[rows_, 0:L], None, 1.0)
                    return out
                if n < (2 * R + 1) * G:
                    return move(vT[:, n - 2 * R * G, :], src[:, 0:L], cols[:, 1:2] if biased else None, 1.0)
                r, c = divmod(n - (2 * R + 1) * G, G // VB)
                dst = vo[:, b, :, :].rearrange("p (g r) d -> p g r d", r=HPG)[:, c * VB:(c + 1) * VB, r, :]
                return move(dst, src[0:L, 0:VB * D].rearrange("p (g d) -> p g d", g=VB), None, 1.0)

            @block.scalar
            def _(act):
                def move(to, frm, bias, scale):
                    if bias is None:
                        return nc.scalar.activation(to, frm, ACT.Copy, scale=scale)
                    return nc.scalar.activation(to, frm, ACT.Identity, bias=bias, scale=scale)

                def read(pieces):
                    for b, n in pieces:
                        if not by_dve[n]:
                            act.wait_ge(projected, b * NP + n + 1)
                            take(move, b, n).then_inc(taken_a, 1)
                read(START)
                for i in range(NS + TLAG):
                    if i < NS:
                        act.wait_ge(centred, i + 1)
                        if i >= RING:
                            act.wait_ge(turned, i - RING + 1)
                        nc.scalar.activation(pr[:, i % RING, :, :], sc[:, i % 2, :, :], ACT.Exp).then_inc(expd, 1)
                    j = i - TLAG
                    if j >= 0:
                        act.wait_ge(turned, j + 1)
                        if j >= RING:
                            act.wait_ge(pv_done, j - RING + 1)
                        nc.scalar.activation(prT[:, j % RING, :], tbank[j % 2][0:L, 0:HB * P], ACT.Copy).then_inc(copied, 1)
                    read(pieces_at(i))

            @block.gpsimd
            def _(pool):
                for i in range(NS):
                    pool.wait_ge(summed, i + 1)
                    p = pr[:, i % RING, :, :]
                    nc.gpsimd.tensor_tensor(p, p, spread(rs[:, i % RING, :], L), ALU.mult).then_inc(normal, 1)

            @block.vector
            def _(dve):
                link = chain(T, dve)

                def move(to, frm, bias, scale):
                    if bias is None:
                        return nc.vector.tensor_scalar(to, frm, scale, None, ALU.mult)
                    return nc.vector.tensor_scalar(to, frm, scale, bias, ALU.mult, ALU.add)

                def rotate(b, n):
                    kind, part = divmod(n, 2)
                    trig, rot, w_ = ((qtrig, qrot, S), (ktrig, krot, L))[kind]
                    if b and part == 0:
                        dve.wait_ge(rotated, 2 * b - 1 + kind)
                    nc.vector.tensor_tensor(rot[:, part, :], pj[(b * NP + n) % 2][:, 0:w_], trig[:, part, :], ALU.mult)\
                        .then_inc(taken_v, 1)
                    if part:
                        dve.wait_ge(taken_v, b * NTV + n + 1)
                        if kind == 0:
                            out = nc.vector.tensor_tensor(q[:, b % 2, 0, :], rot[:, 0, :], rot[:, 1, :], ALU.add)
                        else:
                            for r in range(HPG):
                                rows_ = slice(r * dk, (r + 1) * dk)
                                out = nc.vector.tensor_tensor(k[rows_, b % 2, 0, r, :], rot[rows_, 0, :], rot[rows_, 1, :], ALU.add)
                        out.then_inc(rotated, 1)

                def read(pieces):
                    for b, n in pieces:
                        if by_dve[n]:
                            dve.wait_ge(projected, b * NP + n + 1)
                            if rope and n < 2 * R * G:
                                rotate(b, n)
                            else:
                                take(move, b, n).then_inc(taken_v, 1)
                read(START)
                for i in range(NS + VLAG + 1):
                    if i < NS:
                        b, tile = i // STEPS, i // HT
                        s = sbank[i % 2][:, 0:W].rearrange("p (e l) -> p e l", e=HB)
                        dve.wait_ge(scored, i + 1)
                        if i >= 2:
                            dve.wait_ge(expd, i - 1)
                        z = sc[:, i % 2, :, :]
                        if keep_mask:
                            link(nc.vector.scalar_tensor_tensor(z, s, rms[:, tile:tile + 1], tiled(keep[:, b, :], HB),
                                                                ALU.mult, ALU.mult))
                            link(nc.vector.tensor_tensor(z, z, tiled(fill[:, b, :], HB), ALU.add))
                            s = z
                        link(nc.vector.tensor_reduce(mx[:, i % 2, :], s, axis=AX, op=ALU.max))
                        nc.vector.tensor_tensor(z, s, spread(mx[:, i % 2, :], L), ALU.subtract).then_inc(centred, 1)
                    j = i - 1
                    if 0 <= j < NS:
                        dve.wait_ge(expd, j + 1)
                        link(nc.vector.tensor_reduce(rs[:, j % RING, :], pr[:, j % RING, :, :], axis=AX, op=ALU.add))
                        nc.vector.reciprocal(rs[:, j % RING, :], rs[:, j % RING, :]).then_inc(summed, 1)
                    j = i - VLAG - 1
                    if j >= 0 and j % HT == HT - 1:
                        tile = j // HT
                        dve.wait_ge(pv_done, j + 1)
                        xt = T.X[:, tile, :]
                        nc.vector.tensor_tensor(xt, xt, obank[tile % 2][:, 0:D], ALU.add).then_inc(added, 1)
                    read(pieces_at(i))


def pick_max(nc, link, V, rev, m, c, O):
    groups, n = V.shape[1], V.shape[2]
    link(nc.vector.tensor_reduce(m, V, axis=AX, op=ALU.max))
    link(nc.vector.tensor_tensor(c, V, spread(m, n), ALU.is_ge))
    link(nc.vector.tensor_tensor(c, c, tiled(rev, groups), ALU.mult))
    link(nc.vector.tensor_reduce(m, c, axis=AX, op=ALU.max))
    link(nc.vector.tensor_tensor(O, c, spread(m, n), ALU.is_equal))
    link(nc.vector.scalar_tensor_tensor(V, O, -3.0 * BIG, V, ALU.mult, ALU.add))


def expert_ffn(nc, T, A, name, E, K, route, NSH=1, half_weights=False, add_input=False,
               counted=False):
    I = 64
    PAIRS = E // 2
    SLOTS = 4
    BLK = B
    PRE = NSH * BLK
    PER = SLOTS * BLK
    TURNS = PAIRS // SLOTS
    DLAG, RING = 4, 8
    with Stage(nc, T, name) as st:
        WT = BF16 if half_weights else F32
        router = st.sb("router", [P, E], WT)
        bias = st.sb("bias", [P, E])
        shared_raw = st.sb("shared", [P, NSH, 3 * P], WT)
        score = st.sb("score", [P, NT, E])
        cw = st.sb("cw", [P, NT, E])
        cwT = st.sb("cwT", [E, N])
        wide_router = st.sb("wide_router", [P, E]) if half_weights else router
        x_hi, x_lo = st.sb("x_hi", [P, N], F32R), st.sb("x_lo", [P, N], F32R)
        shared_hi = st.sb("shared_hi", [P, NSH, 3 * P], F32R)
        wslot = [st.sb(f"w{i}", [P, 3 * P], WT) for i in range(SLOTS)]
        w_hi = [st.sb(f"w_hi{i}", [P, 3 * P], F32R) for i in range(SLOTS)]
        if not half_weights:
            shared_lo = st.sb("shared_lo", [P, NSH, 3 * P], F32R)
            w_lo = [st.sb(f"w_lo{i}", [P, 3 * P], F32R) for i in range(SLOTS)]
        arrived = [st.sem(f"arrived{i}") for i in range(SLOTS)]
        w_high = [st.sem(f"w_high{i}") for i in range(SLOTS)]
        w_low = w_high if half_weights else [st.sem(f"w_low{i}") for i in range(SLOTS)]
        x_high, shared_high = st.sem("x_high"), st.sem("shared_high")

        def fetch(sp, s, turn):
            sp.dma_start(wslot[s][:, :], A[f"{name}_pairs"][bass.ds(turn * SLOTS + s, 1), :, :]
                         .rearrange("a p c -> (a p) c")).then_inc(arrived[s], 16)
        mask = st.sb("mask", [P, NT, E])
        T.router_bias = bias
        T.chosen, T.counts = st.sem("chosen"), st.sem("counts")
        loaded = st.sem("loaded")
        loads = [(router[:, :], A[f"{name}_router"]), (bias[:, :], A[f"{name}_bias"]),
                 (shared_raw[:, :, :], A[f"{name}_shared"])]
        if counted:
            tri = st.sb("tri", [P, 2, P])
            loads.append((tri[:, :, :], A["tri"]))
        weights = nc.dram_tensor(f"{name}_weights", (E, N), F32, kind="Internal").ap()
        widened, logits, scored, routed, cw_turned, cw_taken, cw_stored = (
            st.sem(n) for n in ("widened", "logits", "scored", "routed", "cw_turned", "cw_taken", "cw_stored"))
        layernorm(nc, T, T.X[:, :, :], T.LNX[:, :, :], T.LNT[:, :], loads, loaded)

        with Stage(nc, T, f"{name}r") as rt, nc.Block() as block:
            per_bank = 512 // E if E > 32 else NT

            @block.tensor
            def _(pe):
                pe.wait_ge(loaded, 16 * len(loads))
                if half_weights:
                    pe.wait_ge(widened, 1)
                for t in range(NT):
                    bank, at = divmod(t, per_bank)
                    last = nc.tensor.matmul(T.bank[bank][:, at * E:(at + 1) * E], T.LNT[:, t * P:(t + 1) * P],
                                            wide_router[:, :], start=True, stop=True)
                last.then_inc(logits, 1)
                if counted:
                    pe.wait_ge(T.chosen, 1)
                    for i in range(2):
                        nc.tensor.matmul(T.bank[2 + i][:, :], tri[:, i, :], mask[:, :, :].rearrange("p t e -> p (t e)"),
                                         start=True, stop=True).then_inc(T.counts, 1)
                pe.wait_ge(routed, 1)
                for c in range(B):
                    for t in range(TPB):
                        last = nc.tensor.transpose(T.bank[4 + c][0:E, t * P:(t + 1) * P], cw[:, c * TPB + t, :],
                                                   T.ident[:, :])
                    last.then_inc(cw_turned, 1)

            @block.scalar
            def _(act):
                act.wait_ge(loaded, 16 * len(loads))
                if half_weights:
                    nc.scalar.activation(wide_router[:, :], router[:, :], ACT.Copy).then_inc(widened, 1)
                for c in range(B):
                    nc.scalar.activation(x_hi[:, c * S:(c + 1) * S], T.LNT[:, c * S:(c + 1) * S], ACT.Copy).then_inc(x_high, 1)
                act.wait_ge(logits, 1)
                for n in range(0, NT, per_bank):
                    last = nc.scalar.activation(score[:, n:n + per_bank, :],
                                                T.bank[n // per_bank][:, 0:per_bank * E].rearrange("p (t e) -> p t e", e=E),
                                                ACT.Sigmoid)
                last.then_inc(scored, 1)
                nc.scalar.activation(shared_hi[:, :, :], shared_raw[:, :, :], ACT.Copy).then_inc(shared_high, 1)
                if not half_weights:
                    for s in range(SLOTS - 1):
                        act.wait_ge(arrived[s], 16)
                        nc.scalar.activation(w_hi[s][:, :], wslot[s][:, :], ACT.Copy).then_inc(w_high[s], 1)
                for c in range(B):
                    act.wait_ge(cw_turned, c + 1)
                    nc.scalar.activation(cwT[:, c * S:(c + 1) * S], T.bank[4 + c][0:E, :], ACT.Copy).then_inc(cw_taken, 1)

            @block.vector
            def _(dve):
                dve.wait_ge(loaded, 16 * len(loads))
                dve.wait_ge(scored, 1)
                route(nc, T, rt, dve, chain(T, dve), score, mask, cw)
                dve.sem_inc(routed, 1)

            @block.gpsimd
            def _(pool):
                for c in range(B):
                    cols = slice(c * S, (c + 1) * S)
                    pool.wait_ge(x_high, c + 1)
                    nc.gpsimd.tensor_tensor(x_lo[:, cols], T.LNT[:, cols], x_hi[:, cols], ALU.subtract)
                if not half_weights:
                    pool.wait_ge(shared_high, 1)
                    nc.gpsimd.tensor_tensor(shared_lo[:, :, :], shared_raw[:, :, :], shared_hi[:, :, :], ALU.subtract)
                for s in range(SLOTS - 1):
                    if half_weights:
                        pool.wait_ge(arrived[s], 16)
                        nc.gpsimd.tensor_copy(w_hi[s][:, :], wslot[s][:, :]).then_inc(w_high[s], 1)
                    else:
                        pool.wait_ge(w_high[s], 1)
                        nc.gpsimd.tensor_tensor(w_lo[s][:, :], wslot[s][:, :], w_hi[s][:, :], ALU.subtract).then_inc(w_low[s], 1)

            @block.sync
            def _(sp):
                for s in range(SLOTS):
                    fetch(sp, s, 0)
                sp.wait_ge(cw_taken, B)
                sp.dma_start(weights, cwT[:, :]).then_inc(cw_stored, 16)
                sp.wait_ge(cw_stored, 16)

        cslot = [st.sb(f"c{i}", [P, N]) for i in range(SLOTS)]
        gate = st.sb("gate", [P, 2, S])
        prod = st.sb("prod", [P, 2, S])
        hid = st.sb("hid", [P, 4, S])
        hid_hi, hid_lo = st.sb("hid_hi", [P, RING, S], F32R), st.sb("hid_lo", [P, RING, S], F32R)
        outT = st.sb("outT", [P, N])
        cw_here = [st.sem(f"cw_here{i}") for i in range(SLOTS)]
        up_done, gated, multiplied, hidden, hid_high, hid_low, down_done, split_free = (
            st.sem(n) for n in ("up_done", "gated", "multiplied", "hidden", "hid_high", "hid_low", "down_done", "split_free"))
        taken, turned_back, closed = st.sem("taken"), st.sem("turned_back"), st.sem("closed")
        closing = T.ident if add_input else T.zeros
        acc = T.bank[0:BLK]
        gbank, ubank = T.bank[4:6], T.bank[6:8]

        def steps(engine, step):
            for n in range(-PRE, DLAG):
                step(0, n, False)
            with engine.Fori(0, TURNS - 1) as it:
                for n in range(DLAG, DLAG + PER):
                    step(it, n, False)
            for n in range(DLAG, DLAG + PER):
                step(TURNS - 1, n, True)

        def split_at(n, last):
            for s in range(SLOTS - 1):
                if n == (s + 1) * BLK + DLAG + 2 and not last:
                    return s, 1
            return (SLOTS - 1, 0) if n == DLAG + 2 else None

        def halves(n):
            if n < 0:
                e = (n + PRE) // BLK
                return shared_hi[:, e, :], None if half_weights else shared_lo[:, e, :]
            s = n // BLK % SLOTS
            return w_hi[s][:, :], None if half_weights else w_lo[s][:, :]

        with nc.Block() as block:
            @block.sync
            def _(sp):
                def fetch_cw(s, turn):
                    for e in range(2):
                        sp.dma_start(cslot[s][e * I:(e + 1) * I, :],
                                     weights[bass.ds(turn * 2 * SLOTS + 2 * s + e, 1), :].broadcast_to([I, N]))\
                            .then_inc(cw_here[s], 16)
                for s in range(SLOTS):
                    fetch_cw(s, 0)
                with sp.Fori(0, TURNS - 1) as it:
                    for s in range(SLOTS):
                        sp.wait_ge(w_low[s], it + 1)
                        fetch(sp, s, it + 1)
                        sp.wait_ge(down_done, it * PER + PRE + (s + 1) * BLK)
                        fetch_cw(s, it + 1)

            @block.tensor
            def _(pe):
                def product(out, w, w_cols, hi, lo, first, last, lo_ready=None):
                    wh, wl = w
                    nc.tensor.matmul(out, wh[:, w_cols], hi, start=first, stop=False)
                    if wl is not None:
                        nc.tensor.matmul(out, wl[:, w_cols], hi, start=False, stop=False)
                    if lo_ready is not None:
                        pe.wait_ge(hid_low, lo_ready)
                    return nc.tensor.matmul(out, wh[:, w_cols], lo, start=False, stop=last)

                def step(it, n, last):
                    k = it * PER + PRE + n
                    if n < PER or not last:
                        s, blk = n // BLK % SLOTS, n % BLK
                        if n >= 0 and blk == 0:
                            pe.wait_ge(w_low[s], it + n // PER + 1)
                        if n + PRE >= 2:
                            pe.wait_ge(multiplied, k - 1)
                        x = slice(blk * S, (blk + 1) * S)
                        product(gbank[n % 2][:, :], halves(n), slice(0, P), x_hi[:, x], x_lo[:, x], True, True)
                        product(ubank[n % 2][:, :], halves(n), slice(P, 2 * P), x_hi[:, x], x_lo[:, x], True, True)\
                            .then_inc(up_done, 1)
                    m = n - DLAG
                    if m + PRE >= 0:
                        at = (m + PRE) % RING
                        pe.wait_ge(hid_high, k - DLAG + 1)
                        product(acc[m % BLK][:, :], halves(m), slice(2 * P, 3 * P), hid_hi[:, at, :], hid_lo[:, at, :],
                                m + PRE < BLK, False, k - DLAG + 1).then_inc(down_done, 1)
                steps(pe, step)
                for blk in range(BLK):
                    nc.tensor.matmul(acc[blk][:, :], closing[:, :], T.LNT[:, blk * S:(blk + 1) * S], start=False,
                                     stop=True).then_inc(closed, 1)
                for c in range(B):
                    pe.wait_ge(taken, c + 1)
                    for t in range(TPB):
                        last = nc.tensor.transpose(T.bank[4 + c][:, t * P:(t + 1) * P],
                                                   outT[:, c * S + t * P:c * S + (t + 1) * P], T.ident[:, :])
                    last.then_inc(turned_back, 1)

            @block.scalar
            def _(act):
                def step(it, n, last):
                    k = it * PER + PRE + n
                    if n < PER or not last:
                        act.wait_ge(up_done, k + 1)
                        if n + PRE >= 2:
                            act.wait_ge(multiplied, k - 1)
                        nc.scalar.activation(gate[:, n % 2, :], gbank[n % 2][:, :], ACT.Silu).then_inc(gated, 1)
                    m = n - 1
                    if m + PRE >= 0 and (m < PER or not last):
                        act.wait_ge(hidden, k)
                        if n + PRE > DLAG + 1:
                            act.wait_ge(down_done, k - DLAG - 1)
                        nc.scalar.activation(hid_hi[:, (m + PRE) % RING, :], hid[:, (m + PRE) % 4, :], ACT.Copy)\
                            .then_inc(hid_high, 1)
                    if split_at(n, last) and not half_weights:
                        s, ahead = split_at(n, last)
                        act.wait_ge(arrived[s], it * 16 + 16 * ahead + 16)
                        act.wait_ge(down_done, k - DLAG - 1)
                        nc.scalar.activation(w_hi[s][:, :], wslot[s][:, :], ACT.Copy).then_inc(w_high[s], 1)
                steps(act, step)
                for c in range(B):
                    act.wait_ge(closed, c + 1)
                    nc.scalar.activation(outT[:, c * S:(c + 1) * S], acc[c][:, :], ACT.Copy).then_inc(taken, 1)

            @block.gpsimd
            def _(pool):
                def step(it, n, last):
                    k = it * PER + PRE + n
                    if n < PER or not last:
                        pool.wait_ge(hid_high, k + 1)
                        if n + PRE > DLAG + 1:
                            pool.wait_ge(down_done, k - DLAG - 1)
                        at = (n + PRE) % RING
                        nc.gpsimd.tensor_tensor(hid_lo[:, at, :], hid[:, (n + PRE) % 4, :], hid_hi[:, at, :], ALU.subtract)\
                            .then_inc(hid_low, 1)
                    if split_at(n, last):
                        s, ahead = split_at(n, last)
                        if half_weights:
                            pool.wait_ge(arrived[s], it * 16 + 16 * ahead + 16)
                            pool.wait_ge(down_done, k - DLAG - 1)
                            pool.sem_inc(split_free, 1)
                            nc.gpsimd.tensor_copy(w_hi[s][:, :], wslot[s][:, :]).then_inc(w_high[s], 1)
                        else:
                            pool.wait_ge(w_high[s], it + ahead + 1)
                            nc.gpsimd.tensor_tensor(w_lo[s][:, :], wslot[s][:, :], w_hi[s][:, :], ALU.subtract)\
                                .then_inc(w_low[s], 1)
                steps(pool, step)

            @block.vector
            def _(dve):
                def step(it, n, last):
                    if n >= PER and last:
                        return
                    k = it * PER + PRE + n
                    h = hid[:, (n + PRE) % 4, :]
                    if n < 0:
                        dve.wait_ge(gated, k + 1)
                        if k >= 4:
                            dve.wait_ge(hid_low, k - 3)
                        nc.vector.tensor_tensor(h, ubank[n % 2][:, :], gate[:, n % 2, :], ALU.mult).then_inc(hidden, 1)
                        dve.wait_ge(hidden, k + 1)
                        dve.sem_inc(multiplied, 1)
                        return
                    s, blk = n // BLK % SLOTS, n % BLK
                    if blk == 0:
                        dve.wait_ge(cw_here[s], it * 32 + 32 * (n // PER) + 32)
                    dve.wait_ge(gated, k + 1)
                    dve.wait_ge(hidden, k - 1)
                    nc.vector.tensor_tensor(prod[:, n % 2, :], ubank[n % 2][:, :], gate[:, n % 2, :], ALU.mult)\
                        .then_inc(multiplied, 1)
                    dve.wait_ge(multiplied, k + 1)
                    dve.wait_ge(hid_low, k - 3)
                    nc.vector.tensor_tensor(h, prod[:, n % 2, :], cslot[s][:, blk * S:(blk + 1) * S], ALU.mult)\
                        .then_inc(hidden, 1)
                steps(dve, step)
                for c in range(B):
                    dve.wait_ge(turned_back, c + 1)
                    x = T.X[:, c * TPB:(c + 1) * TPB, :]
                    nc.vector.tensor_tensor(x, x, T.bank[4 + c][:, :].rearrange("p (t d) -> p t d", t=TPB), ALU.add)


def top_groups_then_experts(nc, T, rt, link, score, bias, NG, TG, K, mask):
    E = score.shape[2]
    n = E // NG
    V = rt.sb("V", [P, NT, E])
    c = rt.sb("c", [P, NT * E])
    O = rt.sb("O", [P, NT * E])
    m = rt.sb("m", [P, NT * NG])
    best = rt.sb("best", [P, NT * NG])
    gs = rt.sb("gs", [P, NT, NG])
    gm = rt.sb("gm", [P, NT])
    sfc = rt.sb("sfc", [P, NT, E])
    rev = T.rev
    def groups(t):
        return t.rearrange("p (g n) -> p g n", n=n)
    Vg = V[:, :, :].rearrange("p t (g n) -> p (t g) n", n=n)
    flat_gs = gs[:, :, :].rearrange("p t g -> p (t g)")
    link(nc.vector.tensor_tensor(sfc[:, :, :], score[:, :, :], tiled(bias[:, :], NT), ALU.add))
    link(nc.vector.tensor_copy(V[:, :, :], sfc[:, :, :]))
    link(nc.vector.tensor_reduce(best[:, :], Vg, axis=AX, op=ALU.max))
    pick_max(nc, link, Vg, rev[:, 64 - n:64], m[:, :], groups(c[:, :]), groups(O[:, :]))
    link(nc.vector.tensor_reduce(m[:, :], Vg, axis=AX, op=ALU.max))
    link(nc.vector.tensor_tensor(flat_gs, best[:, :], m[:, :], ALU.add))
    g = NT * NG
    if NG >= 8:
        lower_top(nc, rt, link, gs, TG, "group")
    else:
        for _ in range(TG):
            pick_max(nc, link, gs[:, :, :], rev[:, 64 - NG:64], gm[:, :], c[:, 0:g].rearrange("p (t g) -> p t g", g=NG),
                     O[:, 0:g].rearrange("p (t g) -> p t g", g=NG))
    link(nc.vector.tensor_scalar(m[:, :], flat_gs, -2.0 * BIG, BIG, ALU.is_lt, ALU.mult))
    link(nc.vector.tensor_scalar(m[:, :], m[:, :], -BIG, None, ALU.add))
    link(nc.vector.tensor_tensor(Vg, sfc[:, :, :].rearrange("p t (g n) -> p (t g) n", n=n), spread(m[:, :], n), ALU.add))
    lower_top(nc, rt, link, V, K, "expert")
    link(nc.vector.tensor_scalar(mask[:, :, :], V[:, :, :], -2.0 * BIG, None, ALU.is_lt))


def lower_top(nc, rt, link, V, K, name):
    top = rt.sb(f"{name}_top", [P, NT, 8])
    for t in range(NT):
        last = nc.vector.max(top[:, t, :], V[:, t, :])
    link(last)
    if K < 8:
        link(nc.vector.memset(top[:, :, K:8], 3.0e38))
    for t in range(NT):
        last = nc.vector.match_replace(V[:, t, :], top[:, t, :], V[:, t, :], -3.0 * BIG)
    link(last)


def normalized(nc, rt, link, score, mask, cw, scale, floor, clip):
    total = rt.sb("total", [P, NT])
    E = score.shape[2]
    link(nc.vector.tensor_tensor(cw[:, :, :], score[:, :, :], mask[:, :, :], ALU.mult))
    link(nc.vector.tensor_reduce(total[:, :], cw[:, :, :], axis=AX, op=ALU.add))
    link(nc.vector.tensor_scalar(total[:, :], total[:, :], floor, None, ALU.max if clip else ALU.add))
    link(nc.vector.reciprocal(total[:, :], total[:, :]))
    link(nc.vector.tensor_tensor(cw[:, :, :], cw[:, :, :], spread(total[:, :], E), ALU.mult))
    if scale != 1.0:
        link(nc.vector.tensor_scalar(cw[:, :, :], cw[:, :, :], scale, None, ALU.mult))


def l0_moe(nc, T, A):
    def route(nc, T, rt, dve, link, score, mask, cw):
        top_groups_then_experts(nc, T, rt, link, score, T.router_bias, NG=4, TG=2, K=4, mask=mask)
        normalized(nc, rt, link, score, mask, cw, 2.5, 1e-20, False)
    expert_ffn(nc, T, A, "l0m", 16, 4, route, add_input=True)


def l1_moe(nc, T, A):
    def route(nc, T, rt, dve, link, score, mask, cw):
        top_groups_then_experts(nc, T, rt, link, score, T.router_bias, NG=8, TG=4, K=8, mask=mask)
        normalized(nc, rt, link, score, mask, cw, 1.0, 1e-20, False)
    expert_ffn(nc, T, A, "l1m", 64, 8, route, NSH=2)


def l3_moe(nc, T, A):
    E, CAP = 32, 2 * 512 * 4 // 32

    def route(nc, T, rt, dve, link, score, mask, cw):
        V = rt.sb("V", [P, NT, E])
        pos = rt.sb("pos", [P, NT, E])
        before = rt.sb("before", [P, NT, E])
        link(nc.vector.tensor_tensor(V[:, :, :], score[:, :, :], tiled(T.router_bias[:, :], NT), ALU.add))
        lower_top(nc, rt, link, V, 4, "expert")
        nc.vector.tensor_scalar(mask[:, :, :], V[:, :, :], -2.0 * BIG, None, ALU.is_lt).then_inc(T.chosen, 1)
        dve.wait_ge(T.chosen, 1)
        normalized(nc, rt, link, score, mask, cw, 1.0, 1e-12, True)
        dve.wait_ge(T.counts, 2)
        link(nc.vector.memset(before[:, 0, :], 0.0))
        for t in range(1, NT):
            link(nc.vector.tensor_tensor(before[:, t, :], before[:, t - 1, :], T.bank[3][:, (t - 1) * E:t * E], ALU.add))
        link(nc.vector.tensor_tensor(pos[:, :, :], before[:, :, :], T.bank[2][:, :].rearrange("p (t e) -> p t e", e=E), ALU.add))
        link(nc.vector.tensor_scalar(pos[:, :, :], pos[:, :, :], float(CAP), None, ALU.is_lt))
        link(nc.vector.tensor_tensor(cw[:, :, :], cw[:, :, :], pos[:, :, :], ALU.mult))
    expert_ffn(nc, T, A, "l3m", 32, 4, route, half_weights=True, counted=True)


def l1_attention(nc, T, A):
    H, HD = 16, 8
    KW = D + H
    with Stage(nc, T, "l1a") as st:
        wq = st.sb("wq", [P, D])
        wkv = st.sb("wkv", [P, 2 * D])
        wo = st.sb("wo", [P, D])
        bo = st.sb("bo", [P, D])
        same = st.sb("same", [P, KW])
        qm, qe = (st.sb(n, [P, S]) for n in ("qm", "qe"))
        km, ke = (st.sb(n, [P, TPB, D]) for n in ("km", "ke"))
        qf, kf = st.sb("qf", [P, 2, S]), st.sb("kf", [P, 2, TPB, D])
        v = st.sb("v", [P, 2, TPB, D + 1])
        kv = st.sb("kv", [P, KW])
        den = st.sb("den", [P, TPB, H])
        y = st.sb("y", [P, TPB, D])
        yT = st.sb("yT", [P, S])
        names = ("loaded", "projected", "mins", "exps", "features", "kv_done", "kv_ready", "out_done",
                 "den_step", "y_ready", "y_turned", "yT_ready", "proj_done", "added", "ones")
        loaded, projected, mins, exps, features, kv_done, kv_ready, out_done, den_step, y_ready, y_turned, \
            yT_ready, proj_done, added, ones = (st.sem(n) for n in names)
        loads = [(wq[:, :], A["l1a_wq"]), (wkv[:, :], A["l1a_wkv"]), (wo[:, :], A["l1a_wo"]), (bo[:, :], A["l1a_bo"]),
                 (same[:, :], A["l1a_same"])]
        layernorm(nc, T, T.X[:, :, :], T.LNX[:, :, :], T.LNT[:, :], loads, loaded)
        k_psum = [T.bank[1 + i][:, :].rearrange("p (t c) -> p t c", t=2) for i in range(2)]
        o_psum = [T.bank[4 + i][:, 0:2 * KW].rearrange("p (t c) -> p t c", t=2) for i in range(2)]
        with nc.Block() as block:
            @block.scalar
            def _(act):
                def exponentials(b):
                    act.wait_ge(mins, b + 1)
                    if b >= 2:
                        act.wait_ge(kv_done, b - 1)
                    nc.scalar.activation(qe[:, :], qm[:, :], ACT.Exp)
                    nc.scalar.activation(ke[:, :, :], km[:, :, :], ACT.Exp)
                    for i in range(2):
                        last = nc.scalar.activation(v[:, b % 2, 2 * i:2 * i + 2, 0:D], k_psum[i][:, :, D:2 * D], ACT.Copy)
                    last.then_inc(exps, 1)
                act.wait_ge(ones, 1)
                exponentials(0)
                for b in range(B):
                    if b + 1 < B:
                        exponentials(b + 1)
                    act.wait_ge(y_turned, b + 1)
                    nc.scalar.activation(yT[:, :], T.bank[6][:, :], ACT.Copy).then_inc(yT_ready, 1)

            @block.tensor
            def _(pe):
                def project(b):
                    if b:
                        pe.wait_ge(features, b)
                    x = T.LNT[:, b * S:(b + 1) * S]
                    nc.tensor.matmul(T.bank[0][:, :], wq[:, :], x, start=True, stop=True)
                    for t in range(TPB):
                        last = nc.tensor.matmul(k_psum[t // 2][:, t % 2, :], x[:, t * P:(t + 1) * P], wkv[:, :],
                                                start=True, stop=True)
                    last.then_inc(projected, 1)
                pe.wait_ge(loaded, 16 * len(loads))
                project(0)
                for b in range(B):
                    pe.wait_ge(features, b + 1)
                    for t in range(TPB):
                        last = nc.tensor.matmul(T.bank[3][:, 0:D + 1], kf[:, b % 2, t, :], v[:, b % 2, t, :], start=(t == 0),
                                                stop=(t == TPB - 1))
                    last.then_inc(kv_done, 1)
                    if b + 1 < B:
                        project(b + 1)
                    pe.wait_ge(kv_ready, b + 1)
                    for t in range(TPB):
                        last = nc.tensor.matmul(o_psum[t // 2][:, t % 2, :], qf[:, b % 2, t * P:(t + 1) * P], kv[:, :],
                                                start=True, stop=True)
                    last.then_inc(out_done, 1)
                    pe.wait_ge(y_ready, b + 1)
                    for t in range(TPB):
                        last = nc.tensor.transpose(T.bank[6][:, t * P:(t + 1) * P], y[:, t, :], T.ident[:, :])
                    last.then_inc(y_turned, 1)
                    pe.wait_ge(yT_ready, b + 1)
                    if b:
                        pe.wait_ge(added, b)
                    for t in range(TPB):
                        last = nc.tensor.matmul(T.bank[7][:, t * D:(t + 1) * D], yT[:, t * P:(t + 1) * P], wo[:, :],
                                                start=True, stop=True)
                    last.then_inc(proj_done, 1)

            @block.vector
            def _(dve):
                link = chain(T, dve)

                def minima(b):
                    dve.wait_ge(projected, b + 1)
                    nc.vector.tensor_scalar(qm[:, :], T.bank[0][:, :], 0.0, None, ALU.min)
                    for i in range(2):
                        last = nc.vector.tensor_scalar(km[:, 2 * i:2 * i + 2, :], k_psum[i][:, :, 0:D], 0.0, None, ALU.min)
                    last.then_inc(mins, 1)

                def make_features(b):
                    dve.wait_ge(exps, b + 1)
                    if b >= 2:
                        dve.wait_ge(out_done, b - 1)
                    nc.vector.scalar_tensor_tensor(qf[:, b % 2, :], T.bank[0][:, :], 0.0, qe[:, :], ALU.max, ALU.add)
                    for i in range(2):
                        last = nc.vector.scalar_tensor_tensor(kf[:, b % 2, 2 * i:2 * i + 2, :], k_psum[i][:, :, 0:D], 0.0,
                                                              ke[:, 2 * i:2 * i + 2, :], ALU.max, ALU.add)
                    last.then_inc(features, 1)
                nc.vector.memset(v[:, :, :, :], 1.0).then_inc(ones, 1)
                dve.wait_ge(loaded, 16 * len(loads))
                minima(0)
                link(nc.vector.tensor_tensor(T.X[:, :, :], T.X[:, :, :], tiled(bo[:, :], NT), ALU.add))
                make_features(0)
                for b in range(B):
                    dve.wait_ge(kv_done, b + 1)
                    if b:
                        dve.wait_ge(out_done, b)
                    nc.vector.tensor_tensor(kv[:, 0:D], T.bank[3][:, 0:D], same[:, 0:D], ALU.mult)
                    nc.vector.tensor_scalar(kv[:, D:KW], same[:, D:KW], T.bank[3][:, D:D + 1], None, ALU.mult)\
                        .then_inc(kv_ready, 1)
                    if b + 1 < B:
                        minima(b + 1)
                    dve.wait_ge(out_done, b + 1)
                    for i in range(2):
                        last = nc.vector.tensor_scalar(den[:, 2 * i:2 * i + 2, :], o_psum[i][:, :, D:KW], 1e-6, None, ALU.add)
                    last.then_inc(den_step, 1)
                    dve.wait_ge(den_step, b * 2 + 1)
                    nc.vector.reciprocal(den[:, :, :], den[:, :, :]).then_inc(den_step, 1)
                    dve.wait_ge(den_step, b * 2 + 2)
                    if b:
                        dve.wait_ge(y_turned, b)
                    for t in range(TPB):
                        last = nc.vector.tensor_tensor(y[:, t, :].rearrange("p (h d) -> p h d", h=H),
                                                       o_psum[t // 2][:, t % 2, 0:D].rearrange("p (h d) -> p h d", h=H),
                                                       spread(den[:, t, :], HD), ALU.mult)
                    last.then_inc(y_ready, 1)
                    if b + 1 < B:
                        make_features(b + 1)
                    dve.wait_ge(proj_done, b + 1)
                    x = T.X[:, b * TPB:(b + 1) * TPB, :]
                    nc.vector.tensor_tensor(x, x, T.bank[7][:, :].rearrange("p (t c) -> p t c", t=TPB), ALU.add)\
                        .then_inc(added, 1)


def l1_coattention(nc, T, A):
    with Stage(nc, T, "l1c") as st:
        cols = st.sb("cols", [P, 4])
        w = st.sb("w", [P, 4, D])
        bias = st.sb("bias", [P, D])
        c3 = st.sb("c3", [P, B * L])
        w2 = st.sb("w2", [P, P])
        drow = st.sb("drow", [P, B, L])
        sim = st.sb("sim", [P, 2, TPB, L])
        mx = st.sb("mx", [P, NT])
        rs = st.sb("rs", [P, NT])
        prT = st.sb("prT", [L, 2, S])
        hq = st.sb("hq", [P, 2, S])
        ehq = st.sb("ehq", [P, 2, S])
        row = st.sb("row", [1, 2, S])
        rowmax = st.sb("rowmax", [1, B])
        rowsum = st.sb("rowsum", [1, B])
        ecol = st.sb("ecol", [P, NT])
        w14 = st.sb("w14", [P, B, D])
        names = ("loaded", "prepared", "drow_done", "drow_ready", "sim_done", "centred", "expd", "normal", "turned",
                 "prT_ready", "hq_done", "hq_ready", "row_done", "rowmax_ready", "row_exp", "row_ready", "col_done",
                 "col_ready", "hc_done", "w_ready", "out_done", "added")
        loaded, prepared, drow_done, drow_ready, sim_done, centred, expd, normal, turned, prT_ready, hq_done, hq_ready, \
            row_done, rowmax_ready, row_exp, row_ready, col_done, col_ready, hc_done, w_ready, out_done, added = (st.sem(n) for n in names)
        loads = [(cols[:, :], A["l1c_cols"]), (w[:, :, :], A["l1c_w"]), (bias[:, :], A["l1c_bias"])]
        layernorm(nc, T, T.X[:, :, :], T.LNX[:, :, :], T.LNT[:, :], loads, loaded)
        with nc.Block() as block:
            @block.tensor
            def _(pe):
                pe.wait_ge(prepared, 1)
                nc.tensor.matmul(T.bank[0][:, 0:B * L], w2[:, :], T.CTXT[:, :], start=True, stop=True).then_inc(drow_done, 1)
                pe.wait_ge(drow_ready, 1)

                def similarities(b):
                    if b >= 2:
                        pe.wait_ge(centred, b - 1)
                    for t in range(TPB):
                        n = b * TPB + t
                        last = nc.tensor.matmul(T.bank[b % 2][:, t * L:(t + 1) * L], T.LNT[:, n * P:(n + 1) * P],
                                                c3[:, b * L:(b + 1) * L], start=True, stop=True)
                    last.then_inc(sim_done, 1)
                similarities(0)
                for b in range(B):
                    if b + 1 < B:
                        similarities(b + 1)
                    if b:
                        pe.wait_ge(added, b)
                    pe.wait_ge(normal, b + 1)
                    for t in range(TPB):
                        last = nc.tensor.transpose(T.bank[2][0:L, t * P:(t + 1) * P], sim[:, b % 2, t, :], T.ident[:, :])
                    last.then_inc(turned, 1)
                    for t in range(TPB):
                        n = b * TPB + t
                        last = nc.tensor.matmul(T.bank[4][0:1, t * P:(t + 1) * P], mx[:, n:n + 1], T.ident[:, :],
                                                start=True, stop=True)
                    last.then_inc(row_done, 1)
                    pe.wait_ge(prT_ready, b + 1)
                    nc.tensor.matmul(T.bank[3][:, :], T.CTX[:, b, :], prT[:, b % 2, :], start=True, stop=True).then_inc(hq_done, 1)
                    pe.wait_ge(row_ready, b + 1)
                    for t in range(TPB):
                        last = nc.tensor.matmul(T.bank[5][:, t:t + 1], row[0:1, b % 2, t * P:(t + 1) * P],
                                                T.ident[0:1, 0:1], start=True, stop=True)
                    last.then_inc(col_done, 1)
                    pe.wait_ge(col_ready, b + 1)
                    for t in range(TPB):
                        n = b * TPB + t
                        last = nc.tensor.matmul(T.bank[7][:, 0:1], T.LNX[:, n, :], ecol[:, n:n + 1], start=(t == 0),
                                                stop=(t == TPB - 1))
                    last.then_inc(hc_done, 1)
                    pe.wait_ge(w_ready, b + 1)
                    pe.wait_ge(hq_ready, b + 1)
                    for t in range(TPB):
                        n = b * TPB + t
                        cut = slice(t * P, (t + 1) * P)
                        o = T.bank[6][:, t * D:(t + 1) * D]
                        nc.tensor.matmul(o, T.LNT[:, n * P:(n + 1) * P], w14[:, b, :], start=True, stop=False)
                        nc.tensor.matmul(o, hq[:, b % 2, cut], w[:, 1, :], start=False, stop=False)
                        last = nc.tensor.matmul(o, ehq[:, b % 2, cut], w[:, 2, :], start=False, stop=True)
                    last.then_inc(out_done, 1)

            @block.scalar
            def _(act):
                def exponentials(b):
                    act.wait_ge(centred, b + 1)
                    nc.scalar.activation(sim[:, b % 2, :, :], sim[:, b % 2, :, :], ACT.Exp).then_inc(expd, 1)
                exponentials(0)
                for b in range(B):
                    act.wait_ge(turned, b + 1)
                    nc.scalar.activation(prT[:, b % 2, :], T.bank[2][0:L, :], ACT.Copy).then_inc(prT_ready, 1)
                    act.wait_ge(rowmax_ready, b + 1)
                    nc.scalar.activation(row[0:1, b % 2, :], T.bank[4][0:1, :], ACT.Exp, bias=rowmax[0:1, b:b + 1],
                                         accum_out=rowsum[0:1, b:b + 1]).then_inc(row_exp, 1)
                    if b + 1 < B:
                        exponentials(b + 1)
                    act.wait_ge(col_done, b + 1)
                    nc.scalar.activation(ecol[:, b * TPB:(b + 1) * TPB], T.bank[5][:, 0:TPB], ACT.Copy).then_inc(col_ready, 1)

            @block.vector
            def _(dve):
                link = chain(T, dve)
                dve.wait_ge(loaded, 16 * len(loads))
                nc.vector.tensor_scalar(c3[:, :], T.CTXT[:, :], cols[:, 2:3], cols[:, 0:1], ALU.mult, ALU.add)
                nc.vector.tensor_scalar(w2[:, :], T.zeros[:, :], cols[:, 1:2], None, ALU.add).then_inc(prepared, 1)
                link(nc.vector.tensor_tensor(T.X[:, :, :], T.X[:, :, :], tiled(bias[:, :], NT), ALU.add))
                dve.wait_ge(drow_done, 1)
                nc.vector.tensor_scalar(drow[:, :, :], T.bank[0][:, 0:B * L].rearrange("p (b l) -> p b l", b=B),
                                        cols[:, 3:4], None, ALU.add).then_inc(drow_ready, 1)
                dve.wait_ge(drow_ready, 1)

                def centre(b):
                    z = sim[:, b % 2, :, :]
                    m = mx[:, b * TPB:(b + 1) * TPB]
                    dve.wait_ge(sim_done, b + 1)
                    if b >= 2:
                        dve.wait_ge(turned, b - 1)
                    link(nc.vector.tensor_tensor(z, T.bank[b % 2][:, 0:TPB * L].rearrange("p (t l) -> p t l", t=TPB),
                                                 tiled(drow[:, b, :], TPB), ALU.add))
                    link(nc.vector.tensor_reduce(m, z, axis=AX, op=ALU.max))
                    nc.vector.tensor_tensor(z, z, spread(m, L), ALU.subtract).then_inc(centred, 1)

                def normalize(b):
                    z = sim[:, b % 2, :, :]
                    r = rs[:, b * TPB:(b + 1) * TPB]
                    dve.wait_ge(expd, b + 1)
                    link(nc.vector.tensor_reduce(r, z, axis=AX, op=ALU.add))
                    link(nc.vector.reciprocal(r, r))
                    nc.vector.tensor_tensor(z, z, spread(r, L), ALU.mult).then_inc(normal, 1)
                centre(0)
                normalize(0)
                for b in range(B):
                    dve.wait_ge(row_done, b + 1)
                    nc.vector.tensor_reduce(rowmax[0:1, b:b + 1], T.bank[4][0:1, :], axis=AX, op=ALU.max, negate=True)\
                        .then_inc(rowmax_ready, 1)
                    if b + 1 < B:
                        centre(b + 1)
                    dve.wait_ge(row_exp, b + 1)
                    link(nc.vector.reciprocal(rowsum[0:1, b:b + 1], rowsum[0:1, b:b + 1]))
                    nc.vector.tensor_scalar(row[0:1, b % 2, :], row[0:1, b % 2, :], rowsum[0:1, b:b + 1], None, ALU.mult)\
                        .then_inc(row_ready, 1)
                    dve.wait_ge(hq_done, b + 1)
                    nc.vector.tensor_copy(hq[:, b % 2, :], T.bank[3][:, :])
                    nc.vector.tensor_tensor(ehq[:, b % 2, :], T.bank[3][:, :], T.LNT[:, b * S:(b + 1) * S], ALU.mult)\
                        .then_inc(hq_ready, 1)
                    if b + 1 < B:
                        normalize(b + 1)
                    dve.wait_ge(hc_done, b + 1)
                    nc.vector.scalar_tensor_tensor(w14[:, b, :], w[:, 3, :], T.bank[7][:, 0:1], w[:, 0, :], ALU.mult,
                                                   ALU.add).then_inc(w_ready, 1)
                    dve.wait_ge(out_done, b + 1)
                    x = T.X[:, b * TPB:(b + 1) * TPB, :]
                    nc.vector.tensor_tensor(x, x, T.bank[6][:, :].rearrange("p (t d) -> p t d", t=TPB), ALU.add)\
                        .then_inc(added, 1)


def l2_attention(nc, T, A):
    with Stage(nc, T, "l2a") as st:
        w = st.sb("w", [P, 3 * D])
        q, k = st.sb("q", [P, S]), st.sb("k", [P, S])
        v = st.sb("v", [P, 2, TPB, D])
        e = st.sb("e", [P, 2, TPB, S])
        nmx, rs = st.sb("nmx", [P, 2, TPB]), st.sb("rs", [P, 2, TPB])
        names = ("loaded", "projected", "qk_ready", "scored", "max_ready", "expd", "v_scaled", "out_done",
                 "added", "v_step")
        loaded, projected, qk_ready, scored, max_ready, expd, v_scaled, out_done, added, v_step = (
            st.sem(n) for n in names)
        loads = [(w[:, :], A["l2a_w"])]
        layernorm(nc, T, T.X[:, :, :], T.LNX[:, :, :], T.LNT[:, :], loads, loaded)
        with nc.Block() as block:
            @block.tensor
            def _(pe):
                def project(b):
                    x = T.LNT[:, b * S:(b + 1) * S]
                    if b:
                        pe.wait_ge(qk_ready, b)
                    for i in range(2):
                        nc.tensor.matmul(T.bank[i][:, :], w[:, i * D:(i + 1) * D], x, start=True, stop=True)
                    if b:
                        pe.wait_ge(v_scaled, b)
                    for t in range(TPB):
                        last = nc.tensor.matmul(T.bank[2][:, t * D:(t + 1) * D], x[:, t * P:(t + 1) * P], w[:, 2 * D:3 * D],
                                                start=True, stop=True)
                    last.then_inc(projected, 1)

                def scores(b):
                    pe.wait_ge(qk_ready, b + 1)
                    if b:
                        pe.wait_ge(expd, b * TPB)
                    for t in range(TPB):
                        nc.tensor.matmul(T.bank[3 + t][:, :], k[:, t * P:(t + 1) * P], q[:, :], start=True, stop=True)\
                            .then_inc(scored, 1)
                pe.wait_ge(loaded, 16)
                project(0)
                scores(0)
                for b in range(B):
                    if b + 1 < B:
                        project(b + 1)
                        scores(b + 1)
                    pe.wait_ge(v_scaled, b + 1)
                    if b:
                        pe.wait_ge(added, b)
                    for t in range(TPB):
                        for j in range(TPB):
                            last = nc.tensor.matmul(T.bank[7][:, t * D:(t + 1) * D], e[:, b % 2, j, t * P:(t + 1) * P],
                                                    v[:, b % 2, j, :], start=(j == 0), stop=(j == TPB - 1))
                    last.then_inc(out_done, 1)

            @block.scalar
            def _(act):
                def move(b):
                    act.wait_ge(projected, b + 1)
                    if b:
                        act.wait_ge(scored, b * TPB)
                    nc.scalar.activation(q[:, :], T.bank[0][:, :], ACT.Copy, scale=D ** -0.5)
                    nc.scalar.activation(k[:, :], T.bank[1][:, :], ACT.Copy).then_inc(qk_ready, 1)
                move(0)
                for b in range(B):
                    if b >= 2:
                        act.wait_ge(out_done, b - 1)
                    for t in range(TPB):
                        act.wait_ge(max_ready, b * TPB + t + 1)
                        nc.scalar.activation(e[:, b % 2, t, :], T.bank[3 + t][:, :], ACT.Exp, bias=nmx[:, b % 2, t:t + 1],
                                             accum_out=rs[:, b % 2, t:t + 1]).then_inc(expd, 1)
                    if b + 1 < B:
                        move(b + 1)

            @block.vector
            def _(dve):
                def add_output(b):
                    dve.wait_ge(out_done, b + 1)
                    x = T.X[:, b * TPB:(b + 1) * TPB, :]
                    nc.vector.tensor_tensor(x, x, T.bank[7][:, :].rearrange("p (t c) -> p t c", t=TPB), ALU.add)\
                        .then_inc(added, 1)
                for b in range(B):
                    for t in range(TPB):
                        dve.wait_ge(scored, b * TPB + t + 1)
                        nc.vector.tensor_reduce(nmx[:, b % 2, t:t + 1], T.bank[3 + t][:, :], axis=AX, op=ALU.max, negate=True)\
                            .then_inc(max_ready, 1)
                    if b:
                        add_output(b - 1)
                    dve.wait_ge(expd, b * TPB + TPB)
                    nc.vector.reciprocal(rs[:, b % 2, :], rs[:, b % 2, :]).then_inc(v_step, 1)
                    dve.wait_ge(v_step, b + 1)
                    dve.wait_ge(projected, b + 1)
                    nc.vector.tensor_tensor(v[:, b % 2, :, :], T.bank[2][:, :].rearrange("p (t d) -> p t d", t=TPB),
                                            spread(rs[:, b % 2, :], D), ALU.mult).then_inc(v_scaled, 1)
                add_output(B - 1)


def l3_attention(nc, T, A):
    EPS = 1e-9
    with Stage(nc, T, "l3a") as st:
        w = st.sb("w", [P, 3 * D])
        tril = st.sb("tril", [P, 2, P])
        eps = st.sb("eps", [P, P])
        q = st.sb("q", [P, N])
        k = st.sb("k", [P, N])
        v = st.sb("v", [P, NT, D])
        m = st.sb("m", [P, S])
        z = st.sb("z", [P, B, S])
        zT = st.sb("zT", [P, B, S])
        total = st.sb("total", [P, S])
        names = ("loaded", "projected", "taken", "scored", "first", "centred", "expd", "normal", "turned", "zT_ready",
                 "out_done", "added", "eps_ready")
        loaded, projected, taken, scored, first, centred, expd, normal, turned, zT_ready, out_done, added, eps_ready = (
            st.sem(n) for n in names)
        loads = [(w[:, :], A["l3a_w"]), (tril[:, :, :], A["tril"])]
        layernorm(nc, T, T.X[:, :, :], T.LNX[:, :, :], T.LNT[:, :], loads, loaded)
        with nc.Block() as block:
            @block.tensor
            def _(pe):
                pe.wait_ge(loaded, 16 * len(loads))
                for b in range(B):
                    for i in range(3):
                        n = 3 * b + i
                        if n >= 6:
                            pe.wait_ge(taken, n - 5)
                        bank = T.bank[n % 6]
                        xT = T.LNT[:, b * S:(b + 1) * S]
                        if i == 0:
                            last = nc.tensor.matmul(bank[:, :], w[:, 0:D], xT, start=True, stop=True)
                        for t in range(TPB if i else 0):
                            x = xT.rearrange("p (r c) -> p c r", c=TPB)[:, t, :] if i == 1 else xT[:, t * P:(t + 1) * P]
                            last = nc.tensor.matmul(bank[:, t * D:(t + 1) * D], x, w[:, i * D:(i + 1) * D], start=True,
                                                    stop=True)
                        last.then_inc(projected, 1)
                pe.wait_ge(taken, 3 * B)
                pe.wait_ge(eps_ready, 1)

                def scores(t):
                    W = (t + 1) * P
                    if t:
                        pe.wait_ge(centred, t)
                    for b in range(B):
                        last = nc.tensor.matmul(T.bank[b][:, 0:W], q[:, b * S + t * P:b * S + (t + 1) * P],
                                                k[:, b * S:b * S + W], start=True, stop=True)
                    last.then_inc(scored, 1)
                scores(0)
                for t in range(TPB):
                    if t + 1 < TPB:
                        scores(t + 1)
                    pe.wait_ge(normal, t + 1)
                    for b in range(B):
                        n = t * B + b
                        if n >= 2:
                            pe.wait_ge(zT_ready, n - 1)
                        for j in range(t + 1):
                            last = nc.tensor.transpose(T.bank[4 + n % 2][:, j * P:(j + 1) * P], z[:, b, j * P:(j + 1) * P],
                                                       T.ident[:, :])
                        last.then_inc(turned, 1)
                    pe.wait_ge(zT_ready, B * (t + 1))
                    if t >= 2:
                        pe.wait_ge(added, t - 1)
                    for b in range(B):
                        for j in range(TPB):
                            p = zT[:, b, j * P:(j + 1) * P] if j <= t else eps[:, :]
                            last = nc.tensor.matmul(T.bank[6 + t % 2][:, b * D:(b + 1) * D], p, v[:, b * TPB + j, :],
                                                    start=(j == 0), stop=(j == TPB - 1))
                    last.then_inc(out_done, 1)

            @block.scalar
            def _(act):
                for n in range(3 * B):
                    b, i = divmod(n, 3)
                    act.wait_ge(projected, n + 1)
                    src = T.bank[n % 6][:, :]
                    if i == 0:
                        out = nc.scalar.activation(q[:, b * S:(b + 1) * S], src, ACT.Copy, scale=D ** -0.5)
                    elif i == 1:
                        out = nc.scalar.activation(k[:, b * S:(b + 1) * S], src, ACT.Copy)
                    else:
                        out = nc.scalar.activation(v[:, b * TPB:(b + 1) * TPB, :],
                                                   src.rearrange("p (t d) -> p t d", t=TPB), ACT.Copy)
                    out.then_inc(taken, 1)
                for t in range(TPB):
                    W = (t + 1) * P
                    act.wait_ge(scored, t + 1)
                    if t:
                        act.wait_ge(centred, t)
                    nc.scalar.activation(m[:, 0:W], T.bank[0][:, 0:W], ACT.Copy).then_inc(first, 1)
                    act.wait_ge(centred, t + 1)
                    nc.scalar.activation(z[:, :, 0:W], z[:, :, 0:W], ACT.Exp).then_inc(expd, 1)
                    for b in range(B):
                        act.wait_ge(turned, B * t + b + 1)
                        nc.scalar.activation(zT[:, b, 0:W], T.bank[4 + b % 2][:, 0:W], ACT.Copy).then_inc(zT_ready, 1)

            @block.vector
            def _(dve):
                link = chain(T, dve)

                def add_output(t):
                    dve.wait_ge(out_done, t + 1)
                    x = T.X[:, :, :].rearrange("p (b t) d -> p t b d", b=B)[:, t, :, :]
                    nc.vector.tensor_tensor(x, x, T.bank[6 + t % 2][:, :].rearrange("p (b d) -> p b d", b=B), ALU.add)\
                        .then_inc(added, 1)
                nc.vector.memset(eps[:, :], EPS).then_inc(eps_ready, 1)
                dve.wait_ge(loaded, 16 * len(loads))
                for t in range(TPB):
                    W = (t + 1) * P
                    dve.wait_ge(first, t + 1)
                    mm = m[:, 0:W]
                    for b in range(1, B):
                        link(nc.vector.tensor_tensor(mm, T.bank[b][:, 0:W], mm, ALU.max))
                    if t:
                        dve.wait_ge(turned, B * t)
                    for b in range(B):
                        last = nc.vector.tensor_tensor(z[:, b, 0:W], T.bank[b][:, 0:W], mm, ALU.subtract)
                    last.then_inc(centred, 1)
                    if t:
                        add_output(t - 1)
                    dve.wait_ge(expd, t + 1)
                    link(nc.vector.tensor_reduce(total[:, 0:W], z[:, :, 0:W].rearrange("p b w -> p w b"), axis=AX, op=ALU.add))
                    link(nc.vector.reciprocal(total[:, 0:W], total[:, 0:W]))
                    link(nc.vector.tensor_tensor(z[:, :, 0:W], z[:, :, 0:W], tiled(total[:, 0:W], B), ALU.mult))
                    last_block = z[:, :, t * P:W]
                    link(nc.vector.tensor_tensor(last_block, last_block, tiled(tril[:, 0, :], B), ALU.mult))
                    nc.vector.tensor_tensor(last_block, last_block, tiled(tril[:, 1, :], B), ALU.add).then_inc(normal, 1)
                add_output(TPB - 1)


def l2_moe_attention(nc, T, A):
    H, HD, E = 16, 64, 8
    PAIRS, SLOTS = H // 2, 2
    TURNS = PAIRS // SLOTS
    TH = 2 * SLOTS
    PICKS = 14
    GROUPS = SLOTS * B
    UPG = 2 * TPB
    UNITS = GROUPS * UPG
    SPLIT_1, SPLIT_0, PICK = 14, 44, 20
    LEAD = UPG + 2
    PIECES = 4 + UPG
    QK = 4 * P
    WV = QK + 2 * E * HD
    WTOT = WV + 2 * 4 * D
    F = 4 * D
    with Stage(nc, T, "l2m") as st:
        gates = st.sb("gates", [P, NT, 2, H, E])
        ln1, ln2 = st.sb("ln1", [P, 2, D]), st.sb("ln2", [P, 2, D])
        b1, b2 = st.sb("b1", [P, 4]), st.sb("b2", [P, D])
        trig = st.sb("trig", [P, 4, S])
        loaded = st.sem("loaded")
        loads = [(ln1[:, :, :], A["l2m_ln1"]), (ln2[:, :, :], A["l2m_ln2"]), (b1[:, :], A["l2m_b1"]), (b2[:, :], A["l2m_b2"]),
                 (trig[:, :, :], A["l2m_trig"])]

        with Stage(nc, T, "l2h") as sh:
            wsel = sh.sb("wsel", [P, 2 * H * E])
            left = sh.sb("left", [P, NT, 2, TH, E])
            seen = sh.sb("seen", [P, NT, 2, TH, E])
            pick = sh.sb("pick", [P, NT, 2, TH, E])
            best = sh.sb("best", [P, NT * 2 * TH])
            x_hi, x_lo = sh.sb("x_hi", [P, N], F32R), sh.sb("x_lo", [P, N], F32R)
            w_hi = [sh.sb(f"w_hi{i}", [P, WV], F32R) for i in range(SLOTS)]
            w_lo = [sh.sb(f"w_lo{i}", [P, WV], F32R) for i in range(SLOTS)]
            slot = [sh.sb(f"w{i}", [P, WTOT]) for i in range(SLOTS)]
            plain, rotated = sh.sb("plain", [P, 2, S]), sh.sb("rotated", [P, 2, S])
            qk = sh.sb("qk", [P, 2, S])
            qk_hi, qk_lo = sh.sb("qk_hi", [P, 2, 2, S], F32R), sh.sb("qk_lo", [P, 2, 2, S], F32R)
            vg = sh.sb("vg", [P, 2, E, HD])
            vs = sh.sb("vs", [P, 2, E // 2, HD])
            v = sh.sb("v", [P, 2, UPG, HD])
            pr, prT = sh.sb("pr", [P, 2, S]), sh.sb("prT", [P, 2, S])
            og, ogT = sh.sb("og", [P, 2, E, HD]), sh.sb("ogT", [P, 2, S])
            nmx, rs = sh.sb("nmx", [P, 4]), sh.sb("rs", [P, 4])
            go = sh.sb("go", [P, 4, E])
            gv_h = [sh.sb(f"gv{i}", [P, NT, 2, E]) for i in range(SLOTS)]
            go_h = [sh.sb(f"go{i}", [P, NT, 2, E]) for i in range(SLOTS)]
            arrived = [sh.sem(f"arrived{i}") for i in range(SLOTS)]
            logits, squashed, pick_step, x_high, x_low, w_high, w_low, qk_high, qk_low = (
                sh.sem(n) for n in ("logits", "squashed", "pick_step", "x_high", "x_low", "w_high", "w_low", "qk_high", "qk_low"))
            names = ("gates_ready", "made", "read", "roped", "v_step", "v_ready", "scored", "maxed",
                     "expd", "turned", "copied", "pv_done", "o_step", "gated", "g_turned", "g_copied", "y_done", "added")
            gates_ready, made, read, roped, v_step, v_ready, scored, maxed, expd, turned, copied, pv_done, \
                o_step, gated, g_turned, g_copied, y_done, added = (sh.sem(n) for n in names)
            pj, sbank, tbank, obank, ybank = T.bank[0:2], T.bank[2:4], T.bank[4:6], T.bank[6], T.bank[7]

            def pieces_at(i, last):
                g, r = divmod(i, UPG)
                if last and g + 1 >= GROUPS:
                    return []
                return [(g + 1, n) for n in range(PIECES * r // UPG, PIECES * (r + 1) // UPG)]
            START = [(0, n) for n in range(PIECES)]

            def place(n):
                g, u = divmod(n, UPG)
                return g // B % SLOTS, u // TPB, g % B, u % TPB

            def turns(engine, step):
                for i in range(LEAD):
                    step(0, i, False)
                with engine.Fori(0, TURNS - 1) as it:
                    for i in range(LEAD, LEAD + UNITS):
                        step(it, i, False)
                for i in range(LEAD, UNITS + 5):
                    step(TURNS - 1, i, True)

            def due(i, lag, last):
                return i >= lag and (i - lag < UNITS or not last)

            layernorm(nc, T, T.X[:, :, :], T.LNX[:, :, :], T.LNT[:, :], loads + [(wsel[:, :], A["l2m_wsel"])], loaded)
            with nc.Block() as block:
                @block.sync
                def _(sp):
                    for s in range(SLOTS):
                        sp.dma_start(slot[s][:, :], A["l2m_w"][s, :, :]).then_inc(arrived[s], 16)
                    with sp.Fori(0, TURNS - 1) as it:
                        for s in range(SLOTS):
                            sp.wait_ge(y_done, it * UNITS + (s + 1) * UNITS // SLOTS)
                            sp.dma_start(slot[s][:, :], A["l2m_w"][bass.ds(it * SLOTS + SLOTS + s, 1), :, :]
                                         .rearrange("a p c -> (a p) c")).then_inc(arrived[s], 16)

                @block.tensor
                def _(pe):
                    def make(it, g, n):
                        s, b = g // B % SLOTS, g % B
                        at = g * PIECES + n
                        if n == 0 and b == 0:
                            pe.wait_ge(w_low, it * SLOTS + g // GROUPS * SLOTS + s + 1)
                        if at >= 2:
                            pe.wait_ge(read, it * GROUPS * PIECES + at - 1)
                        halves = ((x_hi, w_hi[s]), (x_lo, w_hi[s]), (x_hi, w_lo[s]))
                        for p, (x, w) in enumerate(halves):
                            if n < 4:
                                out = nc.tensor.matmul(pj[at % 2][:, :], w[:, n * P:(n + 1) * P], x[:, b * S:(b + 1) * S],
                                                       start=(p == 0), stop=(p == 2))
                            else:
                                h, t = divmod(n - 4, TPB)
                                out = nc.tensor.matmul(pj[at % 2][:, :], x[:, b * S + t * P:b * S + (t + 1) * P],
                                                       w[:, QK + h * S:QK + (h + 1) * S], start=(p == 0), stop=(p == 2))
                        out.then_inc(made, 1)

                    def step(it, i, last):
                        if due(i, 0, last):
                            g, u = divmod(i, UPG)
                            h, t = divmod(u, TPB)
                            if u == 0:
                                pe.wait_ge(qk_low, it * 2 * GROUPS + 2 * g + 2)
                            if i >= 2:
                                pe.wait_ge(expd, it * UNITS + i - 1)
                            rows = slice(h * HD, (h + 1) * HD)
                            halves = ((qk_hi, qk_hi), (qk_lo, qk_hi), (qk_hi, qk_lo))
                            for p, (q, k) in enumerate(halves):
                                out = nc.tensor.matmul(sbank[i % 2][:, :], q[rows, g % 2, 0, t * P:(t + 1) * P],
                                                       k[rows, g % 2, 1, :], start=(p == 0), stop=(p == 2))
                            out.then_inc(scored, 1)
                        j = i - 1
                        if due(i, 1, last):
                            pe.wait_ge(expd, it * UNITS + j + 1)
                            if j >= 1:
                                pe.wait_ge(copied, it * UNITS + j)
                            for t in range(TPB):
                                out = nc.tensor.transpose(tbank[0][:, t * P:(t + 1) * P], pr[:, j % 2, t * P:(t + 1) * P],
                                                          T.ident[:, :])
                            out.then_inc(turned, 1)
                        j = i - 2
                        if due(i, 2, last):
                            g, u = divmod(j, UPG)
                            pe.wait_ge(copied, it * UNITS + j + 1)
                            if u % TPB == 0:
                                pe.wait_ge(v_ready, it * UNITS + j + TPB)
                            if j >= 1:
                                pe.wait_ge(gated, it * UNITS + j)
                            for t in range(TPB):
                                out = nc.tensor.matmul(obank[:, 0:HD], prT[:, j % 2, t * P:(t + 1) * P],
                                                       v[:, g % 2, u // TPB * TPB + t, :], start=(t == 0),
                                                       stop=(t == TPB - 1))
                            out.then_inc(pv_done, 1)
                        j = i - 3
                        if due(i, 3, last):
                            pe.wait_ge(gated, it * UNITS + j + 1)
                            if j >= 1:
                                pe.wait_ge(g_copied, it * UNITS + j)
                            for t in range(4):
                                out = nc.tensor.transpose(tbank[1][:, t * P:(t + 1) * P],
                                                          og[:, j % 2, 2 * t:2 * t + 2, :].rearrange("p e d -> p (e d)"),
                                                          T.ident[:, :])
                            out.then_inc(g_turned, 1)
                        for g, n in pieces_at(i, last):
                            make(it, g, n)
                        j = i - 4
                        if due(i, 4, last):
                            s, h, _, _ = place(j)
                            pe.wait_ge(g_copied, it * UNITS + j + 1)
                            if j >= 1:
                                pe.wait_ge(added, it * UNITS + j)
                            for t in range(4):
                                at = WV + (h * 4 + t) * D
                                out = nc.tensor.matmul(ybank[:, 0:D], ogT[:, j % 2, t * P:(t + 1) * P],
                                                       slot[s][:, at:at + D], start=(t == 0), stop=(t == 3))
                            out.then_inc(y_done, 1)
                    pe.wait_ge(loaded, 16 * len(loads) + 16)
                    for t in range(NT):
                        nc.tensor.matmul(T.bank[t // 2][:, t % 2 * 256:t % 2 * 256 + 256], T.LNT[:, t * P:(t + 1) * P],
                                         wsel[:, :], start=True, stop=True).then_inc(logits, 1)
                    pe.wait_ge(squashed, NT // 2)
                    pe.wait_ge(x_low, B)
                    for g, n in START:
                        make(0, g, n)
                    turns(pe, step)

                @block.scalar
                def _(act):
                    def split_weights(it, s):
                        act.wait_ge(arrived[s], it * 16 + 16)
                        nc.scalar.activation(w_hi[s][:, :], slot[s][:, 0:WV], ACT.Copy).then_inc(w_high, 1)

                    def split_qk(it, g, kind):
                        act.wait_ge(roped, it * 2 * GROUPS + 2 * g + kind + 1)
                        nc.scalar.activation(qk_hi[:, g % 2, kind, :], qk[:, kind, :], ACT.Copy).then_inc(qk_high, 1)

                    def step(it, i, last):
                        if i == SPLIT_1:
                            act.wait_ge(made, it * GROUPS * PIECES + PIECES)
                            split_weights(it, 1)
                        if i == SPLIT_0 and not last:
                            act.wait_ge(made, it * GROUPS * PIECES + B * PIECES)
                            split_weights(it + 1, 0)
                        if due(i, 0, last):
                            act.wait_ge(maxed, it * UNITS + i + 1)
                            if i >= 2:
                                act.wait_ge(turned, it * UNITS + i - 1)
                            nc.scalar.activation(pr[:, i % 2, :], sbank[i % 2][:, :], ACT.Exp, bias=nmx[:, i % 4:i % 4 + 1],
                                                 accum_out=rs[:, i % 4:i % 4 + 1]).then_inc(expd, 1)
                        j = i - 1
                        if due(i, 1, last):
                            act.wait_ge(turned, it * UNITS + j + 1)
                            if j >= 2:
                                act.wait_ge(pv_done, it * UNITS + j - 1)
                            nc.scalar.activation(prT[:, j % 2, :], tbank[0][:, :], ACT.Copy).then_inc(copied, 1)
                        j = i - 3
                        if due(i, 3, last):
                            act.wait_ge(g_turned, it * UNITS + j + 1)
                            if j >= 2:
                                act.wait_ge(y_done, it * UNITS + j - 1)
                            nc.scalar.activation(ogT[:, j % 2, :], tbank[1][:, :], ACT.Copy).then_inc(g_copied, 1)
                        g, r = divmod(i, UPG)
                        if r in (2, 3) and not (last and g + 1 >= GROUPS):
                            split_qk(it, g + 1, r - 2)
                    for c in range(B):
                        nc.scalar.activation(x_hi[:, c * S:(c + 1) * S], T.LNT[:, c * S:(c + 1) * S], ACT.Copy)\
                            .then_inc(x_high, 1)
                    for i in range(NT // 2):
                        act.wait_ge(logits, 2 * i + 2)
                        nc.scalar.activation(gates[:, 2 * i:2 * i + 2, :, :, :].rearrange("p t v h e -> p (t v h e)"),
                                             T.bank[i][:, :], ACT.Sigmoid).then_inc(squashed, 1)
                    split_weights(0, 0)
                    split_qk(0, 0, 0)
                    split_qk(0, 0, 1)
                    turns(act, step)

                @block.vector
                def _(dve):
                    def pick_gates(it, k):
                        if k:
                            dve.wait_ge(pick_step, it * PICKS + k)
                        V, c, O = (t[:, :, :, :, :].rearrange("p t v h e -> p (t v h) e") for t in (left, seen, pick))
                        m = best[:, :]
                        if k == 0:
                            out = nc.vector.tensor_copy(left[:, :, :, :, :], gates[:, :, :, bass.ds(it * TH, TH), :])
                        elif k == PICKS - 1:
                            out = nc.vector.tensor_scalar(c, V, -2.0 * BIG, None, ALU.is_lt)
                        elif k % 6 == 1:
                            out = nc.vector.tensor_reduce(m, V, axis=AX, op=ALU.max)
                        elif k % 6 == 2:
                            out = nc.vector.tensor_tensor(c, V, spread(m, E), ALU.is_ge)
                        elif k % 6 == 3:
                            out = nc.vector.tensor_tensor(c, c, tiled(T.rev[:, 64 - E:64], NT * 2 * TH), ALU.mult)
                        elif k % 6 == 4:
                            out = nc.vector.tensor_reduce(m, c, axis=AX, op=ALU.max)
                        elif k % 6 == 5:
                            out = nc.vector.tensor_tensor(O, c, spread(m, E), ALU.is_equal)
                        else:
                            out = nc.vector.scalar_tensor_tensor(V, O, -3.0 * BIG, V, ALU.mult, ALU.add)
                        out.then_inc(pick_step, 1)

                    def fetch_gates(it, s, n):
                        heads = bass.ds(it * TH + 2 * s, 2)
                        mine = slice(2 * s, 2 * s + 2)
                        nc.vector.tensor_tensor(gv_h[s][:, :, :, :], gates[:, :, 0, heads, :], seen[:, :, 0, mine, :], ALU.mult)
                        nc.vector.tensor_tensor(go_h[s][:, :, :, :], gates[:, :, 1, heads, :], seen[:, :, 1, mine, :], ALU.mult)\
                            .then_inc(gates_ready, 1)
                        dve.wait_ge(gates_ready, n)

                    def take(it, g, n):
                        s, b = g // B % SLOTS, g % B
                        at = g * PIECES + n
                        dve.wait_ge(made, it * GROUPS * PIECES + at + 1)
                        if n < 4:
                            kind, part = divmod(n, 2)
                            dst = (plain, rotated)[part][:, kind, :]
                            if at >= PIECES and part == 0:
                                dve.wait_ge(roped, it * 2 * GROUPS + 2 * g - 1 + kind)
                            nc.vector.tensor_tensor(dst, pj[at % 2][:, :], trig[:, n, :], ALU.mult).then_inc(read, 1)
                            if part:
                                dve.wait_ge(read, it * GROUPS * PIECES + at + 1)
                                if g:
                                    dve.wait_ge(qk_low, it * 2 * GROUPS + 2 * g - 1 + kind)
                                nc.vector.tensor_tensor(qk[:, kind, :], plain[:, kind, :], rotated[:, kind, :],
                                                        ALU.add).then_inc(roped, 1)
                        else:
                            u = g * UPG + n - 4
                            h, t = divmod(n - 4, TPB)
                            if u >= 2:
                                dve.wait_ge(v_step, it * 2 * UNITS + 2 * u - 3)
                            nc.vector.tensor_tensor(vg[:, u % 2, :, :], pj[at % 2][:, :].rearrange("p (e d) -> p e d", e=E),
                                                    spread(gv_h[s][:, b * TPB + t, h, :], HD), ALU.mult).then_inc(read, 1)

                    def step(it, i, last):
                        j = i - 5
                        if due(i, 5, last):
                            _, _, b, t = place(j)
                            dve.wait_ge(y_done, it * UNITS + j + 1)
                            if j >= TPB:
                                dve.wait_ge(added, it * UNITS + j - TPB + 1)
                            acc = T.LNX[:, b * TPB + t, :]
                            nc.vector.tensor_tensor(acc, acc, ybank[:, 0:D], ALU.add).then_inc(added, 1)
                        if due(i, 0, last):
                            dve.wait_ge(scored, it * UNITS + i + 1)
                            nc.vector.tensor_reduce(nmx[:, i % 4:i % 4 + 1], sbank[i % 2][:, :], axis=AX, op=ALU.max,
                                                    negate=True).then_inc(maxed, 1)
                        j = i - 2
                        if due(i, 2, last):
                            s, h, b, t = place(j)
                            dve.wait_ge(expd, it * UNITS + j + 1)
                            nc.vector.reciprocal(rs[:, j % 4:j % 4 + 1], rs[:, j % 4:j % 4 + 1]).then_inc(o_step, 1)
                            dve.wait_ge(o_step, it * 2 * UNITS + 2 * j + 1)
                            nc.vector.tensor_scalar(go[:, j % 4, :], go_h[s][:, b * TPB + t, h, :], rs[:, j % 4:j % 4 + 1],
                                                    None, ALU.mult).then_inc(o_step, 1)
                            dve.wait_ge(o_step, it * 2 * UNITS + 2 * j + 2)
                            if j >= 2:
                                dve.wait_ge(g_turned, it * UNITS + j - 1)
                            dve.wait_ge(pv_done, it * UNITS + j + 1)
                            nc.vector.tensor_tensor(og[:, j % 2, :, :], tiled(obank[:, 0:HD], E), spread(go[:, j % 4, :], HD),
                                                    ALU.mult).then_inc(gated, 1)
                        if 0 <= i - PICK < PICKS and not last:
                            if i == PICK:
                                dve.wait_ge(gates_ready, it * SLOTS + SLOTS)
                            pick_gates(it + 1, i - PICK)
                        for s in range(SLOTS):
                            if i == (s + 1) * UNITS // SLOTS + 5 and not last:
                                dve.wait_ge(gated, it * UNITS + (s + 1) * UNITS // SLOTS)
                                dve.wait_ge(read, it * GROUPS * PIECES + (s + 1) * B * PIECES)
                                if s == 0:
                                    dve.wait_ge(pick_step, it * PICKS + 2 * PICKS)
                                fetch_gates(it + 1, s, it * SLOTS + SLOTS + s + 1)
                        for g, n in pieces_at(i, last):
                            take(it, g, n)
                    for c in range(B):
                        cols = slice(c * S, (c + 1) * S)
                        dve.wait_ge(x_high, c + 1)
                        nc.vector.tensor_tensor(x_lo[:, cols], T.LNT[:, cols], x_hi[:, cols], ALU.subtract).then_inc(x_low, 1)
                    dve.wait_ge(squashed, NT // 2)
                    for n in range(PICKS):
                        pick_gates(0, n)
                    dve.wait_ge(pick_step, PICKS)
                    for s in range(SLOTS):
                        fetch_gates(0, s, s + 1)
                    for g, n in START:
                        take(0, g, n)
                    turns(dve, step)
                    dve.wait_ge(added, TURNS * UNITS)

                @block.gpsimd
                def _(pool):
                    def split_weights(it, s, later):
                        pool.wait_ge(w_high, it * SLOTS + later * SLOTS + s + 1)
                        nc.gpsimd.tensor_tensor(w_lo[s][:, :], slot[s][:, 0:WV], w_hi[s][:, :], ALU.subtract).then_inc(w_low, 1)

                    def sum_experts(it, u, last):
                        g, n = divmod(u, UPG)
                        if u == SPLIT_1 + UPG:
                            split_weights(it, 1, 0)
                        if u == SPLIT_0 + UPG and not last:
                            split_weights(it, 0, 1)
                        for kind in range(2 if n == 0 else 0):
                            pool.wait_ge(qk_high, it * 2 * GROUPS + 2 * g + kind + 1)
                            nc.gpsimd.tensor_tensor(qk_lo[:, g % 2, kind, :], qk[:, kind, :], qk_hi[:, g % 2, kind, :],
                                                    ALU.subtract).then_inc(qk_low, 1)
                        pool.wait_ge(read, it * GROUPS * PIECES + g * PIECES + 4 + n + 1)
                        nc.gpsimd.tensor_tensor(vs[:, u % 2, :, :], vg[:, u % 2, 0:4, :], vg[:, u % 2, 4:8, :], ALU.add)\
                            .then_inc(v_step, 1)
                        pool.wait_ge(v_step, it * 2 * UNITS + 2 * u + 1)
                        nc.gpsimd.tensor_tensor(vs[:, u % 2, 0:2, :], vs[:, u % 2, 0:2, :], vs[:, u % 2, 2:4, :], ALU.add)\
                            .then_inc(v_step, 1)
                        pool.wait_ge(v_step, it * 2 * UNITS + 2 * u + 2)
                        if g >= 2 and n == 0:
                            pool.wait_ge(pv_done, it * UNITS + (g - 1) * UPG)
                        nc.gpsimd.tensor_tensor(v[:, g % 2, n, :], vs[:, u % 2, 0, :], vs[:, u % 2, 1, :], ALU.add)\
                            .then_inc(v_ready, 1)
                    split_weights(0, 0, 0)
                    for u in range(2 * UPG):
                        sum_experts(0, u, False)
                    with pool.Fori(0, TURNS - 1) as it:
                        for u in range(2 * UPG, 2 * UPG + UNITS):
                            sum_experts(it, u, False)
                    for u in range(2 * UPG, UNITS):
                        sum_experts(TURNS - 1, u, True)

        with Stage(nc, T, "l2f") as sf:
            w1 = sf.sb("w1", [P, F])
            w2 = sf.sb("w2", [P, 4, D])
            hid = sf.sb("hid", [P, 2, 4, S])
            names = ("loaded", "up_done", "hidden", "down_done", "added")
            w_loaded, up_done, hidden, down_done, added = (sf.sem(n) for n in names)
            layernorm(nc, T, T.LNX[:, :, :], T.LNX[:, :, :], T.LNT[:, :], [(w1[:, :], A["l2m_w1"]), (w2[:, :, :], A["l2m_w2"])],
                      w_loaded, ln1[:, 0, :], ln1[:, 1, :])
            with nc.Block() as block:
                @block.tensor
                def _(pe):
                    pe.wait_ge(w_loaded, 32)
                    for c in range(B + 1):
                        for f in range(4 if c < B else 0):
                            n = 4 * c + f
                            if n >= 4:
                                pe.wait_ge(hidden, n - 3)
                            nc.tensor.matmul(T.bank[f][:, :], w1[:, f * P:(f + 1) * P], T.LNT[:, c * S:(c + 1) * S],
                                             start=True, stop=True).then_inc(up_done, 1)
                        if c:
                            d = c - 1
                            pe.wait_ge(hidden, 4 * c)
                            if d >= 2:
                                pe.wait_ge(added, d - 1)
                            for t in range(TPB):
                                for f in range(4):
                                    last = nc.tensor.matmul(T.bank[4 + d % 2][:, t * D:(t + 1) * D],
                                                            hid[:, d % 2, f, t * P:(t + 1) * P], w2[:, f, :], start=(f == 0),
                                                            stop=(f == 3))
                            last.then_inc(down_done, 1)

                @block.scalar
                def _(act):
                    for n in range(4 * B):
                        c, f = divmod(n, 4)
                        act.wait_ge(up_done, n + 1)
                        if c >= 2:
                            act.wait_ge(down_done, c - 1)
                        nc.scalar.activation(hid[:, c % 2, f, :], T.bank[f][:, :], ACT.Relu, bias=b1[:, f:f + 1]).then_inc(hidden, 1)

                @block.vector
                def _(dve):
                    link = chain(T, dve)
                    link(nc.vector.tensor_tensor(T.LNX[:, :, :], T.LNX[:, :, :], tiled(b2[:, :], NT), ALU.add))
                    for c in range(B):
                        dve.wait_ge(down_done, c + 1)
                        x = T.LNX[:, c * TPB:(c + 1) * TPB, :]
                        nc.vector.tensor_tensor(x, x, T.bank[4 + c % 2][:, :].rearrange("p (t d) -> p t d", t=TPB), ALU.add)\
                            .then_inc(added, 1)
        layernorm(nc, T, T.LNX[:, :, :], T.LNX[:, :, :], T.LNT[:, :], gain=ln2[:, 0, :], shift=ln2[:, 1, :])
        with nc.Block() as block:
            @block.vector
            def _(dve):
                nc.vector.tensor_tensor(T.X[:, :, :], T.X[:, :, :], T.LNX[:, :, :], ALU.add)


def build(nc, A, out):
    T = Shared()
    T.dve_steps = T.ln_calls = T.ln_affine_calls = 0
    T.used = []
    with ExitStack() as ctx:
        def sb(name, shape, dt=F32):
            return ctx.enter_context(nc.sbuf_tensor(name, shape, dt))

        T.X = sb("X", [P, NT, D])
        T.LNX = sb("LNX", [P, NT, D])
        T.LNT = sb("LNT", [P, N])
        T.CTX = sb("CTX", [L, B, D])
        T.CTXT = sb("CTXT", [P, B * L])
        T.ident = sb("ident", [P, P])
        T.zeros = sb("zeros", [P, P])
        T.rev = sb("rev", [P, 64])
        T.ln_stats = sb("ln_stats", [P, NT, 6])
        T.ln_mv = sb("ln_mv", [P, NT, 2])
        T.ln_var_eps, T.ln_rstd, T.ln_shift = (sb(n, [P, NT]) for n in ("ln_var_eps", "ln_rstd", "ln_shift"))
        T.bank = [ctx.enter_context(nc.psum_tensor(f"bank{i}", [P, 512], F32)) for i in range(8)]
        T.dve_step, T.ln_var, T.ln_std, T.ln_scaled, T.ln_even, T.ln_odd, T.ln_affine, T.ln_turned, inputs, stored = (
            ctx.enter_context(nc.semaphore(n))
            for n in ("dve_step", "ln_var", "ln_std", "ln_scaled", "ln_even", "ln_odd", "ln_affine", "ln_turned", "inputs", "stored"))
        with nc.Block() as block:
            @block.sync
            def _(sp):
                for to, frm in ((T.X[:, :, :], A["x"]), (T.CTX[:, :, :], A["ctx"]), (T.CTXT[:, :], A["ctxT"]),
                                (T.ident[:, :], A["ident"]), (T.rev[:, :], A["rev"])):
                    sp.dma_start(to, frm).then_inc(inputs, 16)
                sp.wait_ge(inputs, 80)

            @block.vector
            def _(dve):
                nc.vector.memset(T.zeros[:, :], 0.0)

        stages = [
            lambda: l0_attention(nc, T, A),
            lambda: context_attention(nc, T, A, "l0x", H=1, dk=128, HB=1, biased=True),
            lambda: l0_moe(nc, T, A),
            lambda: l1_attention(nc, T, A),
            lambda: l1_coattention(nc, T, A),
            lambda: l1_moe(nc, T, A),
            lambda: l2_attention(nc, T, A),
            lambda: context_attention(nc, T, A, "l2x", H=4, dk=32, HB=4, rope=True, normed=True, keep_mask=True),
            lambda: l2_moe_attention(nc, T, A),
            lambda: l3_attention(nc, T, A),
            lambda: context_attention(nc, T, A, "l3x", H=16, dk=64, HB=4),
            lambda: l3_moe(nc, T, A),
        ]
        for n in STAGES:
            stages[n]()
        with nc.Block() as block:
            @block.sync
            def _(sp):
                sp.dma_start(out, T.X[:, :, :]).then_inc(stored, 16)
                sp.wait_ge(stored, 16)


def _rope_tables(positions, half, base):
    angle = positions[None, :].astype(np.float32) * (base ** (-np.arange(half, dtype=np.float32) / half))[:, None]
    return np.cos(angle.astype(np.float32)), np.sin(angle.astype(np.float32))


def _layouts(a):
    f = {}

    def rep(v, n=P):
        return np.broadcast_to(v.reshape(1, -1), (n, v.size))

    def tok(x):
        return x.reshape(NT, P, D).transpose(1, 0, 2)

    ctx = a["ctx_1024"]
    f["x"] = tok(a["x"])
    f["ctx"] = ctx.transpose(1, 0, 2)
    f["ctxT"] = ctx.transpose(2, 0, 1).reshape(D, B * L)
    f["ident"] = np.eye(P, dtype=np.float32)

    w, bias = a["L0_attn_W_attn"], a["L0_attn_b_attn"]

    def copies(m):
        z = np.broadcast_to(m.reshape(m.shape[:-1] + (8, 4, 1, 8)), m.shape[:-1] + (8, 4, 4, 8))
        return z.reshape(m.shape[:-1] + (8, 128))
    copy = np.arange(P) // 8 % 4
    low = np.stack([-(copy // 2), -(copy % 2)], axis=1).astype(np.float32)
    f["l0a_w"] = np.concatenate([copies(w[:, :256]).reshape(D, 1024), w[:, 256:]], axis=1)
    f["l0a_cols"] = np.concatenate([copies(bias[:256]).T, rep(a["L0_attn_temperature"]), low], axis=1)
    f["l0a_rows"] = np.concatenate([rep(bias[256:]), rep(a["L0_attn_b_proj"])], axis=1)
    f["l0a_wproj"] = a["L0_attn_W_proj"]
    u = np.arange(2 * S - P)[None, :] - (S - P) - np.arange(P)[:, None]
    f["rel"] = np.where(u <= 0, -u, BIG).astype(np.float32)

    f["l0x_wq"] = a["L0_xattn_Wq"].T.reshape(D, 1, 1, P)
    f["l0x_wk"] = a["L0_xattn_Wk"].T.reshape(D, 1, 1, P)
    f["l0x_wv"] = a["L0_xattn_Wv"].T.reshape(D, 1, P)
    f["l0x_wo"] = a["L0_xattn_Wo"].T.reshape(P, 1, D)
    f["l0x_cols"] = np.stack([a["L0_xattn_bq"], a["L0_xattn_bv"]], axis=1)
    f["l0x_rows"] = rep(a["L0_xattn_bo"])

    qw = a["L2_xattn_q_w"].transpose(1, 0, 2)
    kw = np.broadcast_to(a["L2_xattn_kv_w"][0, 0][:, None, :], (D, 4, 32))
    vw = np.broadcast_to(a["L2_xattn_kv_w"][1, 0][:, None, :], (D, 4, 32))

    def halves(m):
        return np.concatenate([m[..., 16:], m[..., :16]], axis=-1)
    f["l2x_wq"] = np.stack([qw.reshape(D, P), halves(qw).reshape(D, P)], axis=1).reshape(D, 2, 1, P)
    f["l2x_wk"] = np.stack([kw.reshape(D, P), halves(kw).reshape(D, P)], axis=1).reshape(D, 2, 1, P)
    f["l2x_wv"] = vw.reshape(D, 1, P)
    f["l2x_wo"] = a["L2_xattn_out_w"].reshape(P, 1, D)
    for n, pos in (("l2x_qtrig", np.arange(L, L + S)), ("l2x_ktrig", np.arange(L))):
        cos, sin = _rope_tables(pos, 16, 10000.0)
        f[n] = np.stack([np.tile(np.concatenate([cos, cos]), (4, 1)), np.tile(np.concatenate([-sin, sin]), (4, 1))], axis=1)
    f["l2x_gain"] = a["L2_xattn_rms_scale"].reshape(D, 1)
    f["l2x_keep"] = np.broadcast_to(a["mask_BxS2_bk0"].astype(np.int32)[None], (P, B, L))

    f["l3x_wq"] = a["L3_xattn_w_q"].reshape(D, 1, 8, P)
    f["l3x_wk"] = a["L3_xattn_w_k"].reshape(D, 1, 8, P)
    f["l3x_wv"] = a["L3_xattn_w_v"].reshape(D, 8, P)
    f["l3x_wo"] = a["L3_xattn_w_o"].reshape(8, P, D).transpose(1, 0, 2)

    def native(g, u, d):
        e = g.shape[0]
        def cols(m):
            return m.reshape(e // 2, 2, D, 64).transpose(0, 2, 1, 3).reshape(e // 2, D, P)
        return np.concatenate([cols(g), cols(u), d.reshape(e // 2, P, D)], axis=2)

    def turned(m):
        return m.transpose(0, 2, 1)
    f["rev"] = rep(np.arange(64, 0, -1, dtype=np.float32))
    f["tri"] = np.stack([np.triu(np.ones((P, P), np.float32), 1), np.ones((P, P), np.float32)], axis=1)
    f["l0m_router"] = a["L0_ffn_gate_w"].T
    f["l0m_bias"] = rep(a["L0_ffn_gate_bias"])
    f["l0m_pairs"] = native(turned(a["L0_ffn_Wg"]), turned(a["L0_ffn_Wu"]), turned(a["L0_ffn_Wd"]))
    f["l0m_shared"] = np.concatenate([a["L0_ffn_Ws_g"].T, a["L0_ffn_Ws_u"].T, a["L0_ffn_Ws_d"].T], axis=1).reshape(D, 1, 3 * P)
    f["l1m_router"] = a["L1_ffn_router_w"].T
    f["l1m_bias"] = rep(a["L1_ffn_e_bias"])
    f["l1m_pairs"] = native(a["L1_ffn_gate_w"], a["L1_ffn_up_w"], a["L1_ffn_down_w"])
    f["l1m_shared"] = np.stack([np.concatenate([a["L1_ffn_sh_gate_w"][:, s], a["L1_ffn_sh_up_w"][:, s],
                                                a["L1_ffn_sh_down_w"][s, :]], axis=1)
                                for s in (slice(0, P), slice(P, 2 * P))], axis=1)
    f["l3m_router"] = a["L3_ffn_gate_w"].T
    f["l3m_bias"] = rep(a["L3_ffn_bias"])
    f["l3m_pairs"] = native(a["L3_ffn_W1"], a["L3_ffn_W3"], a["L3_ffn_W2"])
    half = np.zeros((P, 1, 3 * P), f["l3m_pairs"].dtype)
    half[:, 0, 0:64] = a["L3_ffn_sw1"].T
    half[:, 0, P:P + 64] = a["L3_ffn_sw3"].T
    half[0:64, 0, 2 * P:3 * P] = a["L3_ffn_sw2"].T
    f["l3m_shared"] = half

    f["l1a_wq"] = a["L1_attn_wq"].T
    f["l1a_wkv"] = np.concatenate([a["L1_attn_wk"].T, a["L1_attn_wv"].T], axis=1)
    f["l1a_wo"] = a["L1_attn_wo"].T
    f["l1a_bo"] = rep(a["L1_attn_bo"])
    r = np.arange(P)
    f["l1a_same"] = np.concatenate([r[:, None] // 8 == r[None, :] // 8, r[:, None] // 8 == np.arange(16)[None, :]],
                                   axis=1).astype(np.float32)
    f["l1c_cols"] = np.concatenate([a["L1_xattn_w_sim"].reshape(3, D).T, rep(a["L1_xattn_b_sim"])], axis=1)
    f["l1c_w"] = a["L1_xattn_W_qv"].reshape(4, D, D).transpose(1, 0, 2)
    f["l1c_bias"] = rep(a["L1_xattn_b_qv"])

    f["l2a_w"] = a["L2_attn_W"]

    def pair_cols(m):
        return m.reshape(8, 2, D, 64).transpose(0, 2, 1, 3).reshape(8, D, P)

    def rotated_cols(m):
        return np.concatenate([m[..., 16:32], m[..., :16], m[..., 32:]], axis=-1)
    wq, wk = a["L2_ffn_Wq"], a["L2_ffn_Wk"]
    wv = a["L2_ffn_Wv"].transpose(0, 2, 1, 3).reshape(8, 2, D, 512).transpose(0, 2, 1, 3).reshape(8, D, 1024)
    wo = a["L2_ffn_Wo"].reshape(8, 2, 4, P, D).transpose(0, 3, 1, 2, 4).reshape(8, P, 1024)
    f["l2m_w"] = np.concatenate([pair_cols(wq), pair_cols(rotated_cols(wq)), pair_cols(wk), pair_cols(rotated_cols(wk)), wv, wo],
                                axis=2)
    f["l2m_wsel"] = np.concatenate([a["L2_ffn_Wsel_v"].reshape(P, D).T, a["L2_ffn_Wsel_o"].reshape(P, D).T], axis=1)
    cos, sin = _rope_tables(np.arange(S), 16, 10000.0)
    cos = np.tile(np.concatenate([cos, cos, np.ones((32, S), np.float32)]), (2, 1))
    sin = np.tile(np.concatenate([-sin, sin, np.zeros((32, S), np.float32)]), (2, 1))
    f["l2m_trig"] = np.stack([cos / 8, sin / 8, cos, sin], axis=1).astype(np.float32)
    for n in ("1", "2"):
        f["l2m_ln" + n] = np.stack([rep(a[f"L2_ffn_ln{n}_g"]), rep(a[f"L2_ffn_ln{n}_b"])], axis=1)
    f["l2m_w1"] = a["L2_ffn_W1"]
    f["l2m_b1"] = a["L2_ffn_b1"].reshape(4, P).T
    f["l2m_w2"] = a["L2_ffn_W2"].reshape(4, P, D).transpose(1, 0, 2)
    f["l2m_b2"] = rep(a["L2_ffn_b2"])

    f["l3a_w"] = np.concatenate([a["L3_attn_Wq"].T, a["L3_attn_Wk"].T, a["L3_attn_Wv"].T], axis=1)
    low = np.tril(np.ones((P, P), np.float32))
    f["tril"] = np.stack([low, (1 - low) * np.float32(1e-9)], axis=1)
    return {n: np.ascontiguousarray(v) for n, v in f.items()}


def kernel(**inputs):
    import concourse.bacc as bacc
    from concourse.bass_utils import run_bass_kernel_spmd

    arrays = _layouts({n: np.asarray(v) for n, v in inputs.items()})
    nc = bacc.Bacc("TRN2", target_bir_lowering=False, num_devices=1)
    A = {n: nc.dram_tensor(f"in_{n}", v.shape, mybir.dt.from_np(v.dtype), kind="ExternalInput").ap()
         for n, v in arrays.items()}
    out = nc.dram_tensor("out", (P, NT, D), F32, kind="ExternalOutput").ap()
    build(nc, A, out)
    r = run_bass_kernel_spmd(nc, [{f"in_{n}": v for n, v in arrays.items()}], core_ids=[0])
    return np.ascontiguousarray(r.results[0]["out"].transpose(1, 0, 2)).reshape(B, S, D)
```
